# Optimizing a Trainium2 kernel written in Bass

```python
import numpy as np
import jax
import jax.numpy as jnp

def _softmax(x, axis=-1):
    return jax.nn.softmax(x, axis=axis)

def _gelu(x):
    return jax.nn.gelu(x, approximate=True)

def _silu(x):
    return jax.nn.silu(x)

def _sigmoid(x):
    return jax.nn.sigmoid(x)

def _layernorm(x, axis=-1, eps=1e-05):
    m = jnp.mean(x, axis=axis, keepdims=True)
    v = jnp.var(x, axis=axis, keepdims=True)
    return (x - m) / jnp.sqrt(v + eps)

def _scatter_add(tgt, idx, src, axis=0):
    return tgt.at[idx].add(src)

def _segment_sum(src, seg, n):
    return jax.ops.segment_sum(src, seg, n)
kernel_name = 'mk_xattn_ffn_d4_seqx_r8_5d6018'

def setup_inputs(seed: int=0):
    np.random.seed(seed)
    _w = jnp.asarray

    def _rec_inputs():
        import jax
        import jax.numpy as jnp
        _rk = jax.random.key(seed)
        x = 7.22e-05 + 1 * jax.random.normal(jax.random.fold_in(_rk, 1), (2, 512, 128), jnp.float32)
        _lenS = 512 - jax.random.randint(jax.random.fold_in(_rk, 7), (2,), 0, max(1, 512 // 4) + 1, jnp.int32)
        _lenS2 = 77 - jax.random.randint(jax.random.fold_in(_rk, 8), (2,), 0, max(1, 77 // 4) + 1, jnp.int32)
        _ctx_768P = jax.random.normal(jax.random.fold_in(_rk, 11), (2, 16, 96), jnp.float32)
        _ctx_768c = jax.random.dirichlet(jax.random.fold_in(_rk, 511), 0.3 * jnp.ones((16,), jnp.float32), (2, 77))
        _ctx_768t = jnp.einsum('bsk,bkd->bsd', _ctx_768c, _ctx_768P)
        _ctx_768t = _ctx_768t * jax.lax.rsqrt(jnp.mean(jnp.square(_ctx_768t)) + 1e-12) * 0.953939
        ctx_768 = 3.88148e-05 + 0.999967 * (_ctx_768t + 0.3 * jax.random.normal(jax.random.fold_in(_rk, 611), (2, 77, 96), jnp.float32))
        _validS = jnp.arange(512)[None, :] < _lenS[:, None]
        _validS2 = jnp.arange(77)[None, :] < _lenS2[:, None]
        _causal = jnp.tril(jnp.ones((512, 512), dtype=bool))
        mask_BxS_bf1 = jnp.ones((2, 512), dtype=bool)
        mask_BxS2_bf1 = jnp.ones((2, 77), dtype=bool)
        mask_BxS2_bk0 = jnp.logical_not(jnp.broadcast_to(_validS2[:, :], (2, 77)))
        return (x, ctx_768, mask_BxS_bf1, mask_BxS2_bf1, mask_BxS2_bk0)
    x, ctx_768, mask_BxS_bf1, mask_BxS2_bf1, mask_BxS2_bk0 = _rec_inputs()

    def _L0_xattn_setup():
        import jax, jax.numpy as jnp
        import numpy as np
        B, T, DT, G, DV = (16, 64, 128, 72, 96)
        H, DH = (4, 32)
        INNER = H * DH
        HID = 4 * DT
        N_STATE = 64
        K_TOP = 32

        def layernorm(x, g, b, eps=1e-05):
            m = x.mean(-1, keepdims=True)
            v = x.var(-1, keepdims=True)
            return (x - m) * jax.lax.rsqrt(v + eps) * g + b

        def s4d(x, log_dt, A_re, A_im, C_re, C_im, D_skip):
            Bb, L, D = x.shape
            dt = jnp.exp(log_dt)
            A = A_re + 1j * A_im
            C = C_re + 1j * C_im
            dtA = dt[:, None] * A
            dC = C * (jnp.exp(dtA) - 1.0) / A
            powers = jnp.exp(dtA[:, :, None] * jnp.arange(L))
            K = 2.0 * jnp.einsum('dn,dnl->dl', dC, powers).real
            n = 2 * L
            Kf = jnp.fft.rfft(K, n=n, axis=-1)
            xf = jnp.fft.rfft(x, n=n, axis=1)
            y = jnp.fft.irfft(xf * Kf.T[None], n=n, axis=1)[:, :L]
            return y + x * D_skip
        key = jax.random.key(seed)
        ks = jax.random.split(key, 16)
        s = 0.02
        inp = {'x_text': jax.random.normal(ks[0], (B, T, DT), jnp.float32), 'x_vision': jax.random.normal(ks[1], (B, G, DV), jnp.float32), 'text_mask': jnp.ones((B, T), bool), 'vision_mask': jnp.ones((B, G), bool), 'Wq': jax.random.normal(ks[2], (DT, INNER), jnp.float32) * s, 'Wk': jax.random.normal(ks[3], (DV, INNER), jnp.float32) * s, 'Wv': jax.random.normal(ks[4], (DV, DT), jnp.float32) * s, 'W_film_in': jax.random.normal(ks[5], (DT, 2 * DT), jnp.float32) * s, 'b_film_in': jnp.zeros((2 * DT,), jnp.float32), 'W_film_out': jax.random.normal(ks[6], (DT, 2 * DT), jnp.float32) * s, 'b_film_out': jnp.zeros((2 * DT,), jnp.float32), 'g_norm_in': jnp.ones((DT,), jnp.float32), 'b_norm_in': jnp.zeros((DT,), jnp.float32), 'g_norm_out': jnp.ones((DT,), jnp.float32), 'b_norm_out': jnp.zeros((DT,), jnp.float32), 'g_ffn': jnp.ones((DT,), jnp.float32), 'b_ffn': jnp.zeros((DT,), jnp.float32), 'W1': jax.random.normal(ks[7], (DT, HID), jnp.float32) * s, 'b1': jnp.zeros((HID,), jnp.float32), 'W2': jax.random.normal(ks[8], (HID, DT), jnp.float32) * s, 'b2': jnp.zeros((DT,), jnp.float32), 'log_dt': jnp.log(0.001) + jax.random.uniform(ks[9], (DT,), jnp.float32) * (jnp.log(0.1) - jnp.log(0.001)), 'A_re': -0.5 * jnp.ones((DT, N_STATE), jnp.float32), 'A_im': jnp.tile(jnp.pi * jnp.arange(N_STATE, dtype=jnp.float32), (DT, 1)), 'C_re': jax.random.normal(ks[10], (DT, N_STATE), jnp.float32) * 0.5 ** 0.5, 'C_im': jax.random.normal(ks[11], (DT, N_STATE), jnp.float32) * 0.5 ** 0.5, 'D_skip': jax.random.normal(ks[12], (DT,), jnp.float32), 'mod_gate': jnp.array(0.5, jnp.float32)}
        return inp
    _L0_xattn_all = _L0_xattn_setup()
    _L0_xattn_in = {k: v for k, v in _L0_xattn_all.items() if k in ('Wq', 'Wk', 'Wv', 'W_film_in', 'b_film_in', 'W_film_out', 'b_film_out', 'g_norm_in', 'b_norm_in', 'g_norm_out', 'b_norm_out', 'g_ffn', 'b_ffn', 'W1', 'b1', 'W2', 'b2', 'log_dt', 'A_re', 'A_im', 'C_re', 'C_im', 'D_skip', 'mod_gate')}
    del _L0_xattn_all

    def _L0_ffn_setup():
        import jax, jax.numpy as jnp
        import numpy as np
        N_HEAD = 16
        N_ACTIVE = 4
        D_MODEL = 128
        D_ATTN = 64
        B = 4
        S = 256
        key = jax.random.key(seed)
        ks = jax.random.split(key, 6)
        sc = 1.0 / np.sqrt(D_MODEL).astype(np.float32)
        return {'x': jax.random.normal(ks[0], (B, S, D_MODEL), jnp.float32), 'Wq': jax.random.normal(ks[1], (D_MODEL, N_HEAD * D_ATTN), jnp.float32) * sc, 'bq': jnp.zeros((N_HEAD * D_ATTN,), jnp.float32), 'Wk': jax.random.normal(ks[2], (D_MODEL, N_HEAD * D_ATTN), jnp.float32) * sc, 'bk': jnp.zeros((N_HEAD * D_ATTN,), jnp.float32), 'Wv': jax.random.normal(ks[3], (D_MODEL, N_HEAD * D_ATTN), jnp.float32) * sc, 'bv': jnp.zeros((N_HEAD * D_ATTN,), jnp.float32), 'Wr': jax.random.normal(ks[4], (D_MODEL, N_HEAD), jnp.float32) * sc, 'br': jnp.zeros((N_HEAD,), jnp.float32), 'Wo': jax.random.normal(ks[5], (N_ACTIVE * D_ATTN, D_MODEL), jnp.float32) * (1.0 / np.sqrt(N_ACTIVE * D_ATTN).astype(np.float32)), 'bo': jnp.zeros((D_MODEL,), jnp.float32)}
    _L0_ffn_all = _L0_ffn_setup()
    _L0_ffn_in = {k: v for k, v in _L0_ffn_all.items() if k in ('Wq', 'bq', 'Wk', 'bk', 'Wv', 'bv', 'Wr', 'br', 'Wo', 'bo')}
    del _L0_ffn_all

    def _L1_xattn_setup():
        import jax, jax.numpy as jnp
        import numpy as np
        EPS = 1e-05
        key = jax.random.key(seed)
        ks = jax.random.split(key, 6)
        B, Nq, Nk, Dq, Dk = (16, 256, 256, 128, 96)
        s = lambda d: 1.0 / np.sqrt(d)
        return {'q': jax.random.normal(ks[0], (B, Nq, Dq), dtype=jnp.float32), 'k': jax.random.normal(ks[1], (B, Nk, Dk), dtype=jnp.float32), 'Wq': jax.random.normal(ks[2], (Dq, Dq), dtype=jnp.float32) * s(Dq), 'Wk': jax.random.normal(ks[3], (Dq, Dk), dtype=jnp.float32) * s(Dk), 'Wv': jax.random.normal(ks[4], (Dq, Dk), dtype=jnp.float32) * s(Dk), 'Wo': jax.random.normal(ks[5], (Dq, Dq), dtype=jnp.float32) * s(Dq)}
    _L1_xattn_all = _L1_xattn_setup()
    _L1_xattn_in = {k: v for k, v in _L1_xattn_all.items() if k in ('Wq', 'Wk', 'Wv', 'Wo')}
    del _L1_xattn_all

    def _L1_ffn_setup():
        import jax, jax.numpy as jnp
        import numpy as np
        D_MODEL = 128
        NUM_TILES = 64
        TPC = 8
        NUM_CLUSTERS = NUM_TILES // TPC
        GRID = 16
        COMP_H = 32
        NUM_KNOTS = 8
        EPS_LN = 1e-05

        def _calibrate(scores, knots, temperature):
            K = knots.shape[0]
            normalized = jax.nn.sigmoid(scores / (temperature[0] + 1e-06))
            idx_float = normalized * (K - 1)
            idx_low = jnp.clip(idx_float.astype(jnp.int32), 0, K - 2)
            idx_high = idx_low + 1
            t = idx_float - idx_low.astype(scores.dtype)
            val_low = knots[idx_low]
            val_high = knots[idx_high]
            return val_low + t * (val_high - val_low)

        def _forward(x, signatures_raw, knot_values, temperature, compress_w1, compress_b1, compress_w2, compress_b2, spline_w1, spline_b1, spline_w2, spline_b2, directions, norm_gamma, norm_beta, output_scale):
            B, T, D = x.shape
            xf = x.reshape(-1, D)
            q = jnp.where(signatures_raw > 0.3, 1.0, jnp.where(signatures_raw < -0.3, -1.0, 0.0)).astype(signatures_raw.dtype)
            sigs = signatures_raw + jax.lax.stop_gradient(q - signatures_raw)
            cluster_sigs = jnp.sign(sigs.reshape(NUM_CLUSTERS, TPC, D).mean(axis=1))
            cluster_scores = xf @ cluster_sigs.T
            cluster_gates = _calibrate(cluster_scores, knot_values, temperature)
            cluster_idx = jnp.argmax(cluster_gates, axis=-1)
            tile_scores = xf @ sigs.T
            tile_gates = _calibrate(tile_scores, knot_values, temperature)
            gates_by_cluster = tile_gates.reshape(-1, NUM_CLUSTERS, TPC)
            sel_gates = jnp.take_along_axis(gates_by_cluster, cluster_idx[:, None, None], axis=1)[:, 0, :]
            local_idx = jnp.argmax(sel_gates, axis=-1)
            tile_idx = cluster_idx * TPC + local_idx
            h = jax.nn.gelu(xf @ compress_w1 + compress_b1, approximate=False)
            comp = jnp.tanh(h @ compress_w2 + compress_b2)
            w1 = spline_w1[tile_idx]
            b1 = spline_b1[tile_idx]
            hh = jax.nn.relu(jnp.einsum('ni,nig->ng', comp, w1) + b1)
            w2 = spline_w2[tile_idx]
            b2 = spline_b2[tile_idx]
            mag = jnp.einsum('ng,ngo->no', hh, w2) + b2
            ffn_out = mag * directions[tile_idx] * output_scale[0]
            y = xf + ffn_out
            mu = y.mean(axis=-1, keepdims=True)
            var = ((y - mu) ** 2).mean(axis=-1, keepdims=True)
            y = (y - mu) / jnp.sqrt(var + EPS_LN) * norm_gamma + norm_beta
            return y.reshape(B, T, D)
        key = jax.random.key(seed)
        ks = jax.random.split(key, 12)
        B, T = (4, 512)
        x = jax.random.normal(ks[0], (B, T, D_MODEL), dtype=jnp.float32)
        signatures_raw = jax.random.normal(ks[1], (NUM_TILES, D_MODEL), dtype=jnp.float32) * 0.5
        knot_values = jax.nn.sigmoid(jnp.linspace(-3.0, 3.0, NUM_KNOTS).astype(jnp.float32))
        temperature = jnp.ones((1,), dtype=jnp.float32)
        compress_w1 = jax.random.normal(ks[2], (D_MODEL, COMP_H), dtype=jnp.float32) * (1.0 / np.sqrt(D_MODEL))
        compress_b1 = jnp.zeros((COMP_H,), dtype=jnp.float32)
        compress_w2 = jax.random.normal(ks[3], (COMP_H, 2), dtype=jnp.float32) * (1.0 / np.sqrt(COMP_H))
        compress_b2 = jnp.zeros((2,), dtype=jnp.float32)
        spline_w1 = jax.random.normal(ks[4], (NUM_TILES, 2, GRID), dtype=jnp.float32) * (1.0 / np.sqrt(2.0))
        spline_b1 = jnp.zeros((NUM_TILES, GRID), dtype=jnp.float32)
        spline_w2 = jax.random.normal(ks[5], (NUM_TILES, GRID, 1), dtype=jnp.float32) * (1.0 / np.sqrt(GRID))
        spline_b2 = jnp.zeros((NUM_TILES, 1), dtype=jnp.float32)
        directions = jax.random.normal(ks[6], (NUM_TILES, D_MODEL), dtype=jnp.float32) * 0.02
        norm_gamma = jnp.ones((D_MODEL,), dtype=jnp.float32)
        norm_beta = jnp.zeros((D_MODEL,), dtype=jnp.float32)
        output_scale = jnp.ones((1,), dtype=jnp.float32) * 0.1
        return dict(x=x, signatures_raw=signatures_raw, knot_values=knot_values, temperature=temperature, compress_w1=compress_w1, compress_b1=compress_b1, compress_w2=compress_w2, compress_b2=compress_b2, spline_w1=spline_w1, spline_b1=spline_b1, spline_w2=spline_w2, spline_b2=spline_b2, directions=directions, norm_gamma=norm_gamma, norm_beta=norm_beta, output_scale=output_scale)
    _L1_ffn_all = _L1_ffn_setup()
    _L1_ffn_in = {k: v for k, v in _L1_ffn_all.items() if k in ('signatures_raw', 'knot_values', 'temperature', 'compress_w1', 'compress_b1', 'compress_w2', 'compress_b2', 'spline_w1', 'spline_b1', 'spline_w2', 'spline_b2', 'directions', 'norm_gamma', 'norm_beta', 'output_scale')}
    del _L1_ffn_all

    def _L2_xattn_setup():
        import jax, jax.numpy as jnp
        import numpy as np
        DIM_IN, DIM_LAT, DIM_HEAD = (96, 128, 64)
        INNER = max(DIM_LAT, DIM_IN)
        HEADS = INNER // DIM_HEAD
        SCALE = DIM_HEAD ** (-0.5)
        RMS_EPS = 1e-08
        LN_EPS = 1e-05

        def layernorm(x, g, b):
            mu = jnp.mean(x, axis=-1, keepdims=True)
            var = jnp.mean((x - mu) ** 2, axis=-1, keepdims=True)
            return (x - mu) * jax.lax.rsqrt(var + LN_EPS) * g + b

        def rmsnorm(x, gamma):
            norm = jnp.sqrt(jnp.sum(x * x, axis=-1, keepdims=True)) * x.shape[-1] ** (-0.5)
            return x / jnp.maximum(norm, RMS_EPS) * gamma
        key = jax.random.key(seed)
        ks = jax.random.split(key, 12)
        b, n, m = (4, 512, 64)
        x = jax.random.normal(ks[0], (b, n, DIM_IN), jnp.float32)
        latents = jax.random.normal(ks[1], (b, m, DIM_LAT), jnp.float32)
        mask = jax.random.randint(ks[2], (b, n), 0, 2).astype(bool)
        s = lambda k, sh, fan: jax.random.normal(k, sh, jnp.float32) * fan ** (-0.5)
        return {'x': x, 'latents': latents, 'mask': mask, 'ln_x_g': jnp.ones((DIM_IN,), jnp.float32), 'ln_x_b': jnp.zeros((DIM_IN,), jnp.float32), 'ln_l_g': jnp.ones((DIM_LAT,), jnp.float32), 'ln_l_b': jnp.zeros((DIM_LAT,), jnp.float32), 'qn_g': jnp.ones((DIM_HEAD,), jnp.float32), 'kn_g': jnp.ones((DIM_HEAD,), jnp.float32), 'Wq': s(ks[3], (INNER, DIM_LAT), DIM_LAT), 'Wkv': s(ks[4], (2 * INNER, DIM_IN), DIM_IN), 'Wlkv': s(ks[5], (2 * INNER, DIM_LAT), DIM_LAT), 'Wo': s(ks[6], (DIM_LAT, INNER), INNER), 'bo': jnp.zeros((DIM_LAT,), jnp.float32)}
    _L2_xattn_all = _L2_xattn_setup()
    _L2_xattn_in = {k: v for k, v in _L2_xattn_all.items() if k in ('ln_x_g', 'ln_x_b', 'ln_l_g', 'ln_l_b', 'qn_g', 'kn_g', 'Wq', 'Wkv', 'Wlkv', 'Wo', 'bo')}
    del _L2_xattn_all

    def _L2_ffn_setup():
        import jax, jax.numpy as jnp
        import numpy as np
        B, S, DIM = (2, 256, 128)
        HID = 256
        E, NSH, TOPK = (8, 2, 2)

        def _ffn(x, w1, w2, w3):
            return jax.nn.silu(x @ w1.T) * (x @ w3.T) @ w2.T
        key = jax.random.key(seed)
        ks = jax.random.split(key, 8)
        sc = 0.02
        return {'x': jax.random.normal(ks[0], (B, S, DIM), jnp.float32), 'router_w': jax.random.normal(ks[1], (E, DIM), jnp.float32) * sc, 'expert_bias': jnp.zeros((E,), jnp.float32), 'w1': jax.random.normal(ks[2], (E, HID, DIM), jnp.float32) * sc, 'w3': jax.random.normal(ks[3], (E, HID, DIM), jnp.float32) * sc, 'w2': jax.random.normal(ks[4], (E, DIM, HID), jnp.float32) * sc, 'sw1': jax.random.normal(ks[5], (NSH, HID, DIM), jnp.float32) * sc, 'sw3': jax.random.normal(ks[6], (NSH, HID, DIM), jnp.float32) * sc, 'sw2': jax.random.normal(ks[7], (NSH, DIM, HID), jnp.float32) * sc}
    _L2_ffn_all = _L2_ffn_setup()
    _L2_ffn_in = {k: v for k, v in _L2_ffn_all.items() if k in ('router_w', 'expert_bias', 'w1', 'w3', 'w2', 'sw1', 'sw3', 'sw2')}
    del _L2_ffn_all

    def _L3_xattn_setup():
        import jax, jax.numpy as jnp
        import numpy as np
        HEADS = 16
        DIM_HEAD = 64
        SCALE = DIM_HEAD ** (-0.5)
        QUERY_DIM = 128
        CONTEXT_DIM = 96
        INNER_DIM = HEADS * DIM_HEAD
        key = jax.random.key(seed)
        ks = jax.random.split(key, 7)
        B, Nq, Nk = (8, 512, 77)
        x = jax.random.normal(ks[0], (B, Nq, QUERY_DIM), dtype=jnp.float32)
        context = jax.random.normal(ks[1], (B, Nk, CONTEXT_DIM), dtype=jnp.float32)
        Wq = jax.random.normal(ks[2], (QUERY_DIM, INNER_DIM), dtype=jnp.float32) * QUERY_DIM ** (-0.5)
        Wk = jax.random.normal(ks[3], (CONTEXT_DIM, INNER_DIM), dtype=jnp.float32) * CONTEXT_DIM ** (-0.5)
        Wv = jax.random.normal(ks[4], (CONTEXT_DIM, INNER_DIM), dtype=jnp.float32) * CONTEXT_DIM ** (-0.5)
        Wo = jax.random.normal(ks[5], (INNER_DIM, QUERY_DIM), dtype=jnp.float32) * INNER_DIM ** (-0.5)
        bo = jnp.zeros((QUERY_DIM,), dtype=jnp.float32)
        return {'x': x, 'context': context, 'Wq': Wq, 'Wk': Wk, 'Wv': Wv, 'Wo': Wo, 'bo': bo}
    _L3_xattn_all = _L3_xattn_setup()
    _L3_xattn_in = {k: v for k, v in _L3_xattn_all.items() if k in ('Wq', 'Wk', 'Wv', 'Wo', 'bo')}
    del _L3_xattn_all

    def _L3_ffn_setup():
        import jax, jax.numpy as jnp
        import numpy as np
        EPS = 1e-06
        LN_EPS = 1e-05

        def _absmean_core(W):
            gamma = jnp.mean(jnp.abs(W)) + EPS
            Ws = W / gamma
            Wq = jnp.sign(Ws) * jnp.minimum(jnp.round(jnp.abs(Ws)), 1.0)
            return (Wq, gamma)

        @jax.custom_vjp
        def absmean(W):
            return _absmean_core(W)[0]

        def _absmean_fwd(W):
            Wq, gamma = _absmean_core(W)
            return (Wq, gamma)

        def _absmean_bwd(gamma, g):
            return (g / gamma,)
        absmean.defvjp(_absmean_fwd, _absmean_bwd)

        def layernorm(x, w, b, eps=LN_EPS):
            mu = jnp.mean(x, axis=-1, keepdims=True)
            var = jnp.mean((x - mu) ** 2, axis=-1, keepdims=True)
            return (x - mu) * jax.lax.rsqrt(var + eps) * w + b
        key = jax.random.key(seed)
        k1, k2, k3 = jax.random.split(key, 3)
        d, h = (128, 512)
        B, T = (8, 256)
        return {'x': jax.random.normal(k1, (B, T, d), jnp.float32), 'W_fc': jax.random.normal(k2, (h, d), jnp.float32), 'ln_w': jnp.ones((h,), jnp.float32), 'ln_b': jnp.zeros((h,), jnp.float32), 'W_proj': jax.random.normal(k3, (d, h), jnp.float32)}
    _L3_ffn_all = _L3_ffn_setup()
    _L3_ffn_in = {k: v for k, v in _L3_ffn_all.items() if k in ('W_fc', 'ln_w', 'ln_b', 'W_proj')}
    del _L3_ffn_all
    return {'x': x, 'ctx_768': ctx_768, 'mask_BxS_bf1': mask_BxS_bf1, 'mask_BxS2_bf1': mask_BxS2_bf1, 'mask_BxS2_bk0': mask_BxS2_bk0, 'L0_xattn_Wq': _L0_xattn_in['Wq'], 'L0_xattn_Wk': _L0_xattn_in['Wk'], 'L0_xattn_Wv': _L0_xattn_in['Wv'], 'L0_xattn_W_film_in': _L0_xattn_in['W_film_in'], 'L0_xattn_b_film_in': _L0_xattn_in['b_film_in'], 'L0_xattn_W_film_out': _L0_xattn_in['W_film_out'], 'L0_xattn_b_film_out': _L0_xattn_in['b_film_out'], 'L0_xattn_g_norm_in': _L0_xattn_in['g_norm_in'], 'L0_xattn_b_norm_in': _L0_xattn_in['b_norm_in'], 'L0_xattn_g_norm_out': _L0_xattn_in['g_norm_out'], 'L0_xattn_b_norm_out': _L0_xattn_in['b_norm_out'], 'L0_xattn_g_ffn': _L0_xattn_in['g_ffn'], 'L0_xattn_b_ffn': _L0_xattn_in['b_ffn'], 'L0_xattn_W1': _L0_xattn_in['W1'], 'L0_xattn_b1': _L0_xattn_in['b1'], 'L0_xattn_W2': _L0_xattn_in['W2'], 'L0_xattn_b2': _L0_xattn_in['b2'], 'L0_xattn_log_dt': _L0_xattn_in['log_dt'], 'L0_xattn_A_re': _L0_xattn_in['A_re'], 'L0_xattn_A_im': _L0_xattn_in['A_im'], 'L0_xattn_C_re': _L0_xattn_in['C_re'], 'L0_xattn_C_im': _L0_xattn_in['C_im'], 'L0_xattn_D_skip': _L0_xattn_in['D_skip'], 'L0_xattn_mod_gate': _L0_xattn_in['mod_gate'], 'L0_ffn_Wq': _L0_ffn_in['Wq'], 'L0_ffn_bq': _L0_ffn_in['bq'], 'L0_ffn_Wk': _L0_ffn_in['Wk'], 'L0_ffn_bk': _L0_ffn_in['bk'], 'L0_ffn_Wv': _L0_ffn_in['Wv'], 'L0_ffn_bv': _L0_ffn_in['bv'], 'L0_ffn_Wr': _L0_ffn_in['Wr'], 'L0_ffn_br': _L0_ffn_in['br'], 'L0_ffn_Wo': _L0_ffn_in['Wo'], 'L0_ffn_bo': _L0_ffn_in['bo'], 'L1_xattn_Wq': _L1_xattn_in['Wq'], 'L1_xattn_Wk': _L1_xattn_in['Wk'], 'L1_xattn_Wv': _L1_xattn_in['Wv'], 'L1_xattn_Wo': _L1_xattn_in['Wo'], 'L1_ffn_signatures_raw': _L1_ffn_in['signatures_raw'], 'L1_ffn_knot_values': _L1_ffn_in['knot_values'], 'L1_ffn_temperature': _L1_ffn_in['temperature'], 'L1_ffn_compress_w1': _L1_ffn_in['compress_w1'], 'L1_ffn_compress_b1': _L1_ffn_in['compress_b1'], 'L1_ffn_compress_w2': _L1_ffn_in['compress_w2'], 'L1_ffn_compress_b2': _L1_ffn_in['compress_b2'], 'L1_ffn_spline_w1': _L1_ffn_in['spline_w1'], 'L1_ffn_spline_b1': _L1_ffn_in['spline_b1'], 'L1_ffn_spline_w2': _L1_ffn_in['spline_w2'], 'L1_ffn_spline_b2': _L1_ffn_in['spline_b2'], 'L1_ffn_directions': _L1_ffn_in['directions'], 'L1_ffn_norm_gamma': _L1_ffn_in['norm_gamma'], 'L1_ffn_norm_beta': _L1_ffn_in['norm_beta'], 'L1_ffn_output_scale': _L1_ffn_in['output_scale'], 'L2_xattn_ln_x_g': _L2_xattn_in['ln_x_g'], 'L2_xattn_ln_x_b': _L2_xattn_in['ln_x_b'], 'L2_xattn_ln_l_g': _L2_xattn_in['ln_l_g'], 'L2_xattn_ln_l_b': _L2_xattn_in['ln_l_b'], 'L2_xattn_qn_g': _L2_xattn_in['qn_g'], 'L2_xattn_kn_g': _L2_xattn_in['kn_g'], 'L2_xattn_Wq': _L2_xattn_in['Wq'], 'L2_xattn_Wkv': _L2_xattn_in['Wkv'], 'L2_xattn_Wlkv': _L2_xattn_in['Wlkv'], 'L2_xattn_Wo': _L2_xattn_in['Wo'], 'L2_xattn_bo': _L2_xattn_in['bo'], 'L2_ffn_router_w': _L2_ffn_in['router_w'], 'L2_ffn_expert_bias': _L2_ffn_in['expert_bias'], 'L2_ffn_w1': _L2_ffn_in['w1'], 'L2_ffn_w3': _L2_ffn_in['w3'], 'L2_ffn_w2': _L2_ffn_in['w2'], 'L2_ffn_sw1': _L2_ffn_in['sw1'], 'L2_ffn_sw3': _L2_ffn_in['sw3'], 'L2_ffn_sw2': _L2_ffn_in['sw2'], 'L3_xattn_Wq': _L3_xattn_in['Wq'], 'L3_xattn_Wk': _L3_xattn_in['Wk'], 'L3_xattn_Wv': _L3_xattn_in['Wv'], 'L3_xattn_Wo': _L3_xattn_in['Wo'], 'L3_xattn_bo': _L3_xattn_in['bo'], 'L3_ffn_W_fc': _L3_ffn_in['W_fc'], 'L3_ffn_ln_w': _L3_ffn_in['ln_w'], 'L3_ffn_ln_b': _L3_ffn_in['ln_b'], 'L3_ffn_W_proj': _L3_ffn_in['W_proj']}

def reference(x, ctx_768, mask_BxS_bf1, mask_BxS2_bf1, mask_BxS2_bk0, L0_xattn_Wq, L0_xattn_Wk, L0_xattn_Wv, L0_xattn_W_film_in, L0_xattn_b_film_in, L0_xattn_W_film_out, L0_xattn_b_film_out, L0_xattn_g_norm_in, L0_xattn_b_norm_in, L0_xattn_g_norm_out, L0_xattn_b_norm_out, L0_xattn_g_ffn, L0_xattn_b_ffn, L0_xattn_W1, L0_xattn_b1, L0_xattn_W2, L0_xattn_b2, L0_xattn_log_dt, L0_xattn_A_re, L0_xattn_A_im, L0_xattn_C_re, L0_xattn_C_im, L0_xattn_D_skip, L0_xattn_mod_gate, L0_ffn_Wq, L0_ffn_bq, L0_ffn_Wk, L0_ffn_bk, L0_ffn_Wv, L0_ffn_bv, L0_ffn_Wr, L0_ffn_br, L0_ffn_Wo, L0_ffn_bo, L1_xattn_Wq, L1_xattn_Wk, L1_xattn_Wv, L1_xattn_Wo, L1_ffn_signatures_raw, L1_ffn_knot_values, L1_ffn_temperature, L1_ffn_compress_w1, L1_ffn_compress_b1, L1_ffn_compress_w2, L1_ffn_compress_b2, L1_ffn_spline_w1, L1_ffn_spline_b1, L1_ffn_spline_w2, L1_ffn_spline_b2, L1_ffn_directions, L1_ffn_norm_gamma, L1_ffn_norm_beta, L1_ffn_output_scale, L2_xattn_ln_x_g, L2_xattn_ln_x_b, L2_xattn_ln_l_g, L2_xattn_ln_l_b, L2_xattn_qn_g, L2_xattn_kn_g, L2_xattn_Wq, L2_xattn_Wkv, L2_xattn_Wlkv, L2_xattn_Wo, L2_xattn_bo, L2_ffn_router_w, L2_ffn_expert_bias, L2_ffn_w1, L2_ffn_w3, L2_ffn_w2, L2_ffn_sw1, L2_ffn_sw3, L2_ffn_sw2, L3_xattn_Wq, L3_xattn_Wk, L3_xattn_Wv, L3_xattn_Wo, L3_xattn_bo, L3_ffn_W_fc, L3_ffn_ln_w, L3_ffn_ln_b, L3_ffn_W_proj):
    import jax
    import jax.numpy as jnp

    def _L0_xattn_ref(x_text, x_vision, text_mask, vision_mask, Wq, Wk, Wv, W_film_in, b_film_in, W_film_out, b_film_out, g_norm_in, b_norm_in, g_norm_out, b_norm_out, g_ffn, b_ffn, W1, b1, W2, b2, log_dt, A_re, A_im, C_re, C_im, D_skip, mod_gate):
        import jax, jax.numpy as jnp
        import numpy as np
        B, T, DT, G, DV = (16, 64, 128, 72, 96)
        H, DH = (4, 32)
        INNER = H * DH
        HID = 4 * DT
        N_STATE = 64
        K_TOP = 32

        def layernorm(x, g, b, eps=1e-05):
            m = x.mean(-1, keepdims=True)
            v = x.var(-1, keepdims=True)
            return (x - m) * jax.lax.rsqrt(v + eps) * g + b

        def s4d(x, log_dt, A_re, A_im, C_re, C_im, D_skip):
            Bb, L, D = x.shape
            dt = jnp.exp(log_dt)
            A = A_re + 1j * A_im
            C = C_re + 1j * C_im
            dtA = dt[:, None] * A
            dC = C * (jnp.exp(dtA) - 1.0) / A
            powers = jnp.exp(dtA[:, :, None] * jnp.arange(L))
            K = 2.0 * jnp.einsum('dn,dnl->dl', dC, powers).real
            n = 2 * L
            Kf = jnp.fft.rfft(K, n=n, axis=-1)
            xf = jnp.fft.rfft(x, n=n, axis=1)
            y = jnp.fft.irfft(xf * Kf.T[None], n=n, axis=1)[:, :L]
            return y + x * D_skip
        Bb, Tt, D = x_text.shape
        Gg = x_vision.shape[1]
        Q = (x_text @ Wq).reshape(Bb, Tt, H, DH)
        K = (x_vision @ Wk).reshape(Bb, Gg, H, DH)
        scores = jnp.einsum('bthd,bghd->bhtg', Q, K) / np.sqrt(DH).astype(np.float32)
        scores = jnp.where(vision_mask[:, None, None, :], scores, -jnp.inf)
        topv, topi = jax.lax.top_k(scores, K_TOP)
        probs = jax.nn.softmax(topv, axis=-1)
        bi = jnp.arange(Bb)[:, None, None, None]
        hi = jnp.arange(H)[None, :, None, None]
        ti = jnp.arange(Tt)[None, None, :, None]
        attn = jnp.zeros_like(scores).at[bi, hi, ti, topi].set(probs)
        attn_mean = attn.mean(axis=1)
        V = x_vision @ Wv
        c_t = jnp.einsum('btg,bgd->btd', attn_mean, V)
        c_t = c_t * text_mask[..., None]
        x = layernorm(x_text, g_norm_in, b_norm_in)
        scale_in, shift_in = jnp.split(c_t @ W_film_in + b_film_in, 2, axis=-1)
        x = x * (1.0 + mod_gate * scale_in) + mod_gate * shift_in
        y = s4d(x, log_dt, A_re, A_im, C_re, C_im, D_skip)
        scale_out, shift_out = jnp.split(c_t @ W_film_out + b_film_out, 2, axis=-1)
        y = y * (1.0 + mod_gate * scale_out) + mod_gate * shift_out
        xt = x_text + y
        h = layernorm(xt, g_ffn, b_ffn)
        h = jax.nn.gelu(h @ W1 + b1, approximate=False) @ W2 + b2
        xt = xt + h
        return layernorm(xt, g_norm_out, b_norm_out)

    def _L0_ffn_ref(x, Wq, bq, Wk, bk, Wv, bv, Wr, br, Wo, bo):
        import jax, jax.numpy as jnp
        import numpy as np
        N_HEAD = 16
        N_ACTIVE = 4
        D_MODEL = 128
        D_ATTN = 64
        B = 4
        S = 256
        b, s, _ = x.shape
        dist = jax.nn.softmax(jnp.mean(x @ Wr + br, axis=1), axis=-1)
        _, idx = jax.lax.top_k(dist, N_ACTIVE)
        idx = jnp.sort(idx, axis=-1)

        def proj(W, bias):
            return (x @ W + bias).reshape(b, s, N_HEAD, D_ATTN).transpose(0, 2, 1, 3)
        Q = proj(Wq, bq)
        K = proj(Wk, bk)
        V = proj(Wv, bv)
        gather = lambda t: jnp.take_along_axis(t, idx[:, :, None, None], axis=1)
        Qs, Ks, Vs = (gather(Q), gather(K), gather(V))
        scale = 1.0 / jnp.sqrt(jnp.asarray(D_ATTN, x.dtype))
        score = jax.nn.softmax(jnp.einsum('bhqd,bhkd->bhqk', Qs, Ks) * scale, axis=-1)
        O = jnp.einsum('bhqk,bhkd->bhqd', score, Vs)
        O = O.transpose(0, 2, 1, 3).reshape(b, s, N_ACTIVE * D_ATTN)
        return O @ Wo + bo

    def _L1_xattn_ref(q, k, Wq, Wk, Wv, Wo):
        import jax, jax.numpy as jnp
        import numpy as np
        EPS = 1e-05
        query = q @ Wq.T
        key_p = k @ Wk.T
        value = k @ Wv.T
        sim = jnp.einsum('bqd,bkd->bqk', query, key_p)
        mean = jnp.mean(sim, axis=(1, 2), keepdims=True)
        var = jnp.var(sim, axis=(1, 2), keepdims=True)
        sim = (sim - mean) * jax.lax.rsqrt(var + EPS)
        attn = jax.nn.softmax(sim, axis=-1)
        out = jnp.einsum('bqk,bkd->bqd', attn, value)
        return out @ Wo.T

    def _L1_ffn_ref(x, signatures_raw, knot_values, temperature, compress_w1, compress_b1, compress_w2, compress_b2, spline_w1, spline_b1, spline_w2, spline_b2, directions, norm_gamma, norm_beta, output_scale):
        import jax, jax.numpy as jnp
        import numpy as np
        D_MODEL = 128
        NUM_TILES = 64
        TPC = 8
        NUM_CLUSTERS = NUM_TILES // TPC
        GRID = 16
        COMP_H = 32
        NUM_KNOTS = 8
        EPS_LN = 1e-05

        def _calibrate(scores, knots, temperature):
            K = knots.shape[0]
            normalized = jax.nn.sigmoid(scores / (temperature[0] + 1e-06))
            idx_float = normalized * (K - 1)
            idx_low = jnp.clip(idx_float.astype(jnp.int32), 0, K - 2)
            idx_high = idx_low + 1
            t = idx_float - idx_low.astype(scores.dtype)
            val_low = knots[idx_low]
            val_high = knots[idx_high]
            return val_low + t * (val_high - val_low)

        def _forward(x, signatures_raw, knot_values, temperature, compress_w1, compress_b1, compress_w2, compress_b2, spline_w1, spline_b1, spline_w2, spline_b2, directions, norm_gamma, norm_beta, output_scale):
            B, T, D = x.shape
            xf = x.reshape(-1, D)
            q = jnp.where(signatures_raw > 0.3, 1.0, jnp.where(signatures_raw < -0.3, -1.0, 0.0)).astype(signatures_raw.dtype)
            sigs = signatures_raw + jax.lax.stop_gradient(q - signatures_raw)
            cluster_sigs = jnp.sign(sigs.reshape(NUM_CLUSTERS, TPC, D).mean(axis=1))
            cluster_scores = xf @ cluster_sigs.T
            cluster_gates = _calibrate(cluster_scores, knot_values, temperature)
            cluster_idx = jnp.argmax(cluster_gates, axis=-1)
            tile_scores = xf @ sigs.T
            tile_gates = _calibrate(tile_scores, knot_values, temperature)
            gates_by_cluster = tile_gates.reshape(-1, NUM_CLUSTERS, TPC)
            sel_gates = jnp.take_along_axis(gates_by_cluster, cluster_idx[:, None, None], axis=1)[:, 0, :]
            local_idx = jnp.argmax(sel_gates, axis=-1)
            tile_idx = cluster_idx * TPC + local_idx
            h = jax.nn.gelu(xf @ compress_w1 + compress_b1, approximate=False)
            comp = jnp.tanh(h @ compress_w2 + compress_b2)
            w1 = spline_w1[tile_idx]
            b1 = spline_b1[tile_idx]
            hh = jax.nn.relu(jnp.einsum('ni,nig->ng', comp, w1) + b1)
            w2 = spline_w2[tile_idx]
            b2 = spline_b2[tile_idx]
            mag = jnp.einsum('ng,ngo->no', hh, w2) + b2
            ffn_out = mag * directions[tile_idx] * output_scale[0]
            y = xf + ffn_out
            mu = y.mean(axis=-1, keepdims=True)
            var = ((y - mu) ** 2).mean(axis=-1, keepdims=True)
            y = (y - mu) / jnp.sqrt(var + EPS_LN) * norm_gamma + norm_beta
            return y.reshape(B, T, D)
        return _forward(x, signatures_raw, knot_values, temperature, compress_w1, compress_b1, compress_w2, compress_b2, spline_w1, spline_b1, spline_w2, spline_b2, directions, norm_gamma, norm_beta, output_scale)

    def _L2_xattn_ref(x, latents, mask, ln_x_g, ln_x_b, ln_l_g, ln_l_b, qn_g, kn_g, Wq, Wkv, Wlkv, Wo, bo):
        import jax, jax.numpy as jnp
        import numpy as np
        DIM_IN, DIM_LAT, DIM_HEAD = (96, 128, 64)
        INNER = max(DIM_LAT, DIM_IN)
        HEADS = INNER // DIM_HEAD
        SCALE = DIM_HEAD ** (-0.5)
        RMS_EPS = 1e-08
        LN_EPS = 1e-05

        def layernorm(x, g, b):
            mu = jnp.mean(x, axis=-1, keepdims=True)
            var = jnp.mean((x - mu) ** 2, axis=-1, keepdims=True)
            return (x - mu) * jax.lax.rsqrt(var + LN_EPS) * g + b

        def rmsnorm(x, gamma):
            norm = jnp.sqrt(jnp.sum(x * x, axis=-1, keepdims=True)) * x.shape[-1] ** (-0.5)
            return x / jnp.maximum(norm, RMS_EPS) * gamma
        b, n, _ = x.shape
        m = latents.shape[1]
        xn = layernorm(x, ln_x_g, ln_x_b)
        ln = layernorm(latents, ln_l_g, ln_l_b)
        q = ln @ Wq.T
        kv = jnp.concatenate([xn @ Wkv.T, ln @ Wlkv.T], axis=1)
        k, v = (kv[..., :INNER], kv[..., INNER:])
        split_heads = lambda t: t.reshape(t.shape[0], t.shape[1], HEADS, DIM_HEAD).transpose(0, 2, 1, 3)
        q, k, v = (split_heads(q), split_heads(k), split_heads(v))
        qn = rmsnorm(q, qn_g) * SCALE
        kn = rmsnorm(k, kn_g)
        attn = jnp.einsum('bhid,bhjd->bhij', qn, kn)
        full_mask = jnp.pad(mask, ((0, 0), (0, m)), constant_values=True)
        attn = jnp.where(full_mask[:, None, None, :], attn, -jnp.finfo(attn.dtype).max)
        attn = jax.nn.softmax(attn, axis=-1)
        out = jnp.einsum('bhij,bhjd->bhid', attn, v)
        out = out.transpose(0, 2, 1, 3).reshape(b, m, INNER)
        return out @ Wo.T + bo

    def _L2_ffn_ref(x, router_w, expert_bias, w1, w3, w2, sw1, sw3, sw2):
        import jax, jax.numpy as jnp
        import numpy as np
        B, S, DIM = (2, 256, 128)
        HID = 256
        E, NSH, TOPK = (8, 2, 2)

        def _ffn(x, w1, w2, w3):
            return jax.nn.silu(x @ w1.T) * (x @ w3.T) @ w2.T
        bs, sl, d = x.shape
        xf = x.reshape(-1, d)
        shared = jnp.zeros_like(xf)
        for i in range(sw1.shape[0]):
            shared = shared + _ffn(xf, sw1[i], sw2[i], sw3[i])
        logits = xf @ router_w.T + expert_bias
        rw, sel = jax.lax.top_k(logits, TOPK)
        rw = jax.nn.softmax(rw.astype(jnp.float32), axis=-1).astype(x.dtype)
        onehot = jax.nn.one_hot(sel, E, dtype=x.dtype)
        combine = jnp.einsum('tk,tke->te', rw, onehot)

        def body(acc, ew):
            e1, e3, e2, cw = ew
            acc = acc + cw[:, None] * _ffn(xf, e1, e2, e3)
            return (acc, None)
        out, _ = jax.lax.scan(body, jnp.zeros_like(xf), (w1, w3, w2, combine.T))
        out = out + shared
        return out.reshape(bs, sl, -1)

    def _L3_xattn_ref(x, context, Wq, Wk, Wv, Wo, bo):
        import jax, jax.numpy as jnp
        import numpy as np
        HEADS = 16
        DIM_HEAD = 64
        SCALE = DIM_HEAD ** (-0.5)
        QUERY_DIM = 128
        CONTEXT_DIM = 96
        INNER_DIM = HEADS * DIM_HEAD
        B, Nq, _ = x.shape
        Nk = context.shape[1]
        q = x @ Wq
        k = context @ Wk
        v = context @ Wv
        q = q.reshape(B, Nq, HEADS, DIM_HEAD).transpose(0, 2, 1, 3)
        k = k.reshape(B, Nk, HEADS, DIM_HEAD).transpose(0, 2, 1, 3)
        v = v.reshape(B, Nk, HEADS, DIM_HEAD).transpose(0, 2, 1, 3)
        sim = jnp.einsum('bhid,bhjd->bhij', q, k) * SCALE
        attn = jax.nn.softmax(sim, axis=-1)
        out = jnp.einsum('bhij,bhjd->bhid', attn, v)
        out = out.transpose(0, 2, 1, 3).reshape(B, Nq, INNER_DIM)
        return out @ Wo + bo

    def _L3_ffn_ref(x, W_fc, ln_w, ln_b, W_proj):
        import jax, jax.numpy as jnp
        import numpy as np
        EPS = 1e-06
        LN_EPS = 1e-05

        def _absmean_core(W):
            gamma = jnp.mean(jnp.abs(W)) + EPS
            Ws = W / gamma
            Wq = jnp.sign(Ws) * jnp.minimum(jnp.round(jnp.abs(Ws)), 1.0)
            return (Wq, gamma)

        @jax.custom_vjp
        def absmean(W):
            return _absmean_core(W)[0]

        def _absmean_fwd(W):
            Wq, gamma = _absmean_core(W)
            return (Wq, gamma)

        def _absmean_bwd(gamma, g):
            return (g / gamma,)
        absmean.defvjp(_absmean_fwd, _absmean_bwd)

        def layernorm(x, w, b, eps=LN_EPS):
            mu = jnp.mean(x, axis=-1, keepdims=True)
            var = jnp.mean((x - mu) ** 2, axis=-1, keepdims=True)
            return (x - mu) * jax.lax.rsqrt(var + eps) * w + b
        h = jnp.einsum('btd,hd->bth', x, absmean(W_fc))
        h = jax.nn.gelu(h, approximate=False)
        h = layernorm(h, ln_w, ln_b)
        return jnp.einsum('bth,dh->btd', h, absmean(W_proj))
    x = x + _L0_xattn_ref(_layernorm(x, axis=-1), ctx_768, mask_BxS_bf1, mask_BxS2_bf1, L0_xattn_Wq, L0_xattn_Wk, L0_xattn_Wv, L0_xattn_W_film_in, L0_xattn_b_film_in, L0_xattn_W_film_out, L0_xattn_b_film_out, L0_xattn_g_norm_in, L0_xattn_b_norm_in, L0_xattn_g_norm_out, L0_xattn_b_norm_out, L0_xattn_g_ffn, L0_xattn_b_ffn, L0_xattn_W1, L0_xattn_b1, L0_xattn_W2, L0_xattn_b2, L0_xattn_log_dt, L0_xattn_A_re, L0_xattn_A_im, L0_xattn_C_re, L0_xattn_C_im, L0_xattn_D_skip, L0_xattn_mod_gate)
    x = x + _L0_ffn_ref(_layernorm(x, axis=-1), L0_ffn_Wq, L0_ffn_bq, L0_ffn_Wk, L0_ffn_bk, L0_ffn_Wv, L0_ffn_bv, L0_ffn_Wr, L0_ffn_br, L0_ffn_Wo, L0_ffn_bo)
    x = x + _L1_xattn_ref(_layernorm(x, axis=-1), ctx_768, L1_xattn_Wq, L1_xattn_Wk, L1_xattn_Wv, L1_xattn_Wo)
    x = x + _L1_ffn_ref(_layernorm(x, axis=-1), L1_ffn_signatures_raw, L1_ffn_knot_values, L1_ffn_temperature, L1_ffn_compress_w1, L1_ffn_compress_b1, L1_ffn_compress_w2, L1_ffn_compress_b2, L1_ffn_spline_w1, L1_ffn_spline_b1, L1_ffn_spline_w2, L1_ffn_spline_b2, L1_ffn_directions, L1_ffn_norm_gamma, L1_ffn_norm_beta, L1_ffn_output_scale)
    x = x + _L2_xattn_ref(ctx_768, _layernorm(x, axis=-1), mask_BxS2_bk0, L2_xattn_ln_x_g, L2_xattn_ln_x_b, L2_xattn_ln_l_g, L2_xattn_ln_l_b, L2_xattn_qn_g, L2_xattn_kn_g, L2_xattn_Wq, L2_xattn_Wkv, L2_xattn_Wlkv, L2_xattn_Wo, L2_xattn_bo)
    x = x + _L2_ffn_ref(_layernorm(x, axis=-1), L2_ffn_router_w, L2_ffn_expert_bias, L2_ffn_w1, L2_ffn_w3, L2_ffn_w2, L2_ffn_sw1, L2_ffn_sw3, L2_ffn_sw2)
    x = x + _L3_xattn_ref(_layernorm(x, axis=-1), ctx_768, L3_xattn_Wq, L3_xattn_Wk, L3_xattn_Wv, L3_xattn_Wo, L3_xattn_bo)
    x = x + _L3_ffn_ref(_layernorm(x, axis=-1), L3_ffn_W_fc, L3_ffn_ln_w, L3_ffn_ln_b, L3_ffn_W_proj)
    return x

_drawn_inputs = setup_inputs


def setup_inputs(seed=0):
    import zlib

    import numpy as np

    out = dict(_drawn_inputs(seed))
    spreads = {'L0_xattn_b_film_in': (0.0, 0.1),
     'L0_xattn_b_film_out': (0.0, 0.1),
     'L0_xattn_g_norm_in': (1.0, 0.2),
     'L0_xattn_b_norm_in': (0.0, 0.1),
     'L0_xattn_g_norm_out': (1.0, 0.2),
     'L0_xattn_b_norm_out': (0.0, 0.1),
     'L0_xattn_g_ffn': (1.0, 0.6),
     'L0_xattn_b_ffn': (0.0, 0.8),
     'L0_xattn_b1': (0.0, 0.1),
     'L0_xattn_b2': (0.0, 0.1),
     'L0_xattn_A_re': (-0.5, 0.2),
     'L0_ffn_bq': (0.0, 0.8),
     'L0_ffn_bk': (0.0, 2.0),
     'L0_ffn_bv': (0.0, 0.1),
     'L0_ffn_br': (0.0, 0.1),
     'L0_ffn_bo': (0.0, 0.1),
     'L1_ffn_compress_b1': (0.0, 0.8),
     'L1_ffn_compress_b2': (0.0, 2.0),
     'L1_ffn_spline_b1': (0.0, 0.8),
     'L1_ffn_spline_b2': (0.0, 2.0),
     'L1_ffn_norm_gamma': (1.0, 0.2),
     'L1_ffn_norm_beta': (0.0, 0.1),
     'L2_xattn_ln_x_g': (1.0, 0.6),
     'L2_xattn_ln_x_b': (0.0, 0.8),
     'L2_xattn_ln_l_g': (1.0, 0.567),
     'L2_xattn_ln_l_b': (0.0, 0.1),
     'L2_xattn_qn_g': (1.0, 0.6),
     'L2_xattn_kn_g': (1.0, 0.6),
     'L2_xattn_bo': (0.0, 0.1),
     'L2_ffn_expert_bias': (0.0, 0.8),
     'L3_xattn_bo': (0.0, 0.665),
     'L3_ffn_ln_w': (1.0, 0.2),
     'L3_ffn_ln_b': (0.0, 0.1)}
    factors = {'L0_xattn_Wq': 8.0,
     'L0_xattn_Wk': 8.0,
     'L0_xattn_W1': 3.252,
     'L1_ffn_signatures_raw': 8.0,
     'L1_ffn_knot_values': 8.0,
     'L1_ffn_compress_w1': 8.0,
     'L1_ffn_compress_w2': 8.0,
     'L1_ffn_spline_w1': 8.0,
     'L1_ffn_spline_w2': 8.0,
     'L1_ffn_directions': 8.0,
     'L2_xattn_Wkv': 6.047,
     'L2_ffn_router_w': 8.0,
     'L2_ffn_w1': 8.0,
     'L2_ffn_w3': 8.0,
     'L2_ffn_w2': 8.0,
     'L2_ffn_sw1': 8.0,
     'L2_ffn_sw3': 8.0,
     'L2_ffn_sw2': 8.0}
    for name, (base, spread) in spreads.items():
        noise = np.random.default_rng([zlib.crc32(name.encode()), seed]).standard_normal(out[name].shape)
        drawn = base * np.exp(spread * noise) if base else spread * noise
        out[name] = jnp.asarray(drawn.astype(out[name].dtype))
    for name, factor in factors.items():
        out[name] = (out[name] * factor).astype(out[name].dtype)
    return out
```

```python
import numpy as np

import concourse.bass as bass
from concourse import mybir
from contextlib import ExitStack

F32 = mybir.dt.float32
U32 = mybir.dt.uint32
I32 = mybir.dt.int32
U8 = mybir.dt.uint8
ALU = mybir.AluOpType
ACT = mybir.ActivationFunctionType
AX = mybir.AxisListType

P = 128
NB, S, D = 2, 512, 128
NT = NB * S // P
TB = S // P
NC, DC = 77, 96
TOK = NB * S
H0, KEEP, DH0 = 4, 32, 32
NST = 64
LA, LB = 32, 16
HID0 = 512
HF, CH, DF = 16, 4, 64
NTL, TPC, NCL, GRID, CMP, KN = 64, 8, 8, 16, 32, 8
TABW = 2 * GRID + GRID + GRID + 1 + D
H2, D2 = 2, 64
NE, NSH, HE = 8, 2, 256
H3, D3 = 16, 64
HK3 = H3 * NC
CK3 = -(-HK3 // P)
HID3 = 512
TURN = 6.283184
MAGIC = 1.5 * 2.0 ** 23
NEVER = -3.0e38
MASKED = 1.0e30

PACKS = {
    "ctx": [("ctxT", NB * NC), ("wk0", D), ("wv0", D), ("wqT0", D), ("wfilm", 4 * D), ("ident", P), ("avg", P)],
    "rows": [("g_in", D), ("b_in", D), ("dskip", D), ("b2", D), ("g_out", D), ("b_out", D),
             ("br", HF), ("bo0", D), ("knots", KN), ("temp", 1), ("oscale", 1), ("cb2", 2), ("gam1", D), ("bet1", D),
             ("lnx_g", DC), ("lnx_b", DC), ("bo2", D), ("ebias", NE), ("bo3", D), ("gate", 1), ("iotaa", LA),
             ("rev8", 8), ("iota8", 8), ("iota16", HF), ("rev16", HF)],
    "cols": [("g_ffn", 1), ("b_ffn", 1), ("b1", HID0 // P), ("wf", 4), ("alt", 1), ("quarter", 1), ("sgn", 1),
             ("off2", 1), ("cb1", 1), ("lnl_g", 1), ("lnl_b", 1), ("qn", 1), ("kn", 1), ("ln3w", 4), ("ln3b", 4),
             ("bq2", HF), ("bk2", HF), ("eps", 1), ("half", 4 * NT), ("br_col", 1), ("euler", 1), ("logdt", 1),
             ("qturn", 1), ("oturn", 1)],
    "small0": [("wr", HF), ("wo0", 2 * D)],
    "s4": [("are", D), ("aim", D), ("cre", D), ("cim", D)],
    "dft": [("cos", 4 * S), ("sin", 4 * S)],
    "ffn0": [("w1", HID0), ("w2", HID0)],
    "head0": [("wqkv", HF * 4 * DF)],
    "l1": [("wq1", D), ("wk1", DC), ("wv1", DC), ("wo1T", D), ("sigT", NTL), ("cw1", CMP), ("cw2", 2), ("tab", TABW)],
    "l2": [("ctxr", NB * DC), ("wq2T", D), ("wlkvT", 2 * D), ("wkvT", 2 * D), ("wo2T", H2 * D), ("router", NE)],
    "moe": [("moe", (NE + NSH) * 3 * HE)],
    "l3": [("wqT3", H3 * D3), ("wk3", H3 * D3), ("wv3", H3 * D3), ("wo3", 8 * D)],
    "l3f": [("wfcT", HID3), ("wpT", HID3)],
}
WIDTH = {k: sum(n for _, n in v) for k, v in PACKS.items()}
LOADS = [("ctx", "rows", "cols"), ("s4",), ("dft",), ("ffn0", "small0", "l1", "l2", "l3f"), ("head0",), ("moe", "l3")]
LAST_STAGE = 8
SPLITK = 3
FOLD_EARLY = 4


def program(nc, A, out):
    ctx = ExitStack()
    with ctx:
        def sb(name, *shape, dt=F32):
            return ctx.enter_context(nc.sbuf_tensor(name, list(shape), dt))

        def sem(name):
            return ctx.enter_context(nc.semaphore(name))

        bank = [ctx.enter_context(nc.psum_tensor(f"bank{i}", [P, 512], F32)) for i in range(8)]

        arenaA, arenaB = sb("arenaA", P, 12288), sb("arenaB", P, 14592)

        def part(region, at, *shape):
            n = int(np.prod(shape))
            v = region[:, at:at + n]
            if len(shape) == 1:
                return v
            names = "abcd"[:len(shape)]
            return v.rearrange(f"p ({' '.join(names)}) -> p {' '.join(names)}", **dict(zip(names, shape)))

        packed, loaded, V = {}, {}, {}
        for group in LOADS:
            s = sem("loaded_" + group[0])
            for k in group:
                loaded[k] = (s, 16 * len(group))
        for k in PACKS:
            if k == "moe":
                packed[k] = arenaA[:, 0:WIDTH[k]]
            elif k == "l3":
                packed[k] = arenaA[:, WIDTH["moe"]:WIDTH["moe"] + WIDTH[k]]
            elif k == "head0":
                packed[k] = packed["dft"][:, 0:WIDTH[k]]
            else:
                packed[k] = sb(f"in_{k}", P, WIDTH[k])
            at = 0
            for name, n in PACKS[k]:
                V[name] = packed[k][:, at:at + n]
                at += n
        X = sb("X", P, NT, D)
        xn = sb("xn", P, NT, D)
        xnT = sb("xnT", P, TOK)
        tmp = sb("tmp", P, NT, D)
        tmp2 = sb("tmp2", P, NT, D)
        stats = sb("stats", P, NT, 6)
        mv = sb("mv", P, NT, 2)
        rstd = sb("rstd", P, NT)
        rtmp = sb("rtmp", P, NT)
        masks8 = sb("masks8", P, 2, NB, NC, dt=U8)
        tmask8 = sb("tmask8", P, NT, dt=U8)
        maskb = sb("maskb", P, 2, NB, NC)
        tmask = sb("tmask", P, NT)
        ident, quarter = V["ident"], V["quarter"]

        x_loaded, masks_loaded = sem("x_loaded"), sem("masks_loaded")
        dve_step, act_step, pool_step = sem("dve_step"), sem("act_step"), sem("pool_step")
        ln_moments, ln_rstd, ln_done = sem("ln_moments"), sem("ln_rstd"), sem("ln_done")
        ln_turned, ln_T = sem("ln_turned"), sem("ln_T")

        avg1_mm = sem("avg1_mm")
        bias_added = sem("bias_added")
        c2_powers = sem("c2_powers")
        c2_scaled = sem("c2_scaled")
        c2_stats = sem("c2_stats")
        kern_act = sem("kern_act")
        kern_pe = sem("kern_pe")
        l1f_act = sem("l1f_act")
        l1f_pe = sem("l1f_pe")
        l1f_vec = sem("l1f_vec")
        l1x_vec = sem("l1x_vec")
        route_pe = sem("route_pe")
        route_vec = sem("route_vec")
        s4_act = sem("s4_act")
        s4_pool = sem("s4_pool")
        w3_vec = sem("w3_vec")

        class Steps:

            def __init__(self, eng, s):
                self.eng, self.s, self.n = eng, s, 0

            def link(self, ins):
                self.n += 1
                ins.then_inc(self.s, 1)
                self.eng.wait_ge(self.s, self.n)

        def bc(col, *shape):
            while len(col.shape) < len(shape):
                col = col.unsqueeze(len(col.shape))
            return col.broadcast_to(list(shape))

        def bm(row, n):
            return row.unsqueeze(1).broadcast_to([row.shape[0], n, row.shape[1]])

        def halves():
            return [slice(b * TB, (b + 1) * TB) for b in range(NB)]

        def vec_moments(dve, st, i, src):
            for r in halves():
                for t in range(r.start, r.stop):
                    ins = nc.vector.bn_stats(stats[:, t, :], src[:, t, :])
                st.link(ins)
                for t in range(r.start, r.stop):
                    ins = nc.vector.bn_aggr(mv[:, t, :], stats[:, t, :])
                ins.then_inc(ln_moments, 1)

        def pool_rstd(pool, st, i):
            for b, r in enumerate(halves()):
                pool.wait_ge(ln_moments, NB * i + b + 1)
                st.link(nc.gpsimd.tensor_scalar(rtmp[:, r], mv[:, r, 1], 1e-5, None, ALU.add))
                nc.gpsimd.tensor_tensor(rstd[:, r], rtmp[:, r], V["half"][:, r], ALU.pow).then_inc(ln_rstd, 1)

        def vec_normalise(dve, i, src, dst):
            for b, r in enumerate(halves()):
                dve.wait_ge(ln_rstd, NB * i + b + 1)
                for t in range(r.start, r.stop):
                    nc.vector.tensor_scalar(dst[:, t, :], src[:, t, :], mv[:, t, 0:1], rstd[:, t:t + 1],
                                            ALU.subtract, ALU.mult).then_inc(ln_done, 1)

        def pe_turn(pe, done, before, src):
            for t in range(NT):
                pe.wait_ge(done, before + t + 1)
                ins = nc.tensor.transpose(bank[t // TB][:, (t % TB) * P:(t % TB + 1) * P], src[:, t, :], ident)
                if t % TB == TB - 1:
                    ins.then_inc(ln_turned, 1)

        def act_turned(act, n, scale=None, bias=None):
            for b in range(NB):
                act.wait_ge(ln_turned, NB * n + b + 1)
                dst = xnT[:, b * S:(b + 1) * S]
                if scale is None:
                    ins = nc.scalar.copy(dst, bank[b][:])
                elif bias is None:
                    ins = nc.scalar.activation(dst, bank[b][:], ACT.Copy, scale=scale)
                else:
                    ins = nc.scalar.activation(dst, bank[b][:], ACT.Identity, scale=scale, bias=bias)
                ins.then_inc(ln_T, 1)

        kT0 = sb("kT0", P, NB * NC)
        f0 = sb("f0", P, NB, H0, NC)
        vT0 = sb("vT0", P, NB * NC)
        vfilm = sb("vfilm", NC + 1, NB, 4 * D)
        s0 = part(arenaB, 0, NT, H0, NC)
        r0 = part(arenaB, 2464, NT, H0, NC)
        e0 = part(arenaB, 4928, NT, H0, NC)
        top0 = part(arenaB, 7392, NT, H0, KEEP)
        sum0 = sb("sum0", P, NT, H0)
        w0 = sb("w0", P, NT, H0)
        am = sb("am", P, NT, NC)
        amT = sb("amT", NC + 1, TOK)
        film = part(arenaA, 0, NT, 4, D)
        xk = part(arenaA, 8192, TB, 3, D)
        yc = part(arenaA, 4096, 4, 2, NB * D)
        kf = part(arenaA, 6144, 4, 2, D)
        pr = part(arenaA, 7168, 4, NB * D)
        kny = sb("kny", 1, D)
        yny = sb("yny", 1, NB, D)
        xt = sb("xt", P, NT, D)
        hT0 = part(arenaA, 8192, 4, TOK)
        altrow = arenaA[0:1, 11264:11264 + S]

        masks_ready, ctx0_mm, ctx0_copy, bias_rows = sem("masks_ready"), sem("ctx0_mm"), sem("ctx0_copy"), sem("bias_rows")
        ones_set = sem("ones_set")
        s0_mm, s0_copy, top_ready, shifted0, exp0 = sem("s0_mm"), sem("s0_copy"), sem("top_ready"), sem("shifted0"), sem("exp0")
        am_ready, am_turned, amT_ready, film_mm, film_ready = sem("am_ready"), sem("am_turned"), sem("amT_ready"), sem("film_mm"), sem("film_ready")
        x2_ready = sem("x2_ready")
        dft_mm, kf_ready, spec_used, prod_ready, y_mm, xt_ready = (sem("dft_mm"), sem("kf_ready"), sem("spec_used"),
                                                                    sem("prod_ready"), sem("y_mm"), sem("xt_ready"))
        ff_mm, ff_gelu, ff_out, b2_added = sem("ff_mm"), sem("ff_gelu"), sem("ff_out"), sem("b2_added")

        ang, are, aim, dtb, al, be = (tmp[:, i, :] for i in range(6))
        q = [xt[:, i, :] for i in range(8)]
        big = [arenaA[:, i * D * LA:(i + 1) * D * LA] for i in range(3)]
        hh4 = part(arenaB, 8416, D, LA)
        gg4 = part(arenaB, 12512, D, LB)
        ka = part(arenaA, 8192, D, LB)[0:LA]
        kTl = part(arenaA, 10240, S)
        s4_vec, s4_pe = sem("s4_vec"), sem("s4_pe")

        def sync_loads(sp):
            sp.dma_start(X[:], A["x"].rearrange("(t p) d -> p t d", p=P)).then_inc(x_loaded, 16)
            for k in ("ctx", "rows", "cols"):
                if k == "rows":
                    sp.dma_start(packed[k][:], A[k].rearrange("a n -> (a n)").partition_broadcast(P)).then_inc(loaded[k][0], 16)
                else:
                    sp.dma_start(packed[k][:], A[k]).then_inc(loaded[k][0], 16)
            sp.dma_start(masks8[:], A["masks"].partition_broadcast(P)).then_inc(masks_loaded, 16)
            sp.dma_start(tmask8[:], A["tmask"]).then_inc(masks_loaded, 16)
            for b in range(NB):
                sp.dma_start(vfilm[NC:NC + 1, b, :], A["bfilm"]).then_inc(bias_rows, 16)
            for k in ("s4", "dft", "ffn0", "small0", "l1", "l2", "l3f"):
                sp.dma_start(packed[k][:], A[k]).then_inc(loaded[k][0], 16)
            sp.wait_ge(s4_pool, 4)
            sp.dma_start(altrow, A["altrow"]).then_inc(bias_rows, 16)
            sp.wait_ge(y_mm, TB)
            sp.dma_start(packed["head0"], A["head0"]).then_inc(loaded["head0"][0], 16)
            sp.wait_ge(ff_out, NB)
            for k in ("moe", "l3"):
                sp.dma_start(packed[k], A[k]).then_inc(loaded[k][0], 16)

        def pe_ctx0(pe):
            pe.wait_ge(*loaded["ctx"])
            nc.tensor.matmul(bank[2][:, 0:NB * NC], V["wk0"][0:DC], V["ctxT"][0:DC], start=True, stop=True).then_inc(ctx0_mm, 1)
            nc.tensor.matmul(bank[3][:, 0:NB * NC], V["wv0"][0:DC], V["ctxT"][0:DC], start=True, stop=True).then_inc(ctx0_mm, 1)
            pe.wait_ge(ctx0_copy, 1)
            pe.wait_ge(s4_vec, 2)
            for h in range(H0):
                r = slice(h * DH0, (h + 1) * DH0)
                nc.tensor.matmul(bank[4 + h][:, 0:NB * NC], V["wqT0"][r], kT0[r, :], start=True, stop=True).then_inc(ctx0_mm, 1)
            pe.wait_ge(ctx0_copy, 2)
            for b in range(NB):
                nc.tensor.matmul(bank[2 + b][0:NC, :], vT0[:, b * NC:(b + 1) * NC], V["wfilm"], start=True, stop=True).then_inc(ctx0_mm, 1)

        def act_ctx0(act):
            act.wait_ge(ctx0_mm, 1)
            nc.scalar.copy(kT0[:], bank[2][:, 0:NB * NC]).then_inc(ctx0_copy, 1)
            act.wait_ge(ctx0_mm, 2)
            nc.scalar.copy(vT0[:], bank[3][:, 0:NB * NC]).then_inc(ctx0_copy, 1)
            for h in range(H0):
                act.wait_ge(ctx0_mm, 3 + h)
                nc.scalar.copy(f0[:, :, h, :], bank[4 + h][:, 0:NB * NC].rearrange("p (b k) -> p b k", b=NB)).then_inc(ctx0_copy, 1)
            for b in range(NB):
                act.wait_ge(ctx0_mm, 3 + H0 + b)
                nc.scalar.copy(vfilm[0:NC, b, :], bank[2 + b][0:NC, :]).then_inc(ctx0_copy, 1)

        def pe_scores0(pe):
            for t in range(NT):
                if t == 0:
                    pe.wait_ge(ctx0_copy, 2 + H0 + NB)
                if t % TB == 0:
                    pe.wait_ge(ln_T, t // TB + 1)
                if t >= 4:
                    pe.wait_ge(s0_copy, t - 3)
                nc.tensor.matmul(bank[2 + t % 4][:, 0:H0 * NC], xnT[:, t * P:(t + 1) * P],
                                 f0[:, t // TB].rearrange("p h k -> p (h k)"), start=True, stop=True).then_inc(s0_mm, 1)

        def vec_scores0(dve, st):
            dve.wait_ge(masks_ready, 1)
            for t in range(NT):
                dve.wait_ge(s0_mm, t + 1)
                nc.vector.tensor_tensor(s0[:, t], bank[2 + t % 4][:, 0:H0 * NC].rearrange("p (h k) -> p h k", h=H0),
                                        bm(maskb[:, 0, t // TB, :], H0), ALU.add).then_inc(s0_copy, 1)
            dve.wait_ge(s0_copy, NT)
            for t in range(NT):
                for k in range(KEEP // 8):
                    for h in range(H0):
                        src = s0[:, t, h, :] if k == 0 else r0[:, t, h, :]
                        ins = nc.vector.max(top0[:, t, h, 8 * k:8 * k + 8], src)
                    st.link(ins)
                    for h in range(H0):
                        src = s0[:, t, h, :] if k == 0 else r0[:, t, h, :]
                        ins = nc.vector.match_replace(r0[:, t, h, :], top0[:, t, h, 8 * k:8 * k + 8], src, NEVER)
                    if k == KEEP // 8 - 1:
                        ins.then_inc(top_ready, 1)
                    else:
                        st.link(ins)

        def pool_shift0(pool):
            for t in range(NT):
                pool.wait_ge(top_ready, t + 1)
                nc.gpsimd.tensor_tensor(e0[:, t], s0[:, t], bc(top0[:, t, :, 0], P, H0, NC), ALU.subtract).then_inc(shifted0, 1)

        def act_exp0(act):
            for t in range(NT):
                act.wait_ge(shifted0, t + 1)
                nc.scalar.activation(e0[:, t], e0[:, t], ACT.Exp, scale=float(1.0 / np.sqrt(np.float32(DH0)))).then_inc(exp0, 1)

        def vec_probs0(dve, st):
            for t in range(NT):
                dve.wait_ge(exp0, t + 1)
                ins = nc.vector.scalar_tensor_tensor(e0[:, t], r0[:, t], 0.5 * NEVER, e0[:, t], ALU.is_lt, ALU.mult)
            st.link(ins)
            st.link(nc.vector.tensor_reduce(sum0[:], e0[:], AX.X, ALU.add))
            st.link(nc.vector.reciprocal(w0[:], sum0[:]))
            st.link(nc.vector.tensor_tensor(w0[:], w0[:], bc(tmask[:], P, NT, H0), ALU.mult))
            for t in range(NT):
                ins = nc.vector.tensor_tensor(e0[:, t], e0[:, t], bc(w0[:, t], P, H0, NC), ALU.mult)
            st.link(ins)
            for t in range(NT):
                ins = nc.vector.tensor_reduce(am[:, t, :], e0[:, t].rearrange("p h k -> p k h"), AX.X, ALU.add)
                ins.then_inc(am_ready, 1)

        def pe_film(pe):
            for t in range(NT):
                pe.wait_ge(am_ready, t + 1)
                ins = nc.tensor.transpose(bank[t // TB][0:NC, (t % TB) * P:(t % TB + 1) * P], am[:, t, :], ident)
                if t % TB == TB - 1:
                    ins.then_inc(am_turned, 1)
            pe.wait_ge(bias_rows, 16 * (NB + 1))
            for t in range(NT):
                if t % TB == 0:
                    pe.wait_ge(amT_ready, t // TB + 1)
                if t >= 4:
                    pe.wait_ge(film_ready, t - 3)
                nc.tensor.matmul(bank[2 + t % 4][:], amT[:, t * P:(t + 1) * P], vfilm[:, t // TB, :],
                                 start=True, stop=True).then_inc(film_mm, 1)

        def act_film(act, st):
            act.wait_ge(ones_set, 1)
            for b in range(NB):
                act.wait_ge(am_turned, b + 1)
                nc.scalar.copy(amT[0:NC, b * S:(b + 1) * S], bank[b][0:NC, :]).then_inc(amT_ready, 1)
            for t in range(NT):
                act.wait_ge(film_mm, t + 1)
                src = bank[2 + t % 4][:].rearrange("p (f s d) -> p f s d", f=2, s=2)
                dst = film[:, t].rearrange("p (f s) d -> p f s d", f=2)
                nc.scalar.activation(dst[:, :, 0], src[:, :, 0], ACT.Identity, scale=V["gate"], bias=1.0)
                nc.scalar.activation(dst[:, :, 1], src[:, :, 1], ACT.Copy, scale=V["gate"]).then_inc(film_ready, 1)

        def pool_masks(pool, st):
            nc.gpsimd.memset(amT[:], 1.0).then_inc(ones_set, 1)
            pool.wait_ge(masks_loaded, 32)
            st.link(nc.gpsimd.tensor_copy(maskb[:], masks8[:]))
            st.link(nc.gpsimd.tensor_copy(tmask[:], tmask8[:]))
            st.link(nc.gpsimd.tensor_scalar(maskb[:], maskb[:], 1.0, MASKED, ALU.subtract, ALU.mult))
            nc.gpsimd.tensor_scalar(tmask[:], tmask[:], 1.0 / H0, None, ALU.mult).then_inc(masks_ready, 1)

        dtc, dtd = sb("dtc", P, 1), q[6]

        def pool_dt(pool):
            pool.wait_ge(*loaded["cols"])
            nc.gpsimd.tensor_tensor(dtc[:], V["euler"], V["logdt"], ALU.pow).then_inc(s4_pool, 1)

        def vec_dt(dve):
            dve.wait_ge(s4_pool, 1)
            dve.wait_ge(*loaded["ctx"])
            nc.vector.tensor_scalar(dtd, ident, dtc[:], float(P), ALU.mult, ALU.mult).then_inc(s4_vec, 1)

        def pe_dt(pe):
            pe.wait_ge(s4_vec, 1)
            nc.tensor.matmul(bank[7][:, 0:D], V["avg"], dtd, start=True, stop=True).then_inc(s4_pe, 1)

        steps = V["iotaa"].unsqueeze(1).broadcast_to([P, D, LA])
        uH, rH, eH = (x.rearrange("p (d l) -> p d l", d=D) for x in big)
        uG, rGc = part(arenaA, 0, D, LB), part(arenaA, D * LB, D, LB)
        rGs, eG, sG = (part(arenaB, i * D * LB, D, LB) for i in range(3))

        def vec_s4(dve, st):
            Vv, L = nc.vector, st.link
            tt, ts, stt = Vv.tensor_tensor, Vv.tensor_scalar, Vv.scalar_tensor_tensor

            def phase(r, u, off):
                L(ts(r, u, off, MAGIC, ALU.add, ALU.add))
                return stt(r, r, MAGIC, u, ALU.subtract, ALU.subtract)

            dve.wait_ge(s4_pe, 1)
            Vv.tensor_copy(dtb[:], bank[7][:, 0:D]).then_inc(s4_vec, 1)
            dve.wait_ge(s4_vec, 2)
            dve.wait_ge(*loaded["s4"])
            tt(are[:], dtb[:], V["are"], ALU.mult).then_inc(s4_vec, 1)
            L(tt(aim[:], dtb[:], V["aim"], ALU.mult))
            L(ts(ang[:], aim[:], float(1.0 / (2.0 * np.pi)), None, ALU.mult))
            L(ts(q[1][:], ang[:], MAGIC, MAGIC, ALU.add, ALU.subtract))
            tt(ang[:], ang[:], q[1][:], ALU.subtract).then_inc(s4_vec, 1)
            dve.wait_ge(s4_vec, 4)
            L(stt(uH, bc(ang[:], P, D, LA), float(LB), steps, ALU.mult, ALU.mult))
            phase(rH, uH, V["quarter"]).then_inc(s4_vec, 1)
            dve.wait_ge(s4_vec, 5)
            L(tt(uG, bc(ang[:], P, D, LB), steps[:, :, 0:LB], ALU.mult))
            phase(rGc, uG, V["quarter"]).then_inc(s4_vec, 1)
            phase(rGs, uG, V["off2"]).then_inc(s4_vec, 1)
            em1, s1, s2, inv = q[0][:], q[1][:], q[2][:], q[4][:]
            a, b, c, d = q[3][:], q[5][:], q[6][:], q[7][:]
            L(tt(a, V["are"], V["are"], ALU.mult))
            L(tt(b, V["aim"], V["aim"], ALU.mult))
            L(tt(a, a, b, ALU.add))
            L(Vv.reciprocal(inv, a))
            dve.wait_ge(s4_act, 3)
            L(ts(a, em1, -1.0, 1.0, ALU.mult, ALU.add))
            L(Vv.reciprocal(b, a))
            L(stt(em1, em1, 2.0, b, ALU.mult, ALU.mult))
            L(stt(a, s1, 2.0, s1, ALU.mult, ALU.mult))
            L(tt(b, em1, a, ALU.mult))
            L(tt(b, em1, b, ALU.subtract))
            L(tt(b, b, a, ALU.subtract))
            L(stt(c, em1, 1.0, s2, ALU.add, ALU.mult))
            L(tt(a, b, V["are"], ALU.mult))
            L(tt(d, c, V["aim"], ALU.mult))
            L(tt(a, a, d, ALU.add))
            L(tt(a, a, inv, ALU.mult))
            L(tt(c, c, V["are"], ALU.mult))
            L(tt(d, b, V["aim"], ALU.mult))
            L(tt(c, c, d, ALU.subtract))
            L(tt(c, c, inv, ALU.mult))
            L(tt(b, V["cre"], a, ALU.mult))
            L(tt(d, V["cim"], c, ALU.mult))
            L(tt(b, b, d, ALU.subtract))
            L(ts(al[:], b, 2.0, V["sgn"], ALU.mult, ALU.mult))
            L(tt(b, V["cre"], c, ALU.mult))
            L(tt(d, V["cim"], a, ALU.mult))
            L(tt(b, b, d, ALU.add))
            L(ts(be[:], b, -2.0, None, ALU.mult))
            dve.wait_ge(s4_act, 6)
            L(tt(gg4[:], gg4[:], bc(al[:], P, D, LB), ALU.mult))
            dve.wait_ge(s4_act, 7)
            L(tt(sG, sG, bc(be[:], P, D, LB), ALU.mult))
            L(tt(gg4[:], gg4[:], sG, ALU.add))
            dve.wait_ge(s4_act, 8)
            tt(gg4[:], gg4[:], eG, ALU.mult).then_inc(s4_vec, 1)

        def pool_s4(pool):
            G = nc.gpsimd
            pool.wait_ge(s4_vec, 3)
            G.tensor_tensor(eH, bc(are[:], P, D, LA), steps, ALU.mult).then_inc(s4_pool, 1)
            G.tensor_tensor(eG, bc(are[:], P, D, LB), steps[:, :, 0:LB], ALU.mult).then_inc(s4_pool, 1)
            pool.wait_ge(s4_act, 5)
            G.tensor_tensor(hh4[:], hh4[:], eH, ALU.mult).then_inc(s4_pool, 1)

        def act_s4(act):
            A_ = nc.scalar.activation
            act.wait_ge(s4_vec, 3)
            A_(q[0][:], are[:], ACT.Tanh, scale=0.5).then_inc(s4_act, 1)
            act.wait_ge(s4_vec, 4)
            A_(q[1][:], ang[:], ACT.Sin, scale=0.5 * TURN).then_inc(s4_act, 1)
            A_(q[2][:], ang[:], ACT.Sin, scale=TURN).then_inc(s4_act, 1)
            act.wait_ge(s4_vec, 5)
            A_(hh4[:], rH, ACT.Sin, scale=-TURN, bias=V["qturn"]).then_inc(s4_act, 1)
            act.wait_ge(s4_pool, 2)
            A_(eH, eH, ACT.Exp, scale=float(LB)).then_inc(s4_act, 1)
            act.wait_ge(s4_vec, 6)
            A_(gg4[:], rGc, ACT.Sin, scale=-TURN, bias=V["qturn"]).then_inc(s4_act, 1)
            act.wait_ge(s4_vec, 7)
            A_(sG, rGs, ACT.Sin, scale=-TURN, bias=V["oturn"]).then_inc(s4_act, 1)
            act.wait_ge(s4_pool, 3)
            A_(eG, eG, ACT.Exp).then_inc(s4_act, 1)

        def pe_kernel(pe):
            pe.wait_ge(s4_vec, 8)
            pe.wait_ge(s4_pool, 4)
            pe.wait_ge(s0_copy, NT)
            per = 512 // LB
            for d in range(D):
                ins = nc.tensor.matmul(bank[2 + d // per][0:LA, (d % per) * LB:(d % per + 1) * LB],
                                       hh4[:, d, :], gg4[:, d, :], start=True, stop=True)
                if d % per == per - 1:
                    ins.then_inc(kern_pe, 1)
            pe.wait_ge(kern_act, 4)
            for b in range(LB):
                ins = nc.tensor.transpose(bank[6][:, b * LA:(b + 1) * LA], ka[:, :, b], ident[0:LA, 0:LA])
            ins.then_inc(kern_pe, 1)
            pe.wait_ge(kern_act, 5)
            for j in range(TB):
                ins = nc.tensor.transpose(bank[7][:, j * P:(j + 1) * P], kTl[:, j * P:(j + 1) * P], ident)
            ins.then_inc(kern_pe, 1)

        def act_kernel(act):
            per = 512 // LB
            for i in range(4):
                act.wait_ge(kern_pe, i + 1)
                nc.scalar.copy(ka[:, i * per:(i + 1) * per, :], bank[2 + i][0:LA, :].rearrange("p (d b) -> p d b", b=LB)).then_inc(kern_act, 1)
            act.wait_ge(kern_pe, 5)
            nc.scalar.copy(kTl[:].rearrange("p (a b) -> p a b", b=LB), bank[6][:].rearrange("p (b a) -> p a b", b=LB)).then_inc(kern_act, 1)
            act.wait_ge(kern_pe, 6)
            nc.scalar.copy(xk[:, :, 2, :], bank[7][:].rearrange("p (j d) -> p j d", d=D)).then_inc(kern_act, 1)

        def vec_film(dve, st):
            st.link(nc.vector.tensor_tensor(tmp[:], tmp2[:], bm(V["g_in"], NT), ALU.mult))
            st.link(nc.vector.tensor_tensor(tmp[:], tmp[:], bm(V["b_in"], NT), ALU.add))
            dve.wait_ge(film_ready, NT)
            st.link(nc.vector.tensor_tensor(tmp[:], tmp[:], film[:, :, 0, :], ALU.mult))
            for b in range(NB):
                ins = nc.vector.tensor_tensor(xk[:, :, b, :], tmp[:, b * TB:(b + 1) * TB, :],
                                              film[:, b * TB:(b + 1) * TB, 1, :], ALU.add)
            ins.then_inc(x2_ready, 1)

        def pe_dft(pe):
            pe.wait_ge(*loaded["dft"])
            pe.wait_ge(c2_copy, 3)
            pe.wait_ge(w3_vec, 2)
            pe.wait_ge(kern_act, 6)
            pe.wait_ge(x2_ready, 1)
            for j in range(4):
                for c, m in enumerate(("cos", "sin")):
                    for q4 in range(TB):
                        ins = nc.tensor.matmul(bank[2 * j + c][:, 0:3 * D], V[m][:, q4 * S + j * P:q4 * S + (j + 1) * P],
                                               xk[:, q4].rearrange("p b d -> p (b d)"), start=(q4 == 0), stop=(q4 == TB - 1))
                ins.then_inc(dft_mm, 1)
            pe.wait_ge(spec_used, 1)
            for q4 in range(TB):
                ins = nc.tensor.matmul(bank[0][0:1, 0:3 * D], V["alt"], xk[:, q4].rearrange("p b d -> p (b d)"),
                                       start=(q4 == 0), stop=(q4 == TB - 1))
            ins.then_inc(dft_mm, 1)
            pe.wait_ge(prod_ready, 5)
            for i in range(TB):
                for j in range(4):
                    for c, m in enumerate(("cos", "sin")):
                        nc.tensor.matmul(bank[2 + i][:, 0:NB * D], V[m][:, j * S + i * P:j * S + (i + 1) * P],
                                         yc[:, j, c], start=(j == 0 and c == 0), stop=False)
                nc.tensor.matmul(bank[2 + i][:, 0:NB * D], altrow[0:1, i * P:(i + 1) * P],
                                 yny[0:1].rearrange("p b d -> p (b d)"), start=False, stop=True).then_inc(y_mm, 1)

        def act_dft(act):
            for j in range(4):
                act.wait_ge(dft_mm, j + 1)
                for c in range(2):
                    ins = nc.scalar.activation(kf[:, j, c, :], bank[2 * j + c][:, 2 * D:3 * D], ACT.Copy, scale=V["wf"][:, j:j + 1])
                ins.then_inc(kf_ready, 1)
            act.wait_ge(dft_mm, 5)
            nc.scalar.activation(kny[:], bank[0][0:1, 2 * D:3 * D], ACT.Copy, scale=1.0 / (2 * S)).then_inc(kf_ready, 1)

        def vec_spectrum(dve, st):
            tt = nc.vector.tensor_tensor
            for j in range(4):
                dve.wait_ge(kf_ready, j + 1)
                xc, xs = (bank[2 * j + c][:, 0:NB * D].rearrange("p (b d) -> p b d", b=NB) for c in range(2))
                kc, ks = (bm(kf[:, j, c, :], NB) for c in range(2))
                p = [pr[:, i, :].rearrange("p (b d) -> p b d", b=NB) for i in range(4)]
                if j:
                    dve.wait_ge(prod_ready, j)
                tt(p[0], xc, kc, ALU.mult)
                tt(p[1], xs, ks, ALU.mult)
                tt(p[2], xs, kc, ALU.mult)
                tt(p[3], xc, ks, ALU.mult).then_inc(spec_used, 1)
                dve.wait_ge(spec_used, j + 1)
                tt(yc[:, j, 0], pr[:, 0], pr[:, 1], ALU.subtract)
                tt(yc[:, j, 1], pr[:, 2], pr[:, 3], ALU.add).then_inc(prod_ready, 1)
            dve.wait_ge(kf_ready, 5)
            tt(yny[:], bank[0][0:1, 0:NB * D].rearrange("p (b d) -> p b d", b=NB), bm(kny[:], NB), ALU.mult).then_inc(prod_ready, 1)

        def vec_xt(dve, st):
            tt = nc.vector.tensor_tensor
            for b in range(NB):
                ins = tt(tmp[:, b * TB:(b + 1) * TB, :], xk[:, :, b, :], bm(V["dskip"], TB), ALU.mult)
            st.link(ins)
            tv = tmp[:].rearrange("p (b q) d -> p q b d", b=NB)
            for i in range(TB):
                dve.wait_ge(y_mm, i + 1)
                ins = tt(tv[:, i], bank[2 + i][:, 0:NB * D].rearrange("p (b d) -> p b d", b=NB), tv[:, i], ALU.add)
            st.link(ins)
            st.link(tt(tmp[:], tmp[:], film[:, :, 2, :], ALU.mult))
            st.link(tt(tmp[:], tmp[:], film[:, :, 3, :], ALU.add))
            st.link(tt(xt[:], tmp[:], xn[:], ALU.add))

        def pe_ffn0(pe):
            pe.wait_ge(*loaded["ffn0"])
            n = 0
            for b in range(NB):
                pe.wait_ge(ln_T, NB * 1 + b + 1)
                for c in range(4):
                    if n >= 4:
                        pe.wait_ge(ff_gelu, n - 3)
                    nc.tensor.matmul(bank[2 + n % 4][:], V["w1"][:, c * P:(c + 1) * P], xnT[:, b * S:(b + 1) * S],
                                     start=True, stop=True).then_inc(ff_mm, 1)
                    n += 1
            for b in range(NB):
                pe.wait_ge(ff_gelu, 4 * b + 4)
                for q4 in range(TB):
                    t = b * TB + q4
                    for c in range(4):
                        ins = nc.tensor.matmul(bank[6 + b][:, q4 * P:(q4 + 1) * P], hT0[:, c, t * P:(t + 1) * P],
                                               V["w2"][:, c * P:(c + 1) * P], start=(c == 0), stop=(c == 3))
                ins.then_inc(ff_out, 1)

        def act_ffn0(act):
            n = 0
            for b in range(NB):
                for c in range(4):
                    act.wait_ge(ff_mm, n + 1)
                    nc.scalar.activation(hT0[:, c, b * S:(b + 1) * S], bank[2 + n % 4][:], ACT.Gelu,
                                         bias=V["b1"][:, c:c + 1]).then_inc(ff_gelu, 1)
                    n += 1

        def vec_ffn0(dve, st):
            st.link(nc.vector.tensor_tensor(tmp[:], xt[:], bm(V["b2"], NT), ALU.add))
            for b in range(NB):
                dve.wait_ge(ff_out, b + 1)
                ins = nc.vector.tensor_tensor(xt[:, b * TB:(b + 1) * TB, :], bank[6 + b][:].rearrange("p (q d) -> p q d", d=D),
                                              tmp[:, b * TB:(b + 1) * TB, :], ALU.add)
            st.link(ins)

        def vec_affine_add(dve, st, src, g, b):
            st.link(nc.vector.tensor_tensor(tmp[:], src[:], bm(g, NT), ALU.mult))
            st.link(nc.vector.tensor_tensor(tmp[:], tmp[:], bm(b, NT), ALU.add))
            st.link(nc.vector.tensor_tensor(X[:], X[:], tmp[:], ALU.add))

        wr, wo0 = V["wr"], V["wo0"]
        wqkv = V["wqkv"].rearrange("p (h w c) -> p h w c", h=HF, w=4)
        qT = part(arenaB, 0, NB, 2, S)
        kT = part(arenaB, 2048, NB, 2, S)
        vv0 = part(arenaB, 4096, NT, CH * DF)
        wsel = part(arenaB, 6144, NB, 4, CH, DF)
        pb0 = part(arenaB, 8192, 3, S)
        pT0 = part(arenaB, 9728, 3, S)
        on0 = part(arenaB, 11264, 2, CH * DF)
        oT0 = part(arenaB, 11776, 2, 2 * P)
        bsel = sb("bsel", P, NB, 2, 2)
        dist = sb("dist", HF, NB)
        dt2 = sb("dt2", NB, HF)
        gm = sb("gm", NB, 8)
        gidx = sb("gidx", NB, 8, dt=U32)
        gidf = sb("gidf", NB, 8)
        gsel = sb("gsel", NB, HF)
        gkey = sb("gkey", NB, 8)
        ghead = sb("ghead", NB, 8, dt=I32)
        gsum, gmax = sb("gsum", NB, 1), sb("gmax", NB, 1)
        nmax0, rsum0 = sb("nmax0", P, NT, CH), sb("rsum0", P, NT, CH)
        rinv0 = sb("rinv0", P, NT, CH)
        rt_exp = sem("rt_exp")
        heads_ready, qk_mm, qk_ready, v_mm, v_ready = sem("heads_ready"), sem("qk_mm"), sem("qk_ready"), sem("v_mm"), sem("v_ready")
        sc_mm, sc_max, sc_exp, sc_turned = sem("sc_mm"), sem("sc_max"), sem("sc_exp"), sem("sc_turned")
        pT_dve, pT_act, pv_mm, o_norm, o_turned, oT_ready, wo_mm, x_added = (
            sem("pT_dve"), sem("pT_act"), sem("pv_mm"), sem("o_norm"), sem("o_turned"), sem("oT_ready"), sem("wo_mm"), sem("x_added"))


        def pe_route(pe):
            for b in range(NB):
                pe.wait_ge(ln_T, NB * 2 + b + 1)
                nc.tensor.matmul(bank[2 + b][0:HF, :], wr, xnT[:, b * S:(b + 1) * S], start=True, stop=True).then_inc(route_pe, 1)
            pe.wait_ge(route_vec, 1)
            nc.tensor.transpose(bank[4][0:NB, 0:HF], dist[:], ident[0:HF, 0:HF]).then_inc(route_pe, 1)

        def vec_route(dve, st):
            Vv = nc.vector
            for b in range(NB):
                dve.wait_ge(route_pe, b + 1)
                ins = Vv.tensor_reduce(dist[:, b:b + 1], bank[2 + b][0:HF, :], AX.X, ALU.add)
            st.link(ins)
            Vv.tensor_scalar(dist[:], dist[:], 1.0 / S, V["br_col"][0:HF], ALU.mult, ALU.add).then_inc(route_vec, 1)
            dve.wait_ge(route_pe, 3)
            st.link(Vv.tensor_reduce(gmax[:], bank[4][0:NB, 0:HF], AX.X, ALU.max))
            Vv.tensor_scalar(dt2[:], bank[4][0:NB, 0:HF], gmax[:], None, ALU.subtract).then_inc(route_vec, 1)
            dve.wait_ge(rt_exp, 1)
            st.link(Vv.reciprocal(gmax[:], gsum[:]))
            st.link(Vv.tensor_scalar(dt2[:], dt2[:], gmax[:], None, ALU.mult))
            st.link(Vv.max(gm[:], dt2[:]))
            st.link(Vv.max_index(gidx[:], gm[:], dt2[:]))
            st.link(Vv.tensor_copy(gidf[:], gidx[:]))
            st.link(Vv.tensor_scalar(gsel[:], V["iota16"][0:NB], gidf[:, 0:1], None, ALU.is_equal))
            for j in range(1, CH):
                st.link(Vv.scalar_tensor_tensor(gsel[:], V["iota16"][0:NB], gidf[:, j:j + 1], gsel[:], ALU.is_equal, ALU.add))
            st.link(Vv.tensor_tensor(gsel[:], gsel[:], V["rev16"][0:NB], ALU.mult))
            st.link(Vv.max(gkey[:], gsel[:]))
            st.link(Vv.tensor_scalar(ghead[:], gkey[:], -1.0, float(HF), ALU.mult, ALU.add))
            dve.wait_ge(*loaded["head0"])
            for b in range(NB):
                for j in range(CH):
                    h = dve.value_load(ghead[b:b + 1, j:j + 1], min_val=0, max_val=HF - 1)
                    r = slice(DF * (j % 2), DF * (j % 2 + 1))
                    Vv.tensor_copy(wsel[:, b, :, j, :].unsqueeze(1), wqkv[:, bass.ds(h, 1), :, :])
                    Vv.tensor_scalar(bsel[r, b, j // 2, 0:1], V["bq2"][r, bass.ds(h, 1)], DF ** -0.5, None, ALU.mult)
                    ins = Vv.tensor_copy(bsel[r, b, j // 2, 1:2], V["bk2"][r, bass.ds(h, 1)])
                ins.then_inc(heads_ready, 1)

        def act_route(act):
            act.wait_ge(route_vec, 2)
            nc.scalar.activation(dt2[:], dt2[:], ACT.Exp, accum_out=gsum[:]).then_inc(rt_exp, 1)

        def pe_qkv0(pe):
            n = 0
            for b in range(NB):
                pe.wait_ge(heads_ready, b + 1)
                for pair in range(2):
                    for w in range(2):
                        if n >= 4:
                            pe.wait_ge(qk_ready, n - 3)
                        nc.tensor.matmul(bank[2 + n % 4][:], wsel[:, b, w, 2 * pair:2 * pair + 2, :].rearrange("p j c -> p (j c)"),
                                         xnT[:, b * S:(b + 1) * S], start=True, stop=True).then_inc(qk_mm, 1)
                        n += 1
                for q2 in range(TB // 2):
                    if b == 1:
                        pe.wait_ge(v_ready, q2 + 1)
                    for q1 in range(2):
                        t = b * TB + 2 * q2 + q1
                        ins = nc.tensor.matmul(bank[6 + q2][:, q1 * CH * DF:(q1 + 1) * CH * DF], xnT[:, t * P:(t + 1) * P],
                                               wsel[:, b, 2, :, :].rearrange("p j c -> p (j c)"), start=True, stop=True)
                    ins.then_inc(v_mm, 1)

        def act_qk0(act):
            n = 0
            for b in range(NB):
                for pair in range(2):
                    for w, (dst, sc) in enumerate(((qT, DF ** -0.5), (kT, 1.0))):
                        act.wait_ge(qk_mm, n + 1)
                        nc.scalar.activation(dst[:, b, pair, :], bank[2 + n % 4][:], ACT.Identity, scale=sc,
                                             bias=bsel[:, b, pair, w:w + 1]).then_inc(qk_ready, 1)
                        n += 1

        def vec_v0(dve):
            for m in range(4):
                b = m // 2
                dve.wait_ge(v_mm, m + 1)
                for q1 in range(2):
                    ins = nc.vector.tensor_tensor(vv0[:, 2 * m + q1, :].rearrange("p (j c) -> p j c", j=CH),
                                                  bank[6 + m % 2][:, q1 * CH * DF:(q1 + 1) * CH * DF].rearrange("p (j c) -> p j c", j=CH),
                                                  wsel[:, b, 3, :, :], ALU.add)
                ins.then_inc(v_ready, 1)

        NU = NT * CH
        by_act = lambda n: n % 3 == 0
        acts_to = lambda n: n // 3 + 1
        dves_to = lambda n: n - n // 3

        def pe_attend0(pe):
            pe.wait_ge(qk_ready, 8)
            pe.wait_ge(v_ready, 4)
            for n in range(NU + 10):
                if n < NU:
                    t, h = n // CH, n % CH
                    b, r = t // TB, slice(DF * (h % 2), DF * (h % 2 + 1))
                    if n >= 2:
                        pe.wait_ge(sc_exp, n - 1)
                    nc.tensor.matmul(bank[n % 2][:], qT[r, b, h // 2, (t % TB) * P:(t % TB + 1) * P],
                                     kT[r, b, h // 2, :], start=True, stop=True).then_inc(sc_mm, 1)
                m = n - 1
                if 0 <= m < NU:
                    pe.wait_ge(sc_exp, m + 1)
                    if m >= 2:
                        w = m - 2
                        pe.wait_ge(*((pT_act, acts_to(w)) if by_act(w) else (pT_dve, dves_to(w))))
                    for k in range(TB):
                        ins = nc.tensor.transpose(bank[2 + m % 2][:, k * P:(k + 1) * P], pb0[:, m % 3, k * P:(k + 1) * P], ident)
                    ins.then_inc(sc_turned, 1)
                m = n - 2
                if 0 <= m < NU:
                    t, h = m // CH, m % CH
                    pe.wait_ge(*((pT_act, acts_to(m)) if by_act(m) else (pT_dve, dves_to(m))))
                    if h == 0 and t >= 2:
                        pe.wait_ge(o_norm, t - 1)
                    for k in range(TB):
                        ins = nc.tensor.matmul(bank[4 + t % 2][:, h * DF:(h + 1) * DF], pT0[:, m % 3, k * P:(k + 1) * P],
                                               vv0[:, t // TB * TB + k, h * DF:(h + 1) * DF], start=(k == 0), stop=(k == TB - 1))
                    ins.then_inc(pv_mm, 1)
                if n >= 7 and (n - 7) % CH == 0 and (n - 7) // CH < NT:
                    t = (n - 7) // CH
                    pe.wait_ge(o_norm, t + 1)
                    if t:
                        pe.wait_ge(oT_ready, t)
                    for c in range(2):
                        ins = nc.tensor.transpose(bank[6][:, c * P:(c + 1) * P], on0[:, t % 2, c * P:(c + 1) * P], ident)
                    ins.then_inc(o_turned, 1)
                if n >= 9 and (n - 9) % CH == 0 and (n - 9) // CH < NT:
                    t = (n - 9) // CH
                    pe.wait_ge(oT_ready, t + 1)
                    if t:
                        pe.wait_ge(x_added, t)
                    for c in range(2):
                        ins = nc.tensor.matmul(bank[7][:, 0:P], oT0[:, t % 2, c * P:(c + 1) * P], wo0[:, c * P:(c + 1) * P],
                                               start=(c == 0), stop=(c == 1))
                    ins.then_inc(wo_mm, 1)

        def vec_attend0(dve, st):
            for n in range(NU + 11):
                if n < NU:
                    t, h = n // CH, n % CH
                    dve.wait_ge(sc_mm, n + 1)
                    nc.vector.tensor_reduce(nmax0[:, t, h:h + 1], bank[n % 2][:], AX.X, ALU.max, negate=True).then_inc(sc_max, 1)
                m = n - 1
                if 0 <= m < NU and not by_act(m):
                    dve.wait_ge(sc_turned, m + 1)
                    if m >= 3:
                        dve.wait_ge(pv_mm, m - 2)
                    nc.vector.tensor_copy(pT0[:, m % 3, :], bank[2 + m % 2][:]).then_inc(pT_dve, 1)
                if n >= 6 and (n - 6) % CH == 0 and (n - 6) // CH < NT:
                    t = (n - 6) // CH
                    dve.wait_ge(sc_exp, CH * t + CH)
                    st.link(nc.vector.reciprocal(rinv0[:, t, :], rsum0[:, t, :]))
                    dve.wait_ge(pv_mm, CH * t + CH)
                    if t >= 2:
                        dve.wait_ge(o_turned, t - 1)
                    nc.vector.tensor_tensor(on0[:, t % 2, :].rearrange("p (h c) -> p h c", h=CH),
                                            bank[4 + t % 2][:, 0:CH * DF].rearrange("p (h c) -> p h c", h=CH),
                                            bc(rinv0[:, t, :], P, CH, DF), ALU.mult).then_inc(o_norm, 1)
                if n >= 10 and (n - 10) % CH == 0 and (n - 10) // CH < NT:
                    t = (n - 10) // CH
                    if t == 0:
                        dve.wait_ge(bias_added, 1)
                    dve.wait_ge(wo_mm, t + 1)
                    nc.vector.tensor_tensor(X[:, t, :], bank[7][:, 0:P], tmp[:, t, :], ALU.add).then_inc(x_added, 1)

        def act_attend0(act):
            for n in range(NU + 9):
                if n < NU:
                    t, h = n // CH, n % CH
                    act.wait_ge(sc_max, n + 1)
                    if n >= 3:
                        act.wait_ge(sc_turned, n - 2)
                    nc.scalar.activation(pb0[:, n % 3, :], bank[n % 2][:], ACT.Exp, bias=nmax0[:, t, h:h + 1],
                                         accum_out=rsum0[:, t, h:h + 1]).then_inc(sc_exp, 1)
                m = n - 1
                if 0 <= m < NU and by_act(m):
                    act.wait_ge(sc_turned, m + 1)
                    if m >= 3:
                        act.wait_ge(pv_mm, m - 2)
                    nc.scalar.copy(pT0[:, m % 3, :], bank[2 + m % 2][:]).then_inc(pT_act, 1)
                if n >= 8 and (n - 8) % CH == 0 and (n - 8) // CH < NT:
                    t = (n - 8) // CH
                    act.wait_ge(o_turned, t + 1)
                    if t >= 2:
                        act.wait_ge(wo_mm, t - 1)
                    nc.scalar.copy(oT0[:, t % 2, :], bank[6][:, 0:2 * P]).then_inc(oT_ready, 1)

        def pool_bias(pool, i, row, ready):
            pool.wait_ge(ln_done, NT * (i + 1))
            nc.gpsimd.tensor_tensor(tmp[:], X[:], bm(row, NT), ALU.add).then_inc(ready, 1)

        a1, bm1 = sb("a1", DC, D), sb("bm1", DC, D)
        m1 = sb("m1", P, NB * NC)
        vw1 = sb("vw1", NC, NB, D)
        s1 = part(arenaB, 0, NT, NC)
        e1 = part(arenaB, 1024, NT, NC)
        pT1 = part(arenaB, 2048, TOK)[0:NC]
        st1, mv1 = sb("st1", P, NB, 6), sb("mv1", P, NB, 2)
        mx1, rs1, ri1 = sb("mx1", P, NT), sb("rs1", P, NT), sb("ri1", P, NT)
        vr1, r1 = sb("vr1", P, NB), sb("r1", P, NB)
        fold1_mm, fold1_copy = sem("fold1_mm"), sem("fold1_copy")
        s1_mm, s1_copy, r1_ready = sem("s1_mm"), sem("s1_copy"), sem("r1_ready")
        e1_ready, e1_turned, pT1_ready, y1_mm = sem("e1_ready"), sem("e1_turned"), sem("pT1_ready"), sem("y1_mm")

        def pe_fold1(pe):
            pe.wait_ge(*loaded["l1"])
            pe.wait_ge(s0_copy, NT)
            nc.tensor.matmul(bank[2][0:DC, 0:D], V["wk1"], V["wq1"], start=True, stop=True).then_inc(fold1_mm, 1)
            nc.tensor.matmul(bank[3][0:DC, 0:D], V["wv1"], V["wo1T"], start=True, stop=True).then_inc(fold1_mm, 1)
            pe.wait_ge(fold1_copy, 2)
            nc.tensor.matmul(bank[2][:, 0:NB * NC], a1[:], V["ctxT"][0:DC], start=True, stop=True).then_inc(fold1_mm, 1)
            for b in range(NB):
                ins = nc.tensor.matmul(bank[3][0:NC, b * D:(b + 1) * D], V["ctxT"][0:DC, b * NC:(b + 1) * NC], bm1[:], start=True, stop=True)
            ins.then_inc(fold1_mm, 1)
            pe.wait_ge(fold1_copy, 4)

        def act_fold1(act):
            act.wait_ge(fold1_mm, 1)
            nc.scalar.copy(a1[:], bank[2][0:DC, 0:D]).then_inc(fold1_copy, 1)
            act.wait_ge(fold1_mm, 2)
            nc.scalar.copy(bm1[:], bank[3][0:DC, 0:D]).then_inc(fold1_copy, 1)
            act.wait_ge(fold1_mm, 3)
            nc.scalar.copy(m1[:], bank[2][:, 0:NB * NC]).then_inc(fold1_copy, 1)
            act.wait_ge(fold1_mm, 4)
            nc.scalar.copy(vw1[:], bank[3][0:NC, 0:NB * D].rearrange("p (b d) -> p b d", b=NB)).then_inc(fold1_copy, 1)

        def pe_l1x(pe):
            for b in range(NB):
                pe.wait_ge(ln_T, NB * 3 + b + 1)
                for q4 in range(TB):
                    t = b * TB + q4
                    ins = nc.tensor.matmul(bank[2 + b][:, q4 * NC:(q4 + 1) * NC], xnT[:, t * P:(t + 1) * P],
                                           m1[:, b * NC:(b + 1) * NC], start=True, stop=True)
                ins.then_inc(s1_mm, 1)
            pe.wait_ge(l1x_vec, 1)
            nc.tensor.matmul(bank[4][:, 0:NB], V["avg"], mv1[:, :, 0], start=True, stop=True).then_inc(avg1_mm, 1)
            pe.wait_ge(l1x_vec, 2)
            nc.tensor.matmul(bank[5][:, 0:NB], V["avg"], vr1[:], start=True, stop=True).then_inc(avg1_mm, 1)
            for t in range(NT):
                pe.wait_ge(e1_ready, t + 1)
                if t == 0:
                    pe.wait_ge(l1x_vec, 3)
                ins = nc.tensor.transpose(bank[4 + t // TB][0:NC, (t % TB) * P:(t % TB + 1) * P], e1[:, t, :], ident)
                if t % TB == TB - 1:
                    ins.then_inc(e1_turned, 1)
            for b in range(NB):
                pe.wait_ge(pT1_ready, b + 1)
                for q4 in range(TB):
                    t = b * TB + q4
                    ins = nc.tensor.matmul(bank[6 + b][:, q4 * P:(q4 + 1) * P], pT1[:, t * P:(t + 1) * P], vw1[:, b, :],
                                           start=True, stop=True)
                ins.then_inc(y1_mm, 1)

        def act_l1x(act):
            for b in range(NB):
                act.wait_ge(s1_mm, b + 1)
                nc.scalar.copy(s1[:, b * TB:(b + 1) * TB, :], bank[2 + b][:, 0:TB * NC].rearrange("p (q k) -> p q k", k=NC)).then_inc(s1_copy, 1)
            act.wait_ge(l1x_vec, 4)
            act.wait_ge(r1_ready, 1)
            for t in range(NT):
                nc.scalar.activation(e1[:, t, :], s1[:, t, :], ACT.Exp, scale=r1[:, t // TB:t // TB + 1], bias=mx1[:, t:t + 1],
                                     accum_out=rs1[:, t:t + 1]).then_inc(e1_ready, 1)
            for b in range(NB):
                act.wait_ge(e1_turned, b + 1)
                nc.scalar.copy(pT1[:, b * S:(b + 1) * S], bank[4 + b][0:NC, :]).then_inc(pT1_ready, 1)

        def pool_l1x(pool, st):
            pool.wait_ge(l1x_vec, 3)
            nc.gpsimd.tensor_tensor(r1[:], vr1[:], V["half"][:, 0:NB], ALU.pow).then_inc(r1_ready, 1)

        def vec_l1x(dve, st):
            Vv = nc.vector
            for b in range(NB):
                dve.wait_ge(s1_copy, b + 1)
                ins = Vv.bn_stats(st1[:, b, :], s1[:, b * TB:(b + 1) * TB, :].rearrange("p q k -> p (q k)"))
            st.link(ins)
            for b in range(NB):
                ins = Vv.bn_aggr(mv1[:, b, :], st1[:, b, :])
            ins.then_inc(l1x_vec, 1)
            Vv.tensor_reduce(mx1[:], s1[:], AX.X, ALU.max, negate=True)
            dve.wait_ge(l1x_vec, 1)
            dve.wait_ge(avg1_mm, 1)
            st.link(Vv.tensor_tensor(vr1[:], mv1[:, :, 0], bank[4][:, 0:NB], ALU.subtract))
            st.link(Vv.tensor_tensor(vr1[:], vr1[:], vr1[:], ALU.mult))
            Vv.tensor_tensor(vr1[:], vr1[:], mv1[:, :, 1], ALU.add).then_inc(l1x_vec, 1)
            dve.wait_ge(avg1_mm, 2)
            Vv.tensor_scalar(vr1[:], bank[5][:, 0:NB], 1e-5, None, ALU.add).then_inc(l1x_vec, 1)
            dve.wait_ge(r1_ready, 1)
            Vv.tensor_tensor(mx1[:].rearrange("p (b q) -> p b q", b=NB), mx1[:].rearrange("p (b q) -> p b q", b=NB),
                             bc(r1[:], P, NB, TB), ALU.mult).then_inc(l1x_vec, 1)
            dve.wait_ge(e1_ready, NT)
            st.link(Vv.reciprocal(ri1[:], rs1[:]))
            for t in range(NT):
                if t % TB == 0:
                    dve.wait_ge(y1_mm, t // TB + 1)
                ins = Vv.scalar_tensor_tensor(X[:, t, :], bank[6 + t // TB][:, (t % TB) * P:(t % TB + 1) * P], ri1[:, t:t + 1],
                                              X[:, t, :], ALU.mult, ALU.add)
            st.link(ins)

        NG = NCL + NTL
        sig = sb("sig", P, NG)
        sigq = sb("sigq", P, NTL)
        kd = sb("kd", P, KN - 1)
        rden = sb("rden", P, 1)
        sc1 = part(arenaB, 0, NT, NG)
        fl1 = part(arenaB, 576, NT, NG)
        lo1 = part(arenaB, 1152, NT, NG)
        vl1 = part(arenaB, 1728, NT, NG)
        dv1 = part(arenaB, 2304, NT, NG)
        ga1 = part(arenaB, 2880, NT, NG)
        ta1 = part(arenaB, 3456, NT, NG)
        tb1 = part(arenaB, 4032, NT, NG)
        ohT = part(arenaB, 4608, TOK)[0:NTL]
        got = part(arenaB, 5632, NT, TABW)
        hT1 = part(arenaB, 7176, TOK)[0:CMP]
        oh1 = part(arenaB, 8200, NT, NTL)
        ocl, osl, sg1 = part(arenaB, 8712, NT, NCL), part(arenaB, 8776, NT, TPC), part(arenaB, 8840, NT, TPC)
        cm1, cn1 = part(arenaB, 8904, NT, NCL), part(arenaB, 8968, NT, NCL)
        b81 = sb("b81", P, NT)
        comp = sb("comp", P, NT, 2)
        hh1, hx1 = part(arenaB, 9032, NT, GRID), part(arenaB, 9160, NT, GRID)
        mag = sb("mag", P, NT)
        sig_ready, dv_ready = sem("sig_ready"), sem("dv_ready")


        def vec_sigs(dve, st):
            Vv = nc.vector
            dve.wait_ge(*loaded["l1"])
            raw, sg = V["sigT"], sig[:, NCL:NG]
            st.link(Vv.tensor_scalar(sigq[:], raw, -0.3, None, ALU.is_lt))
            st.link(Vv.scalar_tensor_tensor(sigq[:], raw, 0.3, sigq[:], ALU.is_gt, ALU.subtract))
            st.link(Vv.tensor_tensor(sigq[:], sigq[:], raw, ALU.subtract))
            st.link(Vv.tensor_tensor(sg, sigq[:], raw, ALU.add))
            st.link(Vv.tensor_reduce(sig[:, 0:NCL], sg.rearrange("p (c j) -> p c j", c=NCL), AX.X, ALU.add))
            st.link(Vv.tensor_scalar(sigq[:, 0:NCL], sig[:, 0:NCL], 0.0, None, ALU.is_lt))
            st.link(Vv.scalar_tensor_tensor(sig[:, 0:NCL], sig[:, 0:NCL], 0.0, sigq[:, 0:NCL], ALU.is_gt, ALU.subtract))
            st.link(Vv.tensor_tensor(kd[:], V["knots"][:, 1:KN], V["knots"][:, 0:KN - 1], ALU.subtract))
            st.link(Vv.tensor_scalar(rden[:], V["temp"], 1e-6, None, ALU.add))
            Vv.reciprocal(rden[:], rden[:]).then_inc(sig_ready, 1)

        def pe_l1f(pe):
            pe.wait_ge(sig_ready, 1)
            for b in range(NB):
                pe.wait_ge(ln_T, NB * 4 + b + 1)
                for q4 in range(TB):
                    t = b * TB + q4
                    ins = nc.tensor.matmul(bank[2 + b][:, q4 * NG:(q4 + 1) * NG], xnT[:, t * P:(t + 1) * P], sig[:], start=True, stop=True)
                ins.then_inc(l1f_pe, 1)
            for b in range(NB):
                nc.tensor.matmul(bank[4 + b][0:CMP, :], V["cw1"], xnT[:, b * S:(b + 1) * S], start=True, stop=True).then_inc(l1f_pe, 1)
            pe.wait_ge(l1f_act, NB)
            for t in range(NT):
                ins = nc.tensor.matmul(bank[6][:, 2 * t:2 * t + 2], hT1[:, t * P:(t + 1) * P], V["cw2"][0:CMP], start=True, stop=True)
            ins.then_inc(l1f_pe, 1)
            if LAST_STAGE >= 7:
                pe.wait_ge(*loaded["l3"])
                pe.wait_ge(l1f_vec, 1)
                pe.wait_ge(l1f_vec, 2)
                pe_fold3(pe, 0, FOLD_EARLY)
            pe.wait_ge(l1f_vec, 4)
            for t in range(NT):
                ins = nc.tensor.transpose(bank[t // TB][0:NTL, (t % TB) * P:(t % TB + 1) * P], oh1[:, t, :], ident)
                if t % TB == TB - 1:
                    ins.then_inc(l1f_pe, 1)
            for m in range(NT // 2):
                if m % 2 == 0:
                    pe.wait_ge(l1f_act, m // 2 + 5)
                for k in range(2):
                    t = 2 * m + k
                    ins = nc.tensor.matmul(bank[2 + m][:, k * TABW:(k + 1) * TABW], ohT[:, t * P:(t + 1) * P], V["tab"][0:NTL],
                                           start=True, stop=True)
                ins.then_inc(l1f_pe, 1)
            if LAST_STAGE >= 7:
                pe.wait_ge(l1f_act, NT // 2 + 6)
                pe_fold3(pe, FOLD_EARLY, H3 // 2)

        def act_l1f(act):
            for b in range(NB):
                act.wait_ge(l1f_pe, b + 3)
                nc.scalar.activation(hT1[:, b * S:(b + 1) * S], bank[4 + b][0:CMP, :], ACT.Gelu, bias=V["cb1"][0:CMP]).then_inc(l1f_act, 1)
            act.wait_ge(l1f_vec, 1)
            nc.scalar.activation(sc1[:], sc1[:], ACT.Exp, scale=-1.0).then_inc(l1f_act, 1)
            act.wait_ge(l1f_vec, 2)
            nc.scalar.activation(comp[:], comp[:], ACT.Tanh).then_inc(l1f_act, 1)
            if LAST_STAGE >= 7:
                act_fold3(act, 0, FOLD_EARLY)
            for b in range(NB):
                act.wait_ge(l1f_pe, b + 6)
                nc.scalar.copy(ohT[:, b * S:(b + 1) * S], bank[b][0:NTL, :]).then_inc(l1f_act, 1)
            for m in range(NT // 2):
                act.wait_ge(l1f_pe, m + 8)
                nc.scalar.copy(got[:, 2 * m:2 * m + 2, :], bank[2 + m][:, 0:2 * TABW].rearrange("p (k n) -> p k n", k=2)).then_inc(l1f_act, 1)
            if LAST_STAGE >= 7:
                act_fold3(act, FOLD_EARLY, H3 // 2)

        def pool_l1f(pool, st):
            G = nc.gpsimd
            pool.wait_ge(l1f_vec, 3)
            st.link(G.tensor_scalar(dv1[:], lo1[:], float(SPLITK), kd[:, SPLITK:SPLITK + 1], ALU.is_equal, ALU.mult))
            for k in range(SPLITK + 1, KN - 1):
                st.link(G.tensor_scalar(tb1[:], lo1[:], float(k), kd[:, k:k + 1], ALU.is_equal, ALU.mult))
                ins = G.tensor_tensor(dv1[:], dv1[:], tb1[:], ALU.add)
                if k < KN - 2:
                    st.link(ins)
            ins.then_inc(dv_ready, 1)

        def first_best(dve, st, vals, best, onehot):
            Vv = nc.vector
            rev = bm(V["rev8"], NT)
            st.link(Vv.tensor_reduce(best[:], vals[:], AX.X, ALU.max))
            st.link(Vv.tensor_tensor(onehot[:], vals[:], bc(best[:], P, NT, 8), ALU.is_equal))
            st.link(Vv.tensor_tensor(onehot[:], onehot[:], rev, ALU.mult))
            st.link(Vv.tensor_reduce(best[:], onehot[:], AX.X, ALU.max))
            st.link(Vv.tensor_tensor(onehot[:], onehot[:], bc(best[:], P, NT, 8), ALU.is_equal))

        def vec_l1f(dve, st):
            Vv = nc.vector
            for b in range(NB):
                dve.wait_ge(l1f_pe, b + 1)
                ins = Vv.tensor_scalar(sc1[:, b * TB:(b + 1) * TB, :], bank[2 + b][:, 0:TB * NG].rearrange("p (q k) -> p q k", k=NG),
                                       rden[:], None, ALU.mult)
            ins.then_inc(l1f_vec, 1)
            dve.wait_ge(l1f_pe, 5)
            Vv.tensor_tensor(comp[:], bank[6][:, 0:2 * NT].rearrange("p (t c) -> p t c", c=2), bm(V["cb2"], NT), ALU.add).then_inc(l1f_vec, 1)
            dve.wait_ge(l1f_act, 3)
            st.link(Vv.tensor_scalar(sc1[:], sc1[:], 1.0, None, ALU.add))
            st.link(Vv.reciprocal(fl1[:], sc1[:]))
            st.link(Vv.tensor_scalar(fl1[:], fl1[:], float(KN - 1), None, ALU.mult))
            st.link(Vv.tensor_scalar(lo1[:], fl1[:], 1.0, None, ALU.is_ge))
            for k in range(2, KN - 1):
                ins = Vv.scalar_tensor_tensor(lo1[:], fl1[:], float(k), lo1[:], ALU.is_ge, ALU.add)
                if k < KN - 2:
                    st.link(ins)
            ins.then_inc(l1f_vec, 1)
            dve.wait_ge(l1f_vec, 3)
            st.link(Vv.tensor_tensor(fl1[:], fl1[:], lo1[:], ALU.subtract))
            st.link(Vv.tensor_scalar(vl1[:], lo1[:], 0.0, V["knots"][:, 0:1], ALU.is_equal, ALU.mult))
            for k in range(1, KN - 1):
                st.link(Vv.tensor_scalar(ta1[:], lo1[:], float(k), V["knots"][:, k:k + 1], ALU.is_equal, ALU.mult))
                st.link(Vv.tensor_tensor(vl1[:], vl1[:], ta1[:], ALU.add))
            st.link(Vv.tensor_scalar(ga1[:], lo1[:], 0.0, kd[:, 0:1], ALU.is_equal, ALU.mult))
            for k in range(1, SPLITK):
                st.link(Vv.tensor_scalar(ta1[:], lo1[:], float(k), kd[:, k:k + 1], ALU.is_equal, ALU.mult))
                st.link(Vv.tensor_tensor(ga1[:], ga1[:], ta1[:], ALU.add))
            dve.wait_ge(dv_ready, 1)
            st.link(Vv.tensor_tensor(ga1[:], ga1[:], dv1[:], ALU.add))
            st.link(Vv.tensor_tensor(ga1[:], fl1[:], ga1[:], ALU.mult))
            st.link(Vv.tensor_tensor(ga1[:], vl1[:], ga1[:], ALU.add))
            first_best(dve, st, ga1[:, :, 0:NCL], b81, ocl)
            ins = None
            for t in range(NT):
                ins = Vv.tensor_tensor(oh1[:, t].rearrange("p (c j) -> p c j", c=NCL), ga1[:, t, NCL:NG].rearrange("p (c j) -> p c j", c=NCL),
                                       bc(ocl[:, t], P, NCL, TPC), ALU.mult)
            st.link(ins)
            for t in range(NT):
                ins = Vv.tensor_reduce(sg1[:, t], oh1[:, t].rearrange("p (c j) -> p j c", c=NCL), AX.X, ALU.add)
            st.link(ins)
            first_best(dve, st, sg1, b81, osl)
            for t in range(NT):
                ins = Vv.tensor_tensor(oh1[:, t].rearrange("p (c j) -> p c j", c=NCL), bm(osl[:, t], NCL), bc(ocl[:, t], P, NCL, TPC), ALU.mult)
            ins.then_inc(l1f_vec, 1)
            dve.wait_ge(l1f_act, NT // 2 + 6)
            dve.wait_ge(l1f_act, 4)
            G_ = GRID
            st.link(Vv.tensor_tensor(hh1[:], got[:, :, 0:G_], bc(comp[:, :, 0], P, NT, G_), ALU.mult))
            st.link(Vv.tensor_tensor(hx1[:], got[:, :, G_:2 * G_], bc(comp[:, :, 1], P, NT, G_), ALU.mult))
            st.link(Vv.tensor_tensor(hh1[:], hh1[:], hx1[:], ALU.add))
            st.link(Vv.tensor_tensor(hh1[:], hh1[:], got[:, :, 2 * G_:3 * G_], ALU.add))
            st.link(Vv.tensor_scalar(hh1[:], hh1[:], 0.0, None, ALU.max))
            st.link(Vv.tensor_tensor(hh1[:], hh1[:], got[:, :, 3 * G_:4 * G_], ALU.mult))
            st.link(Vv.tensor_reduce(mag[:], hh1[:], AX.X, ALU.add))
            st.link(Vv.tensor_tensor(mag[:], mag[:], got[:, :, 4 * G_], ALU.add))
            st.link(Vv.tensor_scalar(mag[:], mag[:], V["oscale"], None, ALU.mult))
            for t in range(NT):
                ins = Vv.scalar_tensor_tensor(xt[:, t, :], got[:, t, 4 * G_ + 1:TABW], mag[:, t:t + 1], xn[:, t, :], ALU.mult, ALU.add)
            st.link(ins)

        var2, mv2 = sb("var2", P, NT), sb("mv2", P, NT)

        def pool_rstd_twice(pool, st, i, ready):
            pool.wait_ge(ln_rstd, NB * (i + 1))
            G = nc.gpsimd
            st.link(G.tensor_tensor(var2[:], rstd[:], rstd[:], ALU.mult))
            st.link(G.tensor_tensor(var2[:], var2[:], mv[:, :, 1], ALU.mult))
            st.link(G.tensor_scalar(var2[:], var2[:], 1e-5, None, ALU.add))
            G.tensor_tensor(mv2[:], var2[:], V["half"][:, 0:NT], ALU.pow).then_inc(ready, 1)

        twice_ready = sem("twice_ready")
        final_stage_done, stored = sem("final_stage_done"), sem("stored")

        KL = S
        cn2 = sb("cn2", NC, NB, DC)
        stc, mvc, rdc = sb("stc", NC, NB, 6), sb("mvc", NC, NB, 2), sb("rdc", NC, NB)
        cnT2 = sb("cnT2", DC, NB * NC)
        kvc = sb("kvc", NC, NB, 2 * D)
        sqc, ssc = sb("sqc", NC, NB, D), sb("ssc", NC, NB, H2)
        kcT = sb("kcT", P, NB, NC)
        qkv2 = part(arenaB, 0, NT, 3 * D)
        sq2 = part(arenaB, 3072, NT, 2 * D)
        pT2 = part(arenaB, 3072, 3, 5 * P)
        qT2, kT2 = part(arenaB, 5120, TOK), part(arenaB, 6144, TOK)
        pb2 = part(arenaB, 7168, 3, KL + NC)
        sc2 = [part(v[:].rearrange("p t d -> p (t d)"), 0, TB * H2, NC) for v in (xt, xn)]
        oT2 = part(tmp2[:].rearrange("p t d -> p (t d)"), 0, 2, H2 * P)[0:D2]
        ss2, inv2 = sb("ss2", P, NT, 2 * H2), sb("inv2", P, NT, 2 * H2)
        nma, nmb, nm2 = sb("nma", P, NT * H2), sb("nmb", P, NT * H2), sb("nm2", P, NT * H2)
        rsa, rsb, ri2 = sb("rsa", P, NT, H2), sb("rsb", P, NT, H2), sb("ri2", P, NT, H2)
        c2_mm, c2_copy = sem("c2_mm"), sem("c2_copy")
        lat_done, qkv2_mm, qkv2_copy, ss2_ready, inv2_ready, qk2_scaled, qk2_turned, qkT2_ready = (
            sem("lat_done"), sem("qkv2_mm"), sem("qkv2_copy"), sem("ss2_ready"), sem("inv2_ready"), sem("qk2_scaled"), sem("qk2_turned"), sem("qkT2_ready"))
        a2_mm, a2_max, a2_exp, a2_turned, p2_dve, p2_act, pv2_mm, oT2_ready, wo2_mm, x2_added = (
            sem(f"{n}") for n in ("a2_mm", "a2_max", "a2_exp", "a2_turned", "p2_dve", "p2_act", "pv2_mm",
                                  "oT2_ready", "wo2_mm", "x2_added"))

        def vec_c2_moments(dve, st):
            dve.wait_ge(*loaded["l2"])
            cr = V["ctxr"][0:NC].rearrange("p (b d) -> p b d", b=NB)
            for b in range(NB):
                ins = nc.vector.bn_stats(stc[:, b, :], cr[:, b, :])
            st.link(ins)
            for b in range(NB):
                ins = nc.vector.bn_aggr(mvc[:, b, :], stc[:, b, :])
            ins.then_inc(c2_stats, 1)

        def pool_c2_rstd(pool, st):
            pool.wait_ge(c2_stats, 1)
            st.link(nc.gpsimd.tensor_scalar(rdc[:], mvc[:, :, 1], 1e-5, None, ALU.add))
            nc.gpsimd.tensor_tensor(rdc[:], rdc[:], V["half"][0:NC, 0:NB], ALU.pow).then_inc(c2_powers, 1)

        def vec_c2_norm(dve, st):
            cr = V["ctxr"][0:NC].rearrange("p (b d) -> p b d", b=NB)
            dve.wait_ge(c2_powers, 1)
            for b in range(NB):
                ins = nc.vector.tensor_scalar(cn2[:, b, :], cr[:, b, :], mvc[:, b, 0:1], rdc[:, b:b + 1], ALU.subtract, ALU.mult)
            st.link(ins)
            st.link(nc.vector.tensor_tensor(cn2[:], cn2[:], bm(V["lnx_g"][0:NC], NB), ALU.mult))
            nc.vector.tensor_tensor(cn2[:], cn2[:], bm(V["lnx_b"][0:NC], NB), ALU.add).then_inc(c2_scaled, 1)

        def pe_c2(pe):
            pe.wait_ge(kern_act, 6)
            pe.wait_ge(c2_scaled, 1)
            for b in range(NB):
                ins = nc.tensor.transpose(bank[6][0:DC, b * NC:(b + 1) * NC], cn2[:, b, :], ident[0:NC, 0:NC])
            ins.then_inc(c2_mm, 1)
            pe.wait_ge(c2_copy, 1)
            for b in range(NB):
                ins = nc.tensor.matmul(bank[7][0:NC, b * 2 * D:(b + 1) * 2 * D], cnT2[:, b * NC:(b + 1) * NC], V["wkvT"][0:DC], start=True, stop=True)
            ins.then_inc(c2_mm, 1)

        def act_c2(act):
            act.wait_ge(c2_mm, 1)
            nc.scalar.copy(cnT2[:], bank[6][0:DC, 0:NB * NC]).then_inc(c2_copy, 1)
            act.wait_ge(c2_mm, 2)
            nc.scalar.copy(kvc[:], bank[7][0:NC, :].rearrange("p (b n) -> p b n", b=NB)).then_inc(c2_copy, 1)

        def vec_c2_squares(dve, st):
            dve.wait_ge(c2_copy, 2)
            st.link(nc.vector.tensor_tensor(sqc[:], kvc[:, :, 0:D], kvc[:, :, 0:D], ALU.mult))
            nc.vector.tensor_reduce(ssc[:].rearrange("p b h -> p (b h)"), sqc[:].rearrange("p b (h c) -> p (b h) c", h=H2), AX.X, ALU.add).then_inc(c2_stats, 1)

        def pool_c2_inv(pool, st):
            pool.wait_ge(c2_stats, 2)
            st.link(nc.gpsimd.tensor_scalar(ssc[:], ssc[:], 1.0 / D2, 1e-16, ALU.mult, ALU.max))
            nc.gpsimd.tensor_tensor(ssc[:].rearrange("p b h -> p (b h)"), ssc[:].rearrange("p b h -> p (b h)"),
                                    V["half"][0:NC, 0:NB * H2], ALU.pow).then_inc(c2_powers, 1)

        def vec_c2_scale(dve):
            dve.wait_ge(c2_powers, 2)
            for b in range(NB):
                kk = kvc[:, b, 0:D].rearrange("p (h c) -> p h c", h=H2)
                ins = nc.vector.tensor_tensor(kk, kk, bc(ssc[:, b], NC, H2, D2), ALU.mult)
            ins.then_inc(c2_scaled, 1)

        def pe_c2_keys(pe):
            pe.wait_ge(c2_scaled, 2)
            for b in range(NB):
                ins = nc.tensor.transpose(bank[6][:, b * NC:(b + 1) * NC], kvc[:, b, 0:D], ident[0:NC, 0:NC])
            ins.then_inc(c2_mm, 1)

        def act_c2_keys(act):
            act.wait_ge(c2_mm, 3)
            nc.scalar.activation(kcT[:], bank[6][:, 0:NB * NC].rearrange("p (b k) -> p b k", b=NB), ACT.Copy, scale=V["kn"]).then_inc(c2_copy, 1)

        def vec_latents(dve):
            dve.wait_ge(twice_ready, 2)
            for t in range(NT):
                nc.vector.tensor_scalar(tmp2[:, t, :], xn[:, t, :], mv2[:, t:t + 1], None, ALU.mult).then_inc(lat_done, 1)

        def pe_qkv2(pe):
            at = NB * DC
            for t in range(NT):
                if t % TB == 0:
                    pe.wait_ge(ln_T, NB * 5 + t // TB + 1)
                if t >= 4:
                    pe.wait_ge(qkv2_copy, t - 3)
                nc.tensor.matmul(bank[2 + t % 4][:, 0:3 * D], xnT[:, t * P:(t + 1) * P], packed["l2"][:, at:at + 3 * D],
                                 start=True, stop=True).then_inc(qkv2_mm, 1)
            for w in range(2):
                for b in range(NB):
                    pe.wait_ge(qk2_scaled, b + 1)
                    for q4 in range(TB):
                        ins = nc.tensor.transpose(bank[2 * w + b][:, q4 * P:(q4 + 1) * P], qkv2[:, b * TB + q4, w * D:(w + 1) * D], ident)
                    ins.then_inc(qk2_turned, 1)

        def act_qkv2(act):
            for t in range(NT):
                act.wait_ge(qkv2_mm, t + 1)
                nc.scalar.copy(qkv2[:, t, :], bank[2 + t % 4][:, 0:3 * D]).then_inc(qkv2_copy, 1)
            for w, (dst, g) in enumerate(((qT2, V["qn"]), (kT2, V["kn"]))):
                for b in range(NB):
                    act.wait_ge(qk2_turned, 2 * w + b + 1)
                    nc.scalar.activation(dst[:, b * S:(b + 1) * S], bank[2 * w + b][:], ACT.Copy, scale=g).then_inc(qkT2_ready, 1)

        def vec_qkv2(dve, st):
            for b in range(NB):
                r = slice(b * TB, (b + 1) * TB)
                dve.wait_ge(qkv2_copy, (b + 1) * TB)
                st.link(nc.vector.tensor_tensor(sq2[:, r], qkv2[:, r, 0:2 * D], qkv2[:, r, 0:2 * D], ALU.mult))
                nc.vector.tensor_reduce(ss2[:, r].rearrange("p t g -> p (t g)"), sq2[:, r].rearrange("p t (g c) -> p (t g) c", c=D2),
                                        AX.X, ALU.add).then_inc(ss2_ready, 1)
            for b in range(NB):
                r = range(b * TB, (b + 1) * TB)
                dve.wait_ge(inv2_ready, b + 1)
                for t in r:
                    v = qkv2[:, t, 0:2 * D].rearrange("p (g c) -> p g c", c=D2)
                    ins = nc.vector.tensor_tensor(v, v, bc(inv2[:, t], P, 2 * H2, D2), ALU.mult)
                ins.then_inc(qk2_scaled, 1)

        def pool_qkv2(pool, st):
            for b in range(NB):
                r = slice(b * TB, (b + 1) * TB)
                pool.wait_ge(ss2_ready, b + 1)
                st.link(nc.gpsimd.tensor_scalar(ss2[:, r], ss2[:, r], 1.0 / D2, 1e-16, ALU.mult, ALU.max))
                nc.gpsimd.tensor_tensor(inv2[:, r].rearrange("p t g -> p (t g)"), ss2[:, r].rearrange("p t g -> p (t g)"),
                                        V["half"][:, 0:TB * 2 * H2], ALU.pow).then_inc(inv2_ready, 1)

        NU2 = NT * H2

        def ctx_unit(n):
            t, h = n // H2, n % H2
            return t // TB * TB * H2 + h * TB + t % TB

        def pe_attend2(pe):
            pe.wait_ge(c2_copy, 3)
            for i in range(NB * H2):
                b, h = i // H2, i % H2
                pe.wait_ge(qkT2_ready, b + 1)
                r = slice(D2 * h, D2 * (h + 1))
                for q4 in range(TB):
                    t = b * TB + q4
                    ins = nc.tensor.matmul(bank[4 + i][:, q4 * NC:(q4 + 1) * NC], qT2[r, t * P:(t + 1) * P], kcT[r, b, :], start=True, stop=True)
                ins.then_inc(c2_mm, 1)
            pe.wait_ge(qkT2_ready, 4)
            for n in range(NU2 + 5):
                if n < NU2:
                    t, h = n // H2, n % H2
                    b, r = t // TB, slice(D2 * h, D2 * (h + 1))
                    if n >= 3:
                        pe.wait_ge(a2_exp, n - 2)
                    nc.tensor.matmul(bank[n % 3][:], qT2[r, t * P:(t + 1) * P], kT2[r, b * S:(b + 1) * S], start=True, stop=True).then_inc(a2_mm, 1)
                m = n - 2
                if 0 <= m < NU2:
                    pe.wait_ge(a2_exp, m + 1)
                    if m >= 2:
                        pe.wait_ge(p2_dve, m - 1)
                    for k in range(TB):
                        nc.tensor.transpose(bank[4 + m % 2][:, k * P:(k + 1) * P], pb2[:, m % 3, k * P:(k + 1) * P], ident)
                    if m:
                        pe.wait_ge(p2_act, m)
                    nc.tensor.transpose(bank[3][0:NC, 0:P], pb2[:, m % 3, KL:KL + NC], ident).then_inc(a2_turned, 1)
                m = n - 3
                if 0 <= m < NU2:
                    t, h = m // H2, m % H2
                    pe.wait_ge(p2_dve, m + 1)
                    pe.wait_ge(p2_act, m + 1)
                    if h == 0 and t >= 2:
                        pe.wait_ge(x2_added, t - 1)
                    o = bank[6 + t % 2][0:D2, h * P:(h + 1) * P]
                    for k in range(TB):
                        nc.tensor.matmul(o, qkv2[:, t // TB * TB + k, 2 * D + h * D2:2 * D + (h + 1) * D2], pT2[:, m % 3, k * P:(k + 1) * P],
                                         start=(k == 0), stop=False)
                    nc.tensor.matmul(o, kvc[:, t // TB, D + h * D2:D + (h + 1) * D2], pT2[0:NC, m % 3, TB * P:(TB + 1) * P],
                                     start=False, stop=True).then_inc(pv2_mm, 1)
                if n >= 5 and n % 2 == 1 and (n - 5) // 2 < NT:
                    t = (n - 5) // 2
                    pe.wait_ge(oT2_ready, t + 1)
                    for h in range(H2):
                        ins = nc.tensor.matmul(bank[6 + t % 2][:, (2 + h) * P:(3 + h) * P], oT2[:, t % 2, h * P:(h + 1) * P],
                                               V["wo2T"][0:D2, h * D:(h + 1) * D], start=True, stop=True)
                    ins.then_inc(wo2_mm, 1)

        def vec_attend2(dve, st):
            Vv = nc.vector
            for i in range(NB * H2):
                b, at = i // H2, i % H2 * TB
                dve.wait_ge(c2_mm, 4 + i)
                ins = Vv.tensor_tensor(sc2[b][:, at:at + TB, :], bank[4 + i][:, 0:TB * NC].rearrange("p (u k) -> p u k", k=NC),
                                       bm(maskb[:, 1, b, :], TB), ALU.add)
            st.link(ins)
            for b in range(NB):
                ins = Vv.tensor_reduce(nmb[:, b * TB * H2:(b + 1) * TB * H2], sc2[b], AX.X, ALU.max, negate=True)
            st.link(ins)
            for n in range(NU2 + 6):
                if n >= 6 and n % 2 == 0 and (n - 6) // 2 < NT:
                    t = (n - 6) // 2
                    if t == 0:
                        dve.wait_ge(bias_added, 2)
                    st.link(Vv.tensor_tensor(rsa[:, t], rsa[:, t], rsb[:, t], ALU.add))
                    st.link(Vv.reciprocal(ri2[:, t], rsa[:, t]))
                    dve.wait_ge(wo2_mm, t + 1)
                    o = bank[6 + t % 2]
                    st.link(Vv.scalar_tensor_tensor(X[:, t, :], o[:, 2 * P:3 * P], ri2[:, t, 0:1], tmp[:, t, :], ALU.mult, ALU.add))
                    Vv.scalar_tensor_tensor(X[:, t, :], o[:, 3 * P:4 * P], ri2[:, t, 1:2], X[:, t, :], ALU.mult, ALU.add).then_inc(x2_added, 1)
                if n < NU2:
                    dve.wait_ge(a2_mm, n + 1)
                    st.link(Vv.tensor_reduce(nma[:, n:n + 1], bank[n % 3][:], AX.X, ALU.max, negate=True))
                    Vv.tensor_scalar(nm2[:, n:n + 1], nma[:, n:n + 1], nmb[:, ctx_unit(n):ctx_unit(n) + 1], D2 ** -0.5, ALU.min, ALU.mult).then_inc(a2_max, 1)
                m = n - 2
                if 0 <= m < NU2:
                    dve.wait_ge(a2_turned, m + 1)
                    if m >= 3:
                        dve.wait_ge(pv2_mm, m - 2)
                    Vv.tensor_copy(pT2[:, m % 3, 0:TB * P], bank[4 + m % 2][:]).then_inc(p2_dve, 1)

        def act_attend2(act):
            for n in range(NU2 + 4):
                if n < NU2:
                    t, h = n // H2, n % H2
                    act.wait_ge(a2_max, n + 1)
                    if n >= 3:
                        act.wait_ge(a2_turned, n - 2)
                    nc.scalar.activation(pb2[:, n % 3, 0:KL], bank[n % 3][:], ACT.Exp, bias=nm2[:, n:n + 1], scale=D2 ** -0.5,
                                         accum_out=rsa[:, t, h:h + 1])
                    nc.scalar.activation(pb2[:, n % 3, KL:KL + NC], sc2[t // TB][:, ctx_unit(n) % (TB * H2), :], ACT.Exp, bias=nm2[:, n:n + 1],
                                         scale=D2 ** -0.5, accum_out=rsb[:, t, h:h + 1]).then_inc(a2_exp, 1)
                m = n - 2
                if 0 <= m < NU2:
                    act.wait_ge(a2_turned, m + 1)
                    if m >= 3:
                        act.wait_ge(pv2_mm, m - 2)
                    nc.scalar.copy(pT2[0:NC, m % 3, TB * P:(TB + 1) * P], bank[3][0:NC, 0:P]).then_inc(p2_act, 1)
                if n >= 4 and n % 2 == 0 and (n - 4) // 2 < NT:
                    t = (n - 4) // 2
                    act.wait_ge(pv2_mm, 2 * t + 2)
                    if t >= 2:
                        act.wait_ge(wo2_mm, t - 1)
                    nc.scalar.copy(oT2[:, t % 2], bank[6 + t % 2][0:D2, 0:2 * P]).then_inc(oT2_ready, 1)

        NX = NE + NSH
        WE = 3 * HE
        lg, m8, ix8, ixf = sb("lg", P, NT, NE), sb("m8", P, NT, 8), sb("ix8", P, NT, 8, dt=U32), sb("ixf", P, NT, 8)
        e2x, wa, wb = sb("e2x", P, NT), sb("wa", P, NT), sb("wb", P, NT)
        cw, cwb = sb("cw", P, NT, NE), sb("cwb", P, NT, NE)
        hid2 = part(arenaB, 0, 2, 2, S)
        sil2 = part(arenaB, 2048, 3, S)
        lg_mm, lg_diff, lg_exp = sem("lg_mm"), sem("lg_diff"), sem("lg_exp")
        up_mm, silu_ready, hid_ready, down_mm, moe_added = sem("up_mm"), sem("silu_ready"), sem("hid_ready"), sem("down_mm"), sem("moe_added")

        def pe_moe(pe):
            for t in range(NT):
                if t % TB == 0:
                    pe.wait_ge(ln_T, NB * 6 + t // TB + 1)
                ins = nc.tensor.matmul(bank[7][:, t * NE:(t + 1) * NE], xnT[:, t * P:(t + 1) * P], V["router"], start=True, stop=True)
            ins.then_inc(lg_mm, 1)
            pe.wait_ge(*loaded["moe"])
            for n in range(4 * NX + 2):
                if n < 4 * NX:
                    e, b, c = n // 4, n // 2 % 2, n % 2
                    w = V["moe"][:, e * WE:(e + 1) * WE]
                    if n >= 2:
                        pe.wait_ge(hid_ready, n - 1)
                    nc.tensor.matmul(bank[n % 2][:], w[:, c * P:(c + 1) * P], xnT[:, b * S:(b + 1) * S], start=True, stop=True).then_inc(up_mm, 1)
                    nc.tensor.matmul(bank[2 + n % 2][:], w[:, HE + c * P:HE + (c + 1) * P], xnT[:, b * S:(b + 1) * S],
                                     start=True, stop=True).then_inc(up_mm, 1)
                if n >= 3 and n % 2 == 1:
                    m = (n - 3) // 2
                    w = V["moe"][:, m // 2 * WE:(m // 2 + 1) * WE]
                    pe.wait_ge(hid_ready, 2 * m + 2)
                    if m >= 3:
                        pe.wait_ge(moe_added, m - 2)
                    for q4 in range(TB):
                        for c in range(2):
                            ins = nc.tensor.matmul(bank[4 + m % 3][:, q4 * P:(q4 + 1) * P], hid2[:, m % 2, c, q4 * P:(q4 + 1) * P],
                                                   w[:, 2 * HE + c * P:2 * HE + (c + 1) * P], start=(c == 0), stop=(c == 1))
                    ins.then_inc(down_mm, 1)

        def act_moe(act):
            act.wait_ge(lg_diff, 1)
            nc.scalar.activation(e2x[:], e2x[:], ACT.Exp).then_inc(lg_exp, 1)
            for n in range(4 * NX):
                act.wait_ge(up_mm, 2 * n + 1)
                if n >= 3:
                    act.wait_ge(hid_ready, n - 2)
                nc.scalar.activation(sil2[:, n % 3, :], bank[n % 2][:], ACT.Silu).then_inc(silu_ready, 1)

        def vec_moe(dve, st):
            Vv = nc.vector
            dve.wait_ge(lg_mm, 1)
            st.link(Vv.tensor_tensor(lg[:], bank[7][:, 0:NT * NE].rearrange("p (t e) -> p t e", e=NE), bm(V["ebias"], NT), ALU.add))
            for t in range(NT):
                ins = Vv.max(m8[:, t, :], lg[:, t, :])
            st.link(ins)
            Vv.tensor_tensor(e2x[:], m8[:, :, 1], m8[:, :, 0], ALU.subtract).then_inc(lg_diff, 1)
            for t in range(NT):
                ins = Vv.max_index(ix8[:, t, :], m8[:, t, :], lg[:, t, :])
            st.link(ins)
            st.link(Vv.tensor_copy(ixf[:], ix8[:]))
            dve.wait_ge(lg_exp, 1)
            st.link(Vv.tensor_scalar(wb[:], e2x[:], 1.0, None, ALU.add))
            st.link(Vv.reciprocal(wa[:], wb[:]))
            st.link(Vv.tensor_tensor(wb[:], e2x[:], wa[:], ALU.mult))
            for i, (dst, w) in enumerate(((cw, wa), (cwb, wb))):
                st.link(Vv.tensor_tensor(dst[:], bm(V["iota8"], NT), bc(ixf[:, :, i], P, NT, NE), ALU.is_equal))
                st.link(Vv.tensor_tensor(dst[:], dst[:], bc(w[:], P, NT, NE), ALU.mult))
            st.link(Vv.tensor_tensor(cw[:], cw[:], cwb[:], ALU.add))
            for n in range(4 * NX + 4):
                if n < 4 * NX:
                    b, c, m = n // 2 % 2, n % 2, n // 2
                    dve.wait_ge(silu_ready, n + 1)
                    dve.wait_ge(up_mm, 2 * n + 2)
                    if m >= 2:
                        dve.wait_ge(down_mm, m - 1)
                    Vv.tensor_tensor(hid2[:, m % 2, c, :], sil2[:, n % 3, :], bank[2 + n % 2][:], ALU.mult).then_inc(hid_ready, 1)
                if n >= 4 and n % 2 == 0:
                    m = (n - 4) // 2
                    e, b = m // 2, m % 2
                    dve.wait_ge(down_mm, m + 1)
                    if m >= 2:
                        dve.wait_ge(moe_added, m - 1)
                    if e < NE:
                        for q4 in range(TB):
                            t = b * TB + q4
                            ins = Vv.scalar_tensor_tensor(X[:, t, :], bank[4 + m % 3][:, q4 * P:(q4 + 1) * P], cw[:, t, e:e + 1], X[:, t, :],
                                                          ALU.mult, ALU.add)
                    else:
                        ins = Vv.tensor_tensor(X[:, b * TB:(b + 1) * TB, :], bank[4 + m % 3][:].rearrange("p (q d) -> p q d", d=D),
                                               X[:, b * TB:(b + 1) * TB, :], ALU.add)
                    ins.then_inc(moe_added, 1)

        f3 = part(arenaB, 9400, NB, H3, NC)
        vw3 = part(arenaB, 11864, NB, CK3, D)
        k3, v3 = sb("k3", P, 2, NB * NC), sb("v3", P, 2, NB * NC)
        vws = part(packed["dft"], 0, 2, 2, NB, D)
        HB3 = [(0, 6), (6, 11), (11, 16)]
        p3 = part(arenaB, 0, 2, H3, NC)
        pT3 = part(arenaB, 2464, 2, CK3, P)
        mx3, sm3 = sb("mx3", P, 2, H3), sb("sm3", P, 2, H3)
        kv3_mm, kv3_copy, f3_mm, f3_copy, vw3_out, vw3_in = sem("kv3_mm"), sem("kv3_copy"), sem("f3_mm"), sem("f3_copy"), [sem("vw3_out_even"), sem("vw3_out_odd")], sem("vw3_in")
        s3_mm, s3_shift, s3_exp, s3_norm, s3_turned, pT3_ready, y3_mm, x3_added = (
            sem(n) for n in ("s3_mm", "s3_shift", "s3_exp", "s3_norm", "s3_turned", "pT3_ready", "y3_mm", "x3_added"))

        def pe_fold3(pe, first, last):
            for c in range(first, last):
                cc = slice(c * P, (c + 1) * P)
                if c:
                    pe.wait_ge(kv3_copy, 2 * c)
                nc.tensor.matmul(bank[2][:, 0:NB * NC], V["wk3"][0:DC, cc], V["ctxT"][0:DC], start=True, stop=True).then_inc(kv3_mm, 1)
                nc.tensor.matmul(bank[3][:, 0:NB * NC], V["wv3"][0:DC, cc], V["ctxT"][0:DC], start=True, stop=True).then_inc(kv3_mm, 1)
                pe.wait_ge(kv3_copy, 2 * c + 2)
                if c:
                    pe.wait_ge(f3_copy, 4 * c)
                for i in range(2):
                    r = slice(D3 * i, D3 * (i + 1))
                    nc.tensor.matmul(bank[4 + i][:, 0:NB * NC], V["wqT3"][r, cc], k3[r, c % 2, :], start=True, stop=True).then_inc(f3_mm, 1)
                    for b in range(NB):
                        ins = nc.tensor.matmul(bank[6 + i][0:NC, b * D:(b + 1) * D], v3[r, c % 2, b * NC:(b + 1) * NC], V["wo3"][r, cc],
                                               start=True, stop=True)
                    ins.then_inc(f3_mm, 1)

        def act_fold3(act, first, last):
            for c in range(first, last):
                act.wait_ge(kv3_mm, 2 * c + 1)
                nc.scalar.copy(k3[:, c % 2, :], bank[2][:, 0:NB * NC]).then_inc(kv3_copy, 1)
                act.wait_ge(kv3_mm, 2 * c + 2)
                nc.scalar.copy(v3[:, c % 2, :], bank[3][:, 0:NB * NC]).then_inc(kv3_copy, 1)
                for i in range(2):
                    act.wait_ge(f3_mm, 4 * c + 2 * i + 1)
                    nc.scalar.activation(f3[:, :, 2 * c + i, :], bank[4 + i][:, 0:NB * NC].rearrange("p (b k) -> p b k", b=NB), ACT.Copy,
                                         scale=D3 ** -0.5).then_inc(f3_copy, 1)
                    act.wait_ge(f3_mm, 4 * c + 2 * i + 2)
                    if c >= 2:
                        act.wait_ge(vw3_out[c % 2], 16 * 4 * (c // 2))
                    nc.scalar.copy(vws[0:NC, c % 2, i], bank[6 + i][0:NC, 0:NB * D].rearrange("p (b d) -> p b d", b=NB)).then_inc(f3_copy, 1)

        def sync_fold3(sp):
            for c in range(H3 // 2):
                sp.wait_ge(f3_copy, 4 * c + 4)
                for i in range(2):
                    h = 2 * c + i
                    for b in range(NB):
                        sp.dma_start(A["vw_scratch"][b, h * NC:(h + 1) * NC, :], vws[0:NC, c % 2, i, b]).then_inc(vw3_out[c % 2], 16)
            for c in range(2):
                sp.wait_ge(vw3_out[c], 16 * H3)
            full = HK3 // P
            for b in range(NB):
                sp.dma_start(vw3[:, b, 0:full, :], A["vw_scratch"][b, 0:full * P, :].rearrange("(c p) d -> p c d", p=P)).then_inc(vw3_in, 16)
                sp.dma_start(vw3[0:HK3 - full * P, b, full, :], A["vw_scratch"][b, full * P:HK3, :]).then_inc(vw3_in, 16)

        def pe_attend3(pe):
            pe.wait_ge(vw3_in, 16 * 4)
            pe.wait_ge(ln_T, NB * 8)
            for n in range(NT + 3):
                if n < NT:
                    b = n // TB
                    for i, (h0, h1) in enumerate(HB3):
                        if n:
                            pe.wait_ge(s3_shift, 3 * (n - 1) + i + 1)
                        nc.tensor.matmul(bank[i][:, 0:(h1 - h0) * NC], xnT[:, n * P:(n + 1) * P],
                                         f3[:, b, h0:h1, :].rearrange("p h k -> p (h k)"), start=True, stop=True).then_inc(s3_mm, 1)
                t = n - 1
                if 0 <= t < NT:
                    pe.wait_ge(s3_norm, t + 1)
                    pf = p3[:, t % 2].rearrange("p h k -> p (h k)")
                    for g in range(3):
                        if t:
                            pe.wait_ge(pT3_ready, 3 * (t - 1) + g + 1)
                        for c in range(4 * g, min(4 * g + 4, CK3)):
                            w = min(P, HK3 - c * P)
                            ins = nc.tensor.transpose(bank[3 + g][0:w, (c % 4) * P:(c % 4 + 1) * P], pf[:, c * P:c * P + w], ident)
                        ins.then_inc(s3_turned, 1)
                t = n - 2
                if 0 <= t < NT:
                    pe.wait_ge(pT3_ready, 3 * t + 3)
                    if t >= 2:
                        pe.wait_ge(x3_added, t - 1)
                    for c in range(CK3):
                        w = min(P, HK3 - c * P)
                        ins = nc.tensor.matmul(bank[6 + t % 2][:, 0:P], pT3[0:w, t % 2, c, :], vw3[0:w, t // TB, c, :],
                                               start=(c == 0), stop=(c == CK3 - 1))
                    ins.then_inc(y3_mm, 1)

        LASTW = HK3 - (CK3 - 1) * P

        def act_attend3(act):
            for n in range(NT + 1):
                if n < NT:
                    act.wait_ge(s3_shift, 3 * n + 3)
                    nc.scalar.activation(p3[:, n % 2], p3[:, n % 2], ACT.Exp).then_inc(s3_exp, 1)
                t = n - 1
                if 0 <= t < NT:
                    for g in range(3):
                        act.wait_ge(s3_turned, 3 * t + g + 1)
                        if t >= 2:
                            act.wait_ge(y3_mm, t - 1)
                        if g < 2:
                            nc.scalar.copy(pT3[:, t % 2, 4 * g:4 * g + 4, :], bank[3 + g][:].rearrange("p (c q) -> p c q", q=P)).then_inc(pT3_ready, 1)
                        else:
                            nc.scalar.copy(pT3[:, t % 2, 8, :], bank[5][:, 0:P])
                            nc.scalar.copy(pT3[0:LASTW, t % 2, 9, :], bank[5][0:LASTW, P:2 * P]).then_inc(pT3_ready, 1)

        def vec_attend3(dve, st):
            Vv = nc.vector
            for n in range(NT + 3):
                if n < NT:
                    if n >= 2:
                        dve.wait_ge(s3_turned, 3 * (n - 1))
                    for i, (h0, h1) in enumerate(HB3):
                        dve.wait_ge(s3_mm, 3 * n + i + 1)
                        s = bank[i][:, 0:(h1 - h0) * NC].rearrange("p (h k) -> p h k", k=NC)
                        st.link(Vv.tensor_reduce(mx3[:, n % 2, h0:h1], s, AX.X, ALU.max))
                        Vv.tensor_tensor(p3[:, n % 2, h0:h1, :], s, bc(mx3[:, n % 2, h0:h1], P, h1 - h0, NC), ALU.subtract).then_inc(s3_shift, 1)
                    dve.wait_ge(s3_exp, n + 1)
                    st.link(Vv.tensor_reduce(sm3[:, n % 2], p3[:, n % 2], AX.X, ALU.add))
                    st.link(Vv.reciprocal(sm3[:, n % 2], sm3[:, n % 2]))
                    Vv.tensor_tensor(p3[:, n % 2], p3[:, n % 2], bc(sm3[:, n % 2], P, H3, NC), ALU.mult).then_inc(s3_norm, 1)
                t = n - 2
                if 0 <= t < NT:
                    if t == 0:
                        dve.wait_ge(bias_added, 3)
                    dve.wait_ge(y3_mm, t + 1)
                    Vv.tensor_tensor(X[:, t, :], bank[6 + t % 2][:, 0:P], tmp[:, t, :], ALU.add).then_inc(x3_added, 1)

        wsum, wgam = sb("wsum", P, 2), sb("wgam", P, 2)
        tern = [V["wfcT"], V["wpT"]]
        ternb = part(arenaB, 12512, HID3)
        g3 = part(arenaB, 0, 3, HID3)
        g3n = part(arenaB, 1536, 3, HID3)
        g3T = part(arenaB, 3072, 3, HID3)
        st3, mv3, rd3 = part(arenaB, 4608, NT, 6), part(arenaB, 4656, NT, 2), part(arenaB, 4672, NT)
        wsum_mm, tern_ready = sem("wsum_mm"), sem("tern_ready")
        h3_mm, g3_ready, mv3_ready, rd3_ready, g3_norm, g3_turned, g3T_dve, g3T_act, y4_mm, x4_added = (
            sem(n) for n in ("h3_mm", "g3_ready", "mv3_ready", "rd3_ready", "g3_norm", "g3_turned", "g3T_dve", "g3T_act", "y4_mm", "x4_added"))

        def vec_weights3(dve):
            dve.wait_ge(*loaded["l3f"])
            for i in range(2):
                ins = nc.vector.tensor_reduce(wsum[:, i:i + 1], tern[i], AX.X, ALU.add, apply_absolute_value=True)
            ins.then_inc(w3_vec, 1)

        def pe_weights3(pe):
            pe.wait_ge(w3_vec, 1)
            nc.tensor.matmul(bank[7][:, 0:2], V["avg"], wsum[:], start=True, stop=True).then_inc(wsum_mm, 1)

        def vec_gamma3(dve, st):
            dve.wait_ge(wsum_mm, 1)
            st.link(nc.vector.tensor_scalar(wgam[:], bank[7][:, 0:2], 1.0 / HID3, 1e-6, ALU.mult, ALU.add))
            nc.vector.reciprocal(wgam[:], wgam[:]).then_inc(w3_vec, 1)

        def pool_ternary3(pool, st):
            G = nc.gpsimd
            pool.wait_ge(w3_vec, 2)
            pool.wait_ge(kern_pe, 4)
            for i in range(2):
                st.link(G.tensor_scalar(ternb, tern[i], wgam[:, i:i + 1], -0.5, ALU.mult, ALU.is_lt))
                st.link(G.tensor_scalar(tern[i], tern[i], wgam[:, i:i + 1], 0.5, ALU.mult, ALU.is_gt))
                ins = G.tensor_tensor(tern[i], tern[i], ternb, ALU.subtract)
                if i == 0:
                    st.link(ins)
                else:
                    ins.then_inc(tern_ready, 1)

        def pe_l3f(pe):
            pe.wait_ge(tern_ready, 1)
            for n in range(NT + 4):
                if n < NT:
                    pe.wait_ge(ln_T, NB * 8 + n // TB + 1)
                    if n >= 2:
                        pe.wait_ge(g3_ready, n - 1)
                    nc.tensor.matmul(bank[2 + n % 2][:], xnT[:, n * P:(n + 1) * P], V["wfcT"], start=True, stop=True).then_inc(h3_mm, 1)
                t = n - 2
                if 0 <= t < NT:
                    pe.wait_ge(g3_norm, t + 1)
                    if t >= 2:
                        pe.wait_ge(g3T_dve, t - 1)
                        pe.wait_ge(g3T_act, t - 1)
                    for c in range(4):
                        ins = nc.tensor.transpose(bank[4 + 2 * (t % 2) + c // 2][:, (c % 2) * P:(c % 2 + 1) * P], g3n[:, t % 3, c * P:(c + 1) * P], ident)
                    ins.then_inc(g3_turned, 1)
                t = n - 3
                if 0 <= t < NT:
                    pe.wait_ge(g3T_dve, t + 1)
                    pe.wait_ge(g3T_act, t + 1)
                    if t >= 2:
                        pe.wait_ge(x4_added, t - 1)
                    for c in range(4):
                        ins = nc.tensor.matmul(bank[t % 2][:, 0:P], g3T[:, t % 3, c * P:(c + 1) * P], V["wpT"][:, c * P:(c + 1) * P],
                                               start=(c == 0), stop=(c == 3))
                    ins.then_inc(y4_mm, 1)

        def act_l3f(act):
            for n in range(NT + 3):
                if n < NT:
                    act.wait_ge(h3_mm, n + 1)
                    if n >= 3:
                        act.wait_ge(g3_norm, n - 2)
                    nc.scalar.activation(g3[:, n % 3, :], bank[2 + n % 2][:], ACT.Gelu).then_inc(g3_ready, 1)
                t = n - 2
                if 0 <= t < NT:
                    act.wait_ge(g3_turned, t + 1)
                    if t >= 3:
                        act.wait_ge(y4_mm, t - 2)
                    for c in range(2):
                        ins = nc.scalar.activation(g3T[:, t % 3, c * P:(c + 1) * P], bank[4 + 2 * (t % 2)][:, c * P:(c + 1) * P], ACT.Identity,
                                                   scale=V["ln3w"][:, c:c + 1], bias=V["ln3b"][:, c:c + 1])
                    ins.then_inc(g3T_act, 1)

        def pool_l3f(pool, st):
            for t in range(NT):
                pool.wait_ge(mv3_ready, t + 1)
                st.link(nc.gpsimd.tensor_scalar(rd3[:, t:t + 1], mv3[:, t, 1:2], 1e-5, None, ALU.add))
                nc.gpsimd.tensor_tensor(rd3[:, t:t + 1], rd3[:, t:t + 1], V["half"][:, 0:1], ALU.pow).then_inc(rd3_ready, 1)

        def vec_l3f(dve, st):
            Vv = nc.vector
            for n in range(NT + 4):
                if n < NT:
                    dve.wait_ge(g3_ready, n + 1)
                    st.link(Vv.bn_stats(st3[:, n, :], g3[:, n % 3, :]))
                    Vv.bn_aggr(mv3[:, n, :], st3[:, n, :]).then_inc(mv3_ready, 1)
                t = n - 1
                if 0 <= t < NT:
                    dve.wait_ge(rd3_ready, t + 1)
                    if t >= 3:
                        dve.wait_ge(g3_turned, t - 2)
                    Vv.tensor_scalar(g3n[:, t % 3, :], g3[:, t % 3, :], mv3[:, t, 0:1], rd3[:, t:t + 1], ALU.subtract, ALU.mult).then_inc(g3_norm, 1)
                t = n - 2
                if 0 <= t < NT:
                    dve.wait_ge(g3_turned, t + 1)
                    if t >= 3:
                        dve.wait_ge(y4_mm, t - 2)
                    for c in range(2, 4):
                        ins = Vv.tensor_scalar(g3T[:, t % 3, c * P:(c + 1) * P], bank[5 + 2 * (t % 2)][:, (c - 2) * P:(c - 1) * P],
                                               V["ln3w"][:, c:c + 1], V["ln3b"][:, c:c + 1], ALU.mult, ALU.add)
                    ins.then_inc(g3T_dve, 1)
                t = n - 3
                if 0 <= t < NT:
                    dve.wait_ge(y4_mm, t + 1)
                    Vv.tensor_tensor(X[:, t, :], bank[t % 2][:, 0:P], X[:, t, :], ALU.add).then_inc(x4_added, 1)

        block = ctx.enter_context(nc.Block())

        @block.sync
        def _(sp):
            sync_loads(sp)
            if LAST_STAGE >= 7:
                sync_fold3(sp)
            sp.wait_ge(final_stage_done, 1)
            sp.dma_start(out.rearrange("b (q p) d -> p (b q) d", p=P), X[:]).then_inc(stored, 16)
            sp.wait_ge(stored, 16)

        @block.tensor
        def _(pe):
            pe_dt(pe)
            pe_ctx0(pe)
            pe_turn(pe, ln_done, NT * 0, xn)
            pe_scores0(pe)
            pe_fold1(pe)
            pe_kernel(pe)
            pe_c2(pe)
            pe_film(pe)
            pe_c2_keys(pe)
            pe_weights3(pe)
            pe_dft(pe)
            pe_turn(pe, ln_done, NT * 1, tmp2)
            pe_ffn0(pe)
            if LAST_STAGE >= 2:
                pe_turn(pe, ln_done, NT * 3, xn)
                pe_route(pe)
                pe_qkv0(pe)
                pe_attend0(pe)
            if LAST_STAGE >= 3:
                pe_turn(pe, ln_done, NT * 4, xn)
                pe_l1x(pe)
            if LAST_STAGE >= 4:
                pe_turn(pe, ln_done, NT * 5, xn)
                pe_l1f(pe)
            if LAST_STAGE >= 5:
                pe_turn(pe, lat_done, 0, tmp2)
                pe_qkv2(pe)
                pe_attend2(pe)
            if LAST_STAGE >= 6:
                pe_turn(pe, ln_done, NT * 8, xn)
                pe_moe(pe)
            if LAST_STAGE >= 7:
                pe_turn(pe, ln_done, NT * 9, xn)
                pe_attend3(pe)
            if LAST_STAGE >= 8:
                pe_turn(pe, ln_done, NT * 10, xn)
                pe_l3f(pe)

        @block.scalar
        def _(act):
            st = Steps(act, act_step)
            act_ctx0(act)
            act_turned(act, 0)
            act_s4(act)
            act_fold1(act)
            act_kernel(act)
            act_exp0(act)
            act_c2(act)
            act_film(act, st)
            act_c2_keys(act)
            act_dft(act)
            act_turned(act, 1, V["g_ffn"], V["b_ffn"])
            act_ffn0(act)
            if LAST_STAGE >= 2:
                act_turned(act, 2)
                act_route(act)
                act_qk0(act)
                act_attend0(act)
            if LAST_STAGE >= 3:
                act_turned(act, 3)
                act_l1x(act)
            if LAST_STAGE >= 4:
                act_turned(act, 4)
                act_l1f(act)
            if LAST_STAGE >= 5:
                act_turned(act, 5, V["lnl_g"], V["lnl_b"])
                act_qkv2(act)
                act_attend2(act)
            if LAST_STAGE >= 6:
                act_turned(act, 6)
                act_moe(act)
            if LAST_STAGE >= 7:
                act_turned(act, 7)
                act_attend3(act)
            if LAST_STAGE >= 8:
                act_turned(act, 8)
                act_l3f(act)

        @block.gpsimd
        def _(pool):
            st = Steps(pool, pool_step)
            pool_dt(pool)
            pool_rstd(pool, st, 0)
            pool_rstd_twice(pool, st, 0, twice_ready)
            pool_masks(pool, st)
            pool_s4(pool)
            pool_c2_rstd(pool, st)
            pool_shift0(pool)
            pool_c2_inv(pool, st)
            pool_ternary3(pool, st)
            pool_rstd(pool, st, 1)
            pool_rstd(pool, st, 2)
            if LAST_STAGE >= 2:
                pool_rstd(pool, st, 3)
                pool_bias(pool, 3, V["bo0"], bias_added)
            if LAST_STAGE >= 3:
                pool_rstd(pool, st, 4)
                pool_l1x(pool, st)
            if LAST_STAGE >= 4:
                pool_rstd(pool, st, 5)
                pool_l1f(pool, st)
                pool_rstd(pool, st, 6)
            if LAST_STAGE >= 5:
                pool_rstd(pool, st, 7)
                pool_rstd_twice(pool, st, 7, twice_ready)
                pool_bias(pool, 7, V["bo2"], bias_added)
                pool_qkv2(pool, st)
            if LAST_STAGE >= 6:
                pool_rstd(pool, st, 8)
            if LAST_STAGE >= 7:
                pool_rstd(pool, st, 9)
                pool_bias(pool, 9, V["bo3"], bias_added)
            if LAST_STAGE >= 8:
                pool_rstd(pool, st, 10)
                pool_l3f(pool, st)

        @block.vector
        def _(dve):
            st = Steps(dve, dve_step)
            dve.wait_ge(x_loaded, 16)
            vec_dt(dve)
            vec_moments(dve, st, 0, X)
            vec_normalise(dve, 0, X, xn)
            dve.wait_ge(twice_ready, 1)
            dve.wait_ge(ln_done, NT)
            for t in range(NT):
                ins = nc.vector.tensor_scalar(tmp2[:, t, :], xn[:, t, :], mv2[:, t:t + 1], None, ALU.mult)
            st.link(ins)
            vec_s4(dve, st)
            vec_c2_moments(dve, st)
            vec_scores0(dve, st)
            vec_sigs(dve, st)
            vec_c2_norm(dve, st)
            vec_weights3(dve)
            vec_probs0(dve, st)
            vec_c2_squares(dve, st)
            vec_film(dve, st)
            vec_c2_scale(dve)
            vec_gamma3(dve, st)
            vec_spectrum(dve, st)
            vec_xt(dve, st)
            vec_moments(dve, st, 1, xt)
            vec_normalise(dve, 1, xt, tmp2)
            vec_ffn0(dve, st)
            vec_moments(dve, st, 2, xt)
            vec_normalise(dve, 2, xt, tmp2)
            dve.wait_ge(ln_done, NT * 3)
            vec_affine_add(dve, st, tmp2, V["g_out"], V["b_out"])
            if LAST_STAGE >= 2:
                vec_moments(dve, st, 3, X)
                vec_normalise(dve, 3, X, xn)
                vec_route(dve, st)
                vec_v0(dve)
                vec_attend0(dve, st)
                dve.wait_ge(x_added, NT)
            if LAST_STAGE >= 3:
                vec_moments(dve, st, 4, X)
                vec_normalise(dve, 4, X, xn)
                vec_l1x(dve, st)
            if LAST_STAGE >= 4:
                vec_moments(dve, st, 5, X)
                vec_normalise(dve, 5, X, xn)
                vec_l1f(dve, st)
                vec_moments(dve, st, 6, xt)
                vec_normalise(dve, 6, xt, tmp2)
                dve.wait_ge(ln_done, NT * 7)
                vec_affine_add(dve, st, tmp2, V["gam1"], V["bet1"])
            if LAST_STAGE >= 5:
                vec_moments(dve, st, 7, X)
                vec_normalise(dve, 7, X, xn)
                dve.wait_ge(ln_done, NT * 8)
                vec_latents(dve)
                vec_qkv2(dve, st)
                vec_attend2(dve, st)
                dve.wait_ge(x2_added, NT)
            if LAST_STAGE >= 6:
                vec_moments(dve, st, 8, X)
                vec_normalise(dve, 8, X, xn)
                vec_moe(dve, st)
                dve.wait_ge(moe_added, 2 * NX)
            if LAST_STAGE >= 7:
                vec_moments(dve, st, 9, X)
                vec_normalise(dve, 9, X, xn)
                vec_attend3(dve, st)
                dve.wait_ge(x3_added, NT)
            if LAST_STAGE >= 8:
                vec_moments(dve, st, 10, X)
                vec_normalise(dve, 10, X, xn)
                vec_l3f(dve, st)
                dve.wait_ge(x4_added, NT)
            nc.vector.engine_nop().then_inc(final_stage_done, 1)


def _packed(I):
    f = np.float32

    def pad(a):
        a = np.asarray(a, f)
        o = np.zeros((P, a.shape[1]), f)
        o[:a.shape[0]] = a
        return o

    def chunks(a):
        return a.reshape(-1, P, a.shape[1]).transpose(1, 0, 2).reshape(P, -1)

    ang = 2.0 * np.pi * (np.outer(np.arange(S), np.arange(S)) % (2 * S)) / (2 * S)
    row, col = {}, {}
    it = {
        "ctxT": I["ctx_768"].reshape(NB * NC, DC).T, "wk0": I["L0_xattn_Wk"], "wv0": I["L0_xattn_Wv"],
        "wqT0": I["L0_xattn_Wq"].T, "wfilm": np.concatenate([I["L0_xattn_W_film_in"], I["L0_xattn_W_film_out"]], 1),
        "ident": np.eye(P, dtype=f), "avg": np.full((P, P), 1.0 / P),
        "ctxr": I["ctx_768"].transpose(1, 0, 2).reshape(NC, -1),
        "g_in": I["L0_xattn_g_norm_in"], "b_in": I["L0_xattn_b_norm_in"], "dskip": I["L0_xattn_D_skip"],
        "b2": I["L0_xattn_b2"], "g_out": I["L0_xattn_g_norm_out"], "b_out": I["L0_xattn_b_norm_out"],
        "logdt": I["L0_xattn_log_dt"][:, None], "br": I["L0_ffn_br"], "bo0": I["L0_ffn_bo"], "knots": I["L1_ffn_knot_values"],
        "temp": I["L1_ffn_temperature"], "oscale": I["L1_ffn_output_scale"], "cb2": I["L1_ffn_compress_b2"],
        "gam1": I["L1_ffn_norm_gamma"], "bet1": I["L1_ffn_norm_beta"], "lnx_g": I["L2_xattn_ln_x_g"],
        "lnx_b": I["L2_xattn_ln_x_b"], "bo2": I["L2_xattn_bo"], "ebias": I["L2_ffn_expert_bias"],
        "bo3": I["L3_xattn_bo"], "gate": I["L0_xattn_mod_gate"].reshape(1), "iotaa": np.arange(LA), "rev8": 8 - np.arange(8),
        "iota8": np.arange(8), "iota16": np.arange(HF), "rev16": HF - np.arange(HF),
        "g_ffn": I["L0_xattn_g_ffn"][:, None], "b_ffn": I["L0_xattn_b_ffn"][:, None],
        "b1": I["L0_xattn_b1"].reshape(4, P).T,
        "wf": np.where(np.arange(S) == 0, 1.0, 2.0).reshape(4, P).T / (2 * S),
        "alt": (1.0 - 2.0 * (np.arange(P) % 2))[:, None], "quarter": np.repeat([0.25, 0.0], P // 2)[:, None],
        "off2": np.repeat([0.0, 0.25], P // 2)[:, None], "qturn": TURN * np.repeat([0.25, 0.0], P // 2)[:, None], "oturn": TURN * np.repeat([0.0, 0.25], P // 2)[:, None],
        "sgn": np.repeat([1.0, -1.0], P // 2)[:, None],
        "cb1": I["L1_ffn_compress_b1"][:, None],
        "lnl_g": I["L2_xattn_ln_l_g"][:, None], "lnl_b": I["L2_xattn_ln_l_b"][:, None],
        "qn": np.tile(I["L2_xattn_qn_g"], H2)[:, None], "kn": np.tile(I["L2_xattn_kn_g"], H2)[:, None],
        "ln3w": I["L3_ffn_ln_w"].reshape(4, P).T, "ln3b": I["L3_ffn_ln_b"].reshape(4, P).T,
        "bq2": np.tile(I["L0_ffn_bq"].reshape(HF, DF).T, (2, 1)), "bk2": np.tile(I["L0_ffn_bk"].reshape(HF, DF).T, (2, 1)),
        "eps": np.full((P, 1), 1e-5), "half": np.full((P, 4 * NT), -0.5), "br_col": I["L0_ffn_br"][:, None],
        "euler": np.full((P, 1), np.e),
        "cos": chunks(np.cos(ang)), "sin": chunks(np.sin(ang)),
        "are": np.tile(I["L0_xattn_A_re"].T, (2, 1)), "aim": np.tile(I["L0_xattn_A_im"].T, (2, 1)),
        "cre": np.tile(I["L0_xattn_C_re"].T, (2, 1)), "cim": np.tile(I["L0_xattn_C_im"].T, (2, 1)),
        "w1": I["L0_xattn_W1"], "w2": chunks(I["L0_xattn_W2"]),
        "wqkv": np.stack([I["L0_ffn_Wq"].reshape(D, HF, DF), I["L0_ffn_Wk"].reshape(D, HF, DF),
                          I["L0_ffn_Wv"].reshape(D, HF, DF),
                          np.broadcast_to(I["L0_ffn_bv"].reshape(1, HF, DF), (D, HF, DF))], 2).reshape(D, -1),
        "wr": I["L0_ffn_Wr"], "wo0": chunks(I["L0_ffn_Wo"]),
        "wq1": I["L1_xattn_Wq"], "wk1": I["L1_xattn_Wk"], "wv1": I["L1_xattn_Wv"], "wo1T": I["L1_xattn_Wo"].T,
        "sigT": I["L1_ffn_signatures_raw"].T, "cw1": I["L1_ffn_compress_w1"], "cw2": I["L1_ffn_compress_w2"],
        "tab": np.concatenate([I["L1_ffn_spline_w1"].reshape(NTL, -1), I["L1_ffn_spline_b1"],
                               I["L1_ffn_spline_w2"].reshape(NTL, -1), I["L1_ffn_spline_b2"], I["L1_ffn_directions"]], 1),
        "wq2T": I["L2_xattn_Wq"].T, "wlkvT": I["L2_xattn_Wlkv"].T, "wkvT": I["L2_xattn_Wkv"].T, "wo2T": I["L2_xattn_Wo"].T.reshape(H2, D2, D).transpose(1, 0, 2).reshape(D2, -1),
        "router": I["L2_ffn_router_w"].T,
        "wqT3": chunks(I["L3_xattn_Wq"].T), "wk3": I["L3_xattn_Wk"], "wv3": I["L3_xattn_Wv"], "wo3": chunks(I["L3_xattn_Wo"]),
        "wfcT": I["L3_ffn_W_fc"].T, "wpT": chunks(I["L3_ffn_W_proj"].T),
    }
    w1 = np.concatenate([I["L2_ffn_w1"], I["L2_ffn_sw1"]])
    w3 = np.concatenate([I["L2_ffn_w3"], I["L2_ffn_sw3"]])
    w2 = np.concatenate([I["L2_ffn_w2"], I["L2_ffn_sw2"]])
    it["moe"] = np.concatenate([np.concatenate([w1[e].T, w3[e].T, chunks(w2[e].T)], 1) for e in range(NE + NSH)], 1)
    res = {}
    for k, items in PACKS.items():
        if k == "rows":
            res[k] = np.concatenate([np.asarray(it[n], f).reshape(-1) for n, _ in items])[None]
        else:
            res[k] = np.concatenate([pad(it[n]) for n, _ in items], 1)
        assert res[k].shape[1] == WIDTH[k], k
    res["x"] = I["x"].reshape(TOK, D)
    res["masks"] = np.stack([I["mask_BxS2_bf1"], I["mask_BxS2_bk0"]])
    res["tmask"] = np.ascontiguousarray(I["mask_BxS_bf1"].reshape(NT, P).T)
    res["bfilm"] = np.concatenate([I["L0_xattn_b_film_in"], I["L0_xattn_b_film_out"]])[None]
    res["altrow"] = (1.0 - 2.0 * (np.arange(S) % 2)).astype(f)[None]
    return {k: np.ascontiguousarray(v) for k, v in res.items()}


def kernel(**inputs):
    import concourse.bacc as bacc
    from concourse.bass_utils import run_bass_kernel_spmd

    arrays = _packed({k: np.asarray(v) for k, v in inputs.items()})
    nc = bacc.Bacc("TRN2", target_bir_lowering=False, num_devices=1)
    A = {}
    for name, a in arrays.items():
        A[name] = nc.dram_tensor(f"in_{name}_dram", a.shape, mybir.dt.from_np(a.dtype), kind="ExternalInput").ap()
    A["vw_scratch"] = nc.dram_tensor("vw_scratch", (NB, HK3, D), F32, kind="Internal").ap()
    out = nc.dram_tensor("out_0_dram", (NB, S, D), F32, kind="ExternalOutput").ap()
    program(nc, A, out)
    r = run_bass_kernel_spmd(nc, [{f"in_{k}_dram": v for k, v in arrays.items()}], core_ids=[0])
    return r.results[0]["out_0_dram"]
```

```python
import numpy as np

import concourse.bass as bass
from concourse import mybir
from contextlib import ExitStack

F32 = mybir.dt.float32
U32 = mybir.dt.uint32
I32 = mybir.dt.int32
U8 = mybir.dt.uint8
ALU = mybir.AluOpType
ACT = mybir.ActivationFunctionType
AX = mybir.AxisListType

P = 128
NB, S, D = 2, 512, 128
NT = NB * S // P
TB = S // P
NC, DC = 77, 96
TOK = NB * S
H0, KEEP, DH0 = 4, 32, 32
NST = 64
LA, LB = 32, 16
HID0 = 512
HF, CH, DF = 16, 4, 64
NTL, TPC, NCL, GRID, CMP, KN = 64, 8, 8, 16, 32, 8
TABW = 2 * GRID + GRID + GRID + 1 + D
H2, D2 = 2, 64
NE, NSH, HE = 8, 2, 256
H3, D3 = 16, 64
HK3 = H3 * NC
CK3 = -(-HK3 // P)
HID3 = 512
TURN = 6.283184
MAGIC = 1.5 * 2.0 ** 23
NEVER = -3.0e38
MASKED = 1.0e30

PACKS = {
    "ctx": [("ctxT", NB * NC), ("wk0", D), ("wv0", D), ("wqT0", D), ("wfilm", 4 * D), ("ident", P), ("avg", P)],
    "rows": [("g_in", D), ("b_in", D), ("dskip", D), ("b2", D), ("g_out", D), ("b_out", D),
             ("br", HF), ("bo0", D), ("knots", KN), ("temp", 1), ("oscale", 1), ("cb2", 2), ("gam1", D), ("bet1", D),
             ("lnx_g", DC), ("lnx_b", DC), ("bo2", D), ("ebias", NE), ("bo3", D), ("gate", 1), ("iotaa", LA),
             ("rev8", 8), ("iota8", 8), ("iota16", HF), ("rev16", HF)],
    "cols": [("g_ffn", 1), ("b_ffn", 1), ("b1", HID0 // P), ("wf", 4), ("alt", 1), ("quarter", 1), ("sgn", 1),
             ("off2", 1), ("cb1", 1), ("lnl_g", 1), ("lnl_b", 1), ("qn", 1), ("kn", 1), ("ln3w", 4), ("ln3b", 4),
             ("bq2", HF), ("bk2", HF), ("eps", 1), ("half", 4 * NT), ("br_col", 1), ("euler", 1), ("logdt", 1),
             ("qturn", 1), ("oturn", 1)],
    "small0": [("wr", HF), ("wo0", 2 * D)],
    "s4": [("are", D), ("aim", D), ("cre", D), ("cim", D)],
    "dft": [("cos", 4 * S), ("sin", 4 * S)],
    "ffn0": [("w1", HID0), ("w2", HID0)],
    "head0": [("wqkv", HF * 4 * DF)],
    "l1": [("wq1", D), ("wk1", DC), ("wv1", DC), ("wo1T", D), ("sigT", NTL), ("cw1", CMP), ("cw2", 2), ("tab", TABW)],
    "l2": [("ctxr", NB * DC), ("wq2T", D), ("wlkvT", 2 * D), ("wkvT", 2 * D), ("wo2T", H2 * D), ("router", NE)],
    "moe": [("moe", (NE + NSH) * 3 * HE)],
    "l3": [("wqT3", H3 * D3), ("wk3", H3 * D3), ("wv3", H3 * D3), ("wo3", 8 * D)],
    "l3f": [("wfcT", HID3), ("wpT", HID3)],
}
WIDTH = {k: sum(n for _, n in v) for k, v in PACKS.items()}
LOADS = [("cols", "ctx"), ("rows",), ("s4",), ("l2", "l3f", "l1"), ("dft",), ("ffn0", "small0"), ("head0",), ("moe", "l3")]
LAST_STAGE = 8
SPLITK = 3
FOLD_EARLY = 4


def program(nc, A, out):
    ctx = ExitStack()
    with ctx:
        def sb(name, *shape, dt=F32):
            return ctx.enter_context(nc.sbuf_tensor(name, list(shape), dt))

        def sem(name):
            return ctx.enter_context(nc.semaphore(name))

        bank = [ctx.enter_context(nc.psum_tensor(f"bank{i}", [P, 512], F32)) for i in range(8)]

        arenaA, arenaB = sb("arenaA", P, 12288), sb("arenaB", P, 14592)

        def part(region, at, *shape):
            n = int(np.prod(shape))
            v = region[:, at:at + n]
            if len(shape) == 1:
                return v
            names = "abcd"[:len(shape)]
            return v.rearrange(f"p ({' '.join(names)}) -> p {' '.join(names)}", **dict(zip(names, shape)))

        packed, loaded, V = {}, {}, {}
        for group in LOADS:
            s = sem("loaded_" + group[0])
            for k in group:
                loaded[k] = (s, 16 * len(group))
        for k in PACKS:
            if k == "moe":
                packed[k] = arenaA[:, 0:WIDTH[k]]
            elif k == "l3":
                packed[k] = arenaA[:, WIDTH["moe"]:WIDTH["moe"] + WIDTH[k]]
            elif k == "head0":
                packed[k] = packed["dft"][:, 0:WIDTH[k]]
            else:
                packed[k] = sb(f"in_{k}", P, WIDTH[k])
            at = 0
            for name, n in PACKS[k]:
                V[name] = packed[k][:, at:at + n]
                at += n
        X = sb("X", P, NT, D)
        xn = sb("xn", P, NT, D)
        xnT = sb("xnT", P, TOK)
        tmp = sb("tmp", P, NT, D)
        tmp2 = sb("tmp2", P, NT, D)
        stats = sb("stats", P, NT, 6)
        mv = sb("mv", P, NT, 2)
        rstd = sb("rstd", P, NT)
        rtmp = sb("rtmp", P, NT)
        masks8 = sb("masks8", P, 2, NB, NC, dt=U8)
        tmask8 = sb("tmask8", P, NT, dt=U8)
        maskb = sb("maskb", P, 2, NB, NC)
        tmask = sb("tmask", P, NT)
        ident, quarter = V["ident"], V["quarter"]

        x_loaded, masks_loaded = sem("x_loaded"), sem("masks_loaded")
        dve_step, act_step, pool_step = sem("dve_step"), sem("act_step"), sem("pool_step")
        ln_moments, ln_rstd, ln_done = sem("ln_moments"), sem("ln_rstd"), sem("ln_done")
        ln_turned, ln_T = sem("ln_turned"), sem("ln_T")

        avg1_mm = sem("avg1_mm")
        bias_added = sem("bias_added")
        c2_powers = sem("c2_powers")
        c2_scaled = sem("c2_scaled")
        c2_stats = sem("c2_stats")
        kern_act = sem("kern_act")
        kern_pe = sem("kern_pe")
        l1f_act = sem("l1f_act")
        l1f_pe = sem("l1f_pe")
        l1f_vec = sem("l1f_vec")
        l1x_vec = sem("l1x_vec")
        route_pe = sem("route_pe")
        route_vec = sem("route_vec")
        s4_act = sem("s4_act")
        s4_pool = sem("s4_pool")
        w3_vec = sem("w3_vec")

        class Steps:

            def __init__(self, eng, s):
                self.eng, self.s, self.n = eng, s, 0

            def link(self, ins):
                self.n += 1
                ins.then_inc(self.s, 1)
                self.eng.wait_ge(self.s, self.n)

        def bc(col, *shape):
            while len(col.shape) < len(shape):
                col = col.unsqueeze(len(col.shape))
            return col.broadcast_to(list(shape))

        def bm(row, n):
            return row.unsqueeze(1).broadcast_to([row.shape[0], n, row.shape[1]])

        def halves():
            return [slice(b * TB, (b + 1) * TB) for b in range(NB)]

        def vec_moments(st, src, which=range(NB)):
            for b in which:
                for t in range(b * TB, (b + 1) * TB):
                    ins = nc.vector.bn_stats(stats[:, t, :], src[:, t, :])
                st.link(ins)
                for t in range(b * TB, (b + 1) * TB):
                    ins = nc.vector.bn_aggr(mv[:, t, :], stats[:, t, :])
                ins.then_inc(ln_moments, 1)

        def pool_rstd(pool, st, i):
            for b, r in enumerate(halves()):
                pool.wait_ge(ln_moments, NB * i + b + 1)
                st.link(nc.gpsimd.tensor_scalar(rtmp[:, r], mv[:, r, 1], 1e-5, None, ALU.add))
                nc.gpsimd.tensor_tensor(rstd[:, r], rtmp[:, r], V["half"][:, r], ALU.pow).then_inc(ln_rstd, 1)

        def vec_normalise(dve, i, src, dst, which=range(NB)):
            for b in which:
                dve.wait_ge(ln_rstd, NB * i + b + 1)
                for t in range(b * TB, (b + 1) * TB):
                    nc.vector.tensor_scalar(dst[:, t, :], src[:, t, :], mv[:, t, 0:1], rstd[:, t:t + 1],
                                            ALU.subtract, ALU.mult).then_inc(ln_done, 1)

        def vec_normalise_add(dve, i, src, g):
            for b in range(NB):
                dve.wait_ge(xb_ready, i)
                dve.wait_ge(ln_rstd, NB * LN_ADDED[i - 1] + b + 1)
                r = range(b * TB, (b + 1) * TB)
                for t in r:
                    nc.vector.scalar_tensor_tensor(tmp[:, t, :], src[:, t, :], mv[:, t, 0:1], g, ALU.subtract, ALU.mult).then_inc(ln_done, 1)
                for t in r:
                    dve.wait_ge(ln_done, NT * LN_ADDED[i - 1] + t + 1)
                    ins = nc.vector.scalar_tensor_tensor(X[:, t, :], tmp[:, t, :], rstd[:, t:t + 1], X[:, t, :], ALU.mult, ALU.add)
                ins.then_inc(x_final, 1)

        LN_ADDED = (2, 6)
        xb_ready, x_final, heads_act = sem("xb_ready"), sem("x_final"), sem("heads_act")

        def pool_add_row(pool, row, after):
            pool.wait_ge(ln_done, after)
            nc.gpsimd.tensor_tensor(X[:], X[:], bm(row, NT), ALU.add).then_inc(xb_ready, 1)

        def pe_turn(pe, done, before, src):
            for t in range(NT):
                pe.wait_ge(done, before + t + 1)
                ins = nc.tensor.transpose(bank[t // TB][:, (t % TB) * P:(t % TB + 1) * P], src[:, t, :], ident)
                if t % TB == TB - 1:
                    ins.then_inc(ln_turned, 1)

        def act_turned(act, n, scale=None, bias=None):
            for b in range(NB):
                act.wait_ge(ln_turned, NB * n + b + 1)
                dst = xnT[:, b * S:(b + 1) * S]
                if scale is None:
                    ins = nc.scalar.copy(dst, bank[b][:])
                elif bias is None:
                    ins = nc.scalar.activation(dst, bank[b][:], ACT.Copy, scale=scale)
                else:
                    ins = nc.scalar.activation(dst, bank[b][:], ACT.Identity, scale=scale, bias=bias)
                ins.then_inc(ln_T, 1)

        kT0 = sb("kT0", P, NB * NC)
        f0 = sb("f0", P, NB, H0, NC)
        vT0 = sb("vT0", P, NB * NC)
        vfilm = sb("vfilm", NC + 1, NB, 4 * D)
        s0 = part(arenaB, 0, NT, H0, NC)
        r0 = part(arenaB, 2464, NT, H0, NC)
        e0 = part(arenaB, 4928, NT, H0, NC)
        top0 = part(arenaB, 7392, NT, H0, KEEP)
        sum0 = sb("sum0", P, NT, H0)
        w0 = sb("w0", P, NT, H0)
        am = sb("am", P, NT, NC)
        amT = sb("amT", NC + 1, TOK)
        film = part(arenaA, 0, NT, 4, D)
        xk = part(arenaA, 8192, TB, 3, D)
        yc = part(arenaA, 4096, 4, 2, NB * D)
        kf = part(arenaA, 6144, 4, 2, D)
        pr = part(arenaA, 7168, 4, NB * D)
        kny = sb("kny", 1, D)
        yny = sb("yny", 1, NB, D)
        xt = sb("xt", P, NT, D)
        hT0 = part(arenaA, 8192, 4, TOK)
        altrow = arenaA[0:1, 11776:11776 + S]

        masks_ready, ctx0_mm, ctx0_copy, bias_rows = sem("masks_ready"), sem("ctx0_mm"), sem("ctx0_copy"), sem("bias_rows")
        ones_set = sem("ones_set")
        s0_mm, s0_copy, top_ready, shifted0, exp0 = sem("s0_mm"), sem("s0_copy"), sem("top_ready"), sem("shifted0"), sem("exp0")
        am_ready, am_turned, amT_ready, film_mm, film_ready = sem("am_ready"), sem("am_turned"), sem("amT_ready"), sem("film_mm"), sem("film_ready")
        x2_ready = sem("x2_ready")
        dft_mm, kf_ready, spec_used, prod_ready, y_mm, xt_ready = (sem("dft_mm"), sem("kf_ready"), sem("spec_used"),
                                                                    sem("prod_ready"), sem("y_mm"), sem("xt_ready"))
        ff_mm, ff_gelu, ff_out, b2_added = sem("ff_mm"), sem("ff_gelu"), sem("ff_out"), sem("b2_added")

        dtb = sb("dtb", P, D)
        ang, are, aim, al, be = (tmp[:, i, :] for i in range(5))
        q = [xt[:, i, :] for i in range(8)]
        hh4 = part(arenaB, 8416, D, LA)
        gg4 = part(arenaB, 12512, D, LB)
        ka = part(arenaB, 0, D, LB)[0:LA]
        kTl = part(arenaB, 2048, S)
        s4_vec, s4_pe = sem("s4_vec"), sem("s4_pe")

        def sync_loads(sp):
            for k in ("cols", "ctx"):
                sp.dma_start(packed[k][:], A[k]).then_inc(loaded[k][0], 16)
            sp.dma_start(X[:], A["x"].rearrange("(t p) d -> p t d", p=P)).then_inc(x_loaded, 16)
            sp.dma_start(masks8[:], A["masks"].partition_broadcast(P)).then_inc(masks_loaded, 16)
            sp.dma_start(tmask8[:], A["tmask"]).then_inc(masks_loaded, 16)
            sp.dma_start(packed["rows"][:], A["rows"].rearrange("a n -> (a n)").partition_broadcast(P)).then_inc(loaded["rows"][0], 16)
            for b in range(NB):
                sp.dma_start(vfilm[NC:NC + 1, b, :], A["bfilm"]).then_inc(bias_rows, 16)
            sp.dma_start(altrow, A["altrow"]).then_inc(bias_rows, 16)
            for k in ("s4", "l2", "l3f", "l1", "dft", "ffn0", "small0"):
                sp.dma_start(packed[k][:], A[k]).then_inc(loaded[k][0], 16)
            sp.wait_ge(y_mm, TB)
            sp.dma_start(packed["head0"], A["head0"]).then_inc(loaded["head0"][0], 16)
            sp.wait_ge(ff_out, NB)
            for k in ("moe", "l3"):
                sp.dma_start(packed[k], A[k]).then_inc(loaded[k][0], 16)

        def pe_ctx0(pe):
            pe.wait_ge(*loaded["ctx"])
            nc.tensor.matmul(bank[2][:, 0:NB * NC], V["wk0"][0:DC], V["ctxT"][0:DC], start=True, stop=True).then_inc(ctx0_mm, 1)
            nc.tensor.matmul(bank[3][:, 0:NB * NC], V["wv0"][0:DC], V["ctxT"][0:DC], start=True, stop=True).then_inc(ctx0_mm, 1)
            pe.wait_ge(ctx0_copy, 1)
            pe.wait_ge(s4_vec, 2)
            for h in range(H0):
                r = slice(h * DH0, (h + 1) * DH0)
                nc.tensor.matmul(bank[4 + h][:, 0:NB * NC], V["wqT0"][r], kT0[r, :], start=True, stop=True).then_inc(ctx0_mm, 1)
            pe.wait_ge(ctx0_copy, 2)
            for b in range(NB):
                nc.tensor.matmul(bank[2 + b][0:NC, :], vT0[:, b * NC:(b + 1) * NC], V["wfilm"], start=True, stop=True).then_inc(ctx0_mm, 1)

        def act_ctx0(act):
            act.wait_ge(ctx0_mm, 1)
            nc.scalar.copy(kT0[:], bank[2][:, 0:NB * NC]).then_inc(ctx0_copy, 1)
            act.wait_ge(ctx0_mm, 2)
            nc.scalar.copy(vT0[:], bank[3][:, 0:NB * NC]).then_inc(ctx0_copy, 1)
            for h in range(H0):
                act.wait_ge(ctx0_mm, 3 + h)
                nc.scalar.copy(f0[:, :, h, :], bank[4 + h][:, 0:NB * NC].rearrange("p (b k) -> p b k", b=NB)).then_inc(ctx0_copy, 1)
            for b in range(NB):
                act.wait_ge(ctx0_mm, 3 + H0 + b)
                nc.scalar.copy(vfilm[0:NC, b, :], bank[2 + b][0:NC, :]).then_inc(ctx0_copy, 1)

        def pe_scores0(pe):
            for t in range(NT):
                if t == 0:
                    pe.wait_ge(ctx0_copy, 2 + H0 + NB)
                if t % TB == 0:
                    pe.wait_ge(ln_T, t // TB + 1)
                if t >= 4:
                    pe.wait_ge(s0_copy, t - 3)
                nc.tensor.matmul(bank[2 + t % 4][:, 0:H0 * NC], xnT[:, t * P:(t + 1) * P],
                                 f0[:, t // TB].rearrange("p h k -> p (h k)"), start=True, stop=True).then_inc(s0_mm, 1)

        def vec_scores0(dve, st):
            dve.wait_ge(masks_ready, 1)
            for t in range(NT):
                dve.wait_ge(s0_mm, t + 1)
                nc.vector.tensor_tensor(s0[:, t], bank[2 + t % 4][:, 0:H0 * NC].rearrange("p (h k) -> p h k", h=H0),
                                        bm(maskb[:, 0, t // TB, :], H0), ALU.add).then_inc(s0_copy, 1)
            dve.wait_ge(s0_copy, NT)
            for r in halves():
                for k in range(KEEP // 8):
                    src = s0 if k == 0 else r0
                    for t in range(r.start, r.stop):
                        for h in range(H0):
                            ins = nc.vector.max(top0[:, t, h, 8 * k:8 * k + 8], src[:, t, h, :])
                    st.link(ins)
                    for t in range(r.start, r.stop):
                        for h in range(H0):
                            ins = nc.vector.match_replace(r0[:, t, h, :], top0[:, t, h, 8 * k:8 * k + 8], src[:, t, h, :], NEVER)
                        if k == KEEP // 8 - 1:
                            ins.then_inc(top_ready, 1)
                    if k < KEEP // 8 - 1:
                        st.link(ins)

        def pool_shift0(pool, b):
            for t in range(b * TB, (b + 1) * TB):
                pool.wait_ge(top_ready, t + 1)
                nc.gpsimd.tensor_tensor(e0[:, t], s0[:, t], bc(top0[:, t, :, 0], P, H0, NC), ALU.subtract).then_inc(shifted0, 1)

        def act_exp0(act, b):
            for t in range(b * TB, (b + 1) * TB):
                act.wait_ge(shifted0, t + 1)
                nc.scalar.activation(e0[:, t], e0[:, t], ACT.Exp, scale=float(1.0 / np.sqrt(np.float32(DH0)))).then_inc(exp0, 1)

        def vec_probs0(dve, st):
            for t in range(NT):
                dve.wait_ge(exp0, t + 1)
                ins = nc.vector.scalar_tensor_tensor(e0[:, t], r0[:, t], 0.5 * NEVER, e0[:, t], ALU.is_lt, ALU.mult)
            st.link(ins)
            st.link(nc.vector.tensor_reduce(sum0[:], e0[:], AX.X, ALU.add))
            st.link(nc.vector.reciprocal(w0[:], sum0[:]))
            st.link(nc.vector.tensor_tensor(w0[:], w0[:], bc(tmask[:], P, NT, H0), ALU.mult))
            for t in range(NT):
                ins = nc.vector.tensor_tensor(e0[:, t], e0[:, t], bc(w0[:, t], P, H0, NC), ALU.mult)
            st.link(ins)
            for t in range(NT):
                ins = nc.vector.tensor_reduce(am[:, t, :], e0[:, t].rearrange("p h k -> p k h"), AX.X, ALU.add)
                ins.then_inc(am_ready, 1)

        def pe_film(pe):
            for t in range(NT):
                pe.wait_ge(am_ready, t + 1)
                ins = nc.tensor.transpose(bank[t // TB][0:NC, (t % TB) * P:(t % TB + 1) * P], am[:, t, :], ident)
                if t % TB == TB - 1:
                    ins.then_inc(am_turned, 1)
            pe.wait_ge(bias_rows, 16 * (NB + 1))
            for t in range(NT):
                if t % TB == 0:
                    pe.wait_ge(amT_ready, t // TB + 1)
                if t >= 4:
                    pe.wait_ge(film_ready, t - 3)
                nc.tensor.matmul(bank[2 + t % 4][:], amT[:, t * P:(t + 1) * P], vfilm[:, t // TB, :],
                                 start=True, stop=True).then_inc(film_mm, 1)

        def act_film(act, st):
            act.wait_ge(ones_set, 1)
            for b in range(NB):
                act.wait_ge(am_turned, b + 1)
                nc.scalar.copy(amT[0:NC, b * S:(b + 1) * S], bank[b][0:NC, :]).then_inc(amT_ready, 1)
            for t in range(NT):
                act.wait_ge(film_mm, t + 1)
                src = bank[2 + t % 4][:].rearrange("p (f s d) -> p f s d", f=2, s=2)
                dst = film[:, t].rearrange("p (f s) d -> p f s d", f=2)
                nc.scalar.activation(dst[:, :, 0], src[:, :, 0], ACT.Identity, scale=V["gate"], bias=1.0)
                nc.scalar.activation(dst[:, :, 1], src[:, :, 1], ACT.Copy, scale=V["gate"]).then_inc(film_ready, 1)

        def pool_masks(pool, st):
            nc.gpsimd.memset(amT[:], 1.0).then_inc(ones_set, 1)
            pool.wait_ge(masks_loaded, 32)
            st.link(nc.gpsimd.tensor_copy(maskb[:], masks8[:]))
            st.link(nc.gpsimd.tensor_copy(tmask[:], tmask8[:]))
            st.link(nc.gpsimd.tensor_scalar(maskb[:], maskb[:], 1.0, MASKED, ALU.subtract, ALU.mult))
            nc.gpsimd.tensor_scalar(tmask[:], tmask[:], 1.0 / H0, None, ALU.mult).then_inc(masks_ready, 1)

        dtc, dtd = sb("dtc", P, 1), q[6]

        def pool_dt(pool):
            pool.wait_ge(*loaded["cols"])
            nc.gpsimd.tensor_tensor(dtc[:], V["euler"], V["logdt"], ALU.pow).then_inc(s4_pool, 1)

        def vec_dt(dve):
            dve.wait_ge(s4_pool, 1)
            dve.wait_ge(*loaded["ctx"])
            nc.vector.tensor_scalar(dtd, ident, dtc[:], float(P), ALU.mult, ALU.mult).then_inc(s4_vec, 1)

        def pe_dt(pe):
            pe.wait_ge(s4_vec, 1)
            nc.tensor.matmul(bank[7][:, 0:D], V["avg"], dtd, start=True, stop=True).then_inc(s4_pe, 1)

        steps = V["iotaa"].unsqueeze(1).broadcast_to([P, D, LA])
        vH, kH = part(arenaA, 0, D, LA), part(arenaA, D * LA, D, LA)
        eH, eG = kH, part(arenaA, 9728, D, LB)
        uG, rGc, rGs, sG = (part(arenaB, i * D * LB, D, LB) for i in range(4))

        def vec_dt_row(dve):
            dve.wait_ge(s4_pe, 1)
            nc.vector.tensor_copy(dtb[:], bank[7][:, 0:D]).then_inc(s4_vec, 1)

        def vec_phase(st, r, u, off):
            st.link(nc.vector.tensor_scalar(r, u, off, MAGIC, ALU.add, ALU.add))
            return nc.vector.scalar_tensor_tensor(r, r, MAGIC, u, ALU.subtract, ALU.subtract)

        def vec_s4(dve, st):
            Vv, L = nc.vector, st.link
            tt, ts, stt = Vv.tensor_tensor, Vv.tensor_scalar, Vv.scalar_tensor_tensor
            dve.wait_ge(s4_pool, 3)
            L(tt(uG, bc(ang[:], P, D, LB), steps[:, :, 0:LB], ALU.mult))
            vec_phase(st, rGc, uG, V["quarter"]).then_inc(s4_vec, 1)
            vec_phase(st, rGs, uG, V["off2"]).then_inc(s4_vec, 1)

        def vec_s4_products(dve, st):
            Vv, L = nc.vector, st.link
            tt, ts, stt = Vv.tensor_tensor, Vv.tensor_scalar, Vv.scalar_tensor_tensor
            em1, s1, s2, inv = q[0][:], q[1][:], q[2][:], q[4][:]
            a, b, c, d = q[3][:], q[5][:], q[6][:], q[7][:]
            L(tt(a, V["are"], V["are"], ALU.mult))
            L(tt(b, V["aim"], V["aim"], ALU.mult))
            L(tt(a, a, b, ALU.add))
            L(Vv.reciprocal(inv, a))
            dve.wait_ge(s4_act, 3)
            L(ts(a, em1, -1.0, 1.0, ALU.mult, ALU.add))
            L(Vv.reciprocal(b, a))
            L(stt(em1, em1, 2.0, b, ALU.mult, ALU.mult))
            L(stt(a, s1, 2.0, s1, ALU.mult, ALU.mult))
            L(tt(b, em1, a, ALU.mult))
            L(tt(b, em1, b, ALU.subtract))
            L(tt(b, b, a, ALU.subtract))
            L(stt(c, em1, 1.0, s2, ALU.add, ALU.mult))
            L(tt(a, b, V["are"], ALU.mult))
            L(tt(d, c, V["aim"], ALU.mult))
            L(tt(a, a, d, ALU.add))
            L(tt(a, a, inv, ALU.mult))
            L(tt(c, c, V["are"], ALU.mult))
            L(tt(d, b, V["aim"], ALU.mult))
            L(tt(c, c, d, ALU.subtract))
            L(tt(c, c, inv, ALU.mult))
            L(tt(b, V["cre"], a, ALU.mult))
            L(tt(d, V["cim"], c, ALU.mult))
            L(tt(b, b, d, ALU.subtract))
            L(ts(al[:], b, 2.0, V["sgn"], ALU.mult, ALU.mult))
            L(tt(b, V["cre"], c, ALU.mult))
            L(tt(d, V["cim"], a, ALU.mult))
            L(tt(b, b, d, ALU.add))
            L(ts(be[:], b, -2.0, None, ALU.mult))
            dve.wait_ge(s4_act, 8)
            for i in range(4):
                r = slice(i * D // 4, (i + 1) * D // 4)
                gq, sq, n = gg4[:, r, :], sG[:, r, :], D // 4
                tt(gq, gq, bc(al[:, r], P, n, LB), ALU.mult)
                L(tt(sq, sq, bc(be[:, r], P, n, LB), ALU.mult))
                L(tt(gq, gq, sq, ALU.add))
                tt(gq, gq, eG[:, r, :], ALU.mult).then_inc(s4_vec, 1)

        def pool_s4(pool, st):
            G, L = nc.gpsimd, st.link
            tt, ts = G.tensor_tensor, G.tensor_scalar
            pool.wait_ge(s4_vec, 2)
            pool.wait_ge(*loaded["s4"])
            tt(are[:], dtb[:], V["are"], ALU.mult).then_inc(s4_pool, 1)
            L(tt(aim[:], dtb[:], V["aim"], ALU.mult))
            L(ts(ang[:], aim[:], float(1.0 / (2.0 * np.pi)), None, ALU.mult))
            L(ts(q[1][:], ang[:], MAGIC, MAGIC, ALU.add, ALU.subtract))
            tt(ang[:], ang[:], q[1][:], ALU.subtract).then_inc(s4_pool, 1)
            pool.wait_ge(s4_pool, 3)
            L(tt(vH, bc(ang[:], P, D, LA), steps, ALU.mult))
            L(ts(vH, vH, float(LB), V["quarter"], ALU.mult, ALU.add))
            L(ts(kH, vH, MAGIC, MAGIC, ALU.add, ALU.subtract))
            tt(vH, vH, kH, ALU.subtract).then_inc(s4_pool, 1)

        def pool_s4_decay(pool):
            tt = nc.gpsimd.tensor_tensor
            pool.wait_ge(s4_pool, 4)
            tt(eH, bc(are[:], P, D, LA), steps, ALU.mult).then_inc(s4_pool, 1)
            tt(eG, bc(are[:], P, D, LB), steps[:, :, 0:LB], ALU.mult).then_inc(s4_pool, 1)

        def pool_s4_scale(pool):
            pool.wait_ge(s4_act, 5)
            nc.gpsimd.tensor_tensor(hh4[:], hh4[:], eH, ALU.mult).then_inc(s4_pool, 1)

        def act_s4_rows(act):
            A_ = nc.scalar.activation
            act.wait_ge(s4_pool, 2)
            A_(q[0][:], are[:], ACT.Tanh, scale=0.5).then_inc(s4_act, 1)
            act.wait_ge(s4_pool, 3)
            A_(q[2][:], ang[:], ACT.Sin, scale=TURN).then_inc(s4_act, 1)
            A_(q[1][:], ang[:], ACT.Sin, scale=0.5 * TURN).then_inc(s4_act, 1)
            act_exp0(act, 0)
            act.wait_ge(s4_pool, 4)
            A_(hh4[:], vH, ACT.Sin, scale=TURN).then_inc(s4_act, 1)
            act_exp0(act, 1)
            act.wait_ge(s4_pool, 5)
            A_(eH, eH, ACT.Exp, scale=float(LB)).then_inc(s4_act, 1)
            act.wait_ge(s4_pool, 6)
            A_(eG, eG, ACT.Exp).then_inc(s4_act, 1)

        def act_s4_cols(act):
            A_ = nc.scalar.activation
            act.wait_ge(s4_vec, 3)
            A_(gg4[:], rGc, ACT.Sin, scale=-TURN, bias=V["qturn"]).then_inc(s4_act, 1)
            act.wait_ge(s4_vec, 4)
            A_(sG, rGs, ACT.Sin, scale=-TURN, bias=V["oturn"]).then_inc(s4_act, 1)

        def pe_kernel(pe):
            pe.wait_ge(s4_pool, 7)
            pe.wait_ge(film_ready, NT)
            pe.wait_ge(c2_copy, 3)
            pe.wait_ge(w3_vec, 2)
            per = 512 // LB
            for d in range(D):
                if d % (D // 4) == 0:
                    pe.wait_ge(s4_vec, 5 + d // (D // 4))
                ins = nc.tensor.matmul(bank[4 + d // per][0:LA, (d % per) * LB:(d % per + 1) * LB],
                                       hh4[:, d, :], gg4[:, d, :], start=True, stop=True)
                if d % per == per - 1:
                    ins.then_inc(kern_pe, 1)
            pe.wait_ge(kern_act, 4)
            for b in range(LB):
                ins = nc.tensor.transpose(bank[4][:, b * LA:(b + 1) * LA], ka[:, :, b], ident[0:LA, 0:LA])
            ins.then_inc(kern_pe, 1)
            pe.wait_ge(kern_act, 5)
            for j in range(TB):
                ins = nc.tensor.transpose(bank[5][:, j * P:(j + 1) * P], kTl[:, j * P:(j + 1) * P], ident)
            ins.then_inc(kern_pe, 1)

        def act_kernel(act):
            per = 512 // LB
            for i in range(4):
                act.wait_ge(kern_pe, i + 1)
                nc.scalar.copy(ka[:, i * per:(i + 1) * per, :], bank[4 + i][0:LA, :].rearrange("p (d b) -> p d b", b=LB)).then_inc(kern_act, 1)
            act.wait_ge(kern_pe, 5)
            nc.scalar.copy(kTl[:].rearrange("p (a b) -> p a b", b=LB), bank[4][:].rearrange("p (b a) -> p a b", b=LB)).then_inc(kern_act, 1)
            act.wait_ge(kern_pe, 6)
            nc.scalar.copy(xk[:, :, 2, :], bank[5][:].rearrange("p (j d) -> p j d", d=D)).then_inc(kern_act, 1)

        def vec_affine_in(dve, st):
            dve.wait_ge(*loaded["rows"])
            st.link(nc.vector.tensor_tensor(tmp2[:], tmp2[:], bm(V["g_in"], NT), ALU.mult))
            nc.vector.tensor_tensor(tmp2[:], tmp2[:], bm(V["b_in"], NT), ALU.add).then_inc(x2_ready, 1)

        def vec_film(dve, st):
            dve.wait_ge(x2_ready, 1)
            dve.wait_ge(film_ready, NT)
            st.link(nc.vector.tensor_tensor(tmp2[:], tmp2[:], film[:, :, 0, :], ALU.mult))
            for b in range(NB):
                ins = nc.vector.tensor_tensor(xk[:, :, b, :], tmp2[:, b * TB:(b + 1) * TB, :],
                                              film[:, b * TB:(b + 1) * TB, 1, :], ALU.add)
            ins.then_inc(x2_ready, 1)

        def pe_dft_x(pe):
            pe.wait_ge(*loaded["dft"])
            pe.wait_ge(x2_ready, 2)
            for j in range(4):
                for c, m in enumerate(("cos", "sin")):
                    for q4 in range(TB):
                        ins = nc.tensor.matmul(bank[j][:, c * NB * D:(c + 1) * NB * D], V[m][:, q4 * S + j * P:q4 * S + (j + 1) * P],
                                               xk[:, q4, 0:NB].rearrange("p b d -> p (b d)"), start=(q4 == 0), stop=(q4 == TB - 1))
                ins.then_inc(dft_mm, 1)

        KBANK = (6, 7, 4, 6)

        def pe_dft_k(pe):
            pe.wait_ge(kern_act, 6)
            for j in range(4):
                if j == 3:
                    pe.wait_ge(kf_ready, 1)
                for c, m in enumerate(("cos", "sin")):
                    for q4 in range(TB):
                        ins = nc.tensor.matmul(bank[KBANK[j]][:, c * D:(c + 1) * D], V[m][:, q4 * S + j * P:q4 * S + (j + 1) * P],
                                               xk[:, q4, 2], start=(q4 == 0), stop=(q4 == TB - 1))
                ins.then_inc(dft_mm, 1)
            for q4 in range(TB):
                ins = nc.tensor.matmul(bank[5][0:1, 0:3 * D], V["alt"], xk[:, q4].rearrange("p b d -> p (b d)"),
                                       start=(q4 == 0), stop=(q4 == TB - 1))
            ins.then_inc(dft_mm, 1)

        def pe_dft_back(pe):
            pe.wait_ge(prod_ready, 5)
            for i in range(TB):
                for j in range(4):
                    for c, m in enumerate(("cos", "sin")):
                        nc.tensor.matmul(bank[4 + i][:, 0:NB * D], V[m][:, j * S + i * P:j * S + (i + 1) * P],
                                         yc[:, j, c], start=(j == 0 and c == 0), stop=False)
                nc.tensor.matmul(bank[4 + i][:, 0:NB * D], altrow[0:1, i * P:(i + 1) * P],
                                 yny[0:1].rearrange("p b d -> p (b d)"), start=False, stop=True).then_inc(y_mm, 1)

        def act_dft(act):
            for j in range(4):
                act.wait_ge(dft_mm, 4 + j + 1)
                nc.scalar.activation(kf[:, j].rearrange("p c d -> p (c d)"), bank[KBANK[j]][:, 0:2 * D], ACT.Copy,
                                     scale=V["wf"][:, j:j + 1]).then_inc(kf_ready, 1)
            act.wait_ge(dft_mm, 9)
            nc.scalar.activation(kny[:], bank[5][0:1, 2 * D:3 * D], ACT.Copy, scale=1.0 / (2 * S)).then_inc(kf_ready, 1)

        def vec_spectrum(dve, st):
            tt = nc.vector.tensor_tensor
            for b in range(NB):
                tt(tmp[:, b * TB:(b + 1) * TB, :], xk[:, :, b, :], bm(V["dskip"], TB), ALU.mult)
            for j in range(4):
                dve.wait_ge(kf_ready, j + 1)
                if j:
                    dve.wait_ge(prod_ready, j)
                x = bank[j][:].rearrange("p (n d) -> p n d", d=D)
                p = pr[:].rearrange("p i (b d) -> p (i b) d", d=D)
                tt(p[:, 0:2 * NB], x, bm(kf[:, j, 0, :], 2 * NB), ALU.mult)
                tt(p[:, 2 * NB:4 * NB], x, bm(kf[:, j, 1, :], 2 * NB), ALU.mult).then_inc(spec_used, 1)
                dve.wait_ge(spec_used, j + 1)
                tt(yc[:, j, 0], pr[:, 0], pr[:, 3], ALU.subtract)
                tt(yc[:, j, 1], pr[:, 1], pr[:, 2], ALU.add).then_inc(prod_ready, 1)
            dve.wait_ge(kf_ready, 5)
            tt(yny[:], bank[5][0:1, 0:NB * D].rearrange("p (b d) -> p b d", b=NB), bm(kny[:], NB), ALU.mult).then_inc(prod_ready, 1)

        def vec_xt(dve, st):
            tt = nc.vector.tensor_tensor
            chunks = lambda v: v.rearrange("p (b q) d -> p q b d", b=NB)
            tv, xv, xnv = chunks(tmp[:]), chunks(xt[:]), chunks(xn[:])
            f2, f3_ = chunks(film[:, :, 2, :]), chunks(film[:, :, 3, :])
            for i in range(TB):
                dve.wait_ge(y_mm, i + 1)
                st.link(tt(tv[:, i], bank[4 + i][:, 0:NB * D].rearrange("p (b d) -> p b d", b=NB), tv[:, i], ALU.add))
                st.link(tt(tv[:, i], tv[:, i], f2[:, i], ALU.mult))
                st.link(tt(tv[:, i], tv[:, i], f3_[:, i], ALU.add))
                ins = tt(xv[:, i], tv[:, i], xnv[:, i], ALU.add)
            st.link(ins)

        def pe_ffn0(pe):
            pe.wait_ge(*loaded["ffn0"])
            n = 0
            for b in range(NB):
                pe.wait_ge(ln_T, NB * 1 + b + 1)
                for c in range(4):
                    if n >= 4:
                        pe.wait_ge(ff_gelu, n - 3)
                    nc.tensor.matmul(bank[2 + n % 4][:], V["w1"][:, c * P:(c + 1) * P], xnT[:, b * S:(b + 1) * S],
                                     start=True, stop=True).then_inc(ff_mm, 1)
                    n += 1
            for b in range(NB):
                pe.wait_ge(ff_gelu, 4 * b + 4)
                for q4 in range(TB):
                    t = b * TB + q4
                    for c in range(4):
                        ins = nc.tensor.matmul(bank[6 + b][:, q4 * P:(q4 + 1) * P], hT0[:, c, t * P:(t + 1) * P],
                                               V["w2"][:, c * P:(c + 1) * P], start=(c == 0), stop=(c == 3))
                ins.then_inc(ff_out, 1)

        def act_ffn0(act):
            n = 0
            for b in range(NB):
                for c in range(4):
                    act.wait_ge(ff_mm, n + 1)
                    nc.scalar.activation(hT0[:, c, b * S:(b + 1) * S], bank[2 + n % 4][:], ACT.Gelu,
                                         bias=V["b1"][:, c:c + 1]).then_inc(ff_gelu, 1)
                    n += 1

        def vec_ffn0(dve, st):
            st.link(nc.vector.tensor_tensor(tmp[:], xt[:], bm(V["b2"], NT), ALU.add))
            for b in range(NB):
                dve.wait_ge(ff_out, b + 1)
                ins = nc.vector.tensor_tensor(xt[:, b * TB:(b + 1) * TB, :], bank[6 + b][:].rearrange("p (q d) -> p q d", d=D),
                                              tmp[:, b * TB:(b + 1) * TB, :], ALU.add)
            st.link(ins)

        wr, wo0 = V["wr"], V["wo0"]
        wqkv = V["wqkv"].rearrange("p (h w c) -> p h w c", h=HF, w=4)
        qT = part(arenaB, 0, NB, 2, S)
        kT = part(arenaB, 2048, NB, 2, S)
        vv0 = part(arenaB, 4096, NT, CH * DF)
        wsel = part(arenaB, 6144, NB, 4, CH, DF)
        pb0 = part(arenaB, 8192, 3, S)
        pT0 = part(arenaB, 9728, 3, S)
        on0 = part(arenaB, 11264, 2, CH * DF)
        oT0 = part(arenaB, 11776, 2, 2 * P)
        bsel = sb("bsel", P, NB, 2, 2)
        dist = sb("dist", HF, NB)
        dt2 = sb("dt2", NB, HF)
        gm = sb("gm", NB, 8)
        gidx = sb("gidx", NB, 8, dt=U32)
        gidf = sb("gidf", NB, 8)
        gsel = sb("gsel", NB, HF)
        gkey = sb("gkey", NB, 8)
        ghead = sb("ghead", NB, 8, dt=I32)
        gsum, gmax = sb("gsum", NB, 1), sb("gmax", NB, 1)
        nmax0, rsum0 = sb("nmax0", P, NT, CH), sb("rsum0", P, NT, CH)
        rinv0 = sb("rinv0", P, NT, CH)
        rt_exp = sem("rt_exp")
        heads_ready, qk_mm, qk_ready, v_mm, v_ready = sem("heads_ready"), sem("qk_mm"), sem("qk_ready"), sem("v_mm"), sem("v_ready")
        sc_mm, sc_max, sc_exp, sc_turned = sem("sc_mm"), sem("sc_max"), sem("sc_exp"), sem("sc_turned")
        pT_dve, pT_act, pv_mm, o_norm, o_turned, oT_ready, wo_mm, x_added = (
            sem("pT_dve"), sem("pT_act"), sem("pv_mm"), sem("o_norm"), sem("o_turned"), sem("oT_ready"), sem("wo_mm"), sem("x_added"))


        def pe_route(pe):
            for b in range(NB):
                pe.wait_ge(ln_T, NB * 2 + b + 1)
                nc.tensor.matmul(bank[2 + b][0:HF, :], wr, xnT[:, b * S:(b + 1) * S], start=True, stop=True).then_inc(route_pe, 1)
            pe.wait_ge(route_vec, 1)
            nc.tensor.transpose(bank[4][0:NB, 0:HF], dist[:], ident[0:HF, 0:HF]).then_inc(route_pe, 1)

        def vec_route(dve, st):
            Vv = nc.vector
            for b in range(NB):
                dve.wait_ge(route_pe, b + 1)
                ins = Vv.tensor_reduce(dist[:, b:b + 1], bank[2 + b][0:HF, :], AX.X, ALU.add)
            st.link(ins)
            Vv.tensor_scalar(dist[:], dist[:], 1.0 / S, V["br_col"][0:HF], ALU.mult, ALU.add).then_inc(route_vec, 1)
            dve.wait_ge(route_pe, 3)
            st.link(Vv.tensor_reduce(gmax[:], bank[4][0:NB, 0:HF], AX.X, ALU.max))
            Vv.tensor_scalar(dt2[:], bank[4][0:NB, 0:HF], gmax[:], None, ALU.subtract).then_inc(route_vec, 1)
            dve.wait_ge(rt_exp, 1)
            st.link(Vv.reciprocal(gmax[:], gsum[:]))
            st.link(Vv.tensor_scalar(dt2[:], dt2[:], gmax[:], None, ALU.mult))
            st.link(Vv.max(gm[:], dt2[:]))
            st.link(Vv.max_index(gidx[:], gm[:], dt2[:]))
            st.link(Vv.tensor_copy(gidf[:], gidx[:]))
            st.link(Vv.tensor_scalar(gsel[:], V["iota16"][0:NB], gidf[:, 0:1], None, ALU.is_equal))
            for j in range(1, CH):
                st.link(Vv.scalar_tensor_tensor(gsel[:], V["iota16"][0:NB], gidf[:, j:j + 1], gsel[:], ALU.is_equal, ALU.add))
            st.link(Vv.tensor_tensor(gsel[:], gsel[:], V["rev16"][0:NB], ALU.mult))
            st.link(Vv.max(gkey[:], gsel[:]))
            Vv.tensor_scalar(ghead[:], gkey[:], -1.0, float(HF), ALU.mult, ALU.add).then_inc(route_vec, 1)
            dve.wait_ge(route_vec, 3)
            dve.wait_ge(*loaded["head0"])
            for b in range(NB):
                for j in range(0, CH, 2):
                    h = dve.value_load(ghead[b:b + 1, j:j + 1], min_val=0, max_val=HF - 1)
                    r = slice(DF * (j % 2), DF * (j % 2 + 1))
                    Vv.tensor_copy(wsel[:, b, :, j, :].unsqueeze(1), wqkv[:, bass.ds(h, 1), :, :])
                    Vv.tensor_scalar(bsel[r, b, j // 2, 0:1], V["bq2"][r, bass.ds(h, 1)], DF ** -0.5, None, ALU.mult)
                    ins = Vv.tensor_copy(bsel[r, b, j // 2, 1:2], V["bk2"][r, bass.ds(h, 1)])
                ins.then_inc(heads_ready, 1)

        def act_route(act):
            act.wait_ge(route_vec, 2)
            nc.scalar.activation(dt2[:], dt2[:], ACT.Exp, accum_out=gsum[:]).then_inc(rt_exp, 1)
            act.wait_ge(*loaded["head0"])
            act.wait_ge(route_vec, 3)
            for b in range(NB):
                for j in range(1, CH, 2):
                    h = act.value_load(ghead[b:b + 1, j:j + 1], min_val=0, max_val=HF - 1)
                    r = slice(DF * (j % 2), DF * (j % 2 + 1))
                    nc.scalar.copy(wsel[:, b, :, j, :].unsqueeze(1), wqkv[:, bass.ds(h, 1), :, :])
                    nc.scalar.activation(bsel[r, b, j // 2, 0:1], V["bq2"][r, bass.ds(h, 1)], ACT.Copy, scale=DF ** -0.5)
                    ins = nc.scalar.copy(bsel[r, b, j // 2, 1:2], V["bk2"][r, bass.ds(h, 1)])
                ins.then_inc(heads_act, 1)

        def pe_qkv0(pe):
            n = 0
            for b in range(NB):
                pe.wait_ge(heads_ready, b + 1)
                pe.wait_ge(heads_act, b + 1)
                for pair in range(2):
                    for w in range(2):
                        if n >= 4:
                            pe.wait_ge(qk_ready, n - 3)
                        nc.tensor.matmul(bank[2 + n % 4][:], wsel[:, b, w, 2 * pair:2 * pair + 2, :].rearrange("p j c -> p (j c)"),
                                         xnT[:, b * S:(b + 1) * S], start=True, stop=True).then_inc(qk_mm, 1)
                        n += 1
                for q2 in range(TB // 2):
                    if b == 1:
                        pe.wait_ge(v_ready, q2 + 1)
                    for q1 in range(2):
                        t = b * TB + 2 * q2 + q1
                        ins = nc.tensor.matmul(bank[6 + q2][:, q1 * CH * DF:(q1 + 1) * CH * DF], xnT[:, t * P:(t + 1) * P],
                                               wsel[:, b, 2, :, :].rearrange("p j c -> p (j c)"), start=True, stop=True)
                    ins.then_inc(v_mm, 1)

        def act_qk0(act):
            n = 0
            for b in range(NB):
                for pair in range(2):
                    for w, (dst, sc) in enumerate(((qT, DF ** -0.5), (kT, 1.0))):
                        act.wait_ge(qk_mm, n + 1)
                        nc.scalar.activation(dst[:, b, pair, :], bank[2 + n % 4][:], ACT.Identity, scale=sc,
                                             bias=bsel[:, b, pair, w:w + 1]).then_inc(qk_ready, 1)
                        n += 1

        def vec_v0(dve):
            for m in range(4):
                b = m // 2
                dve.wait_ge(v_mm, m + 1)
                for q1 in range(2):
                    ins = nc.vector.tensor_tensor(vv0[:, 2 * m + q1, :].rearrange("p (j c) -> p j c", j=CH),
                                                  bank[6 + m % 2][:, q1 * CH * DF:(q1 + 1) * CH * DF].rearrange("p (j c) -> p j c", j=CH),
                                                  wsel[:, b, 3, :, :], ALU.add)
                ins.then_inc(v_ready, 1)

        NU = NT * CH
        by_act = lambda n: n % 3 == 0
        acts_to = lambda n: n // 3 + 1
        dves_to = lambda n: n - n // 3

        def pe_attend0(pe):
            pe.wait_ge(qk_ready, 8)
            pe.wait_ge(v_ready, 4)
            for n in range(NU + 10):
                if n < NU:
                    t, h = n // CH, n % CH
                    b, r = t // TB, slice(DF * (h % 2), DF * (h % 2 + 1))
                    if n >= 2:
                        pe.wait_ge(sc_exp, n - 1)
                    nc.tensor.matmul(bank[n % 2][:], qT[r, b, h // 2, (t % TB) * P:(t % TB + 1) * P],
                                     kT[r, b, h // 2, :], start=True, stop=True).then_inc(sc_mm, 1)
                m = n - 1
                if 0 <= m < NU:
                    pe.wait_ge(sc_exp, m + 1)
                    if m >= 2:
                        w = m - 2
                        pe.wait_ge(*((pT_act, acts_to(w)) if by_act(w) else (pT_dve, dves_to(w))))
                    for k in range(TB):
                        ins = nc.tensor.transpose(bank[2 + m % 2][:, k * P:(k + 1) * P], pb0[:, m % 3, k * P:(k + 1) * P], ident)
                    ins.then_inc(sc_turned, 1)
                m = n - 2
                if 0 <= m < NU:
                    t, h = m // CH, m % CH
                    pe.wait_ge(*((pT_act, acts_to(m)) if by_act(m) else (pT_dve, dves_to(m))))
                    if h == 0 and t >= 2:
                        pe.wait_ge(o_norm, t - 1)
                    for k in range(TB):
                        ins = nc.tensor.matmul(bank[4 + t % 2][:, h * DF:(h + 1) * DF], pT0[:, m % 3, k * P:(k + 1) * P],
                                               vv0[:, t // TB * TB + k, h * DF:(h + 1) * DF], start=(k == 0), stop=(k == TB - 1))
                    ins.then_inc(pv_mm, 1)
                if n >= 7 and (n - 7) % CH == 0 and (n - 7) // CH < NT:
                    t = (n - 7) // CH
                    pe.wait_ge(o_norm, t + 1)
                    if t:
                        pe.wait_ge(oT_ready, t)
                    for c in range(2):
                        ins = nc.tensor.transpose(bank[6][:, c * P:(c + 1) * P], on0[:, t % 2, c * P:(c + 1) * P], ident)
                    ins.then_inc(o_turned, 1)
                if n >= 9 and (n - 9) % CH == 0 and (n - 9) // CH < NT:
                    t = (n - 9) // CH
                    pe.wait_ge(oT_ready, t + 1)
                    if t:
                        pe.wait_ge(x_added, t)
                    for c in range(2):
                        ins = nc.tensor.matmul(bank[7][:, 0:P], oT0[:, t % 2, c * P:(c + 1) * P], wo0[:, c * P:(c + 1) * P],
                                               start=(c == 0), stop=(c == 1))
                    ins.then_inc(wo_mm, 1)

        def vec_attend0(dve, st):
            for n in range(NU + 11):
                if n < NU:
                    t, h = n // CH, n % CH
                    dve.wait_ge(sc_mm, n + 1)
                    nc.vector.tensor_reduce(nmax0[:, t, h:h + 1], bank[n % 2][:], AX.X, ALU.max, negate=True).then_inc(sc_max, 1)
                m = n - 1
                if 0 <= m < NU and not by_act(m):
                    dve.wait_ge(sc_turned, m + 1)
                    if m >= 3:
                        dve.wait_ge(pv_mm, m - 2)
                    nc.vector.tensor_copy(pT0[:, m % 3, :], bank[2 + m % 2][:]).then_inc(pT_dve, 1)
                if n >= 6 and (n - 6) % CH == 0 and (n - 6) // CH < NT:
                    t = (n - 6) // CH
                    dve.wait_ge(sc_exp, CH * t + CH)
                    st.link(nc.vector.reciprocal(rinv0[:, t, :], rsum0[:, t, :]))
                    dve.wait_ge(pv_mm, CH * t + CH)
                    if t >= 2:
                        dve.wait_ge(o_turned, t - 1)
                    nc.vector.tensor_tensor(on0[:, t % 2, :].rearrange("p (h c) -> p h c", h=CH),
                                            bank[4 + t % 2][:, 0:CH * DF].rearrange("p (h c) -> p h c", h=CH),
                                            bc(rinv0[:, t, :], P, CH, DF), ALU.mult).then_inc(o_norm, 1)
                if n >= 10 and (n - 10) % CH == 0 and (n - 10) // CH < NT:
                    t = (n - 10) // CH
                    if t == 0:
                        dve.wait_ge(bias_added, 1)
                    dve.wait_ge(wo_mm, t + 1)
                    nc.vector.tensor_tensor(X[:, t, :], bank[7][:, 0:P], tmp[:, t, :], ALU.add).then_inc(x_added, 1)
                if n == 11 + CH * (TB - 1):
                    dve.wait_ge(x_added, TB)
                    vec_moments(st, X, [0])
                if n == 15 + CH * (TB - 1):
                    vec_normalise(dve, 4, X, xn, [0])

        def act_attend0(act):
            for n in range(NU + 9):
                if n < NU:
                    t, h = n // CH, n % CH
                    act.wait_ge(sc_max, n + 1)
                    if n >= 3:
                        act.wait_ge(sc_turned, n - 2)
                    nc.scalar.activation(pb0[:, n % 3, :], bank[n % 2][:], ACT.Exp, bias=nmax0[:, t, h:h + 1],
                                         accum_out=rsum0[:, t, h:h + 1]).then_inc(sc_exp, 1)
                m = n - 1
                if 0 <= m < NU and by_act(m):
                    act.wait_ge(sc_turned, m + 1)
                    if m >= 3:
                        act.wait_ge(pv_mm, m - 2)
                    nc.scalar.copy(pT0[:, m % 3, :], bank[2 + m % 2][:]).then_inc(pT_act, 1)
                if n >= 8 and (n - 8) % CH == 0 and (n - 8) // CH < NT:
                    t = (n - 8) // CH
                    act.wait_ge(o_turned, t + 1)
                    if t >= 2:
                        act.wait_ge(wo_mm, t - 1)
                    nc.scalar.copy(oT0[:, t % 2, :], bank[6][:, 0:2 * P]).then_inc(oT_ready, 1)

        def pool_bias(pool, i, row, ready):
            pool.wait_ge(ln_done, NT * (i + 1))
            nc.gpsimd.tensor_tensor(tmp[:], X[:], bm(row, NT), ALU.add).then_inc(ready, 1)

        a1, bm1 = sb("a1", DC, D), sb("bm1", DC, D)
        m1 = sb("m1", P, NB * NC)
        vw1 = sb("vw1", NC, NB, D)
        s1 = part(arenaB, 0, NT, NC)
        e1 = part(arenaB, 1024, NT, NC)
        pT1 = part(arenaB, 2048, TOK)[0:NC]
        st1, mv1 = sb("st1", P, NB, 6), sb("mv1", P, NB, 2)
        mx1, rs1, ri1 = sb("mx1", P, NT), sb("rs1", P, NT), sb("ri1", P, NT)
        vr1, r1 = sb("vr1", P, NB), sb("r1", P, NB)
        fold1_mm, fold1_copy = sem("fold1_mm"), sem("fold1_copy")
        s1_mm, s1_copy, r1_ready = sem("s1_mm"), sem("s1_copy"), sem("r1_ready")
        e1_ready, e1_turned, pT1_ready, y1_mm = sem("e1_ready"), sem("e1_turned"), sem("pT1_ready"), sem("y1_mm")

        def pe_fold1(pe):
            pe.wait_ge(*loaded["l1"])
            pe.wait_ge(s0_copy, NT)
            nc.tensor.matmul(bank[2][0:DC, 0:D], V["wk1"], V["wq1"], start=True, stop=True).then_inc(fold1_mm, 1)
            nc.tensor.matmul(bank[3][0:DC, 0:D], V["wv1"], V["wo1T"], start=True, stop=True).then_inc(fold1_mm, 1)
            pe.wait_ge(fold1_copy, 2)
            nc.tensor.matmul(bank[2][:, 0:NB * NC], a1[:], V["ctxT"][0:DC], start=True, stop=True).then_inc(fold1_mm, 1)
            for b in range(NB):
                ins = nc.tensor.matmul(bank[3][0:NC, b * D:(b + 1) * D], V["ctxT"][0:DC, b * NC:(b + 1) * NC], bm1[:], start=True, stop=True)
            ins.then_inc(fold1_mm, 1)
            pe.wait_ge(fold1_copy, 4)

        def act_fold1(act):
            act.wait_ge(fold1_mm, 1)
            nc.scalar.copy(a1[:], bank[2][0:DC, 0:D]).then_inc(fold1_copy, 1)
            act.wait_ge(fold1_mm, 2)
            nc.scalar.copy(bm1[:], bank[3][0:DC, 0:D]).then_inc(fold1_copy, 1)
            act.wait_ge(fold1_mm, 3)
            nc.scalar.copy(m1[:], bank[2][:, 0:NB * NC]).then_inc(fold1_copy, 1)
            act.wait_ge(fold1_mm, 4)
            nc.scalar.copy(vw1[:], bank[3][0:NC, 0:NB * D].rearrange("p (b d) -> p b d", b=NB)).then_inc(fold1_copy, 1)

        def pe_l1x(pe):
            for b in range(NB):
                pe.wait_ge(ln_T, NB * 3 + b + 1)
                for q4 in range(TB):
                    t = b * TB + q4
                    ins = nc.tensor.matmul(bank[2 + b][:, q4 * NC:(q4 + 1) * NC], xnT[:, t * P:(t + 1) * P],
                                           m1[:, b * NC:(b + 1) * NC], start=True, stop=True)
                ins.then_inc(s1_mm, 1)
            pe.wait_ge(l1x_vec, 1)
            nc.tensor.matmul(bank[4][:, 0:NB], V["avg"], mv1[:, :, 0], start=True, stop=True).then_inc(avg1_mm, 1)
            pe.wait_ge(l1x_vec, 2)
            nc.tensor.matmul(bank[5][:, 0:NB], V["avg"], vr1[:], start=True, stop=True).then_inc(avg1_mm, 1)
            for t in range(NT):
                pe.wait_ge(e1_ready, t + 1)
                if t == 0:
                    pe.wait_ge(l1x_vec, 3)
                ins = nc.tensor.transpose(bank[4 + t // TB][0:NC, (t % TB) * P:(t % TB + 1) * P], e1[:, t, :], ident)
                if t % TB == TB - 1:
                    ins.then_inc(e1_turned, 1)
            for b in range(NB):
                pe.wait_ge(pT1_ready, b + 1)
                for q4 in range(TB):
                    t = b * TB + q4
                    ins = nc.tensor.matmul(bank[6 + b][:, q4 * P:(q4 + 1) * P], pT1[:, t * P:(t + 1) * P], vw1[:, b, :],
                                           start=True, stop=True)
                ins.then_inc(y1_mm, 1)

        def act_l1x(act):
            for b in range(NB):
                act.wait_ge(s1_mm, b + 1)
                nc.scalar.copy(s1[:, b * TB:(b + 1) * TB, :], bank[2 + b][:, 0:TB * NC].rearrange("p (q k) -> p q k", k=NC)).then_inc(s1_copy, 1)
            act.wait_ge(l1x_vec, 4)
            act.wait_ge(r1_ready, 1)
            for t in range(NT):
                nc.scalar.activation(e1[:, t, :], s1[:, t, :], ACT.Exp, scale=r1[:, t // TB:t // TB + 1], bias=mx1[:, t:t + 1],
                                     accum_out=rs1[:, t:t + 1]).then_inc(e1_ready, 1)
            for b in range(NB):
                act.wait_ge(e1_turned, b + 1)
                nc.scalar.copy(pT1[:, b * S:(b + 1) * S], bank[4 + b][0:NC, :]).then_inc(pT1_ready, 1)

        def pool_l1x(pool, st):
            pool.wait_ge(l1x_vec, 3)
            nc.gpsimd.tensor_tensor(r1[:], vr1[:], V["half"][:, 0:NB], ALU.pow).then_inc(r1_ready, 1)

        def vec_l1x(dve, st):
            Vv = nc.vector
            for b in range(NB):
                dve.wait_ge(s1_copy, b + 1)
                ins = Vv.bn_stats(st1[:, b, :], s1[:, b * TB:(b + 1) * TB, :].rearrange("p q k -> p (q k)"))
            st.link(ins)
            for b in range(NB):
                ins = Vv.bn_aggr(mv1[:, b, :], st1[:, b, :])
            ins.then_inc(l1x_vec, 1)
            Vv.tensor_reduce(mx1[:], s1[:], AX.X, ALU.max, negate=True)
            dve.wait_ge(l1x_vec, 1)
            dve.wait_ge(avg1_mm, 1)
            st.link(Vv.tensor_tensor(vr1[:], mv1[:, :, 0], bank[4][:, 0:NB], ALU.subtract))
            st.link(Vv.tensor_tensor(vr1[:], vr1[:], vr1[:], ALU.mult))
            Vv.tensor_tensor(vr1[:], vr1[:], mv1[:, :, 1], ALU.add).then_inc(l1x_vec, 1)
            dve.wait_ge(avg1_mm, 2)
            Vv.tensor_scalar(vr1[:], bank[5][:, 0:NB], 1e-5, None, ALU.add).then_inc(l1x_vec, 1)
            dve.wait_ge(r1_ready, 1)
            Vv.tensor_tensor(mx1[:].rearrange("p (b q) -> p b q", b=NB), mx1[:].rearrange("p (b q) -> p b q", b=NB),
                             bc(r1[:], P, NB, TB), ALU.mult).then_inc(l1x_vec, 1)
            dve.wait_ge(e1_ready, NT)
            st.link(Vv.reciprocal(ri1[:], rs1[:]))
            for t in range(NT):
                if t % TB == 0:
                    dve.wait_ge(y1_mm, t // TB + 1)
                ins = Vv.scalar_tensor_tensor(X[:, t, :], bank[6 + t // TB][:, (t % TB) * P:(t % TB + 1) * P], ri1[:, t:t + 1],
                                              X[:, t, :], ALU.mult, ALU.add)
            st.link(ins)

        NG = NCL + NTL
        sig = sb("sig", P, NG)
        sigq = sb("sigq", P, NTL)
        kd = sb("kd", P, KN - 1)
        rden = sb("rden", P, 1)
        sc1 = part(arenaB, 0, NT, NG)
        fl1 = part(arenaB, 576, NT, NG)
        lo1 = part(arenaB, 1152, NT, NG)
        vl1 = part(arenaB, 1728, NT, NG)
        dv1 = part(arenaB, 2304, NT, NG)
        ga1 = part(arenaB, 2880, NT, NG)
        ta1 = part(arenaB, 3456, NT, NG)
        tb1 = part(arenaB, 4032, NT, NG)
        ohT = part(arenaB, 4608, TOK)[0:NTL]
        got = part(arenaB, 5632, NT, TABW)
        hT1 = part(arenaB, 7176, TOK)[0:CMP]
        oh1 = part(arenaB, 8200, NT, NTL)
        ocl, osl, sg1 = part(arenaB, 8712, NT, NCL), part(arenaB, 8776, NT, TPC), part(arenaB, 8840, NT, TPC)
        cm1, cn1 = part(arenaB, 8904, NT, NCL), part(arenaB, 8968, NT, NCL)
        b81 = sb("b81", P, NT)
        comp = sb("comp", P, NT, 2)
        hh1, hx1 = part(arenaB, 9032, NT, GRID), part(arenaB, 9160, NT, GRID)
        mag = sb("mag", P, NT)
        sig_ready, dv_ready = sem("sig_ready"), sem("dv_ready")


        def vec_sigs(dve, st):
            Vv = nc.vector
            dve.wait_ge(*loaded["l1"])
            raw, sg = V["sigT"], sig[:, NCL:NG]
            st.link(Vv.tensor_scalar(sigq[:], raw, -0.3, None, ALU.is_lt))
            st.link(Vv.scalar_tensor_tensor(sigq[:], raw, 0.3, sigq[:], ALU.is_gt, ALU.subtract))
            st.link(Vv.tensor_tensor(sigq[:], sigq[:], raw, ALU.subtract))
            st.link(Vv.tensor_tensor(sg, sigq[:], raw, ALU.add))
            st.link(Vv.tensor_reduce(sig[:, 0:NCL], sg.rearrange("p (c j) -> p c j", c=NCL), AX.X, ALU.add))
            st.link(Vv.tensor_scalar(sigq[:, 0:NCL], sig[:, 0:NCL], 0.0, None, ALU.is_lt))
            st.link(Vv.scalar_tensor_tensor(sig[:, 0:NCL], sig[:, 0:NCL], 0.0, sigq[:, 0:NCL], ALU.is_gt, ALU.subtract))
            st.link(Vv.tensor_tensor(kd[:], V["knots"][:, 1:KN], V["knots"][:, 0:KN - 1], ALU.subtract))
            st.link(Vv.tensor_scalar(rden[:], V["temp"], 1e-6, None, ALU.add))
            Vv.reciprocal(rden[:], rden[:]).then_inc(sig_ready, 1)

        def pe_l1f(pe):
            pe.wait_ge(sig_ready, 1)
            for b in range(NB):
                pe.wait_ge(ln_T, NB * 4 + b + 1)
                for q4 in range(TB):
                    t = b * TB + q4
                    ins = nc.tensor.matmul(bank[2 + b][:, q4 * NG:(q4 + 1) * NG], xnT[:, t * P:(t + 1) * P], sig[:], start=True, stop=True)
                ins.then_inc(l1f_pe, 1)
            for b in range(NB):
                nc.tensor.matmul(bank[4 + b][0:CMP, :], V["cw1"], xnT[:, b * S:(b + 1) * S], start=True, stop=True).then_inc(l1f_pe, 1)
            pe.wait_ge(l1f_act, 1 + NB)
            for t in range(NT):
                ins = nc.tensor.matmul(bank[6][:, 2 * t:2 * t + 2], hT1[:, t * P:(t + 1) * P], V["cw2"][0:CMP], start=True, stop=True)
            ins.then_inc(l1f_pe, 1)
            if LAST_STAGE >= 7:
                pe.wait_ge(*loaded["l3"])
                pe.wait_ge(l1f_vec, 3)
                pe_fold3(pe, 0, FOLD_EARLY)
            for b in range(NB):
                pe.wait_ge(l1f_vec, 4 + b)
                for q4 in range(TB):
                    ins = nc.tensor.transpose(bank[b][0:NTL, q4 * P:(q4 + 1) * P], oh1[:, b * TB + q4, :], ident)
                ins.then_inc(l1f_pe, 1)
                for m in range(b * TB // 2, (b + 1) * TB // 2):
                    pe.wait_ge(l1f_act, 5 + 3 * b)
                    for k in range(2):
                        t = 2 * m + k
                        ins = nc.tensor.matmul(bank[2 + m][:, k * TABW:(k + 1) * TABW], ohT[:, t * P:(t + 1) * P], V["tab"][0:NTL],
                                               start=True, stop=True)
                    ins.then_inc(l1f_pe, 1)
            if LAST_STAGE >= 7:
                pe.wait_ge(l1f_act, NT // 2 + 6)
                pe_fold3(pe, FOLD_EARLY, H3 // 2)

        def act_l1f(act):
            act.wait_ge(l1f_vec, 1)
            nc.scalar.activation(sc1[:], sc1[:], ACT.Exp, scale=-1.0).then_inc(l1f_act, 1)
            for b in range(NB):
                act.wait_ge(l1f_pe, b + 3)
                nc.scalar.activation(hT1[:, b * S:(b + 1) * S], bank[4 + b][0:CMP, :], ACT.Gelu, bias=V["cb1"][0:CMP]).then_inc(l1f_act, 1)
            act.wait_ge(l1f_vec, 3)
            nc.scalar.activation(comp[:], comp[:], ACT.Tanh).then_inc(l1f_act, 1)
            if LAST_STAGE >= 7:
                act_fold3(act, 0, FOLD_EARLY)
            for b in range(NB):
                act.wait_ge(l1f_pe, 6 + 3 * b)
                nc.scalar.copy(ohT[:, b * S:(b + 1) * S], bank[b][0:NTL, :]).then_inc(l1f_act, 1)
                for m in range(b * TB // 2, (b + 1) * TB // 2):
                    act.wait_ge(l1f_pe, 7 + m + b)
                    nc.scalar.copy(got[:, 2 * m:2 * m + 2, :], bank[2 + m][:, 0:2 * TABW].rearrange("p (k n) -> p k n", k=2)).then_inc(l1f_act, 1)
            if LAST_STAGE >= 7:
                act_fold3(act, FOLD_EARLY, H3 // 2)

        def pool_l1f(pool, st):
            G = nc.gpsimd
            pool.wait_ge(l1f_vec, 2)
            st.link(G.tensor_scalar(dv1[:], lo1[:], float(SPLITK), kd[:, SPLITK:SPLITK + 1], ALU.is_equal, ALU.mult))
            for k in range(SPLITK + 1, KN - 1):
                st.link(G.tensor_scalar(tb1[:], lo1[:], float(k), kd[:, k:k + 1], ALU.is_equal, ALU.mult))
                ins = G.tensor_tensor(dv1[:], dv1[:], tb1[:], ALU.add)
                if k < KN - 2:
                    st.link(ins)
            ins.then_inc(dv_ready, 1)

        def first_best(dve, st, vals, best, onehot):
            Vv = nc.vector
            rev = bm(V["rev8"], NT)
            st.link(Vv.tensor_reduce(best[:], vals[:], AX.X, ALU.max))
            st.link(Vv.tensor_tensor(onehot[:], vals[:], bc(best[:], P, NT, 8), ALU.is_equal))
            st.link(Vv.tensor_tensor(onehot[:], onehot[:], rev, ALU.mult))
            st.link(Vv.tensor_reduce(best[:], onehot[:], AX.X, ALU.max))
            st.link(Vv.tensor_tensor(onehot[:], onehot[:], bc(best[:], P, NT, 8), ALU.is_equal))

        def vec_l1f(dve, st):
            Vv = nc.vector
            for b in range(NB):
                dve.wait_ge(l1f_pe, b + 1)
                ins = Vv.tensor_scalar(sc1[:, b * TB:(b + 1) * TB, :], bank[2 + b][:, 0:TB * NG].rearrange("p (q k) -> p q k", k=NG),
                                       rden[:], None, ALU.mult)
            ins.then_inc(l1f_vec, 1)
            dve.wait_ge(l1f_act, 1)
            st.link(Vv.tensor_scalar(sc1[:], sc1[:], 1.0, None, ALU.add))
            st.link(Vv.reciprocal(fl1[:], sc1[:]))
            st.link(Vv.tensor_scalar(fl1[:], fl1[:], float(KN - 1), None, ALU.mult))
            st.link(Vv.tensor_scalar(lo1[:], fl1[:], 1.0, None, ALU.is_ge))
            for k in range(2, KN - 1):
                ins = Vv.scalar_tensor_tensor(lo1[:], fl1[:], float(k), lo1[:], ALU.is_ge, ALU.add)
                if k < KN - 2:
                    st.link(ins)
            ins.then_inc(l1f_vec, 1)
            dve.wait_ge(l1f_pe, 5)
            Vv.tensor_tensor(comp[:], bank[6][:, 0:2 * NT].rearrange("p (t c) -> p t c", c=2), bm(V["cb2"], NT), ALU.add).then_inc(l1f_vec, 1)
            dve.wait_ge(l1f_vec, 2)
            st.link(Vv.tensor_tensor(fl1[:], fl1[:], lo1[:], ALU.subtract))
            st.link(Vv.tensor_scalar(vl1[:], lo1[:], 0.0, V["knots"][:, 0:1], ALU.is_equal, ALU.mult))
            for k in range(1, KN - 1):
                st.link(Vv.tensor_scalar(ta1[:], lo1[:], float(k), V["knots"][:, k:k + 1], ALU.is_equal, ALU.mult))
                st.link(Vv.tensor_tensor(vl1[:], vl1[:], ta1[:], ALU.add))
            st.link(Vv.tensor_scalar(ga1[:], lo1[:], 0.0, kd[:, 0:1], ALU.is_equal, ALU.mult))
            for k in range(1, SPLITK):
                st.link(Vv.tensor_scalar(ta1[:], lo1[:], float(k), kd[:, k:k + 1], ALU.is_equal, ALU.mult))
                st.link(Vv.tensor_tensor(ga1[:], ga1[:], ta1[:], ALU.add))
            dve.wait_ge(dv_ready, 1)
            st.link(Vv.tensor_tensor(ga1[:], ga1[:], dv1[:], ALU.add))
            st.link(Vv.tensor_tensor(ga1[:], fl1[:], ga1[:], ALU.mult))
            st.link(Vv.tensor_tensor(ga1[:], vl1[:], ga1[:], ALU.add))
            first_best(dve, st, ga1[:, :, 0:NCL], b81, ocl)
            ins = None
            for t in range(NT):
                ins = Vv.tensor_tensor(oh1[:, t].rearrange("p (c j) -> p c j", c=NCL), ga1[:, t, NCL:NG].rearrange("p (c j) -> p c j", c=NCL),
                                       bc(ocl[:, t], P, NCL, TPC), ALU.mult)
            st.link(ins)
            for t in range(NT):
                ins = Vv.tensor_reduce(sg1[:, t], oh1[:, t].rearrange("p (c j) -> p j c", c=NCL), AX.X, ALU.add)
            st.link(ins)
            first_best(dve, st, sg1, b81, osl)
            for r in halves():
                for t in range(r.start, r.stop):
                    ins = Vv.tensor_tensor(oh1[:, t].rearrange("p (c j) -> p c j", c=NCL), bm(osl[:, t], NCL), bc(ocl[:, t], P, NCL, TPC), ALU.mult)
                ins.then_inc(l1f_vec, 1)
            dve.wait_ge(l1f_act, 4)
            G_ = GRID
            for b, r in enumerate(halves()):
                dve.wait_ge(l1f_act, 7 + 3 * b)
                h, x, g = hh1[:, r], hx1[:, r], got[:, r]
                Vv.tensor_tensor(h, g[:, :, 0:G_], bc(comp[:, r, 0], P, TB, G_), ALU.mult)
                st.link(Vv.tensor_tensor(x, g[:, :, G_:2 * G_], bc(comp[:, r, 1], P, TB, G_), ALU.mult))
                st.link(Vv.tensor_tensor(h, h, x, ALU.add))
                st.link(Vv.tensor_tensor(h, h, g[:, :, 2 * G_:3 * G_], ALU.add))
                st.link(Vv.scalar_tensor_tensor(h, h, 0.0, g[:, :, 3 * G_:4 * G_], ALU.max, ALU.mult))
                st.link(Vv.tensor_reduce(mag[:, r], h, AX.X, ALU.add))
                st.link(Vv.tensor_tensor(mag[:, r], mag[:, r], g[:, :, 4 * G_], ALU.add))
                st.link(Vv.tensor_scalar(mag[:, r], mag[:, r], V["oscale"], None, ALU.mult))
                for t in range(r.start, r.stop):
                    ins = Vv.scalar_tensor_tensor(xt[:, t, :], got[:, t, 4 * G_ + 1:TABW], mag[:, t:t + 1], xn[:, t, :], ALU.mult, ALU.add)
            st.link(ins)

        var2, mv2 = sb("var2", P, NT), sb("mv2", P, NT)

        def pool_rstd_twice(pool, st, i, ready):
            pool.wait_ge(ln_rstd, NB * (i + 1))
            G = nc.gpsimd
            st.link(G.tensor_tensor(var2[:], rstd[:], rstd[:], ALU.mult))
            st.link(G.tensor_tensor(var2[:], var2[:], mv[:, :, 1], ALU.mult))
            st.link(G.tensor_scalar(var2[:], var2[:], 1e-5, None, ALU.add))
            G.tensor_tensor(mv2[:], var2[:], V["half"][:, 0:NT], ALU.pow).then_inc(ready, 1)

        twice_ready = sem("twice_ready")
        final_stage_done, stored = sem("final_stage_done"), sem("stored")

        KL = S
        cn2 = sb("cn2", NC, NB, DC)
        stc, mvc, rdc = sb("stc", NC, NB, 6), sb("mvc", NC, NB, 2), sb("rdc", NC, NB)
        cnT2 = sb("cnT2", DC, NB * NC)
        kvc = sb("kvc", NC, NB, 2 * D)
        sqc, ssc = sb("sqc", NC, NB, D), sb("ssc", NC, NB, H2)
        kcT = sb("kcT", P, NB, NC)
        qkv2 = part(arenaB, 0, NT, 3 * D)
        sq2 = part(arenaB, 3072, NT, 2 * D)
        pT2 = part(arenaB, 3072, 3, 5 * P)
        qT2, kT2 = part(arenaB, 5120, TOK), part(arenaB, 6144, TOK)
        pb2 = part(arenaB, 7168, 3, KL + NC)
        sc2 = [part(v[:].rearrange("p t d -> p (t d)"), 0, TB * H2, NC) for v in (xt, xn)]
        oT2 = part(tmp2[:].rearrange("p t d -> p (t d)"), 0, 2, H2 * P)[0:D2]
        ss2, inv2 = sb("ss2", P, NT, 2 * H2), sb("inv2", P, NT, 2 * H2)
        nma, nmb, nm2 = sb("nma", P, NT * H2), sb("nmb", P, NT * H2), sb("nm2", P, NT * H2)
        rsa, rsb, ri2 = sb("rsa", P, NT, H2), sb("rsb", P, NT, H2), sb("ri2", P, NT, H2)
        c2_mm, c2_copy = sem("c2_mm"), sem("c2_copy")
        lat_done, qkv2_mm, qkv2_copy, ss2_ready, inv2_ready, qk2_scaled, qk2_turned, qkT2_ready = (
            sem("lat_done"), sem("qkv2_mm"), sem("qkv2_copy"), sem("ss2_ready"), sem("inv2_ready"), sem("qk2_scaled"), sem("qk2_turned"), sem("qkT2_ready"))
        a2_mm, a2_max, a2_exp, a2_turned, p2_dve, p2_act, pv2_mm, oT2_ready, wo2_mm, x2_added = (
            sem(f"{n}") for n in ("a2_mm", "a2_max", "a2_exp", "a2_turned", "p2_dve", "p2_act", "pv2_mm",
                                  "oT2_ready", "wo2_mm", "x2_added"))

        def vec_c2_moments(dve, st):
            dve.wait_ge(*loaded["l2"])
            cr = V["ctxr"][0:NC].rearrange("p (b d) -> p b d", b=NB)
            for b in range(NB):
                ins = nc.vector.bn_stats(stc[:, b, :], cr[:, b, :])
            st.link(ins)
            for b in range(NB):
                ins = nc.vector.bn_aggr(mvc[:, b, :], stc[:, b, :])
            ins.then_inc(c2_stats, 1)

        def pool_c2_rstd(pool, st):
            pool.wait_ge(c2_stats, 1)
            st.link(nc.gpsimd.tensor_scalar(rdc[:], mvc[:, :, 1], 1e-5, None, ALU.add))
            nc.gpsimd.tensor_tensor(rdc[:], rdc[:], V["half"][0:NC, 0:NB], ALU.pow).then_inc(c2_powers, 1)

        def vec_c2_norm(dve, st):
            cr = V["ctxr"][0:NC].rearrange("p (b d) -> p b d", b=NB)
            dve.wait_ge(c2_powers, 1)
            for b in range(NB):
                ins = nc.vector.tensor_scalar(cn2[:, b, :], cr[:, b, :], mvc[:, b, 0:1], rdc[:, b:b + 1], ALU.subtract, ALU.mult)
            st.link(ins)
            st.link(nc.vector.tensor_tensor(cn2[:], cn2[:], bm(V["lnx_g"][0:NC], NB), ALU.mult))
            nc.vector.tensor_tensor(cn2[:], cn2[:], bm(V["lnx_b"][0:NC], NB), ALU.add).then_inc(c2_scaled, 1)

        def pe_c2(pe):
            pe.wait_ge(c2_scaled, 1)
            for b in range(NB):
                ins = nc.tensor.transpose(bank[6][0:DC, b * NC:(b + 1) * NC], cn2[:, b, :], ident[0:NC, 0:NC])
            ins.then_inc(c2_mm, 1)
            pe.wait_ge(c2_copy, 1)
            for b in range(NB):
                ins = nc.tensor.matmul(bank[7][0:NC, b * 2 * D:(b + 1) * 2 * D], cnT2[:, b * NC:(b + 1) * NC], V["wkvT"][0:DC], start=True, stop=True)
            ins.then_inc(c2_mm, 1)

        def act_c2(act):
            act.wait_ge(c2_mm, 1)
            nc.scalar.copy(cnT2[:], bank[6][0:DC, 0:NB * NC]).then_inc(c2_copy, 1)
            act.wait_ge(c2_mm, 2)
            nc.scalar.copy(kvc[:], bank[7][0:NC, :].rearrange("p (b n) -> p b n", b=NB)).then_inc(c2_copy, 1)

        def vec_c2_squares(dve, st):
            dve.wait_ge(c2_copy, 2)
            st.link(nc.vector.tensor_tensor(sqc[:], kvc[:, :, 0:D], kvc[:, :, 0:D], ALU.mult))
            nc.vector.tensor_reduce(ssc[:].rearrange("p b h -> p (b h)"), sqc[:].rearrange("p b (h c) -> p (b h) c", h=H2), AX.X, ALU.add).then_inc(c2_stats, 1)

        def pool_c2_inv(pool, st):
            pool.wait_ge(c2_stats, 2)
            st.link(nc.gpsimd.tensor_scalar(ssc[:], ssc[:], 1.0 / D2, 1e-16, ALU.mult, ALU.max))
            nc.gpsimd.tensor_tensor(ssc[:].rearrange("p b h -> p (b h)"), ssc[:].rearrange("p b h -> p (b h)"),
                                    V["half"][0:NC, 0:NB * H2], ALU.pow).then_inc(c2_powers, 1)

        def vec_c2_scale(dve):
            dve.wait_ge(c2_powers, 2)
            for b in range(NB):
                kk = kvc[:, b, 0:D].rearrange("p (h c) -> p h c", h=H2)
                ins = nc.vector.tensor_tensor(kk, kk, bc(ssc[:, b], NC, H2, D2), ALU.mult)
            ins.then_inc(c2_scaled, 1)

        def pe_c2_keys(pe):
            pe.wait_ge(c2_scaled, 2)
            for b in range(NB):
                ins = nc.tensor.transpose(bank[6][:, b * NC:(b + 1) * NC], kvc[:, b, 0:D], ident[0:NC, 0:NC])
            ins.then_inc(c2_mm, 1)

        def act_c2_keys(act):
            act.wait_ge(c2_mm, 3)
            nc.scalar.activation(kcT[:], bank[6][:, 0:NB * NC].rearrange("p (b k) -> p b k", b=NB), ACT.Copy, scale=V["kn"]).then_inc(c2_copy, 1)

        def vec_latents(dve):
            dve.wait_ge(twice_ready, 2)
            for t in range(NT):
                nc.vector.tensor_scalar(tmp2[:, t, :], xn[:, t, :], mv2[:, t:t + 1], None, ALU.mult).then_inc(lat_done, 1)

        def pe_qkv2(pe):
            at = NB * DC
            for t in range(NT):
                if t % TB == 0:
                    pe.wait_ge(ln_T, NB * 5 + t // TB + 1)
                if t >= 4:
                    pe.wait_ge(qkv2_copy, t - 3)
                nc.tensor.matmul(bank[2 + t % 4][:, 0:3 * D], xnT[:, t * P:(t + 1) * P], packed["l2"][:, at:at + 3 * D],
                                 start=True, stop=True).then_inc(qkv2_mm, 1)
            for w in range(2):
                for b in range(NB):
                    pe.wait_ge(qk2_scaled, b + 1)
                    for q4 in range(TB):
                        ins = nc.tensor.transpose(bank[2 * w + b][:, q4 * P:(q4 + 1) * P], qkv2[:, b * TB + q4, w * D:(w + 1) * D], ident)
                    ins.then_inc(qk2_turned, 1)

        def act_qkv2(act):
            for t in range(NT):
                act.wait_ge(qkv2_mm, t + 1)
                nc.scalar.copy(qkv2[:, t, :], bank[2 + t % 4][:, 0:3 * D]).then_inc(qkv2_copy, 1)
            for w, (dst, g) in enumerate(((qT2, V["qn"]), (kT2, V["kn"]))):
                for b in range(NB):
                    act.wait_ge(qk2_turned, 2 * w + b + 1)
                    nc.scalar.activation(dst[:, b * S:(b + 1) * S], bank[2 * w + b][:], ACT.Copy, scale=g).then_inc(qkT2_ready, 1)

        def vec_qkv2(dve, st):
            for b in range(NB):
                r = slice(b * TB, (b + 1) * TB)
                dve.wait_ge(qkv2_copy, (b + 1) * TB)
                st.link(nc.vector.tensor_tensor(sq2[:, r], qkv2[:, r, 0:2 * D], qkv2[:, r, 0:2 * D], ALU.mult))
                nc.vector.tensor_reduce(ss2[:, r].rearrange("p t g -> p (t g)"), sq2[:, r].rearrange("p t (g c) -> p (t g) c", c=D2),
                                        AX.X, ALU.add).then_inc(ss2_ready, 1)
            for b in range(NB):
                r = range(b * TB, (b + 1) * TB)
                dve.wait_ge(inv2_ready, b + 1)
                for t in r:
                    v = qkv2[:, t, 0:2 * D].rearrange("p (g c) -> p g c", c=D2)
                    ins = nc.vector.tensor_tensor(v, v, bc(inv2[:, t], P, 2 * H2, D2), ALU.mult)
                ins.then_inc(qk2_scaled, 1)

        def pool_qkv2(pool, st):
            for b in range(NB):
                r = slice(b * TB, (b + 1) * TB)
                pool.wait_ge(ss2_ready, b + 1)
                st.link(nc.gpsimd.tensor_scalar(ss2[:, r], ss2[:, r], 1.0 / D2, 1e-16, ALU.mult, ALU.max))
                nc.gpsimd.tensor_tensor(inv2[:, r].rearrange("p t g -> p (t g)"), ss2[:, r].rearrange("p t g -> p (t g)"),
                                        V["half"][:, 0:TB * 2 * H2], ALU.pow).then_inc(inv2_ready, 1)

        NU2 = NT * H2

        def ctx_unit(n):
            t, h = n // H2, n % H2
            return t // TB * TB * H2 + h * TB + t % TB

        def pe_attend2(pe):
            pe.wait_ge(c2_copy, 3)
            for i in range(NB * H2):
                b, h = i // H2, i % H2
                pe.wait_ge(qkT2_ready, b + 1)
                r = slice(D2 * h, D2 * (h + 1))
                for q4 in range(TB):
                    t = b * TB + q4
                    ins = nc.tensor.matmul(bank[4 + i][:, q4 * NC:(q4 + 1) * NC], qT2[r, t * P:(t + 1) * P], kcT[r, b, :], start=True, stop=True)
                ins.then_inc(c2_mm, 1)
            pe.wait_ge(qkT2_ready, 4)
            for n in range(NU2 + 5):
                if n < NU2:
                    t, h = n // H2, n % H2
                    b, r = t // TB, slice(D2 * h, D2 * (h + 1))
                    if n >= 3:
                        pe.wait_ge(a2_exp, n - 2)
                    nc.tensor.matmul(bank[n % 3][:], qT2[r, t * P:(t + 1) * P], kT2[r, b * S:(b + 1) * S], start=True, stop=True).then_inc(a2_mm, 1)
                m = n - 2
                if 0 <= m < NU2:
                    pe.wait_ge(a2_exp, m + 1)
                    if m >= 2:
                        pe.wait_ge(p2_dve, m - 1)
                    for k in range(TB):
                        nc.tensor.transpose(bank[4 + m % 2][:, k * P:(k + 1) * P], pb2[:, m % 3, k * P:(k + 1) * P], ident)
                    if m:
                        pe.wait_ge(p2_act, m)
                    nc.tensor.transpose(bank[3][0:NC, 0:P], pb2[:, m % 3, KL:KL + NC], ident).then_inc(a2_turned, 1)
                m = n - 3
                if 0 <= m < NU2:
                    t, h = m // H2, m % H2
                    pe.wait_ge(p2_dve, m + 1)
                    pe.wait_ge(p2_act, m + 1)
                    if h == 0 and t >= 2:
                        pe.wait_ge(x2_added, t - 1)
                    o = bank[6 + t % 2][0:D2, h * P:(h + 1) * P]
                    for k in range(TB):
                        nc.tensor.matmul(o, qkv2[:, t // TB * TB + k, 2 * D + h * D2:2 * D + (h + 1) * D2], pT2[:, m % 3, k * P:(k + 1) * P],
                                         start=(k == 0), stop=False)
                    nc.tensor.matmul(o, kvc[:, t // TB, D + h * D2:D + (h + 1) * D2], pT2[0:NC, m % 3, TB * P:(TB + 1) * P],
                                     start=False, stop=True).then_inc(pv2_mm, 1)
                if n >= 5 and n % 2 == 1 and (n - 5) // 2 < NT:
                    t = (n - 5) // 2
                    pe.wait_ge(oT2_ready, t + 1)
                    for h in range(H2):
                        ins = nc.tensor.matmul(bank[6 + t % 2][:, (2 + h) * P:(3 + h) * P], oT2[:, t % 2, h * P:(h + 1) * P],
                                               V["wo2T"][0:D2, h * D:(h + 1) * D], start=True, stop=True)
                    ins.then_inc(wo2_mm, 1)

        def vec_attend2(dve, st):
            Vv = nc.vector
            for i in range(NB * H2):
                b, at = i // H2, i % H2 * TB
                dve.wait_ge(c2_mm, 4 + i)
                ins = Vv.tensor_tensor(sc2[b][:, at:at + TB, :], bank[4 + i][:, 0:TB * NC].rearrange("p (u k) -> p u k", k=NC),
                                       bm(maskb[:, 1, b, :], TB), ALU.add)
            st.link(ins)
            for b in range(NB):
                ins = Vv.tensor_reduce(nmb[:, b * TB * H2:(b + 1) * TB * H2], sc2[b], AX.X, ALU.max, negate=True)
            st.link(ins)
            for n in range(NU2 + 6):
                if n >= 6 and n % 2 == 0 and (n - 6) // 2 < NT:
                    t = (n - 6) // 2
                    if t == 0:
                        dve.wait_ge(bias_added, 2)
                    st.link(Vv.tensor_tensor(rsa[:, t], rsa[:, t], rsb[:, t], ALU.add))
                    st.link(Vv.reciprocal(ri2[:, t], rsa[:, t]))
                    dve.wait_ge(wo2_mm, t + 1)
                    o = bank[6 + t % 2]
                    st.link(Vv.scalar_tensor_tensor(X[:, t, :], o[:, 2 * P:3 * P], ri2[:, t, 0:1], tmp[:, t, :], ALU.mult, ALU.add))
                    Vv.scalar_tensor_tensor(X[:, t, :], o[:, 3 * P:4 * P], ri2[:, t, 1:2], X[:, t, :], ALU.mult, ALU.add).then_inc(x2_added, 1)
                if n == 7 + 2 * (TB - 1):
                    dve.wait_ge(x2_added, TB)
                    vec_moments(st, X, [0])
                if n < NU2:
                    dve.wait_ge(a2_mm, n + 1)
                    st.link(Vv.tensor_reduce(nma[:, n:n + 1], bank[n % 3][:], AX.X, ALU.max, negate=True))
                    Vv.tensor_scalar(nm2[:, n:n + 1], nma[:, n:n + 1], nmb[:, ctx_unit(n):ctx_unit(n) + 1], D2 ** -0.5, ALU.min, ALU.mult).then_inc(a2_max, 1)
                m = n - 2
                if 0 <= m < NU2:
                    dve.wait_ge(a2_turned, m + 1)
                    if m >= 3:
                        dve.wait_ge(pv2_mm, m - 2)
                    Vv.tensor_copy(pT2[:, m % 3, 0:TB * P], bank[4 + m % 2][:]).then_inc(p2_dve, 1)

        def act_attend2(act):
            for n in range(NU2 + 4):
                if n < NU2:
                    t, h = n // H2, n % H2
                    act.wait_ge(a2_max, n + 1)
                    if n >= 3:
                        act.wait_ge(a2_turned, n - 2)
                    nc.scalar.activation(pb2[:, n % 3, 0:KL], bank[n % 3][:], ACT.Exp, bias=nm2[:, n:n + 1], scale=D2 ** -0.5,
                                         accum_out=rsa[:, t, h:h + 1])
                    nc.scalar.activation(pb2[:, n % 3, KL:KL + NC], sc2[t // TB][:, ctx_unit(n) % (TB * H2), :], ACT.Exp, bias=nm2[:, n:n + 1],
                                         scale=D2 ** -0.5, accum_out=rsb[:, t, h:h + 1]).then_inc(a2_exp, 1)
                m = n - 2
                if 0 <= m < NU2:
                    act.wait_ge(a2_turned, m + 1)
                    if m >= 3:
                        act.wait_ge(pv2_mm, m - 2)
                    nc.scalar.copy(pT2[0:NC, m % 3, TB * P:(TB + 1) * P], bank[3][0:NC, 0:P]).then_inc(p2_act, 1)
                if n >= 4 and n % 2 == 0 and (n - 4) // 2 < NT:
                    t = (n - 4) // 2
                    act.wait_ge(pv2_mm, 2 * t + 2)
                    if t >= 2:
                        act.wait_ge(wo2_mm, t - 1)
                    nc.scalar.copy(oT2[:, t % 2], bank[6 + t % 2][0:D2, 0:2 * P]).then_inc(oT2_ready, 1)

        NX = NE + NSH
        WE = 3 * HE
        lg, m8, ix8, ixf = sb("lg", P, NT, NE), sb("m8", P, NT, 8), sb("ix8", P, NT, 8, dt=U32), sb("ixf", P, NT, 8)
        e2x, wa, wb = sb("e2x", P, NT), sb("wa", P, NT), sb("wb", P, NT)
        cw, cwb = sb("cw", P, NT, NE), sb("cwb", P, NT, NE)
        hid2 = part(arenaB, 0, 2, 2, S)
        sil2 = part(arenaB, 2048, 3, S)
        lg_mm, lg_diff, lg_exp = sem("lg_mm"), sem("lg_diff"), sem("lg_exp")
        up_mm, silu_ready, hid_ready, down_mm, moe_added = sem("up_mm"), sem("silu_ready"), sem("hid_ready"), sem("down_mm"), sem("moe_added")

        def pe_moe(pe):
            for t in range(NT):
                if t % TB == 0:
                    pe.wait_ge(ln_T, NB * 6 + t // TB + 1)
                ins = nc.tensor.matmul(bank[7][:, t * NE:(t + 1) * NE], xnT[:, t * P:(t + 1) * P], V["router"], start=True, stop=True)
            ins.then_inc(lg_mm, 1)
            pe.wait_ge(*loaded["moe"])
            for n in range(4 * NX + 2):
                if n < 4 * NX:
                    e, b, c = n // 4, n // 2 % 2, n % 2
                    w = V["moe"][:, e * WE:(e + 1) * WE]
                    if n >= 2:
                        pe.wait_ge(hid_ready, n - 1)
                    nc.tensor.matmul(bank[n % 2][:], w[:, c * P:(c + 1) * P], xnT[:, b * S:(b + 1) * S], start=True, stop=True).then_inc(up_mm, 1)
                    nc.tensor.matmul(bank[2 + n % 2][:], w[:, HE + c * P:HE + (c + 1) * P], xnT[:, b * S:(b + 1) * S],
                                     start=True, stop=True).then_inc(up_mm, 1)
                if n >= 3 and n % 2 == 1:
                    m = (n - 3) // 2
                    w = V["moe"][:, m // 2 * WE:(m // 2 + 1) * WE]
                    pe.wait_ge(hid_ready, 2 * m + 2)
                    if m >= 3:
                        pe.wait_ge(moe_added, m - 2)
                    for q4 in range(TB):
                        for c in range(2):
                            ins = nc.tensor.matmul(bank[4 + m % 3][:, q4 * P:(q4 + 1) * P], hid2[:, m % 2, c, q4 * P:(q4 + 1) * P],
                                                   w[:, 2 * HE + c * P:2 * HE + (c + 1) * P], start=(c == 0), stop=(c == 1))
                    ins.then_inc(down_mm, 1)

        def act_moe(act):
            act.wait_ge(lg_diff, 1)
            nc.scalar.activation(e2x[:], e2x[:], ACT.Exp).then_inc(lg_exp, 1)
            for n in range(4 * NX):
                act.wait_ge(up_mm, 2 * n + 1)
                if n >= 3:
                    act.wait_ge(hid_ready, n - 2)
                nc.scalar.activation(sil2[:, n % 3, :], bank[n % 2][:], ACT.Silu).then_inc(silu_ready, 1)

        def vec_moe(dve, st):
            Vv = nc.vector
            dve.wait_ge(lg_mm, 1)
            st.link(Vv.tensor_tensor(lg[:], bank[7][:, 0:NT * NE].rearrange("p (t e) -> p t e", e=NE), bm(V["ebias"], NT), ALU.add))
            for t in range(NT):
                ins = Vv.max(m8[:, t, :], lg[:, t, :])
            st.link(ins)
            Vv.tensor_tensor(e2x[:], m8[:, :, 1], m8[:, :, 0], ALU.subtract).then_inc(lg_diff, 1)
            for t in range(NT):
                ins = Vv.max_index(ix8[:, t, :], m8[:, t, :], lg[:, t, :])
            st.link(ins)
            st.link(Vv.tensor_copy(ixf[:], ix8[:]))
            dve.wait_ge(lg_exp, 1)
            st.link(Vv.tensor_scalar(wb[:], e2x[:], 1.0, None, ALU.add))
            st.link(Vv.reciprocal(wa[:], wb[:]))
            st.link(Vv.tensor_tensor(wb[:], e2x[:], wa[:], ALU.mult))
            for i, (dst, w) in enumerate(((cw, wa), (cwb, wb))):
                st.link(Vv.tensor_tensor(dst[:], bm(V["iota8"], NT), bc(ixf[:, :, i], P, NT, NE), ALU.is_equal))
                st.link(Vv.tensor_tensor(dst[:], dst[:], bc(w[:], P, NT, NE), ALU.mult))
            st.link(Vv.tensor_tensor(cw[:], cw[:], cwb[:], ALU.add))
            for n in range(4 * NX + 4):
                if n < 4 * NX:
                    b, c, m = n // 2 % 2, n % 2, n // 2
                    dve.wait_ge(silu_ready, n + 1)
                    dve.wait_ge(up_mm, 2 * n + 2)
                    if m >= 2:
                        dve.wait_ge(down_mm, m - 1)
                    Vv.tensor_tensor(hid2[:, m % 2, c, :], sil2[:, n % 3, :], bank[2 + n % 2][:], ALU.mult).then_inc(hid_ready, 1)
                if n >= 4 and n % 2 == 0:
                    m = (n - 4) // 2
                    e, b = m // 2, m % 2
                    dve.wait_ge(down_mm, m + 1)
                    if m >= 2:
                        dve.wait_ge(moe_added, m - 1)
                    if e < NE:
                        for q4 in range(TB):
                            t = b * TB + q4
                            ins = Vv.scalar_tensor_tensor(X[:, t, :], bank[4 + m % 3][:, q4 * P:(q4 + 1) * P], cw[:, t, e:e + 1], X[:, t, :],
                                                          ALU.mult, ALU.add)
                    else:
                        ins = Vv.tensor_tensor(X[:, b * TB:(b + 1) * TB, :], bank[4 + m % 3][:].rearrange("p (q d) -> p q d", d=D),
                                               X[:, b * TB:(b + 1) * TB, :], ALU.add)
                    ins.then_inc(moe_added, 1)
                if n == 4 * NX:
                    dve.wait_ge(moe_added, 2 * NX - 1)
                    vec_moments(st, X, [0])

        f3 = part(arenaB, 9400, NB, H3, NC)
        vw3 = part(arenaB, 11864, NB, CK3, D)
        k3, v3 = part(packed["dft"], 1024, 2, NB * NC), part(packed["dft"], 1024 + 2 * NB * NC, 2, NB * NC)
        vws = part(packed["dft"], 0, 2, 2, NB, D)
        HB3 = [(0, 6), (6, 11), (11, 16)]
        p3 = part(arenaB, 0, 3, H3, NC)
        pT3 = part(arenaB, 3 * HK3, 2, CK3, P)
        mx3, sm3 = part(arenaB, 6400, 3, H3), part(arenaB, 6448, 3, H3)
        kv3_mm, kv3_copy, f3_mm, f3_copy, vw3_out, vw3_in = sem("kv3_mm"), sem("kv3_copy"), sem("f3_mm"), sem("f3_copy"), [sem("vw3_out_even"), sem("vw3_out_odd")], sem("vw3_in")
        s3_mm, s3_max, s3_exp, s3_norm, s3_turned, pT3_act, pT3_dve, y3_mm, x3_added = (
            sem(n) for n in ("s3_mm", "s3_max", "s3_exp", "s3_norm", "s3_turned", "pT3_act", "pT3_dve", "y3_mm", "x3_added"))

        def pe_fold3(pe, first, last):
            for c in range(first, last):
                cc = slice(c * P, (c + 1) * P)
                if c:
                    pe.wait_ge(kv3_copy, 2 * c)
                nc.tensor.matmul(bank[2][:, 0:NB * NC], V["wk3"][0:DC, cc], V["ctxT"][0:DC], start=True, stop=True).then_inc(kv3_mm, 1)
                nc.tensor.matmul(bank[3][:, 0:NB * NC], V["wv3"][0:DC, cc], V["ctxT"][0:DC], start=True, stop=True).then_inc(kv3_mm, 1)
                pe.wait_ge(kv3_copy, 2 * c + 2)
                if c:
                    pe.wait_ge(f3_copy, 4 * c)
                for i in range(2):
                    r = slice(D3 * i, D3 * (i + 1))
                    nc.tensor.matmul(bank[4 + i][:, 0:NB * NC], V["wqT3"][r, cc], k3[r, c % 2, :], start=True, stop=True).then_inc(f3_mm, 1)
                    for b in range(NB):
                        ins = nc.tensor.matmul(bank[6 + i][0:NC, b * D:(b + 1) * D], v3[r, c % 2, b * NC:(b + 1) * NC], V["wo3"][r, cc],
                                               start=True, stop=True)
                    ins.then_inc(f3_mm, 1)

        def act_fold3(act, first, last):
            for c in range(first, last):
                act.wait_ge(kv3_mm, 2 * c + 1)
                nc.scalar.copy(k3[:, c % 2, :], bank[2][:, 0:NB * NC]).then_inc(kv3_copy, 1)
                act.wait_ge(kv3_mm, 2 * c + 2)
                nc.scalar.copy(v3[:, c % 2, :], bank[3][:, 0:NB * NC]).then_inc(kv3_copy, 1)
                for i in range(2):
                    act.wait_ge(f3_mm, 4 * c + 2 * i + 1)
                    nc.scalar.activation(f3[:, :, 2 * c + i, :], bank[4 + i][:, 0:NB * NC].rearrange("p (b k) -> p b k", b=NB), ACT.Copy,
                                         scale=D3 ** -0.5).then_inc(f3_copy, 1)
                    act.wait_ge(f3_mm, 4 * c + 2 * i + 2)
                    if c >= 2:
                        act.wait_ge(vw3_out[c % 2], 16 * 4 * (c // 2))
                    nc.scalar.copy(vws[0:NC, c % 2, i], bank[6 + i][0:NC, 0:NB * D].rearrange("p (b d) -> p b d", b=NB)).then_inc(f3_copy, 1)

        def sync_fold3(sp):
            for c in range(H3 // 2):
                sp.wait_ge(f3_copy, 4 * c + 4)
                for i in range(2):
                    h = 2 * c + i
                    for b in range(NB):
                        sp.dma_start(A["vw_scratch"][b, h * NC:(h + 1) * NC, :], vws[0:NC, c % 2, i, b]).then_inc(vw3_out[c % 2], 16)
            for c in range(2):
                sp.wait_ge(vw3_out[c], 16 * H3)
            full = HK3 // P
            for b in range(NB):
                sp.dma_start(vw3[:, b, 0:full, :], A["vw_scratch"][b, 0:full * P, :].rearrange("(c p) d -> p c d", p=P)).then_inc(vw3_in, 16)
                sp.dma_start(vw3[0:HK3 - full * P, b, full, :], A["vw_scratch"][b, full * P:HK3, :]).then_inc(vw3_in, 16)

        def pe_attend3(pe):
            pe.wait_ge(vw3_in, 16 * 4)
            pe.wait_ge(ln_T, NB * 8)
            for n in range(NT + 3):
                if n < NT:
                    b = n // TB
                    for i, (h0, h1) in enumerate(HB3):
                        if n:
                            pe.wait_ge(s3_exp, 3 * (n - 1) + i + 1)
                        nc.tensor.matmul(bank[i][:, 0:(h1 - h0) * NC], xnT[:, n * P:(n + 1) * P],
                                         f3[:, b, h0:h1, :].rearrange("p h k -> p (h k)"), start=True, stop=True).then_inc(s3_mm, 1)
                t = n - 2
                if 0 <= t < NT:
                    pe.wait_ge(s3_norm, t + 1)
                    pf = p3[:, t % 3].rearrange("p h k -> p (h k)")
                    for g in range(3):
                        if t:
                            if g < 2:
                                pe.wait_ge(pT3_act, 2 * (t - 1) + g + 1)
                            else:
                                pe.wait_ge(pT3_dve, t)
                        for c in range(4 * g, min(4 * g + 4, CK3)):
                            w = min(P, HK3 - c * P)
                            ins = nc.tensor.transpose(bank[3 + g][0:w, (c % 4) * P:(c % 4 + 1) * P], pf[:, c * P:c * P + w], ident)
                        ins.then_inc(s3_turned, 1)
                t = n - 3
                if 0 <= t < NT:
                    pe.wait_ge(pT3_act, 2 * t + 2)
                    pe.wait_ge(pT3_dve, t + 1)
                    if t >= 2:
                        pe.wait_ge(x3_added, t - 1)
                    for c in range(CK3):
                        w = min(P, HK3 - c * P)
                        ins = nc.tensor.matmul(bank[6 + t % 2][:, 0:P], pT3[0:w, t % 2, c, :], vw3[0:w, t // TB, c, :],
                                               start=(c == 0), stop=(c == CK3 - 1))
                    ins.then_inc(y3_mm, 1)

        LASTW = HK3 - (CK3 - 1) * P

        def act_attend3(act):
            for n in range(NT + 2):
                if n < NT:
                    if n >= 3:
                        act.wait_ge(s3_turned, 3 * (n - 2))
                    for i, (h0, h1) in enumerate(HB3):
                        act.wait_ge(s3_max, 3 * n + i + 1)
                        for h in range(h0, h1 if i < 2 else h0):
                            ins = nc.scalar.activation(p3[:, n % 3, h, :], bank[i][:, (h - h0) * NC:(h - h0 + 1) * NC], ACT.Exp,
                                                       bias=mx3[:, n % 3, h:h + 1], accum_out=sm3[:, n % 3, h:h + 1])
                        if i == 2:
                            ins = nc.scalar.activation(p3[:, n % 3, h0:h1, :], p3[:, n % 3, h0:h1, :], ACT.Exp)
                        ins.then_inc(s3_exp, 1)
                t = n - 2
                if 0 <= t < NT:
                    for g in range(2):
                        act.wait_ge(s3_turned, 3 * t + g + 1)
                        if t >= 2:
                            act.wait_ge(y3_mm, t - 1)
                        nc.scalar.copy(pT3[:, t % 2, 4 * g:4 * g + 4, :], bank[3 + g][:].rearrange("p (c q) -> p c q", q=P)).then_inc(pT3_act, 1)

        def vec_attend3(dve, st):
            Vv = nc.vector
            for n in range(NT + 4):
                if n < NT:
                    if n >= 3:
                        dve.wait_ge(s3_norm, n - 2)
                        dve.wait_ge(s3_turned, 3 * (n - 2))
                    for i, (h0, h1) in enumerate(HB3):
                        dve.wait_ge(s3_mm, 3 * n + i + 1)
                        s = bank[i][:, 0:(h1 - h0) * NC].rearrange("p (h k) -> p h k", k=NC)
                        ins = Vv.tensor_reduce(mx3[:, n % 3, h0:h1], s, AX.X, ALU.max, negate=True)
                        if i == 2:
                            st.link(ins)
                            ins = Vv.tensor_tensor(p3[:, n % 3, h0:h1, :], s, bc(mx3[:, n % 3, h0:h1], P, h1 - h0, NC), ALU.add)
                        ins.then_inc(s3_max, 1)
                t = n - 1
                if 0 <= t < NT:
                    dve.wait_ge(s3_exp, 3 * t + 3)
                    h0, h1 = HB3[2]
                    st.link(Vv.tensor_reduce(sm3[:, t % 3, h0:h1], p3[:, t % 3, h0:h1, :], AX.X, ALU.add))
                    st.link(Vv.reciprocal(sm3[:, t % 3], sm3[:, t % 3]))
                    Vv.tensor_tensor(p3[:, t % 3], p3[:, t % 3], bc(sm3[:, t % 3], P, H3, NC), ALU.mult).then_inc(s3_norm, 1)
                t = n - 2
                if 0 <= t < NT:
                    dve.wait_ge(s3_turned, 3 * t + 3)
                    if t >= 2:
                        dve.wait_ge(y3_mm, t - 1)
                    Vv.tensor_copy(pT3[:, t % 2, 8, :], bank[5][:, 0:P])
                    Vv.tensor_copy(pT3[0:LASTW, t % 2, 9, :], bank[5][0:LASTW, P:2 * P]).then_inc(pT3_dve, 1)
                t = n - 4
                if 0 <= t < NT:
                    if t == 0:
                        dve.wait_ge(bias_added, 3)
                    dve.wait_ge(y3_mm, t + 1)
                    Vv.tensor_tensor(X[:, t, :], bank[6 + t % 2][:, 0:P], tmp[:, t, :], ALU.add).then_inc(x3_added, 1)
                if n == 5 + (TB - 1):
                    dve.wait_ge(x3_added, TB)
                    vec_moments(st, X, [0])
                if n == 7 + (TB - 1):
                    vec_normalise(dve, 10, X, xn, [0])

        wsum, wgam = sb("wsum", P, 2), sb("wgam", P, 2)
        tern = [V["wfcT"], V["wpT"]]
        ternb = part(arenaB, 12512, HID3)
        g3 = part(arenaB, 0, 3, HID3)
        g3n = part(arenaB, 1536, 3, HID3)
        g3T = part(arenaB, 3072, 3, HID3)
        st3, mv3, rd3 = part(arenaB, 4608, NT, 6), part(arenaB, 4656, NT, 2), part(arenaB, 4672, NT)
        wsum_mm, tern_ready = sem("wsum_mm"), sem("tern_ready")
        h3_mm, g3_ready, mv3_ready, rd3_ready, g3_norm, g3_turned, g3T_dve, g3T_act, y4_mm, x4_added = (
            sem(n) for n in ("h3_mm", "g3_ready", "mv3_ready", "rd3_ready", "g3_norm", "g3_turned", "g3T_dve", "g3T_act", "y4_mm", "x4_added"))

        def vec_weights3(dve):
            dve.wait_ge(*loaded["l3f"])
            for i in range(2):
                ins = nc.vector.tensor_reduce(wsum[:, i:i + 1], tern[i], AX.X, ALU.add, apply_absolute_value=True)
            ins.then_inc(w3_vec, 1)

        def pe_weights3(pe):
            pe.wait_ge(w3_vec, 1)
            pe.wait_ge(c2_copy, 2)
            nc.tensor.matmul(bank[7][:, 0:2], V["avg"], wsum[:], start=True, stop=True).then_inc(wsum_mm, 1)

        def vec_gamma3(dve, st):
            dve.wait_ge(wsum_mm, 1)
            st.link(nc.vector.tensor_scalar(wgam[:], bank[7][:, 0:2], 1.0 / HID3, 1e-6, ALU.mult, ALU.add))
            nc.vector.reciprocal(wgam[:], wgam[:]).then_inc(w3_vec, 1)

        def pool_ternary3(pool, st):
            G = nc.gpsimd
            pool.wait_ge(w3_vec, 2)
            pool.wait_ge(kern_pe, 4)
            for i in range(2):
                st.link(G.tensor_scalar(ternb, tern[i], wgam[:, i:i + 1], -0.5, ALU.mult, ALU.is_lt))
                st.link(G.tensor_scalar(tern[i], tern[i], wgam[:, i:i + 1], 0.5, ALU.mult, ALU.is_gt))
                ins = G.tensor_tensor(tern[i], tern[i], ternb, ALU.subtract)
                if i == 0:
                    st.link(ins)
                else:
                    ins.then_inc(tern_ready, 1)

        def pe_l3f(pe):
            pe.wait_ge(tern_ready, 1)
            for n in range(NT + 4):
                if n < NT:
                    pe.wait_ge(ln_T, NB * 8 + n // TB + 1)
                    if n >= 2:
                        pe.wait_ge(g3_ready, n - 1)
                    nc.tensor.matmul(bank[2 + n % 2][:], xnT[:, n * P:(n + 1) * P], V["wfcT"], start=True, stop=True).then_inc(h3_mm, 1)
                t = n - 2
                if 0 <= t < NT:
                    pe.wait_ge(g3_norm, t + 1)
                    if t >= 2:
                        pe.wait_ge(g3T_dve, t - 1)
                        pe.wait_ge(g3T_act, t - 1)
                    for c in range(4):
                        ins = nc.tensor.transpose(bank[4 + 2 * (t % 2) + c // 2][:, (c % 2) * P:(c % 2 + 1) * P], g3n[:, t % 3, c * P:(c + 1) * P], ident)
                    ins.then_inc(g3_turned, 1)
                t = n - 3
                if 0 <= t < NT:
                    pe.wait_ge(g3T_dve, t + 1)
                    pe.wait_ge(g3T_act, t + 1)
                    if t >= 2:
                        pe.wait_ge(x4_added, t - 1)
                    for c in range(4):
                        ins = nc.tensor.matmul(bank[t % 2][:, 0:P], g3T[:, t % 3, c * P:(c + 1) * P], V["wpT"][:, c * P:(c + 1) * P],
                                               start=(c == 0), stop=(c == 3))
                    ins.then_inc(y4_mm, 1)

        def act_l3f(act):
            for n in range(NT + 3):
                if n < NT:
                    act.wait_ge(h3_mm, n + 1)
                    if n >= 3:
                        act.wait_ge(g3_norm, n - 2)
                    nc.scalar.activation(g3[:, n % 3, :], bank[2 + n % 2][:], ACT.Gelu).then_inc(g3_ready, 1)
                t = n - 2
                if 0 <= t < NT:
                    act.wait_ge(g3_turned, t + 1)
                    if t >= 3:
                        act.wait_ge(y4_mm, t - 2)
                    for c in range(2):
                        ins = nc.scalar.activation(g3T[:, t % 3, c * P:(c + 1) * P], bank[4 + 2 * (t % 2)][:, c * P:(c + 1) * P], ACT.Identity,
                                                   scale=V["ln3w"][:, c:c + 1], bias=V["ln3b"][:, c:c + 1])
                    ins.then_inc(g3T_act, 1)

        def pool_l3f(pool, st):
            for t in range(NT):
                pool.wait_ge(mv3_ready, t + 1)
                st.link(nc.gpsimd.tensor_scalar(rd3[:, t:t + 1], mv3[:, t, 1:2], 1e-5, None, ALU.add))
                nc.gpsimd.tensor_tensor(rd3[:, t:t + 1], rd3[:, t:t + 1], V["half"][:, 0:1], ALU.pow).then_inc(rd3_ready, 1)

        def vec_l3f(dve, st):
            Vv = nc.vector
            for n in range(NT + 4):
                if n < NT:
                    dve.wait_ge(g3_ready, n + 1)
                    st.link(Vv.bn_stats(st3[:, n, :], g3[:, n % 3, :]))
                    Vv.bn_aggr(mv3[:, n, :], st3[:, n, :]).then_inc(mv3_ready, 1)
                t = n - 1
                if 0 <= t < NT:
                    dve.wait_ge(rd3_ready, t + 1)
                    if t >= 3:
                        dve.wait_ge(g3_turned, t - 2)
                    Vv.tensor_scalar(g3n[:, t % 3, :], g3[:, t % 3, :], mv3[:, t, 0:1], rd3[:, t:t + 1], ALU.subtract, ALU.mult).then_inc(g3_norm, 1)
                t = n - 2
                if 0 <= t < NT:
                    dve.wait_ge(g3_turned, t + 1)
                    if t >= 3:
                        dve.wait_ge(y4_mm, t - 2)
                    for c in range(2, 4):
                        ins = Vv.tensor_scalar(g3T[:, t % 3, c * P:(c + 1) * P], bank[5 + 2 * (t % 2)][:, (c - 2) * P:(c - 1) * P],
                                               V["ln3w"][:, c:c + 1], V["ln3b"][:, c:c + 1], ALU.mult, ALU.add)
                    ins.then_inc(g3T_dve, 1)
                t = n - 3
                if 0 <= t < NT:
                    dve.wait_ge(y4_mm, t + 1)
                    Vv.tensor_tensor(X[:, t, :], bank[t % 2][:, 0:P], X[:, t, :], ALU.add).then_inc(x4_added, 1)

        block = ctx.enter_context(nc.Block())

        @block.sync
        def _(sp):
            sync_loads(sp)
            if LAST_STAGE >= 7:
                sync_fold3(sp)
            sp.wait_ge(final_stage_done, 1)
            sp.dma_start(out.rearrange("b (q p) d -> p (b q) d", p=P), X[:]).then_inc(stored, 16)
            sp.wait_ge(stored, 16)

        @block.tensor
        def _(pe):
            pe_dt(pe)
            pe_ctx0(pe)
            pe_turn(pe, ln_done, NT * 0, xn)
            pe_scores0(pe)
            pe_fold1(pe)
            pe_c2(pe)
            pe_weights3(pe)
            pe_film(pe)
            pe_c2_keys(pe)
            pe_dft_x(pe)
            pe_kernel(pe)
            pe_dft_k(pe)
            pe_dft_back(pe)
            pe_turn(pe, ln_done, NT * 1, tmp2)
            pe_ffn0(pe)
            if LAST_STAGE >= 2:
                pe_turn(pe, ln_done, NT * 3, xn)
                pe_route(pe)
                pe_qkv0(pe)
                pe_attend0(pe)
            if LAST_STAGE >= 3:
                pe_turn(pe, ln_done, NT * 4, xn)
                pe_l1x(pe)
            if LAST_STAGE >= 4:
                pe_turn(pe, ln_done, NT * 5, xn)
                pe_l1f(pe)
            if LAST_STAGE >= 5:
                pe_turn(pe, lat_done, 0, tmp2)
                pe_qkv2(pe)
                pe_attend2(pe)
            if LAST_STAGE >= 6:
                pe_turn(pe, ln_done, NT * 8, xn)
                pe_moe(pe)
            if LAST_STAGE >= 7:
                pe_turn(pe, ln_done, NT * 9, xn)
                pe_attend3(pe)
            if LAST_STAGE >= 8:
                pe_turn(pe, ln_done, NT * 10, xn)
                pe_l3f(pe)

        @block.scalar
        def _(act):
            st = Steps(act, act_step)
            act_ctx0(act)
            act_turned(act, 0)
            act_fold1(act)
            act_c2(act)
            act_s4_rows(act)
            act_film(act, st)
            act_s4_cols(act)
            act_c2_keys(act)
            act_kernel(act)
            act_dft(act)
            act_turned(act, 1, V["g_ffn"], V["b_ffn"])
            act_ffn0(act)
            if LAST_STAGE >= 2:
                act_turned(act, 2)
                act_route(act)
                act_qk0(act)
                act_attend0(act)
            if LAST_STAGE >= 3:
                act_turned(act, 3)
                act_l1x(act)
            if LAST_STAGE >= 4:
                act_turned(act, 4)
                act_l1f(act)
            if LAST_STAGE >= 5:
                act_turned(act, 5, V["lnl_g"], V["lnl_b"])
                act_qkv2(act)
                act_attend2(act)
            if LAST_STAGE >= 6:
                act_turned(act, 6)
                act_moe(act)
            if LAST_STAGE >= 7:
                act_turned(act, 7)
                act_attend3(act)
            if LAST_STAGE >= 8:
                act_turned(act, 8)
                act_l3f(act)

        @block.gpsimd
        def _(pool):
            st = Steps(pool, pool_step)
            pool_dt(pool)
            pool_rstd(pool, st, 0)
            pool_rstd_twice(pool, st, 0, twice_ready)
            pool_masks(pool, st)
            pool_c2_rstd(pool, st)
            pool_s4(pool, st)
            pool_shift0(pool, 0)
            pool_shift0(pool, 1)
            pool_s4_decay(pool)
            pool_s4_scale(pool)
            pool_c2_inv(pool, st)
            pool.wait_ge(*loaded["rows"])
            pool_add_row(pool, V["b_out"], NT)
            pool_ternary3(pool, st)
            pool_rstd(pool, st, 1)
            pool_rstd(pool, st, 2)
            if LAST_STAGE >= 2:
                pool_rstd(pool, st, 3)
                pool_bias(pool, 3, V["bo0"], bias_added)
            if LAST_STAGE >= 3:
                pool_rstd(pool, st, 4)
                pool_l1x(pool, st)
            if LAST_STAGE >= 4:
                pool_rstd(pool, st, 5)
                pool_add_row(pool, V["bet1"], NT * 6)
                pool_l1f(pool, st)
                pool_rstd(pool, st, 6)
            if LAST_STAGE >= 5:
                pool_rstd(pool, st, 7)
                pool_rstd_twice(pool, st, 7, twice_ready)
                pool_bias(pool, 7, V["bo2"], bias_added)
                pool_qkv2(pool, st)
            if LAST_STAGE >= 6:
                pool_rstd(pool, st, 8)
            if LAST_STAGE >= 7:
                pool_rstd(pool, st, 9)
                pool_bias(pool, 9, V["bo3"], bias_added)
            if LAST_STAGE >= 8:
                pool_rstd(pool, st, 10)
                pool_l3f(pool, st)

        @block.vector
        def _(dve):
            st = Steps(dve, dve_step)
            vec_dt(dve)
            dve.wait_ge(x_loaded, 16)
            vec_moments(st, X)
            vec_dt_row(dve)
            vec_normalise(dve, 0, X, xn)
            dve.wait_ge(twice_ready, 1)
            dve.wait_ge(ln_done, NT)
            for t in range(NT):
                ins = nc.vector.tensor_scalar(tmp2[:, t, :], xn[:, t, :], mv2[:, t:t + 1], None, ALU.mult)
            st.link(ins)
            vec_affine_in(dve, st)
            vec_c2_moments(dve, st)
            vec_weights3(dve)
            vec_sigs(dve, st)
            vec_c2_norm(dve, st)
            vec_scores0(dve, st)
            vec_probs0(dve, st)
            vec_c2_squares(dve, st)
            vec_s4(dve, st)
            vec_c2_scale(dve)
            vec_gamma3(dve, st)
            vec_film(dve, st)
            vec_s4_products(dve, st)
            vec_spectrum(dve, st)
            vec_xt(dve, st)
            vec_moments(st, xt)
            vec_normalise(dve, 1, xt, tmp2)
            vec_ffn0(dve, st)
            vec_moments(st, xt)
            vec_normalise_add(dve, 1, xt, V["g_out"])
            dve.wait_ge(x_final, NB)
            if LAST_STAGE >= 2:
                vec_moments(st, X)
                vec_normalise(dve, 3, X, xn)
                vec_route(dve, st)
                vec_v0(dve)
                vec_attend0(dve, st)
                dve.wait_ge(x_added, NT)
            if LAST_STAGE >= 3:
                vec_moments(st, X, [1])
                vec_normalise(dve, 4, X, xn, [1])
                vec_l1x(dve, st)
            if LAST_STAGE >= 4:
                vec_moments(st, X)
                vec_normalise(dve, 5, X, xn)
                vec_l1f(dve, st)
                vec_moments(st, xt)
                vec_normalise_add(dve, 2, xt, V["gam1"])
                dve.wait_ge(x_final, 2 * NB)
            if LAST_STAGE >= 5:
                vec_moments(st, X)
                vec_normalise(dve, 7, X, xn)
                dve.wait_ge(ln_done, NT * 8)
                vec_latents(dve)
                vec_qkv2(dve, st)
                vec_attend2(dve, st)
                dve.wait_ge(x2_added, NT)
            if LAST_STAGE >= 6:
                vec_moments(st, X, [1])
                vec_normalise(dve, 8, X, xn)
                vec_moe(dve, st)
                dve.wait_ge(moe_added, 2 * NX)
            if LAST_STAGE >= 7:
                vec_moments(st, X, [1])
                vec_normalise(dve, 9, X, xn)
                vec_attend3(dve, st)
                dve.wait_ge(x3_added, NT)
            if LAST_STAGE >= 8:
                vec_moments(st, X, [1])
                vec_normalise(dve, 10, X, xn, [1])
                vec_l3f(dve, st)
                dve.wait_ge(x4_added, NT)
            nc.vector.engine_nop().then_inc(final_stage_done, 1)


def _packed(I):
    f = np.float32

    def pad(a):
        a = np.asarray(a, f)
        o = np.zeros((P, a.shape[1]), f)
        o[:a.shape[0]] = a
        return o

    def chunks(a):
        return a.reshape(-1, P, a.shape[1]).transpose(1, 0, 2).reshape(P, -1)

    ang = 2.0 * np.pi * (np.outer(np.arange(S), np.arange(S)) % (2 * S)) / (2 * S)
    row, col = {}, {}
    it = {
        "ctxT": I["ctx_768"].reshape(NB * NC, DC).T, "wk0": I["L0_xattn_Wk"], "wv0": I["L0_xattn_Wv"],
        "wqT0": I["L0_xattn_Wq"].T, "wfilm": np.concatenate([I["L0_xattn_W_film_in"], I["L0_xattn_W_film_out"]], 1),
        "ident": np.eye(P, dtype=f), "avg": np.full((P, P), 1.0 / P),
        "ctxr": I["ctx_768"].transpose(1, 0, 2).reshape(NC, -1),
        "g_in": I["L0_xattn_g_norm_in"], "b_in": I["L0_xattn_b_norm_in"], "dskip": I["L0_xattn_D_skip"],
        "b2": I["L0_xattn_b2"], "g_out": I["L0_xattn_g_norm_out"], "b_out": I["L0_xattn_b_norm_out"],
        "logdt": I["L0_xattn_log_dt"][:, None], "br": I["L0_ffn_br"], "bo0": I["L0_ffn_bo"], "knots": I["L1_ffn_knot_values"],
        "temp": I["L1_ffn_temperature"], "oscale": I["L1_ffn_output_scale"], "cb2": I["L1_ffn_compress_b2"],
        "gam1": I["L1_ffn_norm_gamma"], "bet1": I["L1_ffn_norm_beta"], "lnx_g": I["L2_xattn_ln_x_g"],
        "lnx_b": I["L2_xattn_ln_x_b"], "bo2": I["L2_xattn_bo"], "ebias": I["L2_ffn_expert_bias"],
        "bo3": I["L3_xattn_bo"], "gate": I["L0_xattn_mod_gate"].reshape(1), "iotaa": np.arange(LA), "rev8": 8 - np.arange(8),
        "iota8": np.arange(8), "iota16": np.arange(HF), "rev16": HF - np.arange(HF),
        "g_ffn": I["L0_xattn_g_ffn"][:, None], "b_ffn": I["L0_xattn_b_ffn"][:, None],
        "b1": I["L0_xattn_b1"].reshape(4, P).T,
        "wf": np.where(np.arange(S) == 0, 1.0, 2.0).reshape(4, P).T / (2 * S),
        "alt": (1.0 - 2.0 * (np.arange(P) % 2))[:, None], "quarter": np.repeat([0.25, 0.0], P // 2)[:, None],
        "off2": np.repeat([0.0, 0.25], P // 2)[:, None], "qturn": TURN * np.repeat([0.25, 0.0], P // 2)[:, None], "oturn": TURN * np.repeat([0.0, 0.25], P // 2)[:, None],
        "sgn": np.repeat([1.0, -1.0], P // 2)[:, None],
        "cb1": I["L1_ffn_compress_b1"][:, None],
        "lnl_g": I["L2_xattn_ln_l_g"][:, None], "lnl_b": I["L2_xattn_ln_l_b"][:, None],
        "qn": np.tile(I["L2_xattn_qn_g"], H2)[:, None], "kn": np.tile(I["L2_xattn_kn_g"], H2)[:, None],
        "ln3w": I["L3_ffn_ln_w"].reshape(4, P).T, "ln3b": I["L3_ffn_ln_b"].reshape(4, P).T,
        "bq2": np.tile(I["L0_ffn_bq"].reshape(HF, DF).T, (2, 1)), "bk2": np.tile(I["L0_ffn_bk"].reshape(HF, DF).T, (2, 1)),
        "eps": np.full((P, 1), 1e-5), "half": np.full((P, 4 * NT), -0.5), "br_col": I["L0_ffn_br"][:, None],
        "euler": np.full((P, 1), np.e),
        "cos": chunks(np.cos(ang)), "sin": chunks(np.sin(ang)),
        "are": np.tile(I["L0_xattn_A_re"].T, (2, 1)), "aim": np.tile(I["L0_xattn_A_im"].T, (2, 1)),
        "cre": np.tile(I["L0_xattn_C_re"].T, (2, 1)), "cim": np.tile(I["L0_xattn_C_im"].T, (2, 1)),
        "w1": I["L0_xattn_W1"], "w2": chunks(I["L0_xattn_W2"]),
        "wqkv": np.stack([I["L0_ffn_Wq"].reshape(D, HF, DF), I["L0_ffn_Wk"].reshape(D, HF, DF),
                          I["L0_ffn_Wv"].reshape(D, HF, DF),
                          np.broadcast_to(I["L0_ffn_bv"].reshape(1, HF, DF), (D, HF, DF))], 2).reshape(D, -1),
        "wr": I["L0_ffn_Wr"], "wo0": chunks(I["L0_ffn_Wo"]),
        "wq1": I["L1_xattn_Wq"], "wk1": I["L1_xattn_Wk"], "wv1": I["L1_xattn_Wv"], "wo1T": I["L1_xattn_Wo"].T,
        "sigT": I["L1_ffn_signatures_raw"].T, "cw1": I["L1_ffn_compress_w1"], "cw2": I["L1_ffn_compress_w2"],
        "tab": np.concatenate([I["L1_ffn_spline_w1"].reshape(NTL, -1), I["L1_ffn_spline_b1"],
                               I["L1_ffn_spline_w2"].reshape(NTL, -1), I["L1_ffn_spline_b2"], I["L1_ffn_directions"]], 1),
        "wq2T": I["L2_xattn_Wq"].T, "wlkvT": I["L2_xattn_Wlkv"].T, "wkvT": I["L2_xattn_Wkv"].T, "wo2T": I["L2_xattn_Wo"].T.reshape(H2, D2, D).transpose(1, 0, 2).reshape(D2, -1),
        "router": I["L2_ffn_router_w"].T,
        "wqT3": chunks(I["L3_xattn_Wq"].T), "wk3": I["L3_xattn_Wk"], "wv3": I["L3_xattn_Wv"], "wo3": chunks(I["L3_xattn_Wo"]),
        "wfcT": I["L3_ffn_W_fc"].T, "wpT": chunks(I["L3_ffn_W_proj"].T),
    }
    w1 = np.concatenate([I["L2_ffn_w1"], I["L2_ffn_sw1"]])
    w3 = np.concatenate([I["L2_ffn_w3"], I["L2_ffn_sw3"]])
    w2 = np.concatenate([I["L2_ffn_w2"], I["L2_ffn_sw2"]])
    it["moe"] = np.concatenate([np.concatenate([w1[e].T, w3[e].T, chunks(w2[e].T)], 1) for e in range(NE + NSH)], 1)
    res = {}
    for k, items in PACKS.items():
        if k == "rows":
            res[k] = np.concatenate([np.asarray(it[n], f).reshape(-1) for n, _ in items])[None]
        else:
            res[k] = np.concatenate([pad(it[n]) for n, _ in items], 1)
        assert res[k].shape[1] == WIDTH[k], k
    res["x"] = I["x"].reshape(TOK, D)
    res["masks"] = np.stack([I["mask_BxS2_bf1"], I["mask_BxS2_bk0"]])
    res["tmask"] = np.ascontiguousarray(I["mask_BxS_bf1"].reshape(NT, P).T)
    res["bfilm"] = np.concatenate([I["L0_xattn_b_film_in"], I["L0_xattn_b_film_out"]])[None]
    res["altrow"] = (1.0 - 2.0 * (np.arange(S) % 2)).astype(f)[None]
    return {k: np.ascontiguousarray(v) for k, v in res.items()}


def kernel(**inputs):
    import concourse.bacc as bacc
    from concourse.bass_utils import run_bass_kernel_spmd

    arrays = _packed({k: np.asarray(v) for k, v in inputs.items()})
    nc = bacc.Bacc("TRN2", target_bir_lowering=False, num_devices=1)
    A = {}
    for name, a in arrays.items():
        A[name] = nc.dram_tensor(f"in_{name}_dram", a.shape, mybir.dt.from_np(a.dtype), kind="ExternalInput").ap()
    A["vw_scratch"] = nc.dram_tensor("vw_scratch", (NB, HK3, D), F32, kind="Internal").ap()
    out = nc.dram_tensor("out_0_dram", (NB, S, D), F32, kind="ExternalOutput").ap()
    program(nc, A, out)
    r = run_bass_kernel_spmd(nc, [{f"in_{k}_dram": v for k, v in arrays.items()}], core_ids=[0])
    return r.results[0]["out_0_dram"]
```

```python
import numpy as np

import concourse.bass as bass
from concourse import mybir
from contextlib import ExitStack

F32 = mybir.dt.float32
U32 = mybir.dt.uint32
I32 = mybir.dt.int32
U8 = mybir.dt.uint8
ALU = mybir.AluOpType
ACT = mybir.ActivationFunctionType
AX = mybir.AxisListType

P = 128
NB, S, D = 2, 512, 128
NT = NB * S // P
TB = S // P
NC, DC = 77, 96
TOK = NB * S
H0, KEEP, DH0 = 4, 32, 32
LA, LB = 32, 16
HID0 = 512
HF, CH, DF = 16, 4, 64
NTL, TPC, NCL, GRID, CMP, KN = 64, 8, 8, 16, 32, 8
TABW = 2 * GRID + GRID + GRID + 1 + D
H2, D2 = 2, 64
NE, NSH, HE = 8, 2, 256
H3, D3 = 16, 64
HK3 = H3 * NC
CK3 = -(-HK3 // P)
HID3 = 512
TURN = 6.283184
MAGIC = 1.5 * 2.0 ** 23
NEVER = -3.0e38
MASKED = 1.0e30

PACKS = {
    "ctx": [("ctxT", NB * NC), ("wk0", D), ("wv0", D), ("wqT0", D), ("wfilm", 4 * D), ("ident", P), ("avg", P)],
    "rows": [("g_in", D), ("b_in", D), ("dskip", D), ("b2", D), ("g_out", D), ("b_out", D),
             ("br", HF), ("bo0", D), ("knots", KN), ("temp", 1), ("oscale", 1), ("cb2", 2), ("gam1", D), ("bet1", D),
             ("lnx_g", DC), ("lnx_b", DC), ("bo2", D), ("ebias", NE), ("bo3", D), ("gate", 1), ("iotaa", LA),
             ("rev8", 8), ("iota8", 8), ("iota16", HF), ("rev16", HF)],
    "cols": [("g_ffn", 1), ("b_ffn", 1), ("b1", HID0 // P), ("wf", 4), ("alt", 1), ("quarter", 1), ("sgn", 1),
             ("off2", 1), ("cb1", 1), ("lnl_g", 1), ("lnl_b", 1), ("qn", 1), ("kn", 1), ("ln3w", 4), ("ln3b", 4),
             ("bq2", HF), ("bk2", HF), ("eps", 1), ("half", 4 * NT), ("br_col", 1), ("euler", 1), ("logdt", 1),
             ("qturn", 1), ("oturn", 1)],
    "small0": [("wr", HF), ("wo0", 2 * D)],
    "s4": [("are", D), ("aim", D), ("cre", D), ("cim", D)],
    "dft": [("cos", 4 * S), ("sin", 4 * S)],
    "ffn0": [("w1", HID0), ("w2", HID0)],
    "head0": [("wqkv", HF * 4 * DF)],
    "l1": [("wq1", D), ("wk1", DC), ("wv1", DC), ("wo1T", D), ("sigT", NTL), ("cw1", CMP), ("cw2", 2), ("tab", TABW)],
    "l2": [("ctxr", NB * DC), ("wq2T", D), ("wlkvT", 2 * D), ("wkvT", 2 * D), ("wo2T", H2 * D), ("router", NE)],
    "moe": [("moe", (NE + NSH) * 3 * HE)],
    "l3": [("wqT3", H3 * D3), ("wk3", H3 * D3), ("wv3", H3 * D3), ("wo3", 8 * D)],
    "l3f": [("wfcT", HID3), ("wpT", HID3)],
}
WIDTH = {k: sum(n for _, n in v) for k, v in PACKS.items()}
LOADS = [("cols", "ctx"), ("rows",), ("s4",), ("l2", "l3f", "l1"), ("dft",), ("ffn0", "small0"), ("head0",), ("moe", "l3")]
FOLD3 = ((0, 1), (1, 3), (3, 7), (7, 8))


def program(nc, A, out):
    ctx = ExitStack()
    with ctx:
        def sb(name, *shape, dt=F32):
            return ctx.enter_context(nc.sbuf_tensor(name, list(shape), dt))

        def sem(name):
            return ctx.enter_context(nc.semaphore(name))

        bank = [ctx.enter_context(nc.psum_tensor(f"bank{i}", [P, 512], F32)) for i in range(8)]

        arenaA, arenaB = sb("arenaA", P, 12288), sb("arenaB", P, 14592)

        def part(region, at, *shape):
            n = int(np.prod(shape))
            v = region[:, at:at + n]
            if len(shape) == 1:
                return v
            names = "abcd"[:len(shape)]
            return v.rearrange(f"p ({' '.join(names)}) -> p {' '.join(names)}", **dict(zip(names, shape)))

        packed, loaded, V = {}, {}, {}
        for group in LOADS:
            s = sem("loaded_" + group[0])
            for k in group:
                loaded[k] = (s, 16 * len(group))
        for k in PACKS:
            if k == "moe":
                packed[k] = arenaA[:, 0:WIDTH[k]]
            elif k == "l3":
                packed[k] = arenaA[:, WIDTH["moe"]:WIDTH["moe"] + WIDTH[k]]
            elif k == "head0":
                packed[k] = packed["dft"][:, 0:WIDTH[k]]
            else:
                packed[k] = sb(f"in_{k}", P, WIDTH[k])
            at = 0
            for name, n in PACKS[k]:
                V[name] = packed[k][:, at:at + n]
                at += n
        X = sb("X", P, NT, D)
        xn = sb("xn", P, NT, D)
        xnT = sb("xnT", P, TOK)
        tmp = sb("tmp", P, NT, D)
        tmp2 = sb("tmp2", P, NT, D)
        stats = sb("stats", P, NT, 6)
        mv = sb("mv", P, NT, 2)
        rstd = sb("rstd", P, NT)
        rtmp = sb("rtmp", P, NT)
        masks8 = sb("masks8", P, 2, NB, NC, dt=U8)
        tmask8 = sb("tmask8", P, NT, dt=U8)
        maskb = sb("maskb", P, 2, NB, NC)
        tmask = sb("tmask", P, NT)
        ident = V["ident"]

        x_loaded, masks_loaded = sem("x_loaded"), sem("masks_loaded")
        dve_step, act_step, pool_step = sem("dve_step"), sem("act_step"), sem("pool_step")
        ln_moments, ln_rstd, ln_done = sem("ln_moments"), sem("ln_rstd"), sem("ln_done")
        ln_turned, ln_T = sem("ln_turned"), sem("ln_T")

        avg1_mm = sem("avg1_mm")
        bias_added = sem("bias_added")
        c2_powers = sem("c2_powers")
        c2_scaled = sem("c2_scaled")
        c2_stats = sem("c2_stats")
        kern_act = sem("kern_act")
        kern_pe = sem("kern_pe")
        l1f_act = sem("l1f_act")
        l1f_pe = sem("l1f_pe")
        l1f_vec = sem("l1f_vec")
        l1x_vec = sem("l1x_vec")
        route_pe = sem("route_pe")
        route_vec = sem("route_vec")
        s4_act = sem("s4_act")
        s4_pool = sem("s4_pool")
        w3_vec = sem("w3_vec")

        class Steps:

            def __init__(self, eng, s):
                self.eng, self.s, self.n = eng, s, 0

            def link(self, ins):
                self.n += 1
                ins.then_inc(self.s, 1)
                self.eng.wait_ge(self.s, self.n)

        def bc(col, *shape):
            while len(col.shape) < len(shape):
                col = col.unsqueeze(len(col.shape))
            return col.broadcast_to(list(shape))

        def bm(row, n):
            return row.unsqueeze(1).broadcast_to([row.shape[0], n, row.shape[1]])

        def halves():
            return [slice(b * TB, (b + 1) * TB) for b in range(NB)]

        def vec_aggregate(b):
            for t in range(b * TB, (b + 1) * TB):
                ins = nc.vector.bn_aggr(mv[:, t, :], stats[:, t, :])
            ins.then_inc(ln_moments, 1)

        def vec_moments(st, src, which=range(NB)):
            for b in which:
                for t in range(b * TB, (b + 1) * TB):
                    ins = nc.vector.bn_stats(stats[:, t, :], src[:, t, :])
                st.link(ins)
                vec_aggregate(b)

        def pool_rstd(pool, st, i):
            for b, r in enumerate(halves()):
                pool.wait_ge(ln_moments, NB * i + b + 1)
                st.link(nc.gpsimd.tensor_scalar(rtmp[:, r], mv[:, r, 1], 1e-5, None, ALU.add))
                nc.gpsimd.tensor_tensor(rstd[:, r], rtmp[:, r], V["half"][:, r], ALU.pow).then_inc(ln_rstd, 1)

        def vec_normalise(dve, i, src, dst, which=range(NB)):
            for b in which:
                dve.wait_ge(ln_rstd, NB * i + b + 1)
                for t in range(b * TB, (b + 1) * TB):
                    nc.vector.tensor_scalar(dst[:, t, :], src[:, t, :], mv[:, t, 0:1], rstd[:, t:t + 1],
                                            ALU.subtract, ALU.mult).then_inc(ln_done, 1)

        def vec_normalise_add(dve, i, src, g, which):
            for b in which:
                dve.wait_ge(xb_ready, i)
                dve.wait_ge(ln_rstd, NB * LN_ADDED[i - 1] + b + 1)
                r = range(b * TB, (b + 1) * TB)
                for t in r:
                    nc.vector.scalar_tensor_tensor(tmp[:, t, :], src[:, t, :], mv[:, t, 0:1], g, ALU.subtract, ALU.mult).then_inc(ln_done, 1)
                for t in r:
                    dve.wait_ge(ln_done, NT * LN_ADDED[i - 1] + t + 1)
                    ins = nc.vector.scalar_tensor_tensor(X[:, t, :], tmp[:, t, :], rstd[:, t:t + 1], X[:, t, :], ALU.mult, ALU.add)
                ins.then_inc(x_final, 1)

        LN_ADDED = (2, 6)
        xb_ready, x_final, heads_act = sem("xb_ready"), sem("x_final"), sem("heads_act")

        def pool_add_row(pool, row, after):
            pool.wait_ge(ln_done, after)
            nc.gpsimd.tensor_tensor(X[:], X[:], bm(row, NT), ALU.add).then_inc(xb_ready, 1)

        def pe_turn(pe, done, before, src, which=range(NB), banks=(0, 1)):
            for t in range(which[0] * TB, (which[-1] + 1) * TB):
                pe.wait_ge(done, before + t + 1)
                ins = nc.tensor.transpose(bank[banks[t // TB]][:, (t % TB) * P:(t % TB + 1) * P], src[:, t, :], ident)
                if t % TB == TB - 1:
                    ins.then_inc(ln_turned, 1)

        def act_turned(act, n, scale=None, bias=None, which=range(NB), banks=(0, 1)):
            for b in which:
                act.wait_ge(ln_turned, NB * n + b + 1)
                dst = xnT[:, b * S:(b + 1) * S]
                if scale is None:
                    ins = nc.scalar.copy(dst, bank[banks[b]][:])
                elif bias is None:
                    ins = nc.scalar.activation(dst, bank[banks[b]][:], ACT.Copy, scale=scale)
                else:
                    ins = nc.scalar.activation(dst, bank[banks[b]][:], ACT.Identity, scale=scale, bias=bias)
                ins.then_inc(ln_T, 1)

        kT0 = sb("kT0", P, NB * NC)
        f0 = sb("f0", P, NB, H0, NC)
        vT0 = sb("vT0", P, NB * NC)
        vfilm = sb("vfilm", NC + 1, NB, 4 * D)
        s0 = part(arenaB, 0, NT, H0, NC)
        r0 = part(arenaB, 2464, NT, H0, NC)
        e0 = part(arenaB, 4928, NT, H0, NC)
        top0 = part(arenaB, 7392, NT, H0, KEEP)
        sum0 = sb("sum0", P, NT, H0)
        w0 = sb("w0", P, NT, H0)
        am = sb("am", P, NT, NC)
        amT = sb("amT", NC + 1, TOK)
        film = part(arenaA, 0, NT, 4, D)
        xk = part(arenaA, 8192, TB, 3, D)
        yc = part(arenaA, 4096, 4, 2, NB * D)
        kf = part(arenaA, 6144, 4, 2, D)
        pr = part(arenaA, 7168, 4, NB * D)
        kny = sb("kny", 1, D)
        yny = sb("yny", 1, NB, D)
        xt = sb("xt", P, NT, D)
        hT0 = part(arenaA, 8192, 4, TOK)
        altrow = arenaA[0:1, 11776:11776 + S]

        masks_ready, ctx0_mm, ctx0_copy, bias_rows = sem("masks_ready"), sem("ctx0_mm"), sem("ctx0_copy"), sem("bias_rows")
        ones_set = sem("ones_set")
        s0_mm, s0_copy, top_ready, exp0 = sem("s0_mm"), sem("s0_copy"), sem("top_ready"), sem("exp0")
        shifted0 = sem("shifted0_pool"), sem("shifted0_dve")
        am_ready, am_turned, amT_ready, film_mm, film_ready = sem("am_ready"), sem("am_turned"), sem("amT_ready"), sem("film_mm"), sem("film_ready")
        x2_ready = sem("x2_ready")
        dft_mm, kf_ready, spec_used = sem("dft_mm"), sem("kf_ready"), sem("spec_used")
        prod_ready, y_mm = sem("prod_ready"), sem("y_mm")
        ff_mm, ff_gelu, ff_out = sem("ff_mm"), sem("ff_gelu"), sem("ff_out")

        dtb = sb("dtb", P, D)
        ang, are, aim, al, be = (tmp[:, i, :] for i in range(5))
        q = [xt[:, i, :] for i in range(8)]
        hh4 = part(arenaB, 8416, D, LA)
        gg4 = part(arenaB, 12512, D, LB)
        ka = part(arenaB, 0, D, LB)[0:LA]
        kTl = part(arenaB, 2048, S)
        s4_vec, s4_pe, s4_inverses = sem("s4_vec"), sem("s4_pe"), sem("s4_inverses")

        def sync_loads(sp):
            for k in ("cols", "ctx"):
                sp.dma_start(packed[k][:], A[k]).then_inc(loaded[k][0], 16)
            sp.dma_start(X[:], A["x"].rearrange("(t p) d -> p t d", p=P)).then_inc(x_loaded, 16)
            sp.dma_start(masks8[:], A["masks"].partition_broadcast(P)).then_inc(masks_loaded, 16)
            sp.dma_start(tmask8[:], A["tmask"]).then_inc(masks_loaded, 16)
            sp.dma_start(packed["rows"][:], A["rows"].rearrange("a n -> (a n)").partition_broadcast(P)).then_inc(loaded["rows"][0], 16)
            for b in range(NB):
                sp.dma_start(vfilm[NC:NC + 1, b, :], A["bfilm"]).then_inc(bias_rows, 16)
            sp.dma_start(altrow, A["altrow"]).then_inc(bias_rows, 16)
            for k in ("s4", "l2", "l3f", "l1", "dft", "ffn0", "small0"):
                sp.dma_start(packed[k][:], A[k]).then_inc(loaded[k][0], 16)
            sp.wait_ge(y_mm, TB)
            sp.dma_start(packed["head0"], A["head0"]).then_inc(loaded["head0"][0], 16)
            sp.wait_ge(ff_out, NB)
            for k in ("moe", "l3"):
                sp.dma_start(packed[k], A[k]).then_inc(loaded[k][0], 16)

        def pe_ctx0(pe):
            pe.wait_ge(*loaded["ctx"])
            nc.tensor.matmul(bank[2][:, 0:NB * NC], V["wk0"][0:DC], V["ctxT"][0:DC], start=True, stop=True).then_inc(ctx0_mm, 1)
            nc.tensor.matmul(bank[3][:, 0:NB * NC], V["wv0"][0:DC], V["ctxT"][0:DC], start=True, stop=True).then_inc(ctx0_mm, 1)
            pe.wait_ge(ctx0_copy, 1)
            pe.wait_ge(s4_vec, 2)
            for h in range(H0):
                r = slice(h * DH0, (h + 1) * DH0)
                nc.tensor.matmul(bank[4 + h][:, 0:NB * NC], V["wqT0"][r], kT0[r, :], start=True, stop=True).then_inc(ctx0_mm, 1)

        def pe_vfilm(pe):
            pe.wait_ge(ctx0_copy, 2 + H0)
            for b in range(NB):
                nc.tensor.matmul(bank[6 + b][0:NC, :], vT0[:, b * NC:(b + 1) * NC], V["wfilm"], start=True, stop=True).then_inc(ctx0_mm, 1)

        def act_ctx0(act):
            act.wait_ge(ctx0_mm, 1)
            nc.scalar.copy(kT0[:], bank[2][:, 0:NB * NC]).then_inc(ctx0_copy, 1)
            act.wait_ge(ctx0_mm, 2)
            nc.scalar.copy(vT0[:], bank[3][:, 0:NB * NC]).then_inc(ctx0_copy, 1)
            for h in range(H0):
                act.wait_ge(ctx0_mm, 3 + h)
                nc.scalar.copy(f0[:, :, h, :], bank[4 + h][:, 0:NB * NC].rearrange("p (b k) -> p b k", b=NB)).then_inc(ctx0_copy, 1)

        def act_vfilm(act):
            for b in range(NB):
                act.wait_ge(ctx0_mm, 3 + H0 + b)
                nc.scalar.copy(vfilm[0:NC, b, :], bank[6 + b][0:NC, :]).then_inc(ctx0_copy, 1)

        def pe_scores0(pe):
            for t in range(NT):
                if t == 0:
                    pe.wait_ge(ctx0_copy, 2 + H0)
                if t % TB == 0:
                    pe.wait_ge(ln_T, t // TB + 1)
                if t >= 4:
                    pe.wait_ge(s0_copy, t - 3)
                nc.tensor.matmul(bank[2 + t % 4][:, 0:H0 * NC], xnT[:, t * P:(t + 1) * P],
                                 f0[:, t // TB].rearrange("p h k -> p (h k)"), start=True, stop=True).then_inc(s0_mm, 1)

        def vec_scores0(dve, st):
            dve.wait_ge(masks_ready, 1)
            for t in range(NT):
                dve.wait_ge(s0_mm, t + 1)
                nc.vector.tensor_tensor(s0[:, t], bank[2 + t % 4][:, 0:H0 * NC].rearrange("p (h k) -> p h k", h=H0),
                                        bm(maskb[:, 0, t // TB, :], H0), ALU.add).then_inc(s0_copy, 1)
            dve.wait_ge(s0_copy, NT)
            for r in halves():
                for k in range(KEEP // 8):
                    src = s0 if k == 0 else r0
                    for t in range(r.start, r.stop):
                        for h in range(H0):
                            ins = nc.vector.max(top0[:, t, h, 8 * k:8 * k + 8], src[:, t, h, :])
                    st.link(ins)
                    for t in range(r.start, r.stop):
                        for h in range(H0):
                            ins = nc.vector.match_replace(r0[:, t, h, :], top0[:, t, h, 8 * k:8 * k + 8], src[:, t, h, :], NEVER)
                        if k == KEEP // 8 - 1:
                            ins.then_inc(top_ready, 1)
                    if k < KEEP // 8 - 1:
                        st.link(ins)

        def pool_shift0(pool):
            for t in range(TB):
                pool.wait_ge(top_ready, t + 1)
                nc.gpsimd.tensor_tensor(e0[:, t], s0[:, t], bc(top0[:, t, :, 0], P, H0, NC), ALU.subtract).then_inc(shifted0[0], 1)

        def vec_shift0(dve):
            for t in range(TB, NT):
                dve.wait_ge(top_ready, t + 1)
                nc.vector.tensor_tensor(e0[:, t], s0[:, t], bc(top0[:, t, :, 0], P, H0, NC), ALU.subtract).then_inc(shifted0[1], 1)

        def act_exp0(act, b):
            for t in range(b * TB, (b + 1) * TB):
                act.wait_ge(shifted0[b], t % TB + 1)
                nc.scalar.activation(e0[:, t], e0[:, t], ACT.Exp, scale=float(1.0 / np.sqrt(np.float32(DH0)))).then_inc(exp0, 1)

        def vec_probs0(dve, st):
            for t in range(NT):
                dve.wait_ge(exp0, t + 1)
                ins = nc.vector.scalar_tensor_tensor(e0[:, t], r0[:, t], 0.5 * NEVER, e0[:, t], ALU.is_lt, ALU.mult)
            st.link(ins)
            st.link(nc.vector.tensor_reduce(sum0[:], e0[:], AX.X, ALU.add))
            st.link(nc.vector.reciprocal(w0[:], sum0[:]))
            st.link(nc.vector.tensor_tensor(w0[:], w0[:], bc(tmask[:], P, NT, H0), ALU.mult))
            for t in range(NT):
                ins = nc.vector.tensor_tensor(e0[:, t], e0[:, t], bc(w0[:, t], P, H0, NC), ALU.mult)
            st.link(ins)
            for t in range(NT):
                ins = nc.vector.tensor_reduce(am[:, t, :], e0[:, t].rearrange("p h k -> p k h"), AX.X, ALU.add)
                ins.then_inc(am_ready, 1)

        def pe_film(pe):
            for t in range(NT):
                pe.wait_ge(am_ready, t + 1)
                ins = nc.tensor.transpose(bank[t // TB][0:NC, (t % TB) * P:(t % TB + 1) * P], am[:, t, :], ident)
                if t % TB == TB - 1:
                    ins.then_inc(am_turned, 1)
            pe.wait_ge(bias_rows, 16 * (NB + 1))
            for n in range(2 * NT):
                f, t = n // NT, n % NT
                if f == 0 and t % TB == 0:
                    pe.wait_ge(amT_ready, t // TB + 1)
                if n >= 4:
                    pe.wait_ge(film_ready, n - 3)
                nc.tensor.matmul(bank[2 + n % 4][:, 0:2 * D], amT[:, t * P:(t + 1) * P], vfilm[:, t // TB, 2 * f * D:2 * (f + 1) * D],
                                 start=True, stop=True).then_inc(film_mm, 1)

        def act_film(act, st):
            act.wait_ge(ones_set, 1)
            for b in range(NB):
                act.wait_ge(am_turned, b + 1)
                nc.scalar.copy(amT[0:NC, b * S:(b + 1) * S], bank[b][0:NC, :]).then_inc(amT_ready, 1)
            for n in range(2 * NT):
                f, t = n // NT, n % NT
                act.wait_ge(film_mm, n + 1)
                src = bank[2 + n % 4]
                nc.scalar.activation(film[:, t, 2 * f], src[:, 0:D], ACT.Identity, scale=V["gate"], bias=1.0)
                nc.scalar.activation(film[:, t, 2 * f + 1], src[:, D:2 * D], ACT.Copy, scale=V["gate"]).then_inc(film_ready, 1)

        def pool_masks(pool, st):
            nc.gpsimd.memset(amT[:], 1.0).then_inc(ones_set, 1)
            pool.wait_ge(masks_loaded, 32)
            st.link(nc.gpsimd.tensor_copy(maskb[:], masks8[:]))
            st.link(nc.gpsimd.tensor_copy(tmask[:], tmask8[:]))
            st.link(nc.gpsimd.tensor_scalar(maskb[:], maskb[:], 1.0, MASKED, ALU.subtract, ALU.mult))
            nc.gpsimd.tensor_scalar(tmask[:], tmask[:], 1.0 / H0, None, ALU.mult).then_inc(masks_ready, 1)

        dtc, dtd = sb("dtc", P, 1), q[6]

        def pool_dt(pool):
            pool.wait_ge(*loaded["cols"])
            nc.gpsimd.tensor_tensor(dtc[:], V["euler"], V["logdt"], ALU.pow).then_inc(s4_pool, 1)

        def vec_dt(dve):
            dve.wait_ge(s4_pool, 1)
            dve.wait_ge(*loaded["ctx"])
            nc.vector.tensor_scalar(dtd, ident, dtc[:], float(P), ALU.mult, ALU.mult).then_inc(s4_vec, 1)

        def pe_dt(pe):
            pe.wait_ge(s4_vec, 1)
            nc.tensor.matmul(bank[7][:, 0:D], V["avg"], dtd, start=True, stop=True).then_inc(s4_pe, 1)

        steps = V["iotaa"].unsqueeze(1).broadcast_to([P, D, LA])
        vH, kH = part(arenaA, 0, D, LA), part(arenaA, D * LA, D, LA)
        eH, eG = kH, part(arenaA, 9728, D, LB)
        uG, rGc, rGs, sG = (part(arenaB, i * D * LB, D, LB) for i in range(4))

        def vec_dt_row(dve):
            dve.wait_ge(s4_pe, 1)
            nc.vector.tensor_copy(dtb[:], bank[7][:, 0:D]).then_inc(s4_vec, 1)

        def vec_phase(st, r, u, off):
            st.link(nc.vector.tensor_scalar(r, u, off, MAGIC, ALU.add, ALU.add))
            return nc.vector.scalar_tensor_tensor(r, r, MAGIC, u, ALU.subtract, ALU.subtract)

        def vec_s4(dve, st):
            Vv, L = nc.vector, st.link
            tt = Vv.tensor_tensor
            dve.wait_ge(s4_pool, 3)
            L(tt(uG, bc(ang[:], P, D, LB), steps[:, :, 0:LB], ALU.mult))
            vec_phase(st, rGc, uG, V["quarter"]).then_inc(s4_vec, 1)

        def vec_s4_quarter(st):
            vec_phase(st, rGs, uG, V["off2"]).then_inc(s4_vec, 1)

        em1, half_sin, full_sin, u0, inv_a2, u1, u2, u3 = (q[i][:] for i in (0, 1, 2, 3, 4, 5, 6, 7))

        def vec_s4_inverses(dve, st):
            Vv, L = nc.vector, st.link
            tt = Vv.tensor_tensor
            dve.wait_ge(*loaded["s4"])
            tt(u0, V["are"], V["are"], ALU.mult)
            L(tt(u1, V["aim"], V["aim"], ALU.mult))
            L(tt(u0, u0, u1, ALU.add))
            Vv.reciprocal(inv_a2, u0)
            dve.wait_ge(s4_act, 1)
            L(Vv.tensor_scalar(u2, em1, -1.0, 1.0, ALU.mult, ALU.add))
            L(Vv.reciprocal(u1, u2))
            Vv.tensor_tensor(u1, u1, em1, ALU.mult).then_inc(s4_inverses, 1)

        def pool_s4_gains(pool, st):
            L = st.link
            tt, ts = nc.gpsimd.tensor_tensor, nc.gpsimd.tensor_scalar
            pool.wait_ge(s4_inverses, 1)
            pool.wait_ge(s4_act, 3)
            ts(em1, u1, 2.0, None, ALU.mult)
            L(tt(u0, half_sin, half_sin, ALU.mult))
            L(ts(u0, u0, 2.0, None, ALU.mult))
            tt(u2, em1, full_sin, ALU.mult)
            L(tt(u1, em1, u0, ALU.mult))
            tt(u2, u2, full_sin, ALU.add)
            L(tt(u1, em1, u1, ALU.subtract))
            L(tt(u1, u1, u0, ALU.subtract))
            tt(u0, u1, V["are"], ALU.mult)
            L(tt(u3, u2, V["aim"], ALU.mult))
            tt(u2, u2, V["are"], ALU.mult)
            L(tt(u0, u0, u3, ALU.add))
            tt(u0, u0, inv_a2, ALU.mult)
            L(tt(u3, u1, V["aim"], ALU.mult))
            L(tt(u2, u2, u3, ALU.subtract))
            L(tt(u2, u2, inv_a2, ALU.mult))
            tt(u1, V["cre"], u0, ALU.mult)
            L(tt(u3, V["cim"], u2, ALU.mult))
            L(tt(u1, u1, u3, ALU.subtract))
            ts(al[:], u1, 2.0, V["sgn"], ALU.mult, ALU.mult)
            tt(u2, V["cre"], u2, ALU.mult)
            L(tt(u3, V["cim"], u0, ALU.mult))
            L(tt(u1, u2, u3, ALU.add))
            ts(be[:], u1, -2.0, None, ALU.mult).then_inc(s4_pool, 1)

        def vec_s4_products(dve, st):
            Vv, L = nc.vector, st.link
            tt = Vv.tensor_tensor
            dve.wait_ge(s4_pool, 8)
            dve.wait_ge(s4_act, 8)
            for i in range(4):
                r = slice(i * D // 4, (i + 1) * D // 4)
                gq, sq, n = gg4[:, r, :], sG[:, r, :], D // 4
                tt(gq, gq, bc(al[:, r], P, n, LB), ALU.mult)
                L(tt(sq, sq, bc(be[:, r], P, n, LB), ALU.mult))
                L(tt(gq, gq, sq, ALU.add))
                tt(gq, gq, eG[:, r, :], ALU.mult).then_inc(s4_vec, 1)

        def pool_s4(pool, st):
            G, L = nc.gpsimd, st.link
            tt, ts = G.tensor_tensor, G.tensor_scalar
            pool.wait_ge(s4_vec, 2)
            pool.wait_ge(*loaded["s4"])
            tt(are[:], dtb[:], V["are"], ALU.mult).then_inc(s4_pool, 1)
            L(tt(aim[:], dtb[:], V["aim"], ALU.mult))
            L(ts(ang[:], aim[:], float(1.0 / (2.0 * np.pi)), None, ALU.mult))
            L(ts(q[1][:], ang[:], MAGIC, MAGIC, ALU.add, ALU.subtract))
            tt(ang[:], ang[:], q[1][:], ALU.subtract).then_inc(s4_pool, 1)
            pool.wait_ge(s4_pool, 3)
            L(tt(vH, bc(ang[:], P, D, LA), steps, ALU.mult))
            L(ts(vH, vH, float(LB), V["quarter"], ALU.mult, ALU.add))
            L(ts(kH, vH, MAGIC, MAGIC, ALU.add, ALU.subtract))
            pool_shift0(pool)
            tt(vH, vH, kH, ALU.subtract).then_inc(s4_pool, 1)

        def pool_s4_decay(pool):
            tt = nc.gpsimd.tensor_tensor
            pool.wait_ge(s4_pool, 4)
            tt(eH, bc(are[:], P, D, LA), steps, ALU.mult).then_inc(s4_pool, 1)
            tt(eG, bc(are[:], P, D, LB), steps[:, :, 0:LB], ALU.mult).then_inc(s4_pool, 1)

        def pool_s4_scale(pool):
            pool.wait_ge(s4_act, 5)
            nc.gpsimd.tensor_tensor(hh4[:], hh4[:], eH, ALU.mult).then_inc(s4_pool, 1)

        def act_s4_rows(act):
            A_ = nc.scalar.activation
            act.wait_ge(s4_pool, 2)
            A_(q[0][:], are[:], ACT.Tanh, scale=0.5).then_inc(s4_act, 1)
            act.wait_ge(s4_pool, 3)
            A_(q[2][:], ang[:], ACT.Sin, scale=TURN).then_inc(s4_act, 1)
            A_(q[1][:], ang[:], ACT.Sin, scale=0.5 * TURN).then_inc(s4_act, 1)
            act_exp0(act, 0)
            act.wait_ge(s4_pool, 4)
            A_(hh4[:], vH, ACT.Sin, scale=TURN).then_inc(s4_act, 1)
            act_exp0(act, 1)
            act.wait_ge(s4_pool, 5)
            A_(eH, eH, ACT.Exp, scale=float(LB)).then_inc(s4_act, 1)
            act.wait_ge(s4_pool, 6)
            A_(eG, eG, ACT.Exp).then_inc(s4_act, 1)

        def act_s4_cols(act):
            A_ = nc.scalar.activation
            act.wait_ge(s4_vec, 3)
            A_(gg4[:], rGc, ACT.Sin, scale=-TURN, bias=V["qturn"]).then_inc(s4_act, 1)
            act.wait_ge(s4_vec, 4)
            A_(sG, rGs, ACT.Sin, scale=-TURN, bias=V["oturn"]).then_inc(s4_act, 1)

        def pe_kernel(pe):
            pe.wait_ge(s4_pool, 7)
            pe.wait_ge(film_ready, 2 * NT)
            pe.wait_ge(w3_vec, 2)
            per = 512 // LB
            for d in range(D):
                if d == 2 * per:
                    pe.wait_ge(c2_copy, 3)
                if d % (D // 4) == 0:
                    pe.wait_ge(s4_vec, 5 + d // (D // 4))
                ins = nc.tensor.matmul(bank[4 + d // per][0:LA, (d % per) * LB:(d % per + 1) * LB],
                                       hh4[:, d, :], gg4[:, d, :], start=True, stop=True)
                if d % per == per - 1:
                    ins.then_inc(kern_pe, 1)

        def pe_kernel_turn(pe):
            pe.wait_ge(kern_act, 4)
            for b in range(LB):
                ins = nc.tensor.transpose(bank[4][:, b * LA:(b + 1) * LA], ka[:, :, b], ident[0:LA, 0:LA])
            ins.then_inc(kern_pe, 1)
            pe.wait_ge(kern_act, 5)
            for j in range(TB):
                ins = nc.tensor.transpose(bank[5][:, j * P:(j + 1) * P], kTl[:, j * P:(j + 1) * P], ident)
            ins.then_inc(kern_pe, 1)

        def act_kernel(act):
            per = 512 // LB
            for i in range(4):
                act.wait_ge(kern_pe, i + 1)
                nc.scalar.copy(ka[:, i * per:(i + 1) * per, :], bank[4 + i][0:LA, :].rearrange("p (d b) -> p d b", b=LB)).then_inc(kern_act, 1)
            act.wait_ge(kern_pe, 5)
            nc.scalar.copy(kTl[:].rearrange("p (a b) -> p a b", b=LB), bank[4][:].rearrange("p (b a) -> p a b", b=LB)).then_inc(kern_act, 1)
            act.wait_ge(kern_pe, 6)
            nc.scalar.copy(xk[:, :, 2, :], bank[5][:].rearrange("p (j d) -> p j d", d=D)).then_inc(kern_act, 1)

        def vec_affine_in(dve, st):
            dve.wait_ge(twice_ready, 1)
            dve.wait_ge(ln_done, NT)
            for t in range(NT):
                ins = nc.vector.tensor_scalar(tmp2[:, t, :], xn[:, t, :], mv2[:, t:t + 1], None, ALU.mult)
            st.link(ins)
            dve.wait_ge(*loaded["rows"])
            st.link(nc.vector.tensor_tensor(tmp2[:], tmp2[:], bm(V["g_in"], NT), ALU.mult))
            nc.vector.tensor_tensor(tmp2[:], tmp2[:], bm(V["b_in"], NT), ALU.add).then_inc(x2_ready, 1)

        def vec_film(dve, st):
            dve.wait_ge(x2_ready, 1)
            dve.wait_ge(film_ready, NT)
            st.link(nc.vector.tensor_tensor(tmp2[:], tmp2[:], film[:, :, 0, :], ALU.mult))
            for b in range(NB):
                ins = nc.vector.tensor_tensor(xk[:, :, b, :], tmp2[:, b * TB:(b + 1) * TB, :],
                                              film[:, b * TB:(b + 1) * TB, 1, :], ALU.add)
            ins.then_inc(x2_ready, 1)

        def pe_dft_x(pe, chunks):
            pe.wait_ge(*loaded["dft"])
            pe.wait_ge(x2_ready, 2)
            pe.wait_ge(film_ready, 2 * NT)
            for j in chunks:
                for c, m in enumerate(("cos", "sin")):
                    for q4 in range(TB):
                        ins = nc.tensor.matmul(bank[j][:, c * NB * D:(c + 1) * NB * D], V[m][:, q4 * S + j * P:q4 * S + (j + 1) * P],
                                               xk[:, q4, 0:NB].rearrange("p b d -> p (b d)"), start=(q4 == 0), stop=(q4 == TB - 1))
                ins.then_inc(dft_mm, 1)

        KBANK = (6, 7, 4, 6)

        def pe_dft_k(pe):
            pe.wait_ge(kern_act, 6)
            for j in range(4):
                if j == 3:
                    pe.wait_ge(kf_ready, 1)
                for c, m in enumerate(("cos", "sin")):
                    for q4 in range(TB):
                        ins = nc.tensor.matmul(bank[KBANK[j]][:, c * D:(c + 1) * D], V[m][:, q4 * S + j * P:q4 * S + (j + 1) * P],
                                               xk[:, q4, 2], start=(q4 == 0), stop=(q4 == TB - 1))
                ins.then_inc(dft_mm, 1)
            for q4 in range(TB):
                ins = nc.tensor.matmul(bank[5][0:1, 0:3 * D], V["alt"], xk[:, q4].rearrange("p b d -> p (b d)"),
                                       start=(q4 == 0), stop=(q4 == TB - 1))
            ins.then_inc(dft_mm, 1)

        def pe_dft_back(pe):
            pe.wait_ge(prod_ready, 5)
            for i in range(TB):
                for j in range(4):
                    for c, m in enumerate(("cos", "sin")):
                        nc.tensor.matmul(bank[4 + i][:, 0:NB * D], V[m][:, j * S + i * P:j * S + (i + 1) * P],
                                         yc[:, j, c], start=(j == 0 and c == 0), stop=False)
                nc.tensor.matmul(bank[4 + i][:, 0:NB * D], altrow[0:1, i * P:(i + 1) * P],
                                 yny[0:1].rearrange("p b d -> p (b d)"), start=False, stop=True).then_inc(y_mm, 1)

        def act_dft(act):
            for j in range(4):
                act.wait_ge(dft_mm, 4 + j + 1)
                nc.scalar.activation(kf[:, j].rearrange("p c d -> p (c d)"), bank[KBANK[j]][:, 0:2 * D], ACT.Copy,
                                     scale=V["wf"][:, j:j + 1]).then_inc(kf_ready, 1)
            act.wait_ge(dft_mm, 9)
            nc.scalar.activation(kny[:], bank[5][0:1, 2 * D:3 * D], ACT.Copy, scale=1.0 / (2 * S)).then_inc(kf_ready, 1)

        def vec_spectrum(dve, st):
            tt = nc.vector.tensor_tensor
            for b in range(NB):
                tt(tmp[:, b * TB:(b + 1) * TB, :], xk[:, :, b, :], bm(V["dskip"], TB), ALU.mult)
            for j in range(4):
                dve.wait_ge(kf_ready, j + 1)
                if j:
                    dve.wait_ge(prod_ready, j)
                x = bank[j][:].rearrange("p (n d) -> p n d", d=D)
                p = pr[:].rearrange("p i (b d) -> p (i b) d", d=D)
                tt(p[:, 0:2 * NB], x, bm(kf[:, j, 0, :], 2 * NB), ALU.mult)
                tt(p[:, 2 * NB:4 * NB], x, bm(kf[:, j, 1, :], 2 * NB), ALU.mult).then_inc(spec_used, 1)
                dve.wait_ge(spec_used, j + 1)
                tt(yc[:, j, 0], pr[:, 0], pr[:, 3], ALU.subtract)
                tt(yc[:, j, 1], pr[:, 1], pr[:, 2], ALU.add).then_inc(prod_ready, 1)
            dve.wait_ge(kf_ready, 5)
            tt(yny[:], bank[5][0:1, 0:NB * D].rearrange("p (b d) -> p b d", b=NB), bm(kny[:], NB), ALU.mult).then_inc(prod_ready, 1)

        def vec_xt(dve, st):
            tt = nc.vector.tensor_tensor
            chunks = lambda v: v.rearrange("p (b q) d -> p q b d", b=NB)
            tv, xv, f2 = chunks(tmp[:]), chunks(xt[:]), chunks(film[:, :, 2, :])
            dve.wait_ge(film_ready, 2 * NT)
            st.link(tt(tmp[:], tmp[:], film[:, :, 2, :], ALU.mult))
            st.link(tt(tmp[:], tmp[:], film[:, :, 3, :], ALU.add))
            st.link(tt(tmp[:], tmp[:], xn[:], ALU.add))
            for i in range(TB):
                dve.wait_ge(y_mm, i + 1)
                st.link(tt(xv[:, i], bank[4 + i][:, 0:NB * D].rearrange("p (b d) -> p b d", b=NB), f2[:, i], ALU.mult))
                st.link(tt(xv[:, i], xv[:, i], tv[:, i], ALU.add))
                for b in range(NB):
                    ins = nc.vector.bn_stats(stats[:, b * TB + i, :], xt[:, b * TB + i, :])
            st.link(ins)
            for b in range(NB):
                vec_aggregate(b)

        def pe_ffn0(pe):
            pe.wait_ge(*loaded["ffn0"])
            n = 0
            for b in range(NB):
                pe.wait_ge(ln_T, NB * 1 + b + 1)
                for c in range(4):
                    if n >= 4:
                        pe.wait_ge(ff_gelu, n - 3)
                    nc.tensor.matmul(bank[2 + n % 4][:], V["w1"][:, c * P:(c + 1) * P], xnT[:, b * S:(b + 1) * S],
                                     start=True, stop=True).then_inc(ff_mm, 1)
                    n += 1
            for b in range(NB):
                pe.wait_ge(ff_gelu, 4 * b + 4)
                for q4 in range(TB):
                    t = b * TB + q4
                    for c in range(4):
                        ins = nc.tensor.matmul(bank[6 + b][:, q4 * P:(q4 + 1) * P], hT0[:, c, t * P:(t + 1) * P],
                                               V["w2"][:, c * P:(c + 1) * P], start=(c == 0), stop=(c == 3))
                ins.then_inc(ff_out, 1)

        def act_ffn0(act):
            n = 0
            for b in range(NB):
                for c in range(4):
                    act.wait_ge(ff_mm, n + 1)
                    nc.scalar.activation(hT0[:, c, b * S:(b + 1) * S], bank[2 + n % 4][:], ACT.Gelu,
                                         bias=V["b1"][:, c:c + 1]).then_inc(ff_gelu, 1)
                    n += 1

        def vec_ffn0(dve, st):
            st.link(nc.vector.tensor_tensor(tmp[:], xt[:], bm(V["b2"], NT), ALU.add))
            for b, r in enumerate(halves()):
                dve.wait_ge(ff_out, b + 1)
                st.link(nc.vector.tensor_tensor(xt[:, r, :], bank[6 + b][:].rearrange("p (q d) -> p q d", d=D), tmp[:, r, :], ALU.add))
                vec_moments(st, xt, [b])
                if b == 0:
                    vec_normalise_add(dve, 1, xt, V["g_out"], [0])
            dve.wait_ge(x_final, 1)
            vec_moments(st, X, [0])
            vec_normalise_add(dve, 1, xt, V["g_out"], [1])
            dve.wait_ge(x_final, 2)
            vec_moments(st, X, [1])

        wr, wo0 = V["wr"], V["wo0"]
        wqkv = V["wqkv"].rearrange("p (h w c) -> p h w c", h=HF, w=4)
        qT = part(arenaB, 0, NB, 2, S)
        kT = part(arenaB, 2048, NB, 2, S)
        vv0 = part(arenaB, 4096, NT, CH * DF)
        wsel = part(arenaB, 6144, NB, 4, CH, DF)
        pb0 = part(arenaB, 8192, 3, S)
        pT0 = part(arenaB, 9728, 3, S)
        on0 = part(arenaB, 11264, 2, CH * DF)
        oT0 = part(arenaB, 11776, 2, 2 * P)
        bsel = sb("bsel", P, NB, 2, 2)
        dist = sb("dist", HF, NB)
        dt2 = sb("dt2", NB, HF)
        gm = sb("gm", NB, 8)
        gidx = sb("gidx", NB, 8, dt=U32)
        gidf = sb("gidf", NB, 8)
        gsel = sb("gsel", NB, HF)
        gkey = sb("gkey", NB, 8)
        ghead = sb("ghead", NB, 8, dt=I32)
        gsum, gmax = sb("gsum", NB, 1), sb("gmax", NB, 1)
        nmax0, rsum0 = sb("nmax0", P, NT, CH), sb("rsum0", P, NT, CH)
        rinv0 = sb("rinv0", P, NT, CH)
        rt_exp = sem("rt_exp")
        heads_ready, qk_mm, qk_ready, v_mm, v_ready = sem("heads_ready"), sem("qk_mm"), sem("qk_ready"), sem("v_mm"), sem("v_ready")
        sc_mm, sc_max, sc_exp, sc_turned = sem("sc_mm"), sem("sc_max"), sem("sc_exp"), sem("sc_turned")
        pT_dve, pT_act, pv_mm, o_norm, o_turned, oT_ready, wo_mm, x_added = (
            sem("pT_dve"), sem("pT_act"), sem("pv_mm"), sem("o_norm"), sem("o_turned"), sem("oT_ready"), sem("wo_mm"), sem("x_added"))

        def pe_route(pe):
            for b in range(NB):
                pe.wait_ge(ln_T, NB * 2 + b + 1)
                nc.tensor.matmul(bank[2 + b][0:HF, :], wr, xnT[:, b * S:(b + 1) * S], start=True, stop=True).then_inc(route_pe, 1)
            pe.wait_ge(route_vec, 1)
            nc.tensor.transpose(bank[4][0:NB, 0:HF], dist[:], ident[0:HF, 0:HF]).then_inc(route_pe, 1)

        def vec_route(dve, st):
            Vv = nc.vector
            for b in range(NB):
                dve.wait_ge(route_pe, b + 1)
                ins = Vv.tensor_reduce(dist[:, b:b + 1], bank[2 + b][0:HF, :], AX.X, ALU.add)
            st.link(ins)
            Vv.tensor_scalar(dist[:], dist[:], 1.0 / S, V["br_col"][0:HF], ALU.mult, ALU.add).then_inc(route_vec, 1)
            dve.wait_ge(route_pe, 3)
            st.link(Vv.tensor_reduce(gmax[:], bank[4][0:NB, 0:HF], AX.X, ALU.max))
            Vv.tensor_scalar(dt2[:], bank[4][0:NB, 0:HF], gmax[:], None, ALU.subtract).then_inc(route_vec, 1)
            dve.wait_ge(rt_exp, 1)
            st.link(Vv.reciprocal(gmax[:], gsum[:]))
            st.link(Vv.tensor_scalar(dt2[:], dt2[:], gmax[:], None, ALU.mult))
            st.link(Vv.max(gm[:], dt2[:]))
            st.link(Vv.max_index(gidx[:], gm[:], dt2[:]))
            st.link(Vv.tensor_copy(gidf[:], gidx[:]))
            st.link(Vv.tensor_scalar(gsel[:], V["iota16"][0:NB], gidf[:, 0:1], None, ALU.is_equal))
            for j in range(1, CH):
                st.link(Vv.scalar_tensor_tensor(gsel[:], V["iota16"][0:NB], gidf[:, j:j + 1], gsel[:], ALU.is_equal, ALU.add))
            st.link(Vv.tensor_tensor(gsel[:], gsel[:], V["rev16"][0:NB], ALU.mult))
            st.link(Vv.max(gkey[:], gsel[:]))
            Vv.tensor_scalar(ghead[:], gkey[:], -1.0, float(HF), ALU.mult, ALU.add).then_inc(route_vec, 1)
            dve.wait_ge(route_vec, 3)
            dve.wait_ge(*loaded["head0"])
            for b in range(NB):
                for j in range(0, CH, 2):
                    h = dve.value_load(ghead[b:b + 1, j:j + 1], min_val=0, max_val=HF - 1)
                    r = slice(DF * (j % 2), DF * (j % 2 + 1))
                    Vv.tensor_copy(wsel[:, b, :, j, :].unsqueeze(1), wqkv[:, bass.ds(h, 1), :, :])
                    Vv.tensor_scalar(bsel[r, b, j // 2, 0:1], V["bq2"][r, bass.ds(h, 1)], DF ** -0.5, None, ALU.mult)
                    ins = Vv.tensor_copy(bsel[r, b, j // 2, 1:2], V["bk2"][r, bass.ds(h, 1)])
                ins.then_inc(heads_ready, 1)

        def act_route(act):
            act.wait_ge(route_vec, 2)
            nc.scalar.activation(dt2[:], dt2[:], ACT.Exp, accum_out=gsum[:]).then_inc(rt_exp, 1)
            act.wait_ge(*loaded["head0"])
            act.wait_ge(route_vec, 3)
            for b in range(NB):
                for j in range(1, CH, 2):
                    h = act.value_load(ghead[b:b + 1, j:j + 1], min_val=0, max_val=HF - 1)
                    r = slice(DF * (j % 2), DF * (j % 2 + 1))
                    nc.scalar.copy(wsel[:, b, :, j, :].unsqueeze(1), wqkv[:, bass.ds(h, 1), :, :])
                    nc.scalar.activation(bsel[r, b, j // 2, 0:1], V["bq2"][r, bass.ds(h, 1)], ACT.Copy, scale=DF ** -0.5)
                    ins = nc.scalar.copy(bsel[r, b, j // 2, 1:2], V["bk2"][r, bass.ds(h, 1)])
                ins.then_inc(heads_act, 1)

        def pe_qkv0(pe):
            n = 0
            for b in range(NB):
                pe.wait_ge(heads_ready, b + 1)
                pe.wait_ge(heads_act, b + 1)
                for pair in range(2):
                    for w in range(2):
                        if n >= 4:
                            pe.wait_ge(qk_ready, n - 3)
                        nc.tensor.matmul(bank[2 + n % 4][:], wsel[:, b, w, 2 * pair:2 * pair + 2, :].rearrange("p j c -> p (j c)"),
                                         xnT[:, b * S:(b + 1) * S], start=True, stop=True).then_inc(qk_mm, 1)
                        n += 1
                for q2 in range(TB // 2):
                    if b == 1:
                        pe.wait_ge(v_ready, q2 + 1)
                    for q1 in range(2):
                        t = b * TB + 2 * q2 + q1
                        ins = nc.tensor.matmul(bank[6 + q2][:, q1 * CH * DF:(q1 + 1) * CH * DF], xnT[:, t * P:(t + 1) * P],
                                               wsel[:, b, 2, :, :].rearrange("p j c -> p (j c)"), start=True, stop=True)
                    ins.then_inc(v_mm, 1)

        def act_qk0(act):
            n = 0
            for b in range(NB):
                for pair in range(2):
                    for w, (dst, sc) in enumerate(((qT, DF ** -0.5), (kT, 1.0))):
                        act.wait_ge(qk_mm, n + 1)
                        nc.scalar.activation(dst[:, b, pair, :], bank[2 + n % 4][:], ACT.Identity, scale=sc,
                                             bias=bsel[:, b, pair, w:w + 1]).then_inc(qk_ready, 1)
                        n += 1

        def vec_v0(dve):
            for m in range(4):
                b = m // 2
                dve.wait_ge(v_mm, m + 1)
                for q1 in range(2):
                    ins = nc.vector.tensor_tensor(vv0[:, 2 * m + q1, :].rearrange("p (j c) -> p j c", j=CH),
                                                  bank[6 + m % 2][:, q1 * CH * DF:(q1 + 1) * CH * DF].rearrange("p (j c) -> p j c", j=CH),
                                                  wsel[:, b, 3, :, :], ALU.add)
                ins.then_inc(v_ready, 1)

        NU = NT * CH
        by_act = lambda n: n % 3 == 0
        acts_to = lambda n: n // 3 + 1
        dves_to = lambda n: n - n // 3

        def pe_attend0(pe):
            pe.wait_ge(qk_ready, 8)
            pe.wait_ge(v_ready, 4)
            for n in range(NU + 10):
                if n < NU:
                    t, h = n // CH, n % CH
                    b, r = t // TB, slice(DF * (h % 2), DF * (h % 2 + 1))
                    if n >= 2:
                        pe.wait_ge(sc_exp, n - 1)
                    nc.tensor.matmul(bank[n % 2][:], qT[r, b, h // 2, (t % TB) * P:(t % TB + 1) * P],
                                     kT[r, b, h // 2, :], start=True, stop=True).then_inc(sc_mm, 1)
                m = n - 1
                if 0 <= m < NU:
                    pe.wait_ge(sc_exp, m + 1)
                    if m >= 2:
                        w = m - 2
                        pe.wait_ge(*((pT_act, acts_to(w)) if by_act(w) else (pT_dve, dves_to(w))))
                    for k in range(TB):
                        ins = nc.tensor.transpose(bank[2 + m % 2][:, k * P:(k + 1) * P], pb0[:, m % 3, k * P:(k + 1) * P], ident)
                    ins.then_inc(sc_turned, 1)
                m = n - 2
                if 0 <= m < NU:
                    t, h = m // CH, m % CH
                    pe.wait_ge(*((pT_act, acts_to(m)) if by_act(m) else (pT_dve, dves_to(m))))
                    if h == 0 and t >= 2:
                        pe.wait_ge(o_norm, t - 1)
                    for k in range(TB):
                        ins = nc.tensor.matmul(bank[4 + t % 2][:, h * DF:(h + 1) * DF], pT0[:, m % 3, k * P:(k + 1) * P],
                                               vv0[:, t // TB * TB + k, h * DF:(h + 1) * DF], start=(k == 0), stop=(k == TB - 1))
                    ins.then_inc(pv_mm, 1)
                if n >= 7 and (n - 7) % CH == 0 and (n - 7) // CH < NT:
                    t = (n - 7) // CH
                    pe.wait_ge(o_norm, t + 1)
                    if t:
                        pe.wait_ge(oT_ready, t)
                    for c in range(2):
                        ins = nc.tensor.transpose(bank[6][:, c * P:(c + 1) * P], on0[:, t % 2, c * P:(c + 1) * P], ident)
                    ins.then_inc(o_turned, 1)
                if n >= 9 and (n - 9) % CH == 0 and (n - 9) // CH < NT:
                    t = (n - 9) // CH
                    pe.wait_ge(oT_ready, t + 1)
                    if t:
                        pe.wait_ge(x_added, t)
                    for c in range(2):
                        ins = nc.tensor.matmul(bank[7][:, 0:P], oT0[:, t % 2, c * P:(c + 1) * P], wo0[:, c * P:(c + 1) * P],
                                               start=(c == 0), stop=(c == 1))
                    ins.then_inc(wo_mm, 1)

        def vec_attend0(dve, st):
            for n in range(NU + 11):
                if n < NU:
                    t, h = n // CH, n % CH
                    dve.wait_ge(sc_mm, n + 1)
                    nc.vector.tensor_reduce(nmax0[:, t, h:h + 1], bank[n % 2][:], AX.X, ALU.max, negate=True).then_inc(sc_max, 1)
                m = n - 1
                if 0 <= m < NU and not by_act(m):
                    dve.wait_ge(sc_turned, m + 1)
                    if m >= 3:
                        dve.wait_ge(pv_mm, m - 2)
                    nc.vector.tensor_copy(pT0[:, m % 3, :], bank[2 + m % 2][:]).then_inc(pT_dve, 1)
                if n >= 6 and (n - 6) % CH == 0 and (n - 6) // CH < NT:
                    t = (n - 6) // CH
                    dve.wait_ge(sc_exp, CH * t + CH)
                    st.link(nc.vector.reciprocal(rinv0[:, t, :], rsum0[:, t, :]))
                    dve.wait_ge(pv_mm, CH * t + CH)
                    if t >= 2:
                        dve.wait_ge(o_turned, t - 1)
                    nc.vector.tensor_tensor(on0[:, t % 2, :].rearrange("p (h c) -> p h c", h=CH),
                                            bank[4 + t % 2][:, 0:CH * DF].rearrange("p (h c) -> p h c", h=CH),
                                            bc(rinv0[:, t, :], P, CH, DF), ALU.mult).then_inc(o_norm, 1)
                if n >= 10 and (n - 10) % CH == 0 and (n - 10) // CH < NT:
                    t = (n - 10) // CH
                    if t == 0:
                        dve.wait_ge(bias_added, 1)
                    dve.wait_ge(wo_mm, t + 1)
                    nc.vector.tensor_tensor(X[:, t, :], bank[7][:, 0:P], tmp[:, t, :], ALU.add).then_inc(x_added, 1)
                if n == 11 + CH * (TB - 1):
                    dve.wait_ge(x_added, TB)
                    vec_moments(st, X, [0])
                if n == 15 + CH * (TB - 1):
                    vec_normalise(dve, 4, X, xn, [0])

        def act_attend0(act):
            for n in range(NU + 9):
                if n < NU:
                    t, h = n // CH, n % CH
                    act.wait_ge(sc_max, n + 1)
                    if n >= 3:
                        act.wait_ge(sc_turned, n - 2)
                    nc.scalar.activation(pb0[:, n % 3, :], bank[n % 2][:], ACT.Exp, bias=nmax0[:, t, h:h + 1],
                                         accum_out=rsum0[:, t, h:h + 1]).then_inc(sc_exp, 1)
                m = n - 1
                if 0 <= m < NU and by_act(m):
                    act.wait_ge(sc_turned, m + 1)
                    if m >= 3:
                        act.wait_ge(pv_mm, m - 2)
                    nc.scalar.copy(pT0[:, m % 3, :], bank[2 + m % 2][:]).then_inc(pT_act, 1)
                if n >= 8 and (n - 8) % CH == 0 and (n - 8) // CH < NT:
                    t = (n - 8) // CH
                    act.wait_ge(o_turned, t + 1)
                    if t >= 2:
                        act.wait_ge(wo_mm, t - 1)
                    nc.scalar.copy(oT0[:, t % 2, :], bank[6][:, 0:2 * P]).then_inc(oT_ready, 1)

        def pool_bias(pool, i, row, ready):
            pool.wait_ge(ln_done, NT * (i + 1))
            nc.gpsimd.tensor_tensor(tmp[:], X[:], bm(row, NT), ALU.add).then_inc(ready, 1)

        a1, bm1 = sb("a1", DC, D), sb("bm1", DC, D)
        m1 = sb("m1", P, NB * NC)
        vw1 = sb("vw1", NC, NB, D)
        s1 = part(arenaB, 0, NT, NC)
        e1 = part(arenaB, 1024, NT, NC)
        pT1 = part(arenaB, 2048, TOK)[0:NC]
        st1, mv1 = sb("st1", P, NB, 6), sb("mv1", P, NB, 2)
        mx1, rs1, ri1 = sb("mx1", P, NT), sb("rs1", P, NT), sb("ri1", P, NT)
        vr1, r1 = sb("vr1", P, NB), sb("r1", P, NB)
        fold1_mm, fold1_copy = sem("fold1_mm"), sem("fold1_copy")
        s1_mm, s1_copy, r1_ready = sem("s1_mm"), sem("s1_copy"), sem("r1_ready")
        e1_ready, e1_turned, pT1_ready, y1_mm = sem("e1_ready"), sem("e1_turned"), sem("pT1_ready"), sem("y1_mm")

        def pe_fold1(pe):
            pe.wait_ge(*loaded["l1"])
            pe.wait_ge(s0_copy, NT)
            nc.tensor.matmul(bank[2][0:DC, 0:D], V["wk1"], V["wq1"], start=True, stop=True).then_inc(fold1_mm, 1)
            nc.tensor.matmul(bank[3][0:DC, 0:D], V["wv1"], V["wo1T"], start=True, stop=True).then_inc(fold1_mm, 1)
            pe.wait_ge(fold1_copy, 2)
            nc.tensor.matmul(bank[2][:, 0:NB * NC], a1[:], V["ctxT"][0:DC], start=True, stop=True).then_inc(fold1_mm, 1)
            for b in range(NB):
                ins = nc.tensor.matmul(bank[3][0:NC, b * D:(b + 1) * D], V["ctxT"][0:DC, b * NC:(b + 1) * NC], bm1[:], start=True, stop=True)
            ins.then_inc(fold1_mm, 1)
            pe.wait_ge(fold1_copy, 4)

        def act_fold1(act):
            act.wait_ge(fold1_mm, 1)
            nc.scalar.copy(a1[:], bank[2][0:DC, 0:D]).then_inc(fold1_copy, 1)
            act.wait_ge(fold1_mm, 2)
            nc.scalar.copy(bm1[:], bank[3][0:DC, 0:D]).then_inc(fold1_copy, 1)
            act.wait_ge(fold1_mm, 3)
            nc.scalar.copy(m1[:], bank[2][:, 0:NB * NC]).then_inc(fold1_copy, 1)
            act.wait_ge(fold1_mm, 4)
            nc.scalar.copy(vw1[:], bank[3][0:NC, 0:NB * D].rearrange("p (b d) -> p b d", b=NB)).then_inc(fold1_copy, 1)

        def pe_l1x(pe):
            for b in range(NB):
                pe_turn(pe, ln_done, NT * 4, xn, [b])
                pe.wait_ge(ln_T, NB * 3 + b + 1)
                for q4 in range(TB):
                    t = b * TB + q4
                    ins = nc.tensor.matmul(bank[2 + b][:, q4 * NC:(q4 + 1) * NC], xnT[:, t * P:(t + 1) * P],
                                           m1[:, b * NC:(b + 1) * NC], start=True, stop=True)
                ins.then_inc(s1_mm, 1)
            pe.wait_ge(l1x_vec, 1)
            nc.tensor.matmul(bank[4][:, 0:NB], V["avg"], mv1[:, :, 0], start=True, stop=True).then_inc(avg1_mm, 1)
            pe.wait_ge(l1x_vec, 2)
            nc.tensor.matmul(bank[5][:, 0:NB], V["avg"], vr1[:], start=True, stop=True).then_inc(avg1_mm, 1)
            for t in range(NT):
                pe.wait_ge(e1_ready, t + 1)
                if t == 0:
                    pe.wait_ge(l1x_vec, 3)
                ins = nc.tensor.transpose(bank[4 + t // TB][0:NC, (t % TB) * P:(t % TB + 1) * P], e1[:, t, :], ident)
                if t % TB == TB - 1:
                    ins.then_inc(e1_turned, 1)
            for b in range(NB):
                pe.wait_ge(pT1_ready, b + 1)
                for q4 in range(TB):
                    t = b * TB + q4
                    ins = nc.tensor.matmul(bank[6 + b][:, q4 * P:(q4 + 1) * P], pT1[:, t * P:(t + 1) * P], vw1[:, b, :],
                                           start=True, stop=True)
                ins.then_inc(y1_mm, 1)

        def act_l1x(act):
            for b in range(NB):
                act_turned(act, 3, which=[b])
                act.wait_ge(s1_mm, b + 1)
                nc.scalar.copy(s1[:, b * TB:(b + 1) * TB, :], bank[2 + b][:, 0:TB * NC].rearrange("p (q k) -> p q k", k=NC)).then_inc(s1_copy, 1)
            act.wait_ge(l1x_vec, 4)
            act.wait_ge(r1_ready, 1)
            for t in range(NT):
                nc.scalar.activation(e1[:, t, :], s1[:, t, :], ACT.Exp, scale=r1[:, t // TB:t // TB + 1], bias=mx1[:, t:t + 1],
                                     accum_out=rs1[:, t:t + 1]).then_inc(e1_ready, 1)
            for b in range(NB):
                act.wait_ge(e1_turned, b + 1)
                nc.scalar.copy(pT1[:, b * S:(b + 1) * S], bank[4 + b][0:NC, :]).then_inc(pT1_ready, 1)

        def pool_l1x(pool, st):
            pool.wait_ge(l1x_vec, 3)
            nc.gpsimd.tensor_tensor(r1[:], vr1[:], V["half"][:, 0:NB], ALU.pow).then_inc(r1_ready, 1)

        def vec_l1x(dve, st):
            Vv = nc.vector
            for b in range(NB):
                dve.wait_ge(s1_copy, b + 1)
                ins = Vv.bn_stats(st1[:, b, :], s1[:, b * TB:(b + 1) * TB, :].rearrange("p q k -> p (q k)"))
            st.link(ins)
            for b in range(NB):
                ins = Vv.bn_aggr(mv1[:, b, :], st1[:, b, :])
            ins.then_inc(l1x_vec, 1)
            Vv.tensor_reduce(mx1[:], s1[:], AX.X, ALU.max, negate=True)
            dve.wait_ge(l1x_vec, 1)
            dve.wait_ge(avg1_mm, 1)
            st.link(Vv.tensor_tensor(vr1[:], mv1[:, :, 0], bank[4][:, 0:NB], ALU.subtract))
            st.link(Vv.tensor_tensor(vr1[:], vr1[:], vr1[:], ALU.mult))
            Vv.tensor_tensor(vr1[:], vr1[:], mv1[:, :, 1], ALU.add).then_inc(l1x_vec, 1)
            dve.wait_ge(avg1_mm, 2)
            Vv.tensor_scalar(vr1[:], bank[5][:, 0:NB], 1e-5, None, ALU.add).then_inc(l1x_vec, 1)
            dve.wait_ge(r1_ready, 1)
            Vv.tensor_tensor(mx1[:].rearrange("p (b q) -> p b q", b=NB), mx1[:].rearrange("p (b q) -> p b q", b=NB),
                             bc(r1[:], P, NB, TB), ALU.mult).then_inc(l1x_vec, 1)
            dve.wait_ge(e1_ready, NT)
            st.link(Vv.reciprocal(ri1[:], rs1[:]))
            for t in range(NT):
                if t % TB == 0:
                    dve.wait_ge(y1_mm, t // TB + 1)
                ins = Vv.scalar_tensor_tensor(X[:, t, :], bank[6 + t // TB][:, (t % TB) * P:(t % TB + 1) * P], ri1[:, t:t + 1],
                                              X[:, t, :], ALU.mult, ALU.add)
            st.link(ins)

        NG = NCL + NTL
        sig = sb("sig", P, NG)
        sigq = sb("sigq", P, NTL)
        kd = sb("kd", P, KN - 1)
        rden = sb("rden", P, 1)
        sc1 = part(arenaB, 0, NT, NG)
        cand = part(arenaB, 576, NT, TPC)
        pick = part(arenaB, 640, NT, TPC, KN - 1)
        held = part(arenaB, 1088, NT, TPC, KN - 1)
        sg, fr, lo, vl, dv, ga = (part(arenaB, 1536 + 64 * i, NT, TPC) for i in range(6))
        ohT = part(arenaB, 4608, TOK)[0:NTL]
        got = part(arenaB, 5632, NT, TABW)
        hT1 = part(arenaB, 7176, TOK)[0:CMP]
        oh1 = part(arenaB, 8200, NT, NTL)
        ocl, osl = part(arenaB, 8712, NT, NCL), part(arenaB, 8776, NT, TPC)
        b81 = sb("b81", P, NT)
        comp = sb("comp", P, NT, 2)
        hh1, hx1 = part(arenaB, 9032, NT, GRID), part(arenaB, 9160, NT, GRID)
        mag = sb("mag", P, NT)
        sig_ready = sem("sig_ready")

        def vec_sigs(dve, st):
            Vv = nc.vector
            dve.wait_ge(*loaded["l1"])
            raw, sg = V["sigT"], sig[:, NCL:NG]
            st.link(Vv.tensor_scalar(sigq[:], raw, -0.3, None, ALU.is_lt))
            st.link(Vv.scalar_tensor_tensor(sigq[:], raw, 0.3, sigq[:], ALU.is_gt, ALU.subtract))
            st.link(Vv.tensor_tensor(sigq[:], sigq[:], raw, ALU.subtract))
            st.link(Vv.tensor_tensor(sg, sigq[:], raw, ALU.add))
            st.link(Vv.tensor_reduce(sig[:, 0:NCL], sg.rearrange("p (c j) -> p c j", c=NCL), AX.X, ALU.add))
            st.link(Vv.tensor_scalar(sigq[:, 0:NCL], sig[:, 0:NCL], 0.0, None, ALU.is_lt))
            st.link(Vv.scalar_tensor_tensor(sig[:, 0:NCL], sig[:, 0:NCL], 0.0, sigq[:, 0:NCL], ALU.is_gt, ALU.subtract))
            st.link(Vv.tensor_tensor(kd[:], V["knots"][:, 1:KN], V["knots"][:, 0:KN - 1], ALU.subtract))
            st.link(Vv.tensor_scalar(rden[:], V["temp"], 1e-6, None, ALU.add))
            Vv.reciprocal(rden[:], rden[:]).then_inc(sig_ready, 1)

        def pe_l1f(pe):
            pe.wait_ge(sig_ready, 1)
            for b in range(NB):
                pe.wait_ge(ln_T, NB * 4 + b + 1)
                for q4 in range(TB):
                    t = b * TB + q4
                    ins = nc.tensor.matmul(bank[2 + b][:, q4 * NG:(q4 + 1) * NG], xnT[:, t * P:(t + 1) * P], sig[:], start=True, stop=True)
                ins.then_inc(l1f_pe, 1)
            for b in range(NB):
                nc.tensor.matmul(bank[4 + b][0:CMP, :], V["cw1"], xnT[:, b * S:(b + 1) * S], start=True, stop=True).then_inc(l1f_pe, 1)
            pe.wait_ge(l1f_act, 1 + NB)
            for t in range(NT):
                ins = nc.tensor.matmul(bank[6][:, 2 * t:2 * t + 2], hT1[:, t * P:(t + 1) * P], V["cw2"][0:CMP], start=True, stop=True)
            ins.then_inc(l1f_pe, 1)
            pe.wait_ge(*loaded["l3"])
            pe.wait_ge(l1f_vec, 2)
            pe_fold3(pe, *FOLD3[0])
            pe_fold3(pe, *FOLD3[1])
            for b in range(NB):
                pe.wait_ge(l1f_vec, 4 + b)
                for q4 in range(TB):
                    ins = nc.tensor.transpose(bank[b][0:NTL, q4 * P:(q4 + 1) * P], oh1[:, b * TB + q4, :], ident)
                ins.then_inc(l1f_pe, 1)
                for m in range(b * TB // 2, (b + 1) * TB // 2):
                    pe.wait_ge(l1f_act, 6 + 3 * b)
                    for k in range(2):
                        t = 2 * m + k
                        ins = nc.tensor.matmul(bank[2 + m][:, k * TABW:(k + 1) * TABW], ohT[:, t * P:(t + 1) * P], V["tab"][0:NTL],
                                               start=True, stop=True)
                    ins.then_inc(l1f_pe, 1)
            pe.wait_ge(l1f_act, NT // 2 + 7)
            pe_fold3(pe, *FOLD3[2])

        def act_l1f(act):
            act.wait_ge(l1f_vec, 1)
            nc.scalar.activation(sg, sc1[:, :, 0:NCL], ACT.Exp, scale=-1.0).then_inc(l1f_act, 1)
            for b in range(NB):
                act.wait_ge(l1f_pe, b + 3)
                nc.scalar.activation(hT1[:, b * S:(b + 1) * S], bank[4 + b][0:CMP, :], ACT.Gelu, bias=V["cb1"][0:CMP]).then_inc(l1f_act, 1)
            act.wait_ge(l1f_vec, 2)
            nc.scalar.activation(comp[:], comp[:], ACT.Tanh).then_inc(l1f_act, 1)
            act_fold3(act, *FOLD3[0])
            act.wait_ge(l1f_vec, 3)
            nc.scalar.activation(sg, cand, ACT.Exp, scale=-1.0).then_inc(l1f_act, 1)
            act_fold3(act, *FOLD3[1])
            for b in range(NB):
                act.wait_ge(l1f_pe, 6 + 3 * b)
                nc.scalar.copy(ohT[:, b * S:(b + 1) * S], bank[b][0:NTL, :]).then_inc(l1f_act, 1)
                for m in range(b * TB // 2, (b + 1) * TB // 2):
                    act.wait_ge(l1f_pe, 7 + m + b)
                    nc.scalar.copy(got[:, 2 * m:2 * m + 2, :], bank[2 + m][:, 0:2 * TABW].rearrange("p (k n) -> p k n", k=2)).then_inc(l1f_act, 1)
            act_fold3(act, *FOLD3[2])

        def vec_gates(st):
            Vv, L = nc.vector, st.link
            wide = lambda v: v.unsqueeze(3).broadcast_to([P, NT, TPC, KN - 1])
            row = lambda v: v.unsqueeze(1).unsqueeze(1).broadcast_to([P, NT, TPC, v.shape[1]])
            L(Vv.tensor_scalar(sg, sg, 1.0, None, ALU.add))
            L(Vv.reciprocal(fr, sg))
            L(Vv.tensor_scalar(fr, fr, float(KN - 1), None, ALU.mult))
            L(Vv.tensor_tensor(pick[:, :, :, 1:], fr.unsqueeze(3).broadcast_to([P, NT, TPC, KN - 2]), row(V["iota8"][:, 1:KN - 1]), ALU.is_ge))
            L(Vv.tensor_reduce(lo, pick[:, :, :, 1:], AX.X, ALU.add))
            Vv.tensor_tensor(fr, fr, lo, ALU.subtract)
            L(Vv.tensor_tensor(pick, wide(lo), row(V["iota8"][:, 0:KN - 1]), ALU.is_equal))
            L(Vv.tensor_tensor(held, pick, row(V["knots"][:, 0:KN - 1]), ALU.mult))
            L(Vv.tensor_reduce(vl, held, AX.X, ALU.add))
            L(Vv.tensor_tensor(held, pick, row(kd[:]), ALU.mult))
            L(Vv.tensor_reduce(dv, held, AX.X, ALU.add))
            L(Vv.tensor_tensor(dv, fr, dv, ALU.mult))
            L(Vv.tensor_tensor(ga, vl, dv, ALU.add))

        def first_best(st, vals, best, onehot):
            Vv = nc.vector
            rev = bm(V["rev8"], NT)
            st.link(Vv.tensor_reduce(best[:], vals[:], AX.X, ALU.max))
            st.link(Vv.tensor_tensor(onehot[:], vals[:], bc(best[:], P, NT, 8), ALU.is_equal))
            st.link(Vv.tensor_tensor(onehot[:], onehot[:], rev, ALU.mult))
            st.link(Vv.tensor_reduce(best[:], onehot[:], AX.X, ALU.max))
            st.link(Vv.tensor_tensor(onehot[:], onehot[:], bc(best[:], P, NT, 8), ALU.is_equal))

        def vec_l1f(dve, st):
            Vv = nc.vector
            for b in range(NB):
                dve.wait_ge(l1f_pe, b + 1)
                ins = Vv.tensor_scalar(sc1[:, b * TB:(b + 1) * TB, :], bank[2 + b][:, 0:TB * NG].rearrange("p (q k) -> p q k", k=NG),
                                       rden[:], None, ALU.mult)
            ins.then_inc(l1f_vec, 1)
            dve.wait_ge(l1f_act, 1)
            vec_gates(st)
            first_best(st, ga, b81, ocl)
            dve.wait_ge(l1f_pe, 5)
            Vv.tensor_tensor(comp[:], bank[6][:, 0:2 * NT].rearrange("p (t c) -> p t c", c=2), bm(V["cb2"], NT), ALU.add).then_inc(l1f_vec, 1)
            for t in range(NT):
                ins = Vv.tensor_tensor(oh1[:, t].rearrange("p (c j) -> p c j", c=NCL), sc1[:, t, NCL:NG].rearrange("p (c j) -> p c j", c=NCL),
                                       bc(ocl[:, t], P, NCL, TPC), ALU.mult)
            st.link(ins)
            Vv.tensor_reduce(cand, oh1[:].rearrange("p t (c j) -> p t j c", c=NCL), AX.X, ALU.add).then_inc(l1f_vec, 1)
            dve.wait_ge(l1f_act, 5)
            vec_gates(st)
            first_best(st, ga, b81, osl)
            for r in halves():
                for t in range(r.start, r.stop):
                    ins = Vv.tensor_tensor(oh1[:, t].rearrange("p (c j) -> p c j", c=NCL), bm(osl[:, t], NCL), bc(ocl[:, t], P, NCL, TPC), ALU.mult)
                ins.then_inc(l1f_vec, 1)
            dve.wait_ge(l1f_act, 4)
            G_ = GRID
            for b, r in enumerate(halves()):
                dve.wait_ge(l1f_act, 8 + 3 * b)
                h, x, g = hh1[:, r], hx1[:, r], got[:, r]
                Vv.tensor_tensor(h, g[:, :, 0:G_], bc(comp[:, r, 0], P, TB, G_), ALU.mult)
                st.link(Vv.tensor_tensor(x, g[:, :, G_:2 * G_], bc(comp[:, r, 1], P, TB, G_), ALU.mult))
                st.link(Vv.tensor_tensor(h, h, x, ALU.add))
                st.link(Vv.tensor_tensor(h, h, g[:, :, 2 * G_:3 * G_], ALU.add))
                st.link(Vv.scalar_tensor_tensor(h, h, 0.0, g[:, :, 3 * G_:4 * G_], ALU.max, ALU.mult))
                st.link(Vv.tensor_reduce(mag[:, r], h, AX.X, ALU.add))
                st.link(Vv.tensor_tensor(mag[:, r], mag[:, r], g[:, :, 4 * G_], ALU.add))
                st.link(Vv.tensor_scalar(mag[:, r], mag[:, r], V["oscale"], None, ALU.mult))
                for t in range(r.start, r.stop):
                    ins = Vv.scalar_tensor_tensor(xt[:, t, :], got[:, t, 4 * G_ + 1:TABW], mag[:, t:t + 1], xn[:, t, :], ALU.mult, ALU.add)
                st.link(ins)
                vec_moments(st, xt, [b])

        var2, mv2 = sb("var2", P, NT), sb("mv2", P, NT)

        def pool_rstd_twice(pool, st, i, both):
            pool.wait_ge(ln_rstd, NB * (i + 1))
            G = nc.gpsimd
            st.link(G.tensor_tensor(var2[:], rstd[:], rstd[:], ALU.mult))
            st.link(G.tensor_tensor(var2[:], var2[:], mv[:, :, 1], ALU.mult))
            st.link(G.tensor_scalar(var2[:], var2[:], 1e-5, None, ALU.add))
            ins = G.tensor_tensor(mv2[:], var2[:], V["half"][:, 0:NT], ALU.pow)
            if both:
                st.link(ins)
                ins = G.tensor_tensor(mv2[:], mv2[:], rstd[:], ALU.mult)
            ins.then_inc(twice_ready, 1)

        twice_ready = sem("twice_ready")
        final_stage_done, stored = sem("final_stage_done"), sem("stored")

        KL = S
        cn2 = sb("cn2", NC, NB, DC)
        stc, mvc, rdc = sb("stc", NC, NB, 6), sb("mvc", NC, NB, 2), sb("rdc", NC, NB)
        cnT2 = sb("cnT2", DC, NB * NC)
        kvc = sb("kvc", NC, NB, 2 * D)
        sqc, ssc = sb("sqc", NC, NB, D), sb("ssc", NC, NB, H2)
        kcT = sb("kcT", P, NB, NC)
        qkv2 = part(arenaB, 0, NT, 3 * D)
        sq2 = part(arenaB, 3072, NT, 2 * D)
        pT2 = part(arenaB, 3072, 3, 5 * P)
        qT2, kT2 = part(arenaB, 5120, TOK), part(arenaB, 6144, TOK)
        pb2 = part(arenaB, 7168, 3, KL + NC)
        sc2 = [part(v[:].rearrange("p t d -> p (t d)"), 0, TB * H2, NC) for v in (xt, xn)]
        oT2 = part(tmp2[:].rearrange("p t d -> p (t d)"), 0, 2, H2 * P)[0:D2]
        ss2, inv2 = sb("ss2", P, NT, 2 * H2), sb("inv2", P, NT, 2 * H2)
        nma, nmb, nm2 = sb("nma", P, NT * H2), sb("nmb", P, NT * H2), sb("nm2", P, NT * H2)
        rsa, rsb, ri2 = sb("rsa", P, NT, H2), sb("rsb", P, NT, H2), sb("ri2", P, NT, H2)
        c2_mm, c2_copy = sem("c2_mm"), sem("c2_copy")
        qkv2_mm, qkv2_copy, ss2_ready, inv2_ready, qk2_scaled, qk2_turned, qkT2_ready = (
            sem("qkv2_mm"), sem("qkv2_copy"), sem("ss2_ready"), sem("inv2_ready"), sem("qk2_scaled"), sem("qk2_turned"), sem("qkT2_ready"))
        a2_mm, a2_max, a2_exp, a2_turned, p2_dve, p2_act, pv2_mm, oT2_ready, wo2_mm, x2_added = (
            sem(f"{n}") for n in ("a2_mm", "a2_max", "a2_exp", "a2_turned", "p2_dve", "p2_act", "pv2_mm",
                                  "oT2_ready", "wo2_mm", "x2_added"))

        def vec_c2_moments(dve, st):
            dve.wait_ge(*loaded["l2"])
            cr = V["ctxr"][0:NC].rearrange("p (b d) -> p b d", b=NB)
            for b in range(NB):
                ins = nc.vector.bn_stats(stc[:, b, :], cr[:, b, :])
            st.link(ins)
            for b in range(NB):
                ins = nc.vector.bn_aggr(mvc[:, b, :], stc[:, b, :])
            ins.then_inc(c2_stats, 1)

        def pool_c2_rstd(pool, st):
            pool.wait_ge(c2_stats, 1)
            st.link(nc.gpsimd.tensor_scalar(rdc[:], mvc[:, :, 1], 1e-5, None, ALU.add))
            nc.gpsimd.tensor_tensor(rdc[:], rdc[:], V["half"][0:NC, 0:NB], ALU.pow).then_inc(c2_powers, 1)

        def vec_c2_norm(dve, st):
            cr = V["ctxr"][0:NC].rearrange("p (b d) -> p b d", b=NB)
            dve.wait_ge(c2_powers, 1)
            for b in range(NB):
                ins = nc.vector.tensor_scalar(cn2[:, b, :], cr[:, b, :], mvc[:, b, 0:1], rdc[:, b:b + 1], ALU.subtract, ALU.mult)
            st.link(ins)
            st.link(nc.vector.tensor_tensor(cn2[:], cn2[:], bm(V["lnx_g"][0:NC], NB), ALU.mult))
            nc.vector.tensor_tensor(cn2[:], cn2[:], bm(V["lnx_b"][0:NC], NB), ALU.add).then_inc(c2_scaled, 1)

        def pe_c2(pe):
            pe.wait_ge(c2_scaled, 1)
            pe.wait_ge(ctx0_copy, 2 + H0 + NB)
            for b in range(NB):
                ins = nc.tensor.transpose(bank[6][0:DC, b * NC:(b + 1) * NC], cn2[:, b, :], ident[0:NC, 0:NC])
            ins.then_inc(c2_mm, 1)
            pe.wait_ge(c2_copy, 1)
            for b in range(NB):
                ins = nc.tensor.matmul(bank[7][0:NC, b * 2 * D:(b + 1) * 2 * D], cnT2[:, b * NC:(b + 1) * NC], V["wkvT"][0:DC], start=True, stop=True)
            ins.then_inc(c2_mm, 1)

        def act_c2(act):
            act.wait_ge(c2_mm, 1)
            nc.scalar.copy(cnT2[:], bank[6][0:DC, 0:NB * NC]).then_inc(c2_copy, 1)
            act.wait_ge(c2_mm, 2)
            nc.scalar.copy(kvc[:], bank[7][0:NC, :].rearrange("p (b n) -> p b n", b=NB)).then_inc(c2_copy, 1)

        def vec_c2_squares(dve, st):
            dve.wait_ge(c2_copy, 2)
            st.link(nc.vector.tensor_tensor(sqc[:], kvc[:, :, 0:D], kvc[:, :, 0:D], ALU.mult))
            nc.vector.tensor_reduce(ssc[:].rearrange("p b h -> p (b h)"), sqc[:].rearrange("p b (h c) -> p (b h) c", h=H2), AX.X, ALU.add).then_inc(c2_stats, 1)

        def pool_c2_inv(pool, st):
            pool.wait_ge(c2_stats, 2)
            st.link(nc.gpsimd.tensor_scalar(ssc[:], ssc[:], 1.0 / D2, 1e-16, ALU.mult, ALU.max))
            nc.gpsimd.tensor_tensor(ssc[:].rearrange("p b h -> p (b h)"), ssc[:].rearrange("p b h -> p (b h)"),
                                    V["half"][0:NC, 0:NB * H2], ALU.pow).then_inc(c2_powers, 1)

        def vec_c2_scale(dve):
            dve.wait_ge(c2_powers, 2)
            for b in range(NB):
                kk = kvc[:, b, 0:D].rearrange("p (h c) -> p h c", h=H2)
                ins = nc.vector.tensor_tensor(kk, kk, bc(ssc[:, b], NC, H2, D2), ALU.mult)
            ins.then_inc(c2_scaled, 1)

        def pe_c2_keys(pe):
            pe.wait_ge(c2_scaled, 2)
            for b in range(NB):
                ins = nc.tensor.transpose(bank[6][:, b * NC:(b + 1) * NC], kvc[:, b, 0:D], ident[0:NC, 0:NC])
            ins.then_inc(c2_mm, 1)

        def act_c2_keys(act):
            act.wait_ge(c2_mm, 3)
            nc.scalar.activation(kcT[:], bank[6][:, 0:NB * NC].rearrange("p (b k) -> p b k", b=NB), ACT.Copy, scale=V["kn"]).then_inc(c2_copy, 1)

        def vec_latents(dve):
            dve.wait_ge(twice_ready, 2)
            for t in range(NT):
                nc.vector.tensor_scalar(tmp2[:, t, :], X[:, t, :], mv[:, t, 0:1], mv2[:, t:t + 1], ALU.subtract, ALU.mult).then_inc(ln_done, 1)

        def pe_qkv2(pe):
            at = NB * DC
            for t in range(NT):
                if t % TB == 0:
                    pe.wait_ge(ln_T, NB * 5 + t // TB + 1)
                if t >= 4:
                    pe.wait_ge(qkv2_copy, t - 3)
                nc.tensor.matmul(bank[2 + t % 4][:, 0:3 * D], xnT[:, t * P:(t + 1) * P], packed["l2"][:, at:at + 3 * D],
                                 start=True, stop=True).then_inc(qkv2_mm, 1)
            pe.wait_ge(qkv2_copy, NT)
            pe_fold3(pe, *FOLD3[3])
            for w in range(2):
                for b in range(NB):
                    pe.wait_ge(qk2_scaled, b + 1)
                    for q4 in range(TB):
                        ins = nc.tensor.transpose(bank[2 * w + b][:, q4 * P:(q4 + 1) * P], qkv2[:, b * TB + q4, w * D:(w + 1) * D], ident)
                    ins.then_inc(qk2_turned, 1)

        def act_qkv2(act):
            for t in range(NT):
                act.wait_ge(qkv2_mm, t + 1)
                nc.scalar.copy(qkv2[:, t, :], bank[2 + t % 4][:, 0:3 * D]).then_inc(qkv2_copy, 1)
            act_fold3(act, *FOLD3[3])
            for w, (dst, g) in enumerate(((qT2, V["qn"]), (kT2, V["kn"]))):
                for b in range(NB):
                    act.wait_ge(qk2_turned, 2 * w + b + 1)
                    nc.scalar.activation(dst[:, b * S:(b + 1) * S], bank[2 * w + b][:], ACT.Copy, scale=g).then_inc(qkT2_ready, 1)

        def vec_qkv2(dve, st):
            for b in range(NB):
                r = slice(b * TB, (b + 1) * TB)
                dve.wait_ge(qkv2_copy, (b + 1) * TB)
                st.link(nc.vector.tensor_tensor(sq2[:, r], qkv2[:, r, 0:2 * D], qkv2[:, r, 0:2 * D], ALU.mult))
                nc.vector.tensor_reduce(ss2[:, r].rearrange("p t g -> p (t g)"), sq2[:, r].rearrange("p t (g c) -> p (t g) c", c=D2),
                                        AX.X, ALU.add).then_inc(ss2_ready, 1)
            for b in range(NB):
                r = range(b * TB, (b + 1) * TB)
                dve.wait_ge(inv2_ready, b + 1)
                for t in r:
                    v = qkv2[:, t, 0:2 * D].rearrange("p (g c) -> p g c", c=D2)
                    ins = nc.vector.tensor_tensor(v, v, bc(inv2[:, t], P, 2 * H2, D2), ALU.mult)
                ins.then_inc(qk2_scaled, 1)

        def pool_qkv2(pool, st):
            for b in range(NB):
                r = slice(b * TB, (b + 1) * TB)
                pool.wait_ge(ss2_ready, b + 1)
                st.link(nc.gpsimd.tensor_scalar(ss2[:, r], ss2[:, r], 1.0 / D2, 1e-16, ALU.mult, ALU.max))
                nc.gpsimd.tensor_tensor(inv2[:, r].rearrange("p t g -> p (t g)"), ss2[:, r].rearrange("p t g -> p (t g)"),
                                        V["half"][:, 0:TB * 2 * H2], ALU.pow).then_inc(inv2_ready, 1)

        NU2 = NT * H2

        def ctx_unit(n):
            t, h = n // H2, n % H2
            return t // TB * TB * H2 + h * TB + t % TB

        def pe_attend2(pe):
            pe.wait_ge(c2_copy, 3)
            for i in range(NB * H2):
                b, h = i // H2, i % H2
                pe.wait_ge(qkT2_ready, b + 1)
                r = slice(D2 * h, D2 * (h + 1))
                for q4 in range(TB):
                    t = b * TB + q4
                    ins = nc.tensor.matmul(bank[4 + i][:, q4 * NC:(q4 + 1) * NC], qT2[r, t * P:(t + 1) * P], kcT[r, b, :], start=True, stop=True)
                ins.then_inc(c2_mm, 1)
            pe.wait_ge(qkT2_ready, 4)
            for n in range(NU2 + 5):
                if n < NU2:
                    t, h = n // H2, n % H2
                    b, r = t // TB, slice(D2 * h, D2 * (h + 1))
                    if n >= 3:
                        pe.wait_ge(a2_exp, n - 2)
                    nc.tensor.matmul(bank[n % 3][:], qT2[r, t * P:(t + 1) * P], kT2[r, b * S:(b + 1) * S], start=True, stop=True).then_inc(a2_mm, 1)
                m = n - 2
                if 0 <= m < NU2:
                    pe.wait_ge(a2_exp, m + 1)
                    if m >= 2:
                        pe.wait_ge(p2_dve, m - 1)
                    for k in range(TB):
                        nc.tensor.transpose(bank[4 + m % 2][:, k * P:(k + 1) * P], pb2[:, m % 3, k * P:(k + 1) * P], ident)
                    if m:
                        pe.wait_ge(p2_act, m)
                    nc.tensor.transpose(bank[3][0:NC, 0:P], pb2[:, m % 3, KL:KL + NC], ident).then_inc(a2_turned, 1)
                m = n - 3
                if 0 <= m < NU2:
                    t, h = m // H2, m % H2
                    pe.wait_ge(p2_dve, m + 1)
                    pe.wait_ge(p2_act, m + 1)
                    if h == 0 and t >= 2:
                        pe.wait_ge(x2_added, t - 1)
                    o = bank[6 + t % 2][0:D2, h * P:(h + 1) * P]
                    for k in range(TB):
                        nc.tensor.matmul(o, qkv2[:, t // TB * TB + k, 2 * D + h * D2:2 * D + (h + 1) * D2], pT2[:, m % 3, k * P:(k + 1) * P],
                                         start=(k == 0), stop=False)
                    nc.tensor.matmul(o, kvc[:, t // TB, D + h * D2:D + (h + 1) * D2], pT2[0:NC, m % 3, TB * P:(TB + 1) * P],
                                     start=False, stop=True).then_inc(pv2_mm, 1)
                if n >= 5 and n % 2 == 1 and (n - 5) // 2 < NT:
                    t = (n - 5) // 2
                    pe.wait_ge(oT2_ready, t + 1)
                    for h in range(H2):
                        ins = nc.tensor.matmul(bank[6 + t % 2][:, (2 + h) * P:(3 + h) * P], oT2[:, t % 2, h * P:(h + 1) * P],
                                               V["wo2T"][0:D2, h * D:(h + 1) * D], start=True, stop=True)
                    ins.then_inc(wo2_mm, 1)

        def vec_attend2(dve, st):
            Vv = nc.vector
            for i in range(NB * H2):
                b, at = i // H2, i % H2 * TB
                dve.wait_ge(c2_mm, 4 + i)
                ins = Vv.tensor_tensor(sc2[b][:, at:at + TB, :], bank[4 + i][:, 0:TB * NC].rearrange("p (u k) -> p u k", k=NC),
                                       bm(maskb[:, 1, b, :], TB), ALU.add)
            st.link(ins)
            for b in range(NB):
                ins = Vv.tensor_reduce(nmb[:, b * TB * H2:(b + 1) * TB * H2], sc2[b], AX.X, ALU.max, negate=True)
            st.link(ins)
            for n in range(NU2 + 6):
                if n >= 6 and n % 2 == 0 and (n - 6) // 2 < NT:
                    t = (n - 6) // 2
                    if t == 0:
                        dve.wait_ge(bias_added, 2)
                    st.link(Vv.tensor_tensor(rsa[:, t], rsa[:, t], rsb[:, t], ALU.add))
                    st.link(Vv.reciprocal(ri2[:, t], rsa[:, t]))
                    dve.wait_ge(wo2_mm, t + 1)
                    o = bank[6 + t % 2]
                    st.link(Vv.scalar_tensor_tensor(X[:, t, :], o[:, 2 * P:3 * P], ri2[:, t, 0:1], tmp[:, t, :], ALU.mult, ALU.add))
                    Vv.scalar_tensor_tensor(X[:, t, :], o[:, 3 * P:4 * P], ri2[:, t, 1:2], X[:, t, :], ALU.mult, ALU.add).then_inc(x2_added, 1)
                if n == 7 + 2 * (TB - 1):
                    dve.wait_ge(x2_added, TB)
                    vec_moments(st, X, [0])
                if n < NU2:
                    dve.wait_ge(a2_mm, n + 1)
                    st.link(Vv.tensor_reduce(nma[:, n:n + 1], bank[n % 3][:], AX.X, ALU.max, negate=True))
                    Vv.tensor_scalar(nm2[:, n:n + 1], nma[:, n:n + 1], nmb[:, ctx_unit(n):ctx_unit(n) + 1], D2 ** -0.5, ALU.min, ALU.mult).then_inc(a2_max, 1)
                m = n - 2
                if 0 <= m < NU2:
                    dve.wait_ge(a2_turned, m + 1)
                    if m >= 3:
                        dve.wait_ge(pv2_mm, m - 2)
                    Vv.tensor_copy(pT2[:, m % 3, 0:TB * P], bank[4 + m % 2][:]).then_inc(p2_dve, 1)

        def act_attend2(act):
            for n in range(NU2 + 4):
                if n < NU2:
                    t, h = n // H2, n % H2
                    act.wait_ge(a2_max, n + 1)
                    if n >= 3:
                        act.wait_ge(a2_turned, n - 2)
                    nc.scalar.activation(pb2[:, n % 3, 0:KL], bank[n % 3][:], ACT.Exp, bias=nm2[:, n:n + 1], scale=D2 ** -0.5,
                                         accum_out=rsa[:, t, h:h + 1])
                    nc.scalar.activation(pb2[:, n % 3, KL:KL + NC], sc2[t // TB][:, ctx_unit(n) % (TB * H2), :], ACT.Exp, bias=nm2[:, n:n + 1],
                                         scale=D2 ** -0.5, accum_out=rsb[:, t, h:h + 1]).then_inc(a2_exp, 1)
                m = n - 2
                if 0 <= m < NU2:
                    act.wait_ge(a2_turned, m + 1)
                    if m >= 3:
                        act.wait_ge(pv2_mm, m - 2)
                    nc.scalar.copy(pT2[0:NC, m % 3, TB * P:(TB + 1) * P], bank[3][0:NC, 0:P]).then_inc(p2_act, 1)
                if n >= 4 and n % 2 == 0 and (n - 4) // 2 < NT:
                    t = (n - 4) // 2
                    act.wait_ge(pv2_mm, 2 * t + 2)
                    if t >= 2:
                        act.wait_ge(wo2_mm, t - 1)
                    nc.scalar.copy(oT2[:, t % 2], bank[6 + t % 2][0:D2, 0:2 * P]).then_inc(oT2_ready, 1)

        NX = NE + NSH
        WE = 3 * HE
        lg, m8, ix8, ixf = sb("lg", P, NT, NE), sb("m8", P, NT, 8), sb("ix8", P, NT, 8, dt=U32), sb("ixf", P, NT, 8)
        e2x, wa, wb = sb("e2x", P, NT), sb("wa", P, NT), sb("wb", P, NT)
        cw, cwb = sb("cw", P, NT, NE), sb("cwb", P, NT, NE)
        hid2 = part(arenaB, 0, 2, 2, S)
        sil2 = part(arenaB, 2048, 3, S)
        lg_mm, lg_diff, lg_exp = sem("lg_mm"), sem("lg_diff"), sem("lg_exp")
        up_mm, silu_ready, hid_ready, down_mm, moe_added = sem("up_mm"), sem("silu_ready"), sem("hid_ready"), sem("down_mm"), sem("moe_added")

        def pe_moe(pe):
            for t in range(NT):
                if t % TB == 0:
                    pe.wait_ge(ln_T, NB * 6 + t // TB + 1)
                ins = nc.tensor.matmul(bank[7][:, t * NE:(t + 1) * NE], xnT[:, t * P:(t + 1) * P], V["router"], start=True, stop=True)
            ins.then_inc(lg_mm, 1)
            pe.wait_ge(*loaded["moe"])
            for n in range(4 * NX + 2):
                if n < 4 * NX:
                    e, b, c = n // 4, n // 2 % 2, n % 2
                    w = V["moe"][:, e * WE:(e + 1) * WE]
                    if n >= 2:
                        pe.wait_ge(hid_ready, n - 1)
                    nc.tensor.matmul(bank[n % 2][:], w[:, c * P:(c + 1) * P], xnT[:, b * S:(b + 1) * S], start=True, stop=True).then_inc(up_mm, 1)
                    nc.tensor.matmul(bank[2 + n % 2][:], w[:, HE + c * P:HE + (c + 1) * P], xnT[:, b * S:(b + 1) * S],
                                     start=True, stop=True).then_inc(up_mm, 1)
                if n >= 3 and n % 2 == 1:
                    m = (n - 3) // 2
                    w = V["moe"][:, m // 2 * WE:(m // 2 + 1) * WE]
                    pe.wait_ge(hid_ready, 2 * m + 2)
                    if m >= 3:
                        pe.wait_ge(moe_added, m - 2)
                    for q4 in range(TB):
                        for c in range(2):
                            ins = nc.tensor.matmul(bank[4 + m % 3][:, q4 * P:(q4 + 1) * P], hid2[:, m % 2, c, q4 * P:(q4 + 1) * P],
                                                   w[:, 2 * HE + c * P:2 * HE + (c + 1) * P], start=(c == 0), stop=(c == 1))
                    ins.then_inc(down_mm, 1)

        def act_moe(act):
            act.wait_ge(lg_diff, 1)
            nc.scalar.activation(e2x[:], e2x[:], ACT.Exp).then_inc(lg_exp, 1)
            for n in range(4 * NX):
                act.wait_ge(up_mm, 2 * n + 1)
                if n >= 3:
                    act.wait_ge(hid_ready, n - 2)
                nc.scalar.activation(sil2[:, n % 3, :], bank[n % 2][:], ACT.Silu).then_inc(silu_ready, 1)

        def vec_moe(dve, st):
            Vv = nc.vector
            dve.wait_ge(lg_mm, 1)
            st.link(Vv.tensor_tensor(lg[:], bank[7][:, 0:NT * NE].rearrange("p (t e) -> p t e", e=NE), bm(V["ebias"], NT), ALU.add))
            for t in range(NT):
                ins = Vv.max(m8[:, t, :], lg[:, t, :])
            st.link(ins)
            Vv.tensor_tensor(e2x[:], m8[:, :, 1], m8[:, :, 0], ALU.subtract).then_inc(lg_diff, 1)
            for t in range(NT):
                ins = Vv.max_index(ix8[:, t, :], m8[:, t, :], lg[:, t, :])
            st.link(ins)
            st.link(Vv.tensor_copy(ixf[:], ix8[:]))
            dve.wait_ge(lg_exp, 1)
            st.link(Vv.tensor_scalar(wb[:], e2x[:], 1.0, None, ALU.add))
            st.link(Vv.reciprocal(wa[:], wb[:]))
            st.link(Vv.tensor_tensor(wb[:], e2x[:], wa[:], ALU.mult))
            for i, (dst, w) in enumerate(((cw, wa), (cwb, wb))):
                st.link(Vv.tensor_tensor(dst[:], bm(V["iota8"], NT), bc(ixf[:, :, i], P, NT, NE), ALU.is_equal))
                st.link(Vv.tensor_tensor(dst[:], dst[:], bc(w[:], P, NT, NE), ALU.mult))
            st.link(Vv.tensor_tensor(cw[:], cw[:], cwb[:], ALU.add))
            for n in range(4 * NX + 4):
                if n < 4 * NX:
                    b, c, m = n // 2 % 2, n % 2, n // 2
                    dve.wait_ge(silu_ready, n + 1)
                    dve.wait_ge(up_mm, 2 * n + 2)
                    if m >= 2:
                        dve.wait_ge(down_mm, m - 1)
                    Vv.tensor_tensor(hid2[:, m % 2, c, :], sil2[:, n % 3, :], bank[2 + n % 2][:], ALU.mult).then_inc(hid_ready, 1)
                if n >= 4 and n % 2 == 0:
                    m = (n - 4) // 2
                    e, b = m // 2, m % 2
                    dve.wait_ge(down_mm, m + 1)
                    if m >= 2:
                        dve.wait_ge(moe_added, m - 1)
                    if e < NE:
                        for q4 in range(TB):
                            t = b * TB + q4
                            ins = Vv.scalar_tensor_tensor(X[:, t, :], bank[4 + m % 3][:, q4 * P:(q4 + 1) * P], cw[:, t, e:e + 1], X[:, t, :],
                                                          ALU.mult, ALU.add)
                    else:
                        ins = Vv.tensor_tensor(X[:, b * TB:(b + 1) * TB, :], bank[4 + m % 3][:].rearrange("p (q d) -> p q d", d=D),
                                               X[:, b * TB:(b + 1) * TB, :], ALU.add)
                    ins.then_inc(moe_added, 1)
                if n == 4 * NX:
                    dve.wait_ge(moe_added, 2 * NX - 1)
                    vec_moments(st, X, [0])

        f3 = part(arenaB, 9400, NB, H3, NC)
        vw3 = part(arenaB, 11864, NB, CK3, D)
        k3, v3 = part(packed["dft"], 1024, 2, NB * NC), part(packed["dft"], 1024 + 2 * NB * NC, 2, NB * NC)
        vws = part(packed["dft"], 0, 2, 2, NB, D)
        HB3 = [(0, 6), (6, 11), (11, 16)]
        p3 = part(arenaB, 0, 3, H3, NC)
        pT3 = part(arenaB, 3 * HK3, 2, CK3, P)
        mx3, sm3 = part(arenaB, 6400, 3, H3), part(arenaB, 6448, 3, H3)
        kv3_mm, kv3_copy, f3_mm, f3_copy, vw3_out, vw3_in = sem("kv3_mm"), sem("kv3_copy"), sem("f3_mm"), sem("f3_copy"), [sem("vw3_out_even"), sem("vw3_out_odd")], sem("vw3_in")
        s3_mm, s3_max, s3_exp, s3_norm, s3_turned, pT3_act, pT3_dve, y3_mm, x3_added = (
            sem(n) for n in ("s3_mm", "s3_max", "s3_exp", "s3_norm", "s3_turned", "pT3_act", "pT3_dve", "y3_mm", "x3_added"))

        def pe_fold3(pe, first, last):
            for n in range(first, last + 1):
                if n < last:
                    cc = slice(n * P, (n + 1) * P)
                    if n:
                        pe.wait_ge(kv3_copy, 2 * n)
                    nc.tensor.matmul(bank[2][:, 0:NB * NC], V["wk3"][0:DC, cc], V["ctxT"][0:DC], start=True, stop=True).then_inc(kv3_mm, 1)
                    nc.tensor.matmul(bank[3][:, 0:NB * NC], V["wv3"][0:DC, cc], V["ctxT"][0:DC], start=True, stop=True).then_inc(kv3_mm, 1)
                c = n - 1
                if c >= first:
                    cc = slice(c * P, (c + 1) * P)
                    pe.wait_ge(kv3_copy, 2 * c + 2)
                    if c:
                        pe.wait_ge(f3_copy, 4 * c)
                    for i in range(2):
                        r = slice(D3 * i, D3 * (i + 1))
                        nc.tensor.matmul(bank[4 + i][:, 0:NB * NC], V["wqT3"][r, cc], k3[r, c % 2, :], start=True, stop=True).then_inc(f3_mm, 1)
                        for b in range(NB):
                            ins = nc.tensor.matmul(bank[6 + i][0:NC, b * D:(b + 1) * D], v3[r, c % 2, b * NC:(b + 1) * NC], V["wo3"][r, cc],
                                                   start=True, stop=True)
                        ins.then_inc(f3_mm, 1)

        def act_fold3(act, first, last):
            for n in range(first, last + 1):
                if n < last:
                    act.wait_ge(kv3_mm, 2 * n + 1)
                    if n >= 2:
                        act.wait_ge(f3_mm, 4 * (n - 1))
                    nc.scalar.copy(k3[:, n % 2, :], bank[2][:, 0:NB * NC]).then_inc(kv3_copy, 1)
                    act.wait_ge(kv3_mm, 2 * n + 2)
                    nc.scalar.copy(v3[:, n % 2, :], bank[3][:, 0:NB * NC]).then_inc(kv3_copy, 1)
                c = n - 1
                if c >= first:
                    for i in range(2):
                        act.wait_ge(f3_mm, 4 * c + 2 * i + 1)
                        nc.scalar.activation(f3[:, :, 2 * c + i, :], bank[4 + i][:, 0:NB * NC].rearrange("p (b k) -> p b k", b=NB), ACT.Copy,
                                             scale=D3 ** -0.5).then_inc(f3_copy, 1)
                        act.wait_ge(f3_mm, 4 * c + 2 * i + 2)
                        if c >= 2:
                            act.wait_ge(vw3_out[c % 2], 16 * 4 * (c // 2))
                        nc.scalar.copy(vws[0:NC, c % 2, i], bank[6 + i][0:NC, 0:NB * D].rearrange("p (b d) -> p b d", b=NB)).then_inc(f3_copy, 1)

        def sync_fold3(sp):
            for c in range(H3 // 2):
                sp.wait_ge(f3_copy, 4 * c + 4)
                for i in range(2):
                    h = 2 * c + i
                    for b in range(NB):
                        sp.dma_start(A["vw_scratch"][b, h * NC:(h + 1) * NC, :], vws[0:NC, c % 2, i, b]).then_inc(vw3_out[c % 2], 16)
            for c in range(2):
                sp.wait_ge(vw3_out[c], 16 * H3)
            full = HK3 // P
            for b in range(NB):
                sp.dma_start(vw3[:, b, 0:full, :], A["vw_scratch"][b, 0:full * P, :].rearrange("(c p) d -> p c d", p=P)).then_inc(vw3_in, 16)
                sp.dma_start(vw3[0:HK3 - full * P, b, full, :], A["vw_scratch"][b, full * P:HK3, :]).then_inc(vw3_in, 16)

        TURN3 = (6, 7)

        def pe_attend3(pe):
            pe.wait_ge(vw3_in, 16 * 4)
            for n in range(NT + 3):
                if n in (0, 2):
                    pe_turn(pe, ln_done, NT * 9, xn, [n // 2], TURN3)
                if n in (0, TB):
                    pe.wait_ge(ln_T, NB * 7 + n // TB + 1)
                if n < NT:
                    b = n // TB
                    for i, (h0, h1) in enumerate(HB3):
                        if n:
                            pe.wait_ge(s3_exp, 3 * (n - 1) + i + 1)
                        nc.tensor.matmul(bank[i][:, 0:(h1 - h0) * NC], xnT[:, n * P:(n + 1) * P],
                                         f3[:, b, h0:h1, :].rearrange("p h k -> p (h k)"), start=True, stop=True).then_inc(s3_mm, 1)
                t = n - 2
                if 0 <= t < NT:
                    pe.wait_ge(s3_norm, t + 1)
                    pf = p3[:, t % 3].rearrange("p h k -> p (h k)")
                    for g in range(3):
                        if t:
                            if g < 2:
                                pe.wait_ge(pT3_act, 2 * (t - 1) + g + 1)
                            else:
                                pe.wait_ge(pT3_dve, t)
                        for c in range(4 * g, min(4 * g + 4, CK3)):
                            w = min(P, HK3 - c * P)
                            ins = nc.tensor.transpose(bank[3 + g][0:w, (c % 4) * P:(c % 4 + 1) * P], pf[:, c * P:c * P + w], ident)
                        ins.then_inc(s3_turned, 1)
                t = n - 3
                if 0 <= t < NT:
                    pe.wait_ge(pT3_act, 2 * t + 2)
                    pe.wait_ge(pT3_dve, t + 1)
                    if t >= 2:
                        pe.wait_ge(x3_added, t - 1)
                    for c in range(CK3):
                        w = min(P, HK3 - c * P)
                        ins = nc.tensor.matmul(bank[6 + t % 2][:, 0:P], pT3[0:w, t % 2, c, :], vw3[0:w, t // TB, c, :],
                                               start=(c == 0), stop=(c == CK3 - 1))
                    ins.then_inc(y3_mm, 1)

        LASTW = HK3 - (CK3 - 1) * P

        def act_attend3(act):
            for n in range(NT + 2):
                if n in (0, 2):
                    act_turned(act, 7, which=[n // 2], banks=TURN3)
                if n < NT:
                    if n >= 3:
                        act.wait_ge(s3_turned, 3 * (n - 2))
                    for i, (h0, h1) in enumerate(HB3):
                        act.wait_ge(s3_max, 3 * n + i + 1)
                        for h in range(h0, h1 if i < 2 else h0):
                            ins = nc.scalar.activation(p3[:, n % 3, h, :], bank[i][:, (h - h0) * NC:(h - h0 + 1) * NC], ACT.Exp,
                                                       bias=mx3[:, n % 3, h:h + 1], accum_out=sm3[:, n % 3, h:h + 1])
                        if i == 2:
                            ins = nc.scalar.activation(p3[:, n % 3, h0:h1, :], p3[:, n % 3, h0:h1, :], ACT.Exp)
                        ins.then_inc(s3_exp, 1)
                t = n - 2
                if 0 <= t < NT:
                    for g in range(2):
                        act.wait_ge(s3_turned, 3 * t + g + 1)
                        if t >= 2:
                            act.wait_ge(y3_mm, t - 1)
                        nc.scalar.copy(pT3[:, t % 2, 4 * g:4 * g + 4, :], bank[3 + g][:].rearrange("p (c q) -> p c q", q=P)).then_inc(pT3_act, 1)

        def vec_attend3(dve, st):
            Vv = nc.vector
            for n in range(NT + 4):
                if n < NT:
                    if n >= 3:
                        dve.wait_ge(s3_norm, n - 2)
                        dve.wait_ge(s3_turned, 3 * (n - 2))
                    for i, (h0, h1) in enumerate(HB3):
                        dve.wait_ge(s3_mm, 3 * n + i + 1)
                        s = bank[i][:, 0:(h1 - h0) * NC].rearrange("p (h k) -> p h k", k=NC)
                        ins = Vv.tensor_reduce(mx3[:, n % 3, h0:h1], s, AX.X, ALU.max, negate=True)
                        if i == 2:
                            st.link(ins)
                            ins = Vv.tensor_tensor(p3[:, n % 3, h0:h1, :], s, bc(mx3[:, n % 3, h0:h1], P, h1 - h0, NC), ALU.add)
                        ins.then_inc(s3_max, 1)
                t = n - 1
                if 0 <= t < NT:
                    dve.wait_ge(s3_exp, 3 * t + 3)
                    h0, h1 = HB3[2]
                    st.link(Vv.tensor_reduce(sm3[:, t % 3, h0:h1], p3[:, t % 3, h0:h1, :], AX.X, ALU.add))
                    st.link(Vv.reciprocal(sm3[:, t % 3], sm3[:, t % 3]))
                    Vv.tensor_tensor(p3[:, t % 3], p3[:, t % 3], bc(sm3[:, t % 3], P, H3, NC), ALU.mult).then_inc(s3_norm, 1)
                t = n - 2
                if 0 <= t < NT:
                    dve.wait_ge(s3_turned, 3 * t + 3)
                    if t >= 2:
                        dve.wait_ge(y3_mm, t - 1)
                    Vv.tensor_copy(pT3[:, t % 2, 8, :], bank[5][:, 0:P])
                    Vv.tensor_copy(pT3[0:LASTW, t % 2, 9, :], bank[5][0:LASTW, P:2 * P]).then_inc(pT3_dve, 1)
                t = n - 4
                if 0 <= t < NT:
                    if t == 0:
                        dve.wait_ge(bias_added, 3)
                    dve.wait_ge(y3_mm, t + 1)
                    Vv.tensor_tensor(X[:, t, :], bank[6 + t % 2][:, 0:P], tmp[:, t, :], ALU.add).then_inc(x3_added, 1)
                if n == 5 + (TB - 1):
                    dve.wait_ge(x3_added, TB)
                    vec_moments(st, X, [0])
                if n == 7 + (TB - 1):
                    vec_normalise(dve, 10, X, xn, [0])

        wsum, wgam = sb("wsum", P, 2), sb("wgam", P, 2)
        tern = [V["wfcT"], V["wpT"]]
        ternb = part(arenaB, 12512, HID3)
        g3 = part(arenaB, 0, 3, HID3)
        g3n = part(arenaB, 1536, 3, HID3)
        g3T = part(arenaB, 3072, 3, HID3)
        st3, mv3, rd3 = part(arenaB, 4608, NT, 6), part(arenaB, 4656, NT, 2), part(arenaB, 4672, NT)
        wsum_mm, tern_ready = sem("wsum_mm"), sem("tern_ready")
        h3_mm, g3_ready, mv3_ready, rd3_ready, g3_norm, g3_turned, g3T_dve, g3T_act, y4_mm, x4_added = (
            sem(n) for n in ("h3_mm", "g3_ready", "mv3_ready", "rd3_ready", "g3_norm", "g3_turned", "g3T_dve", "g3T_act", "y4_mm", "x4_added"))

        def vec_weights3(dve):
            dve.wait_ge(*loaded["l3f"])
            for i in range(2):
                ins = nc.vector.tensor_reduce(wsum[:, i:i + 1], tern[i], AX.X, ALU.add, apply_absolute_value=True)
            ins.then_inc(w3_vec, 1)

        def pe_weights3(pe):
            pe.wait_ge(w3_vec, 1)
            pe.wait_ge(c2_copy, 2)
            nc.tensor.matmul(bank[7][:, 0:2], V["avg"], wsum[:], start=True, stop=True).then_inc(wsum_mm, 1)

        def vec_gamma3(dve, st):
            dve.wait_ge(wsum_mm, 1)
            st.link(nc.vector.tensor_scalar(wgam[:], bank[7][:, 0:2], 1.0 / HID3, 1e-6, ALU.mult, ALU.add))
            nc.vector.reciprocal(wgam[:], wgam[:]).then_inc(w3_vec, 1)

        def pool_ternary3(pool, st):
            G = nc.gpsimd
            pool.wait_ge(w3_vec, 2)
            pool.wait_ge(kern_pe, 4)
            for i in range(2):
                st.link(G.tensor_scalar(ternb, tern[i], wgam[:, i:i + 1], -0.5, ALU.mult, ALU.is_lt))
                st.link(G.tensor_scalar(tern[i], tern[i], wgam[:, i:i + 1], 0.5, ALU.mult, ALU.is_gt))
                ins = G.tensor_tensor(tern[i], tern[i], ternb, ALU.subtract)
                if i == 0:
                    st.link(ins)
                else:
                    ins.then_inc(tern_ready, 1)

        def pe_l3f(pe):
            pe.wait_ge(tern_ready, 1)
            for n in range(NT + 4):
                if n < NT:
                    if n % TB == 0:
                        pe_turn(pe, ln_done, NT * 10, xn, [n // TB])
                    pe.wait_ge(ln_T, NB * 8 + n // TB + 1)
                    if n >= 2:
                        pe.wait_ge(g3_ready, n - 1)
                    nc.tensor.matmul(bank[2 + n % 2][:], xnT[:, n * P:(n + 1) * P], V["wfcT"], start=True, stop=True).then_inc(h3_mm, 1)
                t = n - 2
                if 0 <= t < NT:
                    pe.wait_ge(g3_norm, t + 1)
                    if t >= 2:
                        pe.wait_ge(g3T_dve, t - 1)
                        pe.wait_ge(g3T_act, t - 1)
                    for c in range(4):
                        ins = nc.tensor.transpose(bank[4 + 2 * (t % 2) + c // 2][:, (c % 2) * P:(c % 2 + 1) * P], g3n[:, t % 3, c * P:(c + 1) * P], ident)
                    ins.then_inc(g3_turned, 1)
                t = n - 3
                if 0 <= t < NT:
                    pe.wait_ge(g3T_dve, t + 1)
                    pe.wait_ge(g3T_act, t + 1)
                    if t >= 2:
                        pe.wait_ge(x4_added, t - 1)
                    for c in range(4):
                        ins = nc.tensor.matmul(bank[t % 2][:, 0:P], g3T[:, t % 3, c * P:(c + 1) * P], V["wpT"][:, c * P:(c + 1) * P],
                                               start=(c == 0), stop=(c == 3))
                    ins.then_inc(y4_mm, 1)

        def act_l3f(act):
            for n in range(NT + 3):
                if n < NT:
                    if n % TB == 0:
                        act_turned(act, 8, which=[n // TB])
                    act.wait_ge(h3_mm, n + 1)
                    if n >= 3:
                        act.wait_ge(g3_norm, n - 2)
                    nc.scalar.activation(g3[:, n % 3, :], bank[2 + n % 2][:], ACT.Gelu).then_inc(g3_ready, 1)
                t = n - 2
                if 0 <= t < NT:
                    act.wait_ge(g3_turned, t + 1)
                    if t >= 3:
                        act.wait_ge(y4_mm, t - 2)
                    for c in range(2):
                        ins = nc.scalar.activation(g3T[:, t % 3, c * P:(c + 1) * P], bank[4 + 2 * (t % 2)][:, c * P:(c + 1) * P], ACT.Identity,
                                                   scale=V["ln3w"][:, c:c + 1], bias=V["ln3b"][:, c:c + 1])
                    ins.then_inc(g3T_act, 1)

        def pool_l3f(pool, st):
            for t in range(NT):
                pool.wait_ge(mv3_ready, t + 1)
                st.link(nc.gpsimd.tensor_scalar(rd3[:, t:t + 1], mv3[:, t, 1:2], 1e-5, None, ALU.add))
                nc.gpsimd.tensor_tensor(rd3[:, t:t + 1], rd3[:, t:t + 1], V["half"][:, 0:1], ALU.pow).then_inc(rd3_ready, 1)

        def vec_l3f(dve, st):
            Vv = nc.vector
            for n in range(NT + 4):
                if n < NT:
                    dve.wait_ge(g3_ready, n + 1)
                    st.link(Vv.bn_stats(st3[:, n, :], g3[:, n % 3, :]))
                    Vv.bn_aggr(mv3[:, n, :], st3[:, n, :]).then_inc(mv3_ready, 1)
                t = n - 1
                if 0 <= t < NT:
                    dve.wait_ge(rd3_ready, t + 1)
                    if t >= 3:
                        dve.wait_ge(g3_turned, t - 2)
                    Vv.tensor_scalar(g3n[:, t % 3, :], g3[:, t % 3, :], mv3[:, t, 0:1], rd3[:, t:t + 1], ALU.subtract, ALU.mult).then_inc(g3_norm, 1)
                t = n - 2
                if 0 <= t < NT:
                    dve.wait_ge(g3_turned, t + 1)
                    if t >= 3:
                        dve.wait_ge(y4_mm, t - 2)
                    for c in range(2, 4):
                        ins = Vv.tensor_scalar(g3T[:, t % 3, c * P:(c + 1) * P], bank[5 + 2 * (t % 2)][:, (c - 2) * P:(c - 1) * P],
                                               V["ln3w"][:, c:c + 1], V["ln3b"][:, c:c + 1], ALU.mult, ALU.add)
                    ins.then_inc(g3T_dve, 1)
                t = n - 3
                if 0 <= t < NT:
                    dve.wait_ge(y4_mm, t + 1)
                    Vv.tensor_tensor(X[:, t, :], bank[t % 2][:, 0:P], X[:, t, :], ALU.add).then_inc(x4_added, 1)

        block = ctx.enter_context(nc.Block())

        @block.sync
        def _(sp):
            sync_loads(sp)
            sync_fold3(sp)
            sp.wait_ge(final_stage_done, 1)
            sp.dma_start(out.rearrange("b (q p) d -> p (b q) d", p=P), X[:]).then_inc(stored, 16)
            sp.wait_ge(stored, 16)

        @block.tensor
        def _(pe):
            pe_dt(pe)
            pe_ctx0(pe)
            pe_turn(pe, ln_done, NT * 0, xn)
            pe_scores0(pe)
            pe_vfilm(pe)
            pe_fold1(pe)
            pe_c2(pe)
            pe_weights3(pe)
            pe_film(pe)
            pe_dft_x(pe, range(3))
            pe_c2_keys(pe)
            pe_kernel(pe)
            pe_dft_x(pe, [3])
            pe_kernel_turn(pe)
            pe_dft_k(pe)
            pe_dft_back(pe)
            pe_turn(pe, ln_done, NT * 1, tmp2)
            pe_ffn0(pe)
            pe_turn(pe, ln_done, NT * 3, xn)
            pe_route(pe)
            pe_qkv0(pe)
            pe_attend0(pe)
            pe_l1x(pe)
            pe_turn(pe, ln_done, NT * 5, xn)
            pe_l1f(pe)
            pe_turn(pe, ln_done, NT * 7, tmp2)
            pe_qkv2(pe)
            pe_attend2(pe)
            pe_turn(pe, ln_done, NT * 8, xn)
            pe_moe(pe)
            pe_attend3(pe)
            pe_l3f(pe)

        @block.scalar
        def _(act):
            st = Steps(act, act_step)
            act_ctx0(act)
            act_turned(act, 0)
            act_vfilm(act)
            act_fold1(act)
            act_c2(act)
            act_s4_rows(act)
            act_film(act, st)
            act_s4_cols(act)
            act_c2_keys(act)
            act_kernel(act)
            act_dft(act)
            act_turned(act, 1, V["g_ffn"], V["b_ffn"])
            act_ffn0(act)
            act_turned(act, 2)
            act_route(act)
            act_qk0(act)
            act_attend0(act)
            act_l1x(act)
            act_turned(act, 4)
            act_l1f(act)
            act_turned(act, 5, V["lnl_g"], V["lnl_b"])
            act_qkv2(act)
            act_attend2(act)
            act_turned(act, 6)
            act_moe(act)
            act_attend3(act)
            act_l3f(act)

        @block.gpsimd
        def _(pool):
            st = Steps(pool, pool_step)
            pool_dt(pool)
            pool_rstd(pool, st, 0)
            pool_masks(pool, st)
            pool_c2_rstd(pool, st)
            pool_rstd_twice(pool, st, 0, False)
            pool_s4(pool, st)
            pool_s4_decay(pool)
            pool_s4_scale(pool)
            pool_c2_inv(pool, st)
            pool_s4_gains(pool, st)
            pool.wait_ge(*loaded["rows"])
            pool_add_row(pool, V["b_out"], NT)
            pool_ternary3(pool, st)
            pool_rstd(pool, st, 1)
            pool_rstd(pool, st, 2)
            pool_rstd(pool, st, 3)
            pool_bias(pool, 3, V["bo0"], bias_added)
            pool_rstd(pool, st, 4)
            pool_l1x(pool, st)
            pool_rstd(pool, st, 5)
            pool_add_row(pool, V["bet1"], NT * 6)
            pool_rstd(pool, st, 6)
            pool_rstd(pool, st, 7)
            pool_rstd_twice(pool, st, 7, True)
            pool_bias(pool, 7, V["bo2"], bias_added)
            pool_qkv2(pool, st)
            pool_rstd(pool, st, 8)
            pool_rstd(pool, st, 9)
            pool_bias(pool, 9, V["bo3"], bias_added)
            pool_rstd(pool, st, 10)
            pool_l3f(pool, st)

        @block.vector
        def _(dve):
            st = Steps(dve, dve_step)
            vec_dt(dve)
            dve.wait_ge(x_loaded, 16)
            vec_moments(st, X)
            vec_dt_row(dve)
            vec_normalise(dve, 0, X, xn)
            vec_c2_moments(dve, st)
            vec_weights3(dve)
            vec_sigs(dve, st)
            vec_c2_norm(dve, st)
            vec_scores0(dve, st)
            vec_shift0(dve)
            vec_s4_inverses(dve, st)
            vec_probs0(dve, st)
            vec_c2_squares(dve, st)
            vec_affine_in(dve, st)
            vec_s4(dve, st)
            vec_film(dve, st)
            vec_s4_quarter(st)
            vec_c2_scale(dve)
            vec_gamma3(dve, st)
            vec_s4_products(dve, st)
            vec_spectrum(dve, st)
            vec_xt(dve, st)
            vec_normalise(dve, 1, xt, tmp2)
            vec_ffn0(dve, st)
            vec_normalise(dve, 3, X, xn)
            vec_route(dve, st)
            vec_v0(dve)
            vec_attend0(dve, st)
            dve.wait_ge(x_added, NT)
            vec_moments(st, X, [1])
            vec_normalise(dve, 4, X, xn, [1])
            vec_l1x(dve, st)
            vec_moments(st, X)
            vec_normalise(dve, 5, X, xn)
            vec_l1f(dve, st)
            for b in range(NB):
                vec_normalise_add(dve, 2, xt, V["gam1"], [b])
                dve.wait_ge(x_final, NB + b + 1)
                vec_moments(st, X, [b])
            vec_latents(dve)
            vec_qkv2(dve, st)
            vec_attend2(dve, st)
            dve.wait_ge(x2_added, NT)
            vec_moments(st, X, [1])
            vec_normalise(dve, 8, X, xn)
            vec_moe(dve, st)
            vec_normalise(dve, 9, X, xn, [0])
            dve.wait_ge(moe_added, 2 * NX)
            vec_moments(st, X, [1])
            vec_normalise(dve, 9, X, xn, [1])
            vec_attend3(dve, st)
            dve.wait_ge(x3_added, NT)
            vec_moments(st, X, [1])
            vec_normalise(dve, 10, X, xn, [1])
            vec_l3f(dve, st)
            dve.wait_ge(x4_added, NT)
            nc.vector.engine_nop().then_inc(final_stage_done, 1)


def _packed(I):
    f = np.float32

    def pad(a):
        a = np.asarray(a, f)
        o = np.zeros((P, a.shape[1]), f)
        o[:a.shape[0]] = a
        return o

    def chunks(a):
        return a.reshape(-1, P, a.shape[1]).transpose(1, 0, 2).reshape(P, -1)

    ang = 2.0 * np.pi * (np.outer(np.arange(S), np.arange(S)) % (2 * S)) / (2 * S)
    it = {
        "ctxT": I["ctx_768"].reshape(NB * NC, DC).T, "wk0": I["L0_xattn_Wk"], "wv0": I["L0_xattn_Wv"],
        "wqT0": I["L0_xattn_Wq"].T, "wfilm": np.concatenate([I["L0_xattn_W_film_in"], I["L0_xattn_W_film_out"]], 1),
        "ident": np.eye(P, dtype=f), "avg": np.full((P, P), 1.0 / P),
        "ctxr": I["ctx_768"].transpose(1, 0, 2).reshape(NC, -1),
        "g_in": I["L0_xattn_g_norm_in"], "b_in": I["L0_xattn_b_norm_in"], "dskip": I["L0_xattn_D_skip"],
        "b2": I["L0_xattn_b2"], "g_out": I["L0_xattn_g_norm_out"], "b_out": I["L0_xattn_b_norm_out"],
        "logdt": I["L0_xattn_log_dt"][:, None], "br": I["L0_ffn_br"], "bo0": I["L0_ffn_bo"], "knots": I["L1_ffn_knot_values"],
        "temp": I["L1_ffn_temperature"], "oscale": I["L1_ffn_output_scale"], "cb2": I["L1_ffn_compress_b2"],
        "gam1": I["L1_ffn_norm_gamma"], "bet1": I["L1_ffn_norm_beta"], "lnx_g": I["L2_xattn_ln_x_g"],
        "lnx_b": I["L2_xattn_ln_x_b"], "bo2": I["L2_xattn_bo"], "ebias": I["L2_ffn_expert_bias"],
        "bo3": I["L3_xattn_bo"], "gate": I["L0_xattn_mod_gate"].reshape(1), "iotaa": np.arange(LA), "rev8": 8 - np.arange(8),
        "iota8": np.arange(8), "iota16": np.arange(HF), "rev16": HF - np.arange(HF),
        "g_ffn": I["L0_xattn_g_ffn"][:, None], "b_ffn": I["L0_xattn_b_ffn"][:, None],
        "b1": I["L0_xattn_b1"].reshape(4, P).T,
        "wf": np.where(np.arange(S) == 0, 1.0, 2.0).reshape(4, P).T / (2 * S),
        "alt": (1.0 - 2.0 * (np.arange(P) % 2))[:, None], "quarter": np.repeat([0.25, 0.0], P // 2)[:, None],
        "off2": np.repeat([0.0, 0.25], P // 2)[:, None], "qturn": TURN * np.repeat([0.25, 0.0], P // 2)[:, None], "oturn": TURN * np.repeat([0.0, 0.25], P // 2)[:, None],
        "sgn": np.repeat([1.0, -1.0], P // 2)[:, None],
        "cb1": I["L1_ffn_compress_b1"][:, None],
        "lnl_g": I["L2_xattn_ln_l_g"][:, None], "lnl_b": I["L2_xattn_ln_l_b"][:, None],
        "qn": np.tile(I["L2_xattn_qn_g"], H2)[:, None], "kn": np.tile(I["L2_xattn_kn_g"], H2)[:, None],
        "ln3w": I["L3_ffn_ln_w"].reshape(4, P).T, "ln3b": I["L3_ffn_ln_b"].reshape(4, P).T,
        "bq2": np.tile(I["L0_ffn_bq"].reshape(HF, DF).T, (2, 1)), "bk2": np.tile(I["L0_ffn_bk"].reshape(HF, DF).T, (2, 1)),
        "eps": np.full((P, 1), 1e-5), "half": np.full((P, 4 * NT), -0.5), "br_col": I["L0_ffn_br"][:, None],
        "euler": np.full((P, 1), np.e),
        "cos": chunks(np.cos(ang)), "sin": chunks(np.sin(ang)),
        "are": np.tile(I["L0_xattn_A_re"].T, (2, 1)), "aim": np.tile(I["L0_xattn_A_im"].T, (2, 1)),
        "cre": np.tile(I["L0_xattn_C_re"].T, (2, 1)), "cim": np.tile(I["L0_xattn_C_im"].T, (2, 1)),
        "w1": I["L0_xattn_W1"], "w2": chunks(I["L0_xattn_W2"]),
        "wqkv": np.stack([I["L0_ffn_Wq"].reshape(D, HF, DF), I["L0_ffn_Wk"].reshape(D, HF, DF),
                          I["L0_ffn_Wv"].reshape(D, HF, DF),
                          np.broadcast_to(I["L0_ffn_bv"].reshape(1, HF, DF), (D, HF, DF))], 2).reshape(D, -1),
        "wr": I["L0_ffn_Wr"], "wo0": chunks(I["L0_ffn_Wo"]),
        "wq1": I["L1_xattn_Wq"], "wk1": I["L1_xattn_Wk"], "wv1": I["L1_xattn_Wv"], "wo1T": I["L1_xattn_Wo"].T,
        "sigT": I["L1_ffn_signatures_raw"].T, "cw1": I["L1_ffn_compress_w1"], "cw2": I["L1_ffn_compress_w2"],
        "tab": np.concatenate([I["L1_ffn_spline_w1"].reshape(NTL, -1), I["L1_ffn_spline_b1"],
                               I["L1_ffn_spline_w2"].reshape(NTL, -1), I["L1_ffn_spline_b2"], I["L1_ffn_directions"]], 1),
        "wq2T": I["L2_xattn_Wq"].T, "wlkvT": I["L2_xattn_Wlkv"].T, "wkvT": I["L2_xattn_Wkv"].T, "wo2T": I["L2_xattn_Wo"].T.reshape(H2, D2, D).transpose(1, 0, 2).reshape(D2, -1),
        "router": I["L2_ffn_router_w"].T,
        "wqT3": chunks(I["L3_xattn_Wq"].T), "wk3": I["L3_xattn_Wk"], "wv3": I["L3_xattn_Wv"], "wo3": chunks(I["L3_xattn_Wo"]),
        "wfcT": I["L3_ffn_W_fc"].T, "wpT": chunks(I["L3_ffn_W_proj"].T),
    }
    w1 = np.concatenate([I["L2_ffn_w1"], I["L2_ffn_sw1"]])
    w3 = np.concatenate([I["L2_ffn_w3"], I["L2_ffn_sw3"]])
    w2 = np.concatenate([I["L2_ffn_w2"], I["L2_ffn_sw2"]])
    it["moe"] = np.concatenate([np.concatenate([w1[e].T, w3[e].T, chunks(w2[e].T)], 1) for e in range(NE + NSH)], 1)
    res = {}
    for k, items in PACKS.items():
        if k == "rows":
            res[k] = np.concatenate([np.asarray(it[n], f).reshape(-1) for n, _ in items])[None]
        else:
            res[k] = np.concatenate([pad(it[n]) for n, _ in items], 1)
        assert res[k].shape[1] == WIDTH[k], k
    res["x"] = I["x"].reshape(TOK, D)
    res["masks"] = np.stack([I["mask_BxS2_bf1"], I["mask_BxS2_bk0"]])
    res["tmask"] = np.ascontiguousarray(I["mask_BxS_bf1"].reshape(NT, P).T)
    res["bfilm"] = np.concatenate([I["L0_xattn_b_film_in"], I["L0_xattn_b_film_out"]])[None]
    res["altrow"] = (1.0 - 2.0 * (np.arange(S) % 2)).astype(f)[None]
    return {k: np.ascontiguousarray(v) for k, v in res.items()}


def kernel(**inputs):
    import concourse.bacc as bacc
    from concourse.bass_utils import run_bass_kernel_spmd

    arrays = _packed({k: np.asarray(v) for k, v in inputs.items()})
    nc = bacc.Bacc("TRN2", target_bir_lowering=False, num_devices=1)
    A = {}
    for name, a in arrays.items():
        A[name] = nc.dram_tensor(f"in_{name}_dram", a.shape, mybir.dt.from_np(a.dtype), kind="ExternalInput").ap()
    A["vw_scratch"] = nc.dram_tensor("vw_scratch", (NB, HK3, D), F32, kind="Internal").ap()
    out = nc.dram_tensor("out_0_dram", (NB, S, D), F32, kind="ExternalOutput").ap()
    program(nc, A, out)
    r = run_bass_kernel_spmd(nc, [{f"in_{k}_dram": v for k, v in arrays.items()}], core_ids=[0])
    return r.results[0]["out_0_dram"]
```
